# Optimizing a Trainium2 kernel written in Bass

```python
import numpy as np
import jax
import jax.numpy as jnp

def _softmax(x, axis=-1):
    return jax.nn.softmax(x, axis=axis)

def _gelu(x):
    return jax.nn.gelu(x, approximate=True)

def _silu(x):
    return jax.nn.silu(x)

def _sigmoid(x):
    return jax.nn.sigmoid(x)

def _layernorm(x, axis=-1, eps=1e-05):
    m = jnp.mean(x, axis=axis, keepdims=True)
    v = jnp.var(x, axis=axis, keepdims=True)
    return (x - m) / jnp.sqrt(v + eps)

def _scatter_add(tgt, idx, src, axis=0):
    return tgt.at[idx].add(src)

def _segment_sum(src, seg, n):
    return jax.ops.segment_sum(src, seg, n)
kernel_name = 'mk_gnn_resnorm_d4_gnn_r32_96f92c'

def setup_inputs(seed: int=0):
    np.random.seed(seed)
    _w = jnp.asarray

    def _rec_inputs():
        import jax
        import jax.numpy as jnp
        _gk = jax.random.key(seed)
        x = -0.000202 + 1 * jax.random.normal(jax.random.fold_in(_gk, 1), (50000, 128), jnp.float32)
        src = jax.random.randint(jax.random.fold_in(_gk, 2), (25000,), 0, 50000, jnp.int32)
        dst = jnp.minimum((50000 * jax.random.uniform(jax.random.fold_in(_gk, 3), (25000,)) ** 2.0).astype(jnp.int32), 49999)
        _o = jnp.argsort(dst, stable=True)
        src = src[_o]
        dst = dst[_o]
        edge_attr_128 = -5.16925e-05 + 1.00005 * jax.random.normal(jax.random.fold_in(_gk, 12), (25000, 128), jnp.float32)
        return (x, src, dst, edge_attr_128)
    x, src, dst, edge_attr_128 = _rec_inputs()

    def _L0_gnn_setup():
        import jax, jax.numpy as jnp
        import numpy as np
        N_NODES = 50000
        N_EDGES = 20000
        D = 128
        BN_EPS = 1e-05
        key = jax.random.key(seed)
        k1, k2, k3 = jax.random.split(key, 3)
        x = jax.random.normal(k1, (N_NODES, D), dtype=jnp.float32)
        W = jax.random.normal(k2, (D, D), dtype=jnp.float32) * (1.0 / np.sqrt(D))
        b = jnp.zeros((D,), dtype=jnp.float32)
        gamma = jnp.ones((D,), dtype=jnp.float32)
        beta = jnp.zeros((D,), dtype=jnp.float32)
        edge_index = jax.random.randint(k3, (2, N_EDGES), 0, N_NODES, dtype=jnp.int64)
        return {'x': x, 'W': W, 'b': b, 'gamma': gamma, 'beta': beta, 'edge_index': edge_index}
    _L0_gnn_all = _L0_gnn_setup()
    _L0_gnn_in = {k: v for k, v in _L0_gnn_all.items() if k in ('W', 'b', 'gamma', 'beta')}
    del _L0_gnn_all

    def _L1_gnn_setup():
        import jax, jax.numpy as jnp
        import numpy as np
        N_NODES = 50000
        N_EDGES = 25000
        IN_FEATS = 128
        OUT_FEATS = 128
        K = 8
        ITERATIONS = 4
        TAU = 1.0
        key = jax.random.key(seed)
        k1, k2, k3 = jax.random.split(key, 3)
        x = jax.random.normal(k1, (N_NODES, IN_FEATS), dtype=jnp.float32)
        edge_index = jax.random.randint(k2, (2, N_EDGES), 0, N_NODES, dtype=jnp.int64)
        std = 1.414 * np.sqrt(2.0 / (IN_FEATS + OUT_FEATS))
        weight = jax.random.normal(k3, (IN_FEATS, OUT_FEATS), dtype=jnp.float32) * std
        bias = jnp.zeros((OUT_FEATS,), dtype=jnp.float32)
        return {'x': x, 'edge_index': edge_index, 'weight': weight, 'bias': bias}
    _L1_gnn_all = _L1_gnn_setup()
    _L1_gnn_in = {k: v for k, v in _L1_gnn_all.items() if k in ('weight', 'bias')}
    del _L1_gnn_all

    def _L2_gnn_setup():
        import jax, jax.numpy as jnp
        import numpy as np
        N, E, H, NH, HD = (50000, 25000, 128, 8, 16)

        def _layernorm(x, g, b, eps=1e-05):
            mu = jnp.mean(x, axis=-1, keepdims=True)
            var = jnp.mean(jnp.square(x - mu), axis=-1, keepdims=True)
            return (x - mu) * jax.lax.rsqrt(var + eps) * g + b
        key = jax.random.key(seed)
        ks = jax.random.split(key, 24)
        w = lambda k, shape, s=0.05: jax.random.normal(k, shape, jnp.float32) * s
        return {'x': jax.random.normal(ks[0], (N, H), jnp.float32), 'edge_index': jax.random.randint(ks[1], (2, E), 0, N, dtype=jnp.int64), 'curv': jax.random.normal(ks[2], (E, H), jnp.float32), 'Wq': w(ks[3], (H, H)), 'bq': jnp.zeros((H,), jnp.float32), 'Wk': w(ks[4], (H, H)), 'bk': jnp.zeros((H,), jnp.float32), 'Wv': w(ks[5], (H, H)), 'bv': jnp.zeros((H,), jnp.float32), 'Wo': w(ks[6], (H, H)), 'bo': jnp.zeros((H,), jnp.float32), 'Wc': w(ks[7], (H, NH)), 'bc': jnp.zeros((NH,), jnp.float32), 'W1': w(ks[8], (H, 4 * H)), 'b1': jnp.zeros((4 * H,), jnp.float32), 'W2': w(ks[9], (4 * H, H)), 'b2': jnp.zeros((H,), jnp.float32), 'g1': jnp.ones((H,), jnp.float32), 'be1': jnp.zeros((H,), jnp.float32), 'g2': jnp.ones((H,), jnp.float32), 'be2': jnp.zeros((H,), jnp.float32)}
    _L2_gnn_all = _L2_gnn_setup()
    _L2_gnn_in = {k: v for k, v in _L2_gnn_all.items() if k in ('Wq', 'bq', 'Wk', 'bk', 'Wv', 'bv', 'Wo', 'bo', 'Wc', 'bc', 'W1', 'b1', 'W2', 'b2', 'g1', 'be1', 'g2', 'be2')}
    del _L2_gnn_all

    def _L3_gnn_setup():
        import jax, jax.numpy as jnp
        import numpy as np
        N_NODES = 3125
        N_EDGES = 50000
        D = 128
        LN_EPS = 1e-05
        key = jax.random.key(seed)
        ks = jax.random.split(key, 6)
        h = jax.random.normal(ks[0], (N_NODES, D), dtype=jnp.float32)
        W = jax.random.normal(ks[1], (D, D), dtype=jnp.float32) * (1.0 / np.sqrt(D))
        b = jax.random.normal(ks[2], (D,), dtype=jnp.float32) * 0.02
        alpha = jnp.zeros((), dtype=jnp.float32)
        gamma = jnp.ones((D,), dtype=jnp.float32)
        beta = jnp.zeros((D,), dtype=jnp.float32)
        src = jax.random.randint(ks[3], (N_EDGES,), 0, N_NODES, dtype=jnp.int32)
        dst = jax.random.randint(ks[4], (N_EDGES,), 0, N_NODES, dtype=jnp.int32)
        return {'h': h, 'W': W, 'b': b, 'alpha': alpha, 'gamma': gamma, 'beta': beta, 'src': src, 'dst': dst}
    _L3_gnn_all = _L3_gnn_setup()
    _L3_gnn_in = {k: v for k, v in _L3_gnn_all.items() if k in ('W', 'b', 'alpha', 'gamma', 'beta')}
    del _L3_gnn_all
    return {'x': x, 'src': src, 'dst': dst, 'edge_attr_128': edge_attr_128, 'L0_gnn_W': _L0_gnn_in['W'], 'L0_gnn_b': _L0_gnn_in['b'], 'L0_gnn_gamma': _L0_gnn_in['gamma'], 'L0_gnn_beta': _L0_gnn_in['beta'], 'L1_gnn_weight': _L1_gnn_in['weight'], 'L1_gnn_bias': _L1_gnn_in['bias'], 'L2_gnn_Wq': _L2_gnn_in['Wq'], 'L2_gnn_bq': _L2_gnn_in['bq'], 'L2_gnn_Wk': _L2_gnn_in['Wk'], 'L2_gnn_bk': _L2_gnn_in['bk'], 'L2_gnn_Wv': _L2_gnn_in['Wv'], 'L2_gnn_bv': _L2_gnn_in['bv'], 'L2_gnn_Wo': _L2_gnn_in['Wo'], 'L2_gnn_bo': _L2_gnn_in['bo'], 'L2_gnn_Wc': _L2_gnn_in['Wc'], 'L2_gnn_bc': _L2_gnn_in['bc'], 'L2_gnn_W1': _L2_gnn_in['W1'], 'L2_gnn_b1': _L2_gnn_in['b1'], 'L2_gnn_W2': _L2_gnn_in['W2'], 'L2_gnn_b2': _L2_gnn_in['b2'], 'L2_gnn_g1': _L2_gnn_in['g1'], 'L2_gnn_be1': _L2_gnn_in['be1'], 'L2_gnn_g2': _L2_gnn_in['g2'], 'L2_gnn_be2': _L2_gnn_in['be2'], 'L3_gnn_W': _L3_gnn_in['W'], 'L3_gnn_b': _L3_gnn_in['b'], 'L3_gnn_alpha': _L3_gnn_in['alpha'], 'L3_gnn_gamma': _L3_gnn_in['gamma'], 'L3_gnn_beta': _L3_gnn_in['beta']}

def reference(x, src, dst, edge_attr_128, L0_gnn_W, L0_gnn_b, L0_gnn_gamma, L0_gnn_beta, L1_gnn_weight, L1_gnn_bias, L2_gnn_Wq, L2_gnn_bq, L2_gnn_Wk, L2_gnn_bk, L2_gnn_Wv, L2_gnn_bv, L2_gnn_Wo, L2_gnn_bo, L2_gnn_Wc, L2_gnn_bc, L2_gnn_W1, L2_gnn_b1, L2_gnn_W2, L2_gnn_b2, L2_gnn_g1, L2_gnn_be1, L2_gnn_g2, L2_gnn_be2, L3_gnn_W, L3_gnn_b, L3_gnn_alpha, L3_gnn_gamma, L3_gnn_beta):
    import jax
    import jax.numpy as jnp

    def _L0_gnn_ref(x, W, b, gamma, beta, edge_index):
        import jax, jax.numpy as jnp
        import numpy as np
        N_NODES = 50000
        N_EDGES = 20000
        D = 128
        BN_EPS = 1e-05
        N = x.shape[0]
        xw = x @ W
        loops = jnp.arange(N, dtype=edge_index.dtype)
        src = jnp.concatenate([edge_index[0], loops])
        dst = jnp.concatenate([edge_index[1], loops])
        ones = jnp.ones(src.shape[0], dtype=x.dtype)
        deg = jax.ops.segment_sum(ones, dst, num_segments=N)
        dinv = jnp.where(deg > 0, jax.lax.rsqrt(deg), 0.0)
        norm = dinv[src] * dinv[dst]
        msg = xw[src] * norm[:, None]
        h = jax.ops.segment_sum(msg, dst, num_segments=N) + b
        mean = jnp.mean(h, axis=0)
        var = jnp.mean(jnp.square(h - mean), axis=0)
        h = (h - mean) * jax.lax.rsqrt(var + BN_EPS) * gamma + beta
        h = jax.nn.relu(h)
        h = x + h
        return h

    def _L1_gnn_ref(x, edge_index, weight, bias):
        import jax, jax.numpy as jnp
        import numpy as np
        N_NODES = 50000
        N_EDGES = 25000
        IN_FEATS = 128
        OUT_FEATS = 128
        K = 8
        ITERATIONS = 4
        TAU = 1.0
        N = x.shape[0]
        d = OUT_FEATS // K
        h = jax.nn.leaky_relu(x @ weight + bias)
        h = h.reshape(N, K, d)
        h_normed = h / jnp.sqrt(jnp.sum(h * h, axis=-1, keepdims=True))
        row = edge_index[0]
        col = edge_index[1]
        h_src = h_normed
        h_dst = h_normed
        for _ in range(ITERATIONS):
            scores = jnp.sum(h_dst[row] * h_src[col], axis=-1) / TAU
            m = jax.ops.segment_max(scores, row, num_segments=N)
            ex = jnp.exp(scores - m[row])
            denom = jax.ops.segment_sum(ex, row, num_segments=N)
            alpha = ex / denom[row]
            agg = jax.ops.segment_sum(h_src[col] * alpha[:, :, None], row, num_segments=N)
            node_attr = agg + h_normed
            h_dst = node_attr / jnp.sqrt(jnp.sum(node_attr * node_attr, axis=-1, keepdims=True))
        return h_dst.reshape(N, -1)

    def _L2_gnn_ref(x, edge_index, curv, Wq, bq, Wk, bk, Wv, bv, Wo, bo, Wc, bc, W1, b1, W2, b2, g1, be1, g2, be2):
        import jax, jax.numpy as jnp
        import numpy as np
        N, E, H, NH, HD = (50000, 25000, 128, 8, 16)

        def _layernorm(x, g, b, eps=1e-05):
            mu = jnp.mean(x, axis=-1, keepdims=True)
            var = jnp.mean(jnp.square(x - mu), axis=-1, keepdims=True)
            return (x - mu) * jax.lax.rsqrt(var + eps) * g + b
        num_nodes = x.shape[0]
        src, tgt = (edge_index[0], edge_index[1])
        x_norm = _layernorm(x, g1, be1)
        q = (x_norm @ Wq + bq).reshape(num_nodes, NH, HD)
        k = (x_norm @ Wk + bk).reshape(num_nodes, NH, HD)
        v = (x_norm @ Wv + bv).reshape(num_nodes, NH, HD)
        scores = jnp.einsum('ehd,ehd->eh', q[src], k[tgt]) / np.sqrt(HD).astype(np.float32)
        scores = scores + (curv @ Wc + bc)
        smax = jax.ops.segment_max(scores, tgt, num_segments=num_nodes)
        p = jnp.exp(scores - smax[tgt])
        ssum = jax.ops.segment_sum(p, tgt, num_segments=num_nodes)
        probs = p / ssum[tgt]
        messages = (probs[:, :, None] * v[tgt]).reshape(scores.shape[0], -1)
        out = jnp.zeros_like(x).at[src].add(messages)
        out = out @ Wo + bo
        x = x + out
        x_norm2 = _layernorm(x, g2, be2)
        ffn_out = jax.nn.relu(x_norm2 @ W1 + b1) @ W2 + b2
        return x + ffn_out

    def _L3_gnn_ref(h, W, b, alpha, gamma, beta, src, dst):
        import jax, jax.numpy as jnp
        import numpy as np
        N_NODES = 3125
        N_EDGES = 50000
        D = 128
        LN_EPS = 1e-05
        N = h.shape[0]
        h_neigh = jax.ops.segment_sum(h[src], dst, num_segments=N)
        deg = jax.ops.segment_sum(jnp.ones_like(dst, dtype=h.dtype), dst, num_segments=N)
        out = (h_neigh + h) / (deg + 1.0)[:, None]
        out = out @ W.T + b
        a = jax.nn.sigmoid(alpha)
        out = out * a + h * (1.0 - a)
        mu = jnp.mean(out, axis=-1, keepdims=True)
        var = jnp.var(out, axis=-1, keepdims=True)
        out = (out - mu) * jax.lax.rsqrt(var + LN_EPS) * gamma + beta
        return out
    edge_index = jnp.stack([src, dst])
    x = _layernorm(x + _L0_gnn_ref(x, L0_gnn_W, L0_gnn_b, L0_gnn_gamma, L0_gnn_beta, edge_index), axis=-1)
    x = _layernorm(x + _L1_gnn_ref(x, edge_index, L1_gnn_weight, L1_gnn_bias), axis=-1)
    x = _layernorm(x + _L2_gnn_ref(x, edge_index, edge_attr_128, L2_gnn_Wq, L2_gnn_bq, L2_gnn_Wk, L2_gnn_bk, L2_gnn_Wv, L2_gnn_bv, L2_gnn_Wo, L2_gnn_bo, L2_gnn_Wc, L2_gnn_bc, L2_gnn_W1, L2_gnn_b1, L2_gnn_W2, L2_gnn_b2, L2_gnn_g1, L2_gnn_be1, L2_gnn_g2, L2_gnn_be2), axis=-1)
    x = _layernorm(x + _L3_gnn_ref(x, L3_gnn_W, L3_gnn_b, L3_gnn_alpha, L3_gnn_gamma, L3_gnn_beta, src, dst), axis=-1)
    return x

_drawn_inputs = setup_inputs


def setup_inputs(seed=0):
    import zlib

    import numpy as np

    out = dict(_drawn_inputs(seed))
    spreads = {'L0_gnn_b': (0.0, 2.0),
     'L0_gnn_gamma': (1.0, 0.2),
     'L0_gnn_beta': (0.0, 0.1),
     'L1_gnn_bias': (0.0, 0.429),
     'L2_gnn_bq': (0.0, 2.0),
     'L2_gnn_bk': (0.0, 2.0),
     'L2_gnn_bv': (0.0, 0.432),
     'L2_gnn_bo': (0.0, 0.1),
     'L2_gnn_bc': (0.0, 2.0),
     'L2_gnn_b1': (0.0, 0.1),
     'L2_gnn_b2': (0.0, 0.1),
     'L2_gnn_g1': (1.0, 0.6),
     'L2_gnn_be1': (0.0, 0.766),
     'L2_gnn_g2': (1.0, 0.2),
     'L2_gnn_be2': (0.0, 0.43),
     'L3_gnn_gamma': (1.0, 0.2),
     'L3_gnn_beta': (0.0, 0.1)}
    factors = {'edge_attr_128': 4.756,
     'L2_gnn_Wq': 7.514,
     'L2_gnn_Wk': 7.525,
     'L2_gnn_Wc': 4.753,
     'L3_gnn_b': 7.677}
    for name, (base, spread) in spreads.items():
        noise = np.random.default_rng([zlib.crc32(name.encode()), seed]).standard_normal(out[name].shape)
        drawn = base * np.exp(spread * noise) if base else spread * noise
        out[name] = jnp.asarray(drawn.astype(out[name].dtype))
    for name, factor in factors.items():
        out[name] = (out[name] * factor).astype(out[name].dtype)
    return out
```

```python
from contextlib import ExitStack

import concourse.bass as bass
from concourse import mybir

F32 = mybir.dt.float32
BF16 = mybir.dt.bfloat16
I32 = mybir.dt.int32
ALU = mybir.AluOpType
ACT = mybir.ActivationFunctionType
AX = mybir.AxisListType

P = 128
D = 128
N = 50000
E = 25000
NH = 8
HD = D // NH
T = 200
EP = T * P
TB = 100
GT = 4
EG = T // GT
NJ = 8
NG = N // (P * NJ)
TAILP = (N - NG * P * NJ) // NJ
NCOL = (NG + 1) * NJ
PAD_ID = N
EPS = 1e-5
BIG = 1.0e30
FAR = 1 << 20


def after(n, k=1):
    return n * k + k


class Ctx:

    def __init__(self, nc, stack):
        self.nc, self.stack = nc, stack
        self.sems = []
        self.dram = {}

    def sb(self, stack, name, shape, dt=F32):
        return stack.enter_context(self.nc.sbuf_tensor(name, shape, dt))

    def ps(self, stack, name, shape, dt=F32):
        return stack.enter_context(self.nc.psum_tensor(name, shape, dt))

    def sem(self, stack, name):
        return stack.enter_context(self.nc.semaphore(name))


def clear_semaphores(nc, sems):
    with nc.Block() as block:
        @block.gpsimd
        def _(pool):
            for s in sems:
                pool.sem_clear(s)


def ids_phase(k):
    nc = k.nc
    with ExitStack() as st:
        rows = k.sb(st, "ids_rows_i", [TB, 2, 2, P], I32)
        rows_f = k.sb(st, "ids_rows_f", [TB, 2, 2, P])
        low = k.sb(st, "ids_low_i", [TB, 2, 2, P], I32)
        low_f = k.sb(st, "ids_low_f", [TB, 2, 2, P])
        cols_i = k.sb(st, "ids_cols_i", [P, 2, T], I32)
        part = k.sb(st, "ids_part_i", [P, 2, 2, T], I32)
        minus = k.sb(st, "ids_minus", [1, 1])
        pt = k.ps(st, "ids_pt", [P, 2, 2, 256])
        padded = k.sem(st, "ids_padded")
        loaded = k.sem(st, "ids_loaded")
        step = k.sem(st, "ids_step")
        turned = k.sem(st, "ids_turned")
        stored = k.sem(st, "ids_stored")
        with nc.Block() as block:
            @block.sync
            def _(sp):
                sp.wait_ge(padded, 1)
                full = (E // P - TB)
                for a, ids in enumerate((k.src, k.dst)):
                    sp.dma_start(rows[:, a, 0, :], ids[0:TB * P].rearrange("(r e) -> r e", e=P)).then_inc(loaded, 16)
                    sp.dma_start(rows[0:full, a, 1, :],
                                 ids[TB * P:(TB + full) * P].rearrange("(r e) -> r e", e=P)).then_inc(loaded, 16)
                    sp.dma_start(rows[full:full + 1, a, 1, 0:E - (TB + full) * P],
                                 ids[(TB + full) * P:E].rearrange("(r e) -> r e", r=1)).then_inc(loaded, 16)
                sp.wait_ge(step, 3)
                for a, row in enumerate((k.src_row, k.dst_row)):
                    sp.dma_start(row[0:EP].rearrange("(b r e) -> r b e", b=2, e=P), rows_f[:, a]).then_inc(stored, 16)
                sp.dma_start(k.low_row[0:EP].rearrange("(b r e) -> r b e", b=2, e=P), low_f[:, 0]).then_inc(stored, 16)
                sp.dma_start(k.dst_row[EP:EP + 1].rearrange("(r e) -> r e", r=1), minus[:, :]).then_inc(stored, 16)
                sp.wait_ge(stored, 64)

            @block.vector
            def _(dve):
                nc.vector.memset(minus[:, :], -1.0)
                nc.vector.memset(rows[:, :, :, :], PAD_ID).then_inc(padded, 1)
                dve.wait_ge(loaded, 96)
                nc.vector.tensor_copy(rows_f[:, :, :, :], rows[:, :, :, :]).then_inc(step, 1)
                nc.vector.tensor_scalar(low[:, :, :, :], rows[:, :, :, :], 3, 127, ALU.arith_shift_right,
                                        ALU.bitwise_and).then_inc(step, 1)
                dve.wait_ge(step, 2)
                nc.vector.tensor_copy(low_f[:, :, :, :], low[:, :, :, :]).then_inc(step, 1)
                dve.wait_ge(turned, 1)
                nc.vector.tensor_copy(k.id_col[:, 0, :, :], pt[:, :, 0, 0:T]).then_inc(step, 1)
                nc.vector.tensor_copy(cols_i[:, :, :], pt[:, :, 0, 0:T]).then_inc(step, 1)
                nc.vector.tensor_copy(k.low_col[:, :, :], pt[:, :, 1, 0:T]).then_inc(step, 1)
                dve.wait_ge(step, 5)
                nc.vector.tensor_scalar(part[:, 0, :, :], cols_i[:, :, :], 10, 3, ALU.arith_shift_right,
                                        ALU.arith_shift_left).then_inc(step, 1)
                nc.vector.tensor_scalar(part[:, 1, :, :], cols_i[:, :, :], 7, None, ALU.bitwise_and).then_inc(step, 1)
                nc.vector.tensor_scalar(k.node_idx[:, :, :], k.id_col[:, 0, :, :], float(N - 1), None, ALU.min)
                dve.wait_ge(step, 8)
                nc.vector.tensor_tensor(k.high_col[:, :, :], part[:, 0, :, :], part[:, 1, :, :],
                                        ALU.add).then_inc(step, 1)
                dve.wait_ge(step, 9)

            @block.tensor
            def _(pe):
                pe.wait_ge(step, 3)
                for a in range(2):
                    for b in range(2):
                        nc.tensor.transpose(pt[:, a, 0, b * TB:(b + 1) * TB], rows_f[:, a, b, :], k.ident[0:TB, 0:TB])
                        last = nc.tensor.transpose(pt[:, a, 1, b * TB:(b + 1) * TB], low_f[:, a, b, :],
                                                   k.ident[0:TB, 0:TB])
                last.then_inc(turned, 1)
        k.done = [padded, loaded, step, turned, stored]
        clear_semaphores(nc, k.done)


def constants_phase(k):
    nc = k.nc
    with ExitStack() as st:
        it = k.sb(st, "cst_iota", [P, P], I32)
        ih = k.sb(st, "cst_iota_high", [P, NCOL], I32)
        ip = k.sb(st, "cst_iota_part", [P, 1], I32)
        made = k.sem(st, "cst_made")
        step = k.sem(st, "cst_step")
        with nc.Block() as block:
            @block.gpsimd
            def _(pool):
                nc.gpsimd.iota(it[:, :], pattern=[[1, P]], base=0, channel_multiplier=0).then_inc(made, 1)
                nc.gpsimd.iota(ih[:, :], pattern=[[1, NCOL]], base=0, channel_multiplier=0).then_inc(made, 1)
                nc.gpsimd.iota(ip[:, :], pattern=[[0, 1]], base=0, channel_multiplier=1).then_inc(made, 1)

            @block.vector
            def _(dve):
                nc.vector.memset(k.ones[:, :], 1.0).then_inc(step, 1)
                nc.vector.memset(k.zeros[:, :], 0.0).then_inc(step, 1)
                nc.vector.memset(k.eps[:, :], EPS).then_inc(step, 1)
                dve.wait_ge(made, 3)
                nc.vector.tensor_copy(k.iota_row[:, :], it[:, :]).then_inc(step, 1)
                nc.vector.tensor_copy(k.iota_high[:, :], ih[:, :]).then_inc(step, 1)
                nc.vector.tensor_copy(k.iota_part[:, :], ip[:, :]).then_inc(step, 1)
                dve.wait_ge(step, 6)
                nc.vector.tensor_scalar(k.ident[:, :], k.iota_row[:, :], k.iota_part[:, 0:1], None,
                                        ALU.is_equal).then_inc(step, 1)
                nc.vector.tensor_scalar(k.before[:, :], k.iota_row[:, :], k.iota_part[:, 0:1], None,
                                        ALU.is_gt).then_inc(step, 1)
                nc.vector.tensor_scalar(k.earlier[:, :], k.iota_row[:, :], k.iota_part[:, 0:1], None,
                                        ALU.is_lt).then_inc(step, 1)
                nc.vector.tensor_scalar(k.last_part[:, :], k.iota_part[:, :], float(P - 1), None,
                                        ALU.is_equal).then_inc(step, 1)
                dve.wait_ge(step, 10)
        clear_semaphores(nc, [made, step])


def count_phase(k):
    nc = k.nc
    with ExitStack() as st:
        hot_low = k.sb(st, "cnt_hot_low", [P, 2, 2, P], BF16)
        hot_high = k.sb(st, "cnt_hot_high", [P, 2, 2, NCOL], BF16)
        scan = k.sb(st, "cnt_scan", [P, NCOL])
        count = k.sb(st, "cnt_count", [P, NCOL])
        root = k.sb(st, "cnt_root", [P, NCOL])
        one_col = k.sb(st, "cnt_one", [P, NCOL])
        table = [k.ps(st, f"cnt_table{a}", [P, 512]) for a in range(2)]
        base = k.ps(st, "cnt_base", [P, 512])
        hot = k.sem(st, "cnt_hot")
        used = k.sem(st, "cnt_used")
        step = k.sem(st, "cnt_step")
        based = k.sem(st, "cnt_based")
        rooted = k.sem(st, "cnt_rooted")
        with nc.Block() as block:
            @block.vector
            def _(dve):
                with dve.Fori(0, T // 2) as i:
                    for u in range(2):
                        n = i * 2 + u
                        dve.wait_ge(used, after(n))
                        for a in range(2):
                            nc.vector.tensor_scalar(hot_low[:, u, a, :], k.iota_row[:, :],
                                                    k.low_col[:, a, bass.ds(n, 1)], None, ALU.is_equal)
                            nc.vector.tensor_scalar(hot_high[:, u, a, :], k.iota_high[:, :],
                                                    k.high_col[:, a, bass.ds(n, 1)], None,
                                                    ALU.is_equal).then_inc(hot, 1)
                nc.vector.memset(one_col[:, :], 1.0).then_inc(step, 1)
                dve.wait_ge(used, T + 2)
                nc.vector.tensor_copy(count[:, :], table[0][:, 0:NCOL]).then_inc(step, 1)
                nc.vector.tensor_scalar(k.degree[:, :], table[1][:, 0:NCOL], 1.0, None, ALU.add).then_inc(step, 1)
                dve.wait_ge(step, 3)
                nc.vector.tensor_tensor_scan(scan[:, :], one_col[:, :], count[:, :], 0.0, ALU.mult,
                                             ALU.add).then_inc(step, 1)
                dve.wait_ge(rooted, 1)
                nc.vector.reciprocal(k.dinv[:, :], root[:, :]).then_inc(step, 1)
                nc.vector.reciprocal(k.dinv2[:, :], k.degree[:, :]).then_inc(step, 1)
                dve.wait_ge(step, 6)
                dve.wait_ge(based, 1)
                nc.vector.tensor_tensor(scan[:, :], scan[:, :], count[:, :], ALU.subtract).then_inc(step, 1)
                dve.wait_ge(step, 7)
                nc.vector.tensor_scalar(k.start[:, :], scan[:, :], base[:, 0:1], None, ALU.add).then_inc(step, 1)
                dve.wait_ge(step, 8)

            @block.scalar
            def _(act):
                act.wait_ge(step, 3)
                nc.scalar.activation(root[:, :], k.degree[:, :], ACT.Sqrt).then_inc(rooted, 1)

            @block.tensor
            def _(pe):
                for a in range(2):
                    nc.tensor.matmul(table[a][:, 0:NCOL], k.zeros[:, 0:P], k.zeros[:, 0:NCOL], start=True, stop=False,
                                     skip_group_check=True)
                pe.sem_inc(used, 2)
                with pe.Fori(0, T // 2) as i:
                    for u in range(2):
                        n = i * 2 + u
                        pe.wait_ge(hot, after(n, 2))
                        for a in range(2):
                            mm = nc.tensor.matmul(table[a][:, 0:NCOL], hot_low[:, u, a, :], hot_high[:, u, a, :],
                                                  start=False, stop=False, skip_group_check=True)
                        mm.then_inc(used, 1)
                pe.wait_ge(step, 4)
                nc.tensor.matmul(base[:, 0:1], k.before[:, :], scan[:, NCOL - 1:NCOL], start=True,
                                 stop=True).then_inc(based, 1)
        clear_semaphores(nc, [hot, used, step, based, rooted])


def paced(eng, k, sem, value):
    eng.wait_ge(sem, value)
    eng.sem_inc(k.paces, 1)


def rank_phase(k):
    nc = k.nc
    with ExitStack() as st:
        row_b = k.sb(st, "rank_row_b", [P, 2, 2, GT * P])
        hot_low = k.sb(st, "rank_hot_low", [P, 2, P], BF16)
        hot_high = k.sb(st, "rank_hot_high", [P, 2, NCOL], BF16)
        low_hot = k.sb(st, "rank_low_hot", [P, 2, P])
        twin = k.sb(st, "rank_twin", [P, 2, P])
        table_sb = k.sb(st, "rank_table_sb", [P, 2, NCOL])
        picked = k.sb(st, "rank_picked", [P, 2, NCOL])
        parts = k.sb(st, "rank_parts", [P, 2, 2])
        ids_s = k.sb(st, "rank_ids_s", [P, 2 * GT])
        dinv_s = k.sb(st, "rank_dinv_s", [P, 2 * GT])
        eid = k.sb(st, "rank_eid", [P, T], I32)
        load4 = k.sb(st, "rank_payload", [P, T, 4], I32)
        rank = k.sb(st, "rank_rank", [P, 2 * GT], I32)
        load_s = k.sb(st, "rank_payload_slot", [P, 2 * GT, 4], I32)
        table = k.ps(st, "rank_table", [P, 512])
        look = [k.ps(st, f"rank_look{b}", [P, 2, 512]) for b in range(2)]
        names = ["numbered", "filled", "row_ready0", "row_ready1", "row_free", "hot", "marked", "copied", "added",
                 "looked", "look_free", "ids", "twins", "picks", "ranked", "slot_free0", "slot_free1"]
        s = {x: k.sem(st, "rank_" + x) for x in names}
        out0 = k.scatter_count
        k.scatter_count += (EG // 2) * 16 * GT
        sems = list(s.values())
        s.update(sent0=k.scattered[0], sent1=k.scattered[1])
        with nc.Block() as block:
            @block.sync
            def _(sp):
                with sp.Fori(0, EG // 2) as i:
                    for u in range(2):
                        g = i * 2 + u
                        sp.wait_ge(s["row_free"], after(g))
                        for a, row in enumerate((k.low_row, k.src_row)):
                            sp.dma_start(row_b[:, u, a, :],
                                         row[bass.ds(g * (GT * P), GT * P)].partition_broadcast(P))\
                              .then_inc(s[f"row_ready{u}"], 16)

            @block.gpsimd
            def _(pool):
                nc.gpsimd.iota(eid[:, :], pattern=[[P, T]], base=0, channel_multiplier=1).then_inc(s["numbered"], 1)
                with pool.Fori(0, EG // 2) as i:
                    for u in range(2):
                        paced(pool, k, s["ranked"], after(i * 2 + u, GT))
                        for j in range(GT):
                            q = u * GT + j
                            nc.gpsimd.indirect_dma_start(
                                out=k.sorted4[:, :], out_offset=bass.IndirectOffsetOnAxis(ap=rank[:, q:q + 1], axis=0),
                                in_=load_s[:, q, :], in_offset=None).then_inc(s[f"sent{u}"], 16)
                    for u in range(2):
                        pool.wait_ge(s[f"sent{u}"], i * (16 * GT) + (out0 + 16 * GT))
                        pool.sem_inc(s[f"slot_free{u}"], 1)

            @block.vector
            def _(dve):
                dve.wait_ge(s["numbered"], 1)
                nc.vector.memset(load4[:, :, 3], 0)
                nc.vector.tensor_copy(load4[:, :, 2], eid[:, :])
                for a in range(2):
                    nc.vector.tensor_copy(load4[:, :, a], k.id_col[:, 0, a, :]).then_inc(s["filled"], 1)
                dve.wait_ge(s["filled"], 2)
                dve.sem_inc(s["row_free"], 2)
                dve.sem_inc(s["look_free"], 2)

                def one_hots(i, u, j):
                    n = i * (2 * GT) + u * GT + j
                    b = j % 2
                    dve.wait_ge(s["added"], n + 1)
                    nc.vector.tensor_scalar(hot_low[:, b, :], k.iota_row[:, :], k.low_col[:, 0, bass.ds(n, 1)],
                                            None, ALU.is_equal)
                    nc.vector.tensor_scalar(hot_high[:, b, :], k.iota_high[:, :], k.high_col[:, 0, bass.ds(n, 1)],
                                            None, ALU.is_equal).then_inc(s["hot"], 1)
                    if j == 0:
                        dve.wait_ge(s[f"row_ready{u}"], i * 32 + 32)
                        nc.vector.tensor_copy(ids_s[:, u * GT:(u + 1) * GT],
                                              k.id_col[:, 0, 0, bass.ds(n, GT)]).then_inc(s["ids"], 1)
                        dve.wait_ge(s["ids"], i * 2 + u + 1)
                    nc.vector.tensor_scalar(low_hot[:, b, :], row_b[:, u, 0, j * P:(j + 1) * P],
                                            k.iota_part[:, 0:1], None, ALU.is_equal).then_inc(s["marked"], 1)
                    nc.vector.scalar_tensor_tensor(
                        twin[:, b, :], row_b[:, u, 1, j * P:(j + 1) * P], ids_s[:, u * GT + j:u * GT + j + 1],
                        k.earlier[:, :], ALU.is_equal, ALU.mult,
                        accum_out=parts[:, b, 0:1]).then_inc(s["twins"], 1)
                    if j == GT - 1:
                        dve.wait_ge(s["twins"], n + 1)
                        dve.sem_inc(s["row_free"], 1)

                def read_back(i, u, j):
                    n = i * (2 * GT) + u * GT + j
                    b = j % 2
                    q = u * GT + j
                    dve.wait_ge(s["looked"], n + 1)
                    nc.vector.tensor_tensor_reduce(picked[:, 0, :], look[b][:, 0, 0:NCOL], hot_high[:, b, :], 1.0, 0.0,
                                                   ALU.mult, ALU.add, parts[:, b, 1:2]).then_inc(s["picks"], 1)
                    nc.vector.tensor_tensor_reduce(picked[:, 1, :], look[b][:, 1, 0:NCOL], hot_high[:, b, :], 1.0, 0.0,
                                                   ALU.mult, ALU.add, dinv_s[:, q:q + 1])\
                        .then_inc(s["look_free"], 1)
                    if j == 0:
                        dve.wait_ge(s[f"slot_free{u}"], i + 1)
                    dve.wait_ge(s["picks"], n + 1)
                    dve.wait_ge(s["twins"], n + 1)
                    if j == GT - 1:
                        dve.wait_ge(s["look_free"], n + 3)
                        nc.vector.tensor_copy(k.dinv_src[:, bass.ds(n - (GT - 1), GT)],
                                              dinv_s[:, u * GT:(u + 1) * GT])
                    nc.vector.tensor_copy(load_s[:, q, :], load4[:, bass.ds(n, 1), :])
                    nc.vector.tensor_tensor(rank[:, q:q + 1], parts[:, b, 0:1], parts[:, b, 1:2],
                                            ALU.add).then_inc(s["ranked"], 1)

                dve.sem_inc(s["slot_free0"], 1)
                dve.sem_inc(s["slot_free1"], 1)
                with dve.Fori(0, EG // 2) as i:
                    for u in range(2):
                        for j in range(GT):
                            one_hots(i, u, j)
                            read_back(i, u, j)

            @block.scalar
            def _(act):
                with act.Fori(0, T // 2) as i:
                    for b in range(2):
                        n = i * 2 + b
                        act.wait_ge(s["added"], n + 2)
                        nc.scalar.activation(table_sb[:, b, :], table[:, 0:NCOL], ACT.Copy).then_inc(s["copied"], 1)

            @block.tensor
            def _(pe):
                pe.sem_inc(s["added"], 1)
                nc.tensor.matmul(table[:, 0:NCOL], k.ident[:, :], k.start[:, :], start=True, stop=False,
                                 skip_group_check=True).then_inc(s["added"], 1)
                with pe.Fori(0, T // 2) as i:
                    for b in range(2):
                        n = i * 2 + b
                        pe.wait_ge(s["hot"], n + 1)
                        pe.wait_ge(s["copied"], n + 1)
                        pe.wait_ge(s["look_free"], n + 1)
                        pe.wait_ge(s["marked"], n + 1)
                        nc.tensor.matmul(look[b][:, 0, 0:NCOL], low_hot[:, b, :], table_sb[:, b, :], start=True,
                                         stop=True)
                        nc.tensor.matmul(look[b][:, 1, 0:NCOL], low_hot[:, b, :], k.dinv[:, :], start=True,
                                         stop=True).then_inc(s["looked"], 1)
                        nc.tensor.matmul(table[:, 0:NCOL], hot_low[:, b, :], hot_high[:, b, :], start=False,
                                         stop=False, skip_group_check=True).then_inc(s["added"], 1)
        clear_semaphores(nc, sems)


def order_phase(k, order, tag):
    nc = k.nc
    sorted_ = order.payload is not None
    with ExitStack() as st:
        row4 = k.sb(st, tag + "_row4", [TB, 2, P, 4], I32)
        row3 = k.sb(st, tag + "_row3", [TB, 2, 3, P])
        nxt = k.sb(st, tag + "_next", [TB, 2, P])
        minus = k.sb(st, tag + "_minus", [1, 1])
        cols = k.sb(st, tag + "_cols", [P, 4, T])
        same = k.sb(st, tag + "_same", [P, T])
        pt = k.ps(st, tag + "_pt", [P, 4, 512])
        s = {x: k.sem(st, f"{tag}_{x}") for x in ("loaded", "stored", "step", "turned", "shifted")}
        with nc.Block() as block:
            @block.sync
            def _(sp):
                if sorted_:
                    sp.dma_start(row4[:, :, :, :], order.payload.rearrange("(b r e) c -> r b e c", b=2, e=P))\
                      .then_inc(s["loaded"], 16)
                    sp.wait_ge(s["step"], 4)
                    sp.dma_start(order.id_row[0:EP].rearrange("(b r e) -> r b e", b=2, e=P), row3[:, :, 0, :])\
                      .then_inc(s["stored"], 16)
                    sp.dma_start(order.id_row[EP:EP + 1].rearrange("(r e) -> r e", r=1), minus[:, :])\
                      .then_inc(s["stored"], 16)
                    sp.wait_ge(s["stored"], 32)
                sp.dma_start(nxt[:, :, :], order.id_row[1:EP + 1].rearrange("(b r e) -> r b e", b=2, e=P))\
                  .then_inc(s["shifted"], 16)
                sp.wait_ge(s["shifted"], 16)

            @block.vector
            def _(dve):
                at = 0
                if sorted_:
                    nc.vector.memset(minus[:, :], -1.0).then_inc(s["step"], 1)
                    dve.wait_ge(s["loaded"], 16)
                    for c in range(3):
                        nc.vector.tensor_copy(row3[:, :, c, :], row4[:, :, :, c]).then_inc(s["step"], 1)
                    dve.wait_ge(s["turned"], 1)
                    for c in range(3):
                        nc.vector.tensor_copy(cols[:, c, :], pt[:, c, 0:T]).then_inc(s["step"], 1)
                    dve.wait_ge(s["step"], 7)
                    nc.vector.tensor_copy(order.id_col[:, :], cols[:, 0, :]).then_inc(s["step"], 1)
                    nc.vector.tensor_copy(order.eid[:, :], cols[:, 2, :]).then_inc(s["step"], 1)
                    for c, out in ((0, order.cap_own), (1, order.cap_far)):
                        nc.vector.tensor_scalar(same[:, :], cols[:, c, :], float(N - 1), None,
                                                ALU.min).then_inc(s["step"], 1)
                        at = 10 + 2 * c
                        dve.wait_ge(s["step"], at)
                        nc.vector.tensor_scalar(out[:, :], same[:, :], 2.0, 1.0, ALU.mult,
                                                ALU.add).then_inc(s["step"], 1)
                        dve.wait_ge(s["step"], at + 1)
                    at = 13
                dve.wait_ge(s["turned"], 2)
                nc.vector.tensor_copy(cols[:, 3, :], pt[:, 3, 0:T]).then_inc(s["step"], 1)
                nc.vector.memset(order.prev_col[:, 0:1], -5.0).then_inc(s["step"], 1)
                nc.vector.tensor_scalar(order.prev_col[:, 1:T], order.id_col[:, 0:T - 1], 5.0, k.last_part[:, 0:1],
                                        ALU.add, ALU.mult).then_inc(s["step"], 1)
                dve.wait_ge(s["step"], at + 3)
                nc.vector.tensor_scalar(order.prev_col[:, 1:T], order.prev_col[:, 1:T], -5.0, None,
                                        ALU.add).then_inc(s["step"], 1)
                nc.vector.tensor_tensor(same[:, :], order.id_col[:, :], cols[:, 3, :],
                                        ALU.is_equal).then_inc(s["step"], 1)
                dve.wait_ge(s["step"], at + 5)
                nc.vector.scalar_tensor_tensor(cols[:, 3, :], same[:, :], float(FAR), order.id_col[:, :], ALU.mult,
                                               ALU.add).then_inc(s["step"], 1)
                dve.wait_ge(s["step"], at + 6)
                nc.vector.tensor_copy(order.last_idx[:, :], cols[:, 3, :]).then_inc(s["step"], 1)
                if sorted_:
                    nc.vector.tensor_scalar(order.last_cap[:, :], cols[:, 3, :], 2.0, 1.0, ALU.mult,
                                            ALU.add).then_inc(s["step"], 1)

            @block.tensor
            def _(pe):
                if sorted_:
                    pe.wait_ge(s["step"], 4)
                    for c in range(3):
                        for b in range(2):
                            last = nc.tensor.transpose(pt[:, c, b * TB:(b + 1) * TB], row3[:, b, c, :],
                                                       k.ident[0:TB, 0:TB])
                    last.then_inc(s["turned"], 1)
                else:
                    pe.sem_inc(s["turned"], 1)
                pe.wait_ge(s["shifted"], 16)
                for b in range(2):
                    last = nc.tensor.transpose(pt[:, 3, b * TB:(b + 1) * TB], nxt[:, b, :], k.ident[0:TB, 0:TB])
                last.then_inc(s["turned"], 1)
        clear_semaphores(nc, list(s.values()))


def segment_sum_phase(k, order, table, width, index, dest, tag, weigh, project=None, bias=None):
    nc = k.nc
    with ExitStack() as st:
        rows = k.sb(st, tag + "_rows", [P, 2, GT, width])
        index_s = k.sb(st, tag + "_index", [P, 2, GT], I32)
        last_s = k.sb(st, tag + "_last", [P, 2, GT], I32)
        row_b = k.sb(st, tag + "_row_b", [P, 2, GT, P])
        same = k.sb(st, tag + "_same", [P, 2, GT, P])
        cross = k.sb(st, tag + "_cross", [P, 2, GT, P])
        vals = k.sb(st, tag + "_vals", [P, 2, GT, D]) if weigh else rows
        sums = k.sb(st, tag + "_sums", [P, 2, GT, D])
        acc = [k.ps(st, f"{tag}_acc{j}", [P, 512]) for j in range(GT)]
        if project is not None:
            turned_sb = k.sb(st, tag + "_turned_sb", [P, 2, GT, P])
            sent = k.sb(st, tag + "_sent", [P, 2, GT, D])
            pt = [k.ps(st, f"{tag}_pt{u}", [P, GT, P]) for u in range(2)]
            pp = [k.ps(st, f"{tag}_pp{u}", [P, GT, D]) for u in range(2)]
        else:
            sent = sums
        names = ["index", "rows_free", "row_ready0", "row_ready1", "row_free", "masks", "masks_free",
                 "weighed", "summed", "copied", "sent_free", "start", "turned", "turned_copied",
                 "projected", "project_copied", "picked"]
        s = {x: k.sem(st, f"{tag}_{x}") for x in names}
        in0, out0 = k.gather_count, k.scatter_count
        k.gather_count += (EG // 2) * 16 * GT
        k.scatter_count += (EG // 2) * 16 * GT
        sems = list(s.values())
        s.update(got0=k.gathered[0], got1=k.gathered[1], put0=k.scattered[0], put1=k.scattered[1])
        with nc.Block() as block:
            @block.sync
            def _(sp):
                with sp.Fori(0, EG // 2) as i:
                    for u in range(2):
                        g = i * 2 + u
                        sp.wait_ge(s["row_free"], after(g))
                        sp.dma_start(row_b[:, u, :, :].rearrange("p t e -> p (t e)"),
                                     order.id_row[bass.ds(g * (GT * P), GT * P)].partition_broadcast(P))\
                          .then_inc(s[f"row_ready{u}"], 16)

            @block.gpsimd
            def _(pool):
                pool.sem_inc(s["sent_free"], 2)
                with pool.Fori(0, EG // 2) as i:
                    for u in range(2):
                        g = i * 2 + u
                        pool.wait_ge(s["rows_free"], after(g))
                        pool.sem_inc(k.paces, 1)
                        nc.gpsimd.tensor_copy(index_s[:, u, :], index[:, bass.ds(g * GT, GT)])
                        nc.gpsimd.tensor_copy(last_s[:, u, :], order.last_idx[:, bass.ds(g * GT, GT)])\
                            .then_inc(s["index"], 1)
                        paced(pool, k, s["index"], after(g))
                        for j in range(GT):
                            nc.gpsimd.indirect_dma_start(
                                out=rows[:, u, j, :], out_offset=None, in_=table,
                                in_offset=bass.IndirectOffsetOnAxis(ap=index_s[:, u, j:j + 1], axis=0))\
                                .then_inc(s[f"got{u}"], 16)
                    for u in range(2):
                        paced(pool, k, s["project_copied" if project is not None else "copied"],
                              after(i * 2 + u) if project is not None else after(i * 2 + u, GT) + 1)
                        for j in range(GT):
                            nc.gpsimd.indirect_dma_start(
                                out=dest, out_offset=bass.IndirectOffsetOnAxis(ap=last_s[:, u, j:j + 1], axis=0),
                                in_=sent[:, u, j, :], in_offset=None, bounds_check=N - 1, oob_is_err=False)\
                                .then_inc(s[f"put{u}"], 16)
                    for u in range(2):
                        pool.wait_ge(s[f"put{u}"], i * (16 * GT) + (out0 + 16 * GT))
                        pool.sem_inc(s["sent_free"], 1)

            @block.vector
            def _(dve):
                nc.vector.memset(sums[:, 1, GT - 1, :], 0.0).then_inc(s["start"], 1)
                dve.wait_ge(s["start"], 1)
                dve.sem_inc(s["row_free"], 2)
                if weigh:
                    dve.sem_inc(s["rows_free"], 2)
                with dve.Fori(0, EG // 2) as i:
                    for u in range(2):
                        g = i * 2 + u
                        dve.wait_ge(s["masks_free"], after(g))
                        dve.wait_ge(s[f"row_ready{u}"], i * 16 + 16)
                        cols = [c[:, bass.ds(g * GT, GT)].unsqueeze(2).broadcast_to([P, GT, P])
                                for c in (order.id_col, order.prev_col)]
                        nc.vector.tensor_tensor(same[:, u, :, :], row_b[:, u, :, :], cols[0], ALU.is_equal)
                        nc.vector.tensor_tensor(cross[:, u, :, :], row_b[:, u, :, :], cols[1],
                                                ALU.is_equal).then_inc(s["masks"], 1)
                        dve.wait_ge(s["masks"], after(g))
                        dve.sem_inc(s["row_free"], 1)
                        dve.wait_ge(s[f"got{u}"], i * (16 * GT) + (in0 + 16 * GT))
                        if weigh:
                            weigh(dve, vals[:, u, :, :], rows[:, u, :, :], g).then_inc(s["weighed"], 1)
                            dve.wait_ge(s["weighed"], after(g))
                            dve.sem_inc(s["rows_free"], 1)

            @block.scalar
            def _(act):
                act.sem_inc(s["copied"], 1)
                with act.Fori(0, EG // 2) as i:
                    for u in range(2):
                        g = i * 2 + u
                        for j in range(GT):
                            if j == 0:
                                act.wait_ge(s["sent_free"], after(g))
                            act.wait_ge(s["summed"], g * GT + j + 1)
                            nc.scalar.activation(sums[:, u, j, :], acc[j][:, 0:D], ACT.Copy)\
                                .then_inc(s["copied"], 1)
                        if project is not None:
                            act.wait_ge(s["turned"], after(g))
                            nc.scalar.activation(turned_sb[:, u, :, :], pt[u][:, :, :], ACT.Copy)\
                                .then_inc(s["turned_copied"], 1)
                            act.wait_ge(s["projected"], after(g))
                            nc.scalar.activation(sent[:, u, :, :], pp[u][:, :, :], ACT.Copy)\
                                .then_inc(s["project_copied"], 1)

            @block.tensor
            def _(pe):
                pe.wait_ge(s["start"], 1)
                pe.sem_inc(s["masks_free"], 2)
                if not weigh:
                    pe.sem_inc(s["rows_free"], 2)
                with pe.Fori(0, EG // 2) as i:
                    for u in range(2):
                        g = i * 2 + u
                        pe.wait_ge(s["masks"], after(g))
                        if weigh:
                            pe.wait_ge(s["weighed"], after(g))
                        else:
                            pe.wait_ge(s[f"got{u}"], i * (16 * GT) + (in0 + 16 * GT))
                        for j in range(GT):
                            nc.tensor.matmul(acc[j][:, 0:D], same[:, u, j, :], vals[:, u, j, :], start=True,
                                             stop=False)
                            before = sums[:, u, j - 1, :] if j else sums[:, 1 - u, GT - 1, :]
                            pe.wait_ge(s["copied"], g * GT + j + 1)
                            mm = nc.tensor.matmul(acc[j][:, 0:D], cross[:, u, j, :], before, start=False, stop=True)
                            mm.then_inc(s["summed"], 1)
                        pe.wait_ge(s["summed"], after(g, GT))
                        pe.sem_inc(s["masks_free"], 1)
                        if not weigh:
                            pe.sem_inc(s["rows_free"], 1)
                        if project is not None:
                            pe.wait_ge(s["copied"], after(g, GT) + 1)
                            for j in range(GT):
                                mm = nc.tensor.transpose(pt[u][:, j, :], sums[:, u, j, :], k.ident[:, :])
                            mm.then_inc(s["turned"], 1)
                            pe.wait_ge(s["turned_copied"], after(g))
                            for j in range(GT):
                                nc.tensor.matmul(pp[u][:, j, :], turned_sb[:, u, j, :], project, start=True, stop=False)
                                mm = nc.tensor.matmul(pp[u][:, j, :], k.ones[0:1, :], bias, start=False, stop=True)
                            mm.then_inc(s["projected"], 1)
        clear_semaphores(nc, sems)


def zero_phase(k, tables):
    nc = k.nc
    with ExitStack() as st:
        stored = k.sem(st, "zero_stored")
        with nc.Block() as block:
            @block.sync
            def _(sp):
                for m, table in enumerate(tables):
                    with sp.Fori(0, NG) as g:
                        sp.dma_start(table[bass.ds(g * (P * NJ), P * NJ), :].rearrange("(p j) d -> p (j d)", p=P),
                                     k.zeros[:, :]).then_inc(stored, 16)
                    sp.dma_start(table[NG * P * NJ:N, :].rearrange("(p j) d -> p (j d)", p=TAILP),
                                 k.zeros[0:TAILP, :]).then_inc(stored, 16)
                sp.wait_ge(stored, 16 * (NG + 1) * len(tables))
        clear_semaphores(nc, [stored])


class Order:

    def __init__(self, id_row, id_col, prev_col, last_idx, payload=None, eid=None, cap_own=None, cap_far=None,
                 last_cap=None):
        self.id_row, self.id_col, self.prev_col, self.last_idx = id_row, id_col, prev_col, last_idx
        self.payload, self.eid, self.cap_own, self.cap_far, self.last_cap = payload, eid, cap_own, cap_far, last_cap


class Chain:

    def __init__(self, eng, sem, steps):
        self.eng, self.sem, self.steps = eng, sem, steps

    def begin(self, n):
        self.n, self.count = n, 0

    def link(self, ins):
        self.count += 1
        ins.then_inc(self.sem, 1)
        self.eng.wait_ge(self.sem, self.n * self.steps + self.count)

    def end(self):
        assert self.count == self.steps


def node_groups(eng, stages):
    with eng.Fori(0, NG // 2) as i:
        for stage in stages:
            for u in range(2):
                stage(i * 2 + u, i, u, P)
    for stage in stages:
        stage(NG, NG // 2, 0, TAILP)


def node_rows(table, n, p, width=D):
    at = slice(n * P * NJ, n * P * NJ + p * NJ) if isinstance(n, int) else bass.ds(n * (P * NJ), P * NJ)
    return table[at, :].rearrange("(p j) d -> p j d", p=p)


class Linear:

    def __init__(self, k, st, tag, weight, bias=None, cols=NJ, out=None, spare=None):
        self.k, self.weight, self.bias, self.cols = k, weight, bias, cols
        banks = cols // 4
        self.turned_ps = spare or [k.ps(st, f"{tag}_tps{b}", [P, 4, P]) for b in range(banks)]
        self.out = out or [k.ps(st, f"{tag}_out{b}", [P, 4, D]) for b in range(banks)]
        self.turned_sb = k.sb(st, f"{tag}_tsb", [P, cols, P])
        self.turned = k.sem(st, tag + "_turned")
        self.copied = k.sem(st, tag + "_copied")
        self.made = k.sem(st, tag + "_made")
        self.free = k.sem(st, tag + "_free")
        self.sems = [self.turned, self.copied, self.made, self.free]

    def turn(self, pe, n, p, rows):
        pe.wait_ge(self.copied, n + 1)
        for j in range(self.cols):
            mm = self.k.nc.tensor.transpose(self.turned_ps[j // 4][:, j % 4, 0:p], rows[0:p, j, :],
                                            self.k.ident[0:p, 0:p])
        mm.then_inc(self.turned, 1)

    def copy(self, act, n, p):
        act.wait_ge(self.turned, n + 1)
        act.wait_ge(self.made, n + 1)
        for b in range(self.cols // 4):
            ins = self.k.nc.scalar.activation(self.turned_sb[:, 4 * b:4 * b + 4, 0:p],
                                              self.turned_ps[b][:, :, 0:p], ACT.Copy)
        ins.then_inc(self.copied, 1)

    def product(self, pe, n, p):
        pe.wait_ge(self.copied, n + 2)
        pe.wait_ge(self.free, n + 1)
        for j in range(self.cols):
            mm = self.k.nc.tensor.matmul(self.out[j // 4][0:p, j % 4, :], self.turned_sb[:, j, 0:p], self.weight,
                                         start=True, stop=self.bias is None)
            if self.bias is not None:
                mm = self.k.nc.tensor.matmul(self.out[j // 4][0:p, j % 4, :], self.k.ones[0:1, 0:p], self.bias,
                                             start=False, stop=True)
        mm.then_inc(self.made, 1)


class Norm:

    STEPS = 4

    def __init__(self, k, st, tag, cols=NJ, eps=EPS, slots=2):
        self.k, self.cols, self.eps = k, cols, eps
        self.stats = k.sb(st, tag + "_stats", [P, slots, cols, 6])
        self.mean = k.sb(st, tag + "_mean", [P, slots, cols])
        self.gap = k.sb(st, tag + "_gap", [P, slots, cols])
        self.var = k.sb(st, tag + "_var", [P, slots, cols])
        self.root = k.sb(st, tag + "_root", [P, slots, cols])
        self.scale = k.sb(st, tag + "_scale", [P, slots, cols])
        self.bias = k.sb(st, tag + "_bias", [P, 1])
        self.seen = k.sem(st, tag + "_seen")
        self.rooted = k.sem(st, tag + "_rooted")
        self.scaled = k.sem(st, tag + "_scaled")
        self.steps = k.sem(st, tag + "_steps")
        self.set = k.sem(st, tag + "_set")
        self.sems = [self.seen, self.rooted, self.scaled, self.steps, self.set]

    def prepare(self, dve):
        self.chain = Chain(dve, self.steps, self.STEPS)
        self.k.nc.vector.memset(self.bias[:, :], self.eps).then_inc(self.set, 1)

    def statistics(self, dve, n, u, p, rows):
        v, c, s = self.k.nc.vector, self.chain, self.stats
        c.begin(n)
        for j in range(self.cols):
            ins = v.bn_stats(s[0:p, u, j, :], rows[0:p, j, :])
        c.link(ins)
        v.tensor_tensor(self.mean[0:p, u, :], s[0:p, u, :, 1], s[0:p, u, :, 4], ALU.add)
        v.tensor_tensor(self.gap[0:p, u, :], s[0:p, u, :, 1], s[0:p, u, :, 4], ALU.subtract)
        c.link(v.tensor_tensor(self.var[0:p, u, :], s[0:p, u, :, 2], s[0:p, u, :, 5], ALU.add))
        c.link(v.tensor_tensor(self.gap[0:p, u, :], self.gap[0:p, u, :], self.gap[0:p, u, :], ALU.mult))
        c.link(v.scalar_tensor_tensor(self.var[0:p, u, :], self.gap[0:p, u, :], D / 4.0, self.var[0:p, u, :],
                                      ALU.mult, ALU.add))
        c.end()
        v.tensor_scalar(self.mean[0:p, u, :], self.mean[0:p, u, :], 0.5, None, ALU.mult).then_inc(self.seen, 1)

    def square_root(self, act, n, u, p, factor=1.0):
        act.wait_ge(self.seen, n + 1)
        act.wait_ge(self.set, 1)
        self.k.nc.scalar.activation(self.root[0:p, u, :], self.var[0:p, u, :], ACT.Sqrt, bias=self.bias[0:p, 0:1],
                                    scale=factor / D).then_inc(self.rooted, 1)

    def normalise(self, dve, n, u, p, out, rows):
        dve.wait_ge(self.rooted, n + 1)
        self.k.nc.vector.reciprocal(self.scale[0:p, u, :], self.root[0:p, u, :]).then_inc(self.scaled, 1)
        dve.wait_ge(self.scaled, n + 1)
        for j in range(self.cols):
            ins = self.k.nc.vector.tensor_scalar(out[0:p, j, :], rows[0:p, j, :], self.mean[0:p, u, j:j + 1],
                                                 self.scale[0:p, u, j:j + 1], ALU.subtract, ALU.mult)
        return ins


class Propagated:

    def __init__(self, k, st, tag):
        self.k = k
        self.x = k.sb(st, tag + "_x", [P, 2, NJ, D])
        self.agg = k.sb(st, tag + "_agg", [P, 2, NJ, D])
        self.y = k.sb(st, tag + "_y", [P, 2, NJ, D + 1])
        self.ready = [k.sem(st, f"{tag}_ready{u}") for u in range(2)]
        self.free = k.sem(st, tag + "_free")
        self.scaled = k.sem(st, tag + "_scaled")
        self.owned = k.sem(st, tag + "_owned")
        self.made = k.sem(st, tag + "_made")
        self.used = k.sem(st, tag + "_used")
        self.sems = self.ready + [self.free, self.scaled, self.owned, self.made, self.used]

    def load(self, sp, n, i, u, p):
        sp.wait_ge(self.free, n + 1)
        sp.dma_start(self.x[0:p, u, :, :], node_rows(self.k.x, n, p)).then_inc(self.ready[u], 16)
        sp.dma_start(self.agg[0:p, u, :, :], node_rows(self.k.agg, n, p)).then_inc(self.ready[u], 16)

    def per_node(self, column, n, p):
        c = column[0:p, n * NJ:n * NJ + NJ] if isinstance(n, int) else column[0:p, bass.ds(n * NJ, NJ)]
        return c.unsqueeze(2).broadcast_to([p, NJ, D])

    def scale(self, pool, n, i, u, p):
        paced(pool, self.k, self.ready[u], i * 32 + 32)
        self.k.nc.gpsimd.tensor_tensor(self.agg[0:p, u, :, :], self.agg[0:p, u, :, :],
                                       self.per_node(self.k.dinv, n, p), ALU.mult).then_inc(self.scaled, 1)

    def make(self, dve, n, i, u, p):
        dve.wait_ge(self.ready[u], i * 32 + 32)
        dve.wait_ge(self.used, n + 1)
        y = self.y[0:p, u, :, 0:D]
        self.k.nc.vector.tensor_tensor(y, self.x[0:p, u, :, :], self.per_node(self.k.dinv2, n, p),
                                       ALU.mult).then_inc(self.owned, 1)
        dve.wait_ge(self.scaled, n + 1)
        dve.wait_ge(self.owned, n + 1)
        self.k.nc.vector.tensor_tensor(y, y, self.agg[0:p, u, :, :], ALU.add).then_inc(self.made, 1)


def moments_phase(k):
    nc = k.nc
    with ExitStack() as st:
        prop = Propagated(k, st, "mom_y")
        w = k.sb(st, "mom_w", [P, D])
        gb = k.sb(st, "mom_gb", [P, 2, D])
        cov = k.sb(st, "mom_cov", [P, D + 1])
        mean = k.sb(st, "mom_mean", [P, 1])
        mean_b = k.sb(st, "mom_mean_b", [P, P])
        mean_r = k.sb(st, "mom_mean_r", [1, P])
        wz = k.sb(st, "mom_wz", [P, D])
        work = k.sb(st, "mom_work", [P, 4, D])
        acc = k.ps(st, "mom_acc", [P, 512])
        tps = k.ps(st, "mom_tps", [P, 512])
        outer = k.ps(st, "mom_outer", [P, 512])
        zp = k.ps(st, "mom_z", [P, 512])
        vb = k.ps(st, "mom_var", [P, 512])
        mb = k.ps(st, "mom_mean_h", [P, 512])
        s = {x: k.sem(st, "mom_" + x) for x in ("wloaded", "summed", "step", "pstep", "astep", "begun")}
        with nc.Block() as block:
            @block.sync
            def _(sp):
                sp.dma_start(w[:, :], k.a["L0_gnn_W"]).then_inc(s["wloaded"], 16)
                sp.dma_start(gb[:, 0, :], k.a["L0_gnn_gamma"].partition_broadcast(P)).then_inc(s["wloaded"], 16)
                sp.dma_start(gb[:, 1, :], k.a["L0_gnn_beta"].partition_broadcast(P)).then_inc(s["wloaded"], 16)
                node_groups(sp, [lambda n, i, u, p: prop.load(sp, n, i, u, p)])

            @block.gpsimd
            def _(pool):
                node_groups(pool, [lambda n, i, u, p: prop.scale(pool, n, i, u, p)])

            @block.vector
            def _(dve):
                dve.sem_inc(prop.free, 2)
                nc.vector.memset(prop.y[:, :, :, D:D + 1], 1.0).then_inc(s["begun"], 1)

                def make(n, i, u, p):
                    prop.make(dve, n, i, u, p)
                    dve.wait_ge(prop.made, n + 1)
                    dve.sem_inc(prop.free, 1)

                node_groups(dve, [make])
                dve.wait_ge(s["summed"], 1)
                dve.wait_ge(s["wloaded"], 48)
                c = Chain(dve, s["step"], 13)
                c.begin(0)
                c.link(nc.vector.tensor_scalar(cov[:, :], acc[:, 0:D + 1], 1.0 / N, None, ALU.mult))
                c.link(nc.vector.tensor_copy(mean[:, :], cov[:, D:D + 1]))
                c.link(nc.vector.tensor_scalar(mean_b[:, :], k.ones[:, :], mean[:, 0:1], None, ALU.mult))
                dve.wait_ge(s["pstep"], 1)
                c.link(nc.vector.tensor_copy(mean_r[:, :], tps[0:1, 0:P]))
                dve.wait_ge(s["pstep"], 2)
                c.link(nc.vector.tensor_tensor(cov[:, 0:D], cov[:, 0:D], outer[:, 0:P], ALU.subtract))
                dve.wait_ge(s["pstep"], 3)
                c.link(nc.vector.tensor_tensor(wz[:, :], w[:, :], zp[:, 0:D], ALU.mult))
                dve.wait_ge(s["astep"], 1)
                c.link(nc.vector.reciprocal(work[:, 1, :], work[:, 0, :]))
                c.link(nc.vector.tensor_tensor(work[:, 2, :], work[:, 1, :], gb[:, 0, :], ALU.mult))
                c.link(nc.vector.tensor_scalar(work[:, 2, :], work[:, 2, :], 0.5, None, ALU.mult))
                c.link(nc.vector.tensor_tensor(k.gcn_w[:, :], w[:, :], work[:, 2, :], ALU.mult))
                dve.wait_ge(s["pstep"], 5)
                c.link(nc.vector.tensor_tensor(work[:, 3, :], mb[:, 0:D], work[:, 2, :], ALU.mult))
                c.link(nc.vector.tensor_scalar(gb[:, 1, :], gb[:, 1, :], 0.5, None, ALU.mult))
                c.link(nc.vector.tensor_tensor(k.gcn_c[:, :], gb[:, 1, :], work[:, 3, :], ALU.subtract))
                c.end()

            @block.scalar
            def _(act):
                act.wait_ge(s["pstep"], 4)
                nc.scalar.activation(work[:, 0, :], vb[:, 0:D], ACT.Sqrt, bias=k.eps[:, 0:1]).then_inc(s["astep"], 1)

            @block.tensor
            def _(pe):
                nc.tensor.matmul(acc[:, 0:D + 1], k.zeros[:, 0:P], k.zeros[:, 0:D + 1], start=True, stop=False,
                                 skip_group_check=True)
                pe.sem_inc(prop.used, 2)
                pe.wait_ge(s["begun"], 1)

                def add(n, i, u, p):
                    pe.wait_ge(prop.made, n + 1)
                    for j in range(NJ):
                        mm = nc.tensor.matmul(acc[:, 0:D + 1], prop.y[0:p, u, j, 0:D], prop.y[0:p, u, j, :],
                                              start=False, stop=False, skip_group_check=True)
                    mm.then_inc(prop.used, 1)

                node_groups(pe, [add])
                pe.wait_ge(prop.used, NG + 3)
                pe.sem_inc(s["summed"], 1)
                pe.wait_ge(s["step"], 3)
                nc.tensor.transpose(tps[0:1, 0:P], mean[:, 0:1], k.ident[:, :]).then_inc(s["pstep"], 1)
                pe.wait_ge(s["step"], 4)
                nc.tensor.matmul(outer[:, 0:P], mean_r[:, :], mean_r[:, :], start=True, stop=True)\
                    .then_inc(s["pstep"], 1)
                pe.wait_ge(s["step"], 5)
                nc.tensor.matmul(zp[:, 0:D], cov[:, 0:D], w[:, :], start=True, stop=True).then_inc(s["pstep"], 1)
                pe.wait_ge(s["step"], 6)
                nc.tensor.matmul(vb[:, 0:D], k.ones[:, :], wz[:, :], start=True, stop=True).then_inc(s["pstep"], 1)
                nc.tensor.matmul(mb[:, 0:D], mean_b[:, :], w[:, :], start=True, stop=True).then_inc(s["pstep"], 1)
        clear_semaphores(nc, prop.sems + list(s.values()))


def load_constants(k, names):
    nc = k.nc
    with ExitStack() as st:
        got = k.sem(st, "const_got")
        with nc.Block() as block:
            @block.sync
            def _(sp):
                for dst, src in names:
                    sp.dma_start(dst, src).then_inc(got, 16)
                sp.wait_ge(got, 16 * len(names))
        clear_semaphores(nc, [got])


def capsules_phase(k):
    nc = k.nc
    with ExitStack() as st:
        w1 = k.sb(st, "cap_w1", [P, D])
        b1 = k.sb(st, "cap_b1", [1, D])
        load_constants(k, [(w1[:, :], k.a["L1_gnn_weight"]),
                           (b1[:, :], k.a["L1_gnn_bias"].rearrange("(r d) -> r d", r=1))])
        prop = Propagated(k, st, "cap_y")
        conv = Linear(k, st, "cap_conv", k.gcn_w[:, :], k.gcn_c[0:1, :])
        caps = Linear(k, st, "cap_caps", w1[:, :], b1[:, :])
        norm = Norm(k, st, "cap_norm", eps=EPS / 4)
        both = k.sb(st, "cap_both", [P, 2, NJ, 2, D])
        u1 = k.sb(st, "cap_u", [P, 2, NJ, D])
        leak = k.sb(st, "cap_leak", [P, NJ, D])
        square = k.sb(st, "cap_square", [P, NJ, D])
        length = k.sb(st, "cap_length", [P, 3, NJ * NH])
        names = ["added", "added2", "normed", "stored0", "stored1", "out_free", "leaked", "bent", "squared", "reduced",
                 "sized", "inverted", "scaled", "square_free"]
        s = {x: k.sem(st, "cap_" + x) for x in names}
        with nc.Block() as block:
            @block.sync
            def _(sp):
                def store(n, i, u, p):
                    sp.wait_ge(s["scaled"], n + 1)
                    sp.dma_start(node_rows(k.layer1, n, p, 2 * D),
                                 both[0:p, u, :, :, :].rearrange("p j c d -> p j (c d)")).then_inc(s[f"stored{u}"], 16)

                def stored(n, i, u, p):
                    sp.wait_ge(s[f"stored{u}"], i * 16 + 16)
                    sp.sem_inc(s["out_free"], 1)

                sp.sem_inc(s["out_free"], 2)
                node_groups(sp, [lambda n, i, u, p: prop.load(sp, n, i, u, p), store, stored])

            @block.gpsimd
            def _(pool):
                node_groups(pool, [lambda n, i, u, p: prop.scale(pool, n, i, u, p)])

            @block.vector
            def _(dve):
                dve.sem_inc(prop.free, 2)
                dve.sem_inc(conv.free, 1)
                dve.sem_inc(caps.free, 1)
                dve.sem_inc(s["square_free"], 1)
                norm.prepare(dve)

                def add(n, i, u, p):
                    dve.wait_ge(conv.made, n + 2)
                    for b in range(2):
                        ins = nc.vector.scalar_tensor_tensor(
                            u1[0:p, u, 4 * b:4 * b + 4, :], conv.out[b][0:p, :, :], 0.0,
                            prop.x[0:p, u, 4 * b:4 * b + 4, :], ALU.max, ALU.add)
                    ins.then_inc(s["added"], 1)
                    dve.wait_ge(s["added"], n + 1)
                    dve.sem_inc(conv.free, 1)
                    dve.sem_inc(prop.free, 1)
                    norm.statistics(dve, n, u, p, u1[:, u, :, :])

                def normalise(n, i, u, p):
                    dve.wait_ge(s["out_free"], n + 1)
                    norm.normalise(dve, n, u, p, both[:, u, :, 0, :], u1[:, u, :, :]).then_inc(s["normed"], 1)

                def bend(n, i, u, p):
                    dve.wait_ge(s["leaked"], n + 1)
                    for b in range(2):
                        ins = nc.vector.tensor_tensor(both[0:p, u, 4 * b:4 * b + 4, 1, :], caps.out[b][0:p, :, :],
                                                      leak[0:p, 4 * b:4 * b + 4, :], ALU.max)
                    ins.then_inc(s["bent"], 1)
                    dve.wait_ge(s["bent"], n + 1)
                    dve.sem_inc(caps.free, 1)
                    dve.wait_ge(s["squared"], n + 1)
                    nc.vector.tensor_reduce(length[0:p, 0, :],
                                            square[0:p, :, :].rearrange("p j (h d) -> p (j h) d", h=NH), AX.X,
                                            ALU.add).then_inc(s["reduced"], 1)
                    dve.wait_ge(s["sized"], n + 1)
                    nc.vector.reciprocal(length[0:p, 2, :], length[0:p, 1, :]).then_inc(s["inverted"], 1)
                    dve.wait_ge(s["inverted"], n + 1)
                    for b in range(2):
                        half = both[0:p, u, 4 * b:4 * b + 4, 1, :].rearrange("p j (h d) -> p j h d", h=NH)
                        size = length[0:p, 2, 4 * b * NH:(4 * b + 4) * NH].rearrange("p (j h) -> p j h", h=NH)\
                            .unsqueeze(3).broadcast_to([p, 4, NH, HD])
                        ins = nc.vector.tensor_tensor(half, half, size, ALU.mult)
                    ins.then_inc(s["scaled"], 1)

                node_groups(dve, [lambda n, i, u, p: prop.make(dve, n, i, u, p), add, normalise, bend])

            @block.scalar
            def _(act):
                act.sem_inc(conv.copied, 1)
                act.sem_inc(caps.copied, 1)

                def root(n, i, u, p):
                    norm.square_root(act, n, u, p)

                def leaked(n, i, u, p):
                    act.wait_ge(caps.made, n + 2)
                    for b in range(2):
                        ins = nc.scalar.activation(leak[0:p, 4 * b:4 * b + 4, :], caps.out[b][0:p, :, :], ACT.Copy,
                                                   scale=0.01)
                    ins.then_inc(s["leaked"], 1)
                    act.wait_ge(s["bent"], n + 1)
                    nc.scalar.activation(square[0:p, :, :], both[0:p, u, :, 1, :], ACT.Square).then_inc(s["squared"], 1)
                    act.wait_ge(s["reduced"], n + 1)
                    nc.scalar.activation(length[0:p, 1, :], length[0:p, 0, :], ACT.Sqrt).then_inc(s["sized"], 1)

                node_groups(act, [lambda n, i, u, p: conv.copy(act, n, p), root,
                                  lambda n, i, u, p: caps.copy(act, n, p), leaked])

            @block.tensor
            def _(pe):
                pe.sem_inc(conv.made, 1)
                pe.sem_inc(caps.made, 1)
                pe.sem_inc(prop.used, 2)

                def conv_turn(n, i, u, p):
                    pe.wait_ge(prop.made, n + 1)
                    conv.turn(pe, n, p, prop.y[:, u, :, 0:D])
                    pe.wait_ge(conv.turned, n + 1)
                    pe.sem_inc(prop.used, 1)

                def caps_turn(n, i, u, p):
                    pe.wait_ge(s["normed"], n + 1)
                    caps.turn(pe, n, p, both[:, u, :, 0, :])

                node_groups(pe, [conv_turn, lambda n, i, u, p: conv.product(pe, n, p), caps_turn,
                                 lambda n, i, u, p: caps.product(pe, n, p)])
        clear_semaphores(nc, prop.sems + conv.sems + caps.sems + norm.sems + list(s.values()))


def routing_setup_phase(k, o):
    nc = k.nc
    with ExitStack() as st:
        pick = k.sb(st, "rs_pick", [P, 2, P])
        pick2 = k.sb(st, "rs_pick2", [P, 2])
        ends = k.sb(st, "rs_ends", [P, 2, T])
        ends_t = k.sb(st, "rs_ends_t", [TB, 2, 2])
        place = k.sb(st, "rs_place", [P, 2])
        order = k.sb(st, "rs_order", [TB, 2, 2, T])
        pe_ends = [k.ps(st, f"rs_ends_ps{a}", [P, 512]) for a in range(2)]
        pe_two = k.ps(st, "rs_two_ps", [P, 512])
        pe_t = k.ps(st, "rs_t_ps", [P, 2, 2, P])
        s = {x: k.sem(st, "rs_" + x) for x in ("step", "picked", "turned")}
        with nc.Block() as block:
            @block.vector
            def _(dve):
                v = nc.vector
                c = Chain(dve, s["step"], 14)
                c.begin(0)
                c.link(v.tensor_scalar(pick2[:, 0:1], k.iota_part[:, :], 0.0, None, ALU.is_equal))
                c.link(v.tensor_copy(pick2[:, 1:2], k.last_part[:, :]))
                c.link(v.tensor_scalar(pick[:, 0, :], k.ones[:, :], pick2[:, 0:1], None, ALU.mult))
                c.link(v.tensor_scalar(pick[:, 1, :], k.ones[:, :], pick2[:, 1:2], None, ALU.mult))
                dve.wait_ge(s["picked"], 1)
                c.link(v.tensor_copy(ends[:, 0, :], pe_ends[0][:, 0:T]))
                c.link(v.tensor_copy(ends[:, 1, :], pe_ends[1][:, 0:T]))
                c.link(v.tensor_copy(k.ends2[:, :], pe_two[0:2, 0:T]))
                c.link(v.tensor_tensor(k.end_mask[:, :, 0], o.id_col[:, :], ends[:, 0, :], ALU.is_equal))
                c.link(v.tensor_tensor(k.end_mask[:, :, 1], o.id_col[:, :], ends[:, 1, :], ALU.is_equal))
                dve.wait_ge(s["turned"], 1)
                c.link(v.tensor_copy(ends_t[:, :, :], pe_t[0:TB, :, :, 0]))
                c.link(v.tensor_copy(place[:, 0:1], k.iota_part[:, :]))
                c.link(v.tensor_scalar(place[:, 1:2], k.iota_part[:, :], float(TB), None, ALU.add))
                for b in range(2):
                    v.tensor_scalar(order[:, 0, b, :], k.iota_high[0:TB, 0:T], place[0:TB, b:b + 1], None, ALU.is_gt)
                    ins = v.tensor_scalar(order[:, 1, b, :], k.iota_high[0:TB, 0:T], place[0:TB, b:b + 1], None,
                                          ALU.is_lt)
                c.link(ins)
                for b in range(2):
                    v.scalar_tensor_tensor(k.handed[:, 0, b, :], ends[0:TB, 0, :], ends_t[:, 1, b:b + 1],
                                           order[:, 0, b, :], ALU.is_equal, ALU.mult)
                    ins = v.scalar_tensor_tensor(k.handed[:, 1, b, :], ends[0:TB, 1, :], ends_t[:, 0, b:b + 1],
                                                 order[:, 1, b, :], ALU.is_equal, ALU.mult)
                c.link(ins)
                c.end()

            @block.tensor
            def _(pe):
                pe.wait_ge(s["step"], 4)
                for a in range(2):
                    nc.tensor.matmul(pe_ends[a][:, 0:T], pick[:, a, :], o.id_col[:, :], start=True, stop=True)
                nc.tensor.matmul(pe_two[0:2, 0:T], pick2[:, :], o.id_col[:, :], start=True, stop=True)\
                    .then_inc(s["picked"], 1)
                pe.wait_ge(s["step"], 6)
                for a in range(2):
                    for b in range(2):
                        last = nc.tensor.transpose(pe_t[0:TB, a, b, :], ends[:, a, b * TB:(b + 1) * TB], k.ident[:, :])
                last.then_inc(s["turned"], 1)
        clear_semaphores(nc, list(s.values()))


def exchange_phase(k, tag):
    nc = k.nc
    with ExitStack() as st:
        part = k.sb(st, tag + "_part", [TB, 2, 2, D])
        total = k.sb(st, tag + "_total", [TB, 2, 2, D])
        ps = [k.ps(st, f"{tag}_ps{a}", [P, 2, D]) for a in range(2)]
        s = {x: k.sem(st, f"{tag}_{x}") for x in ("got", "made", "out", "put")}
        with nc.Block() as block:
            @block.sync
            def _(sp):
                for a in range(2):
                    for b in range(2):
                        sp.dma_start(part[:, a, b, :], k.end_sums[a, b * TB:(b + 1) * TB, :]).then_inc(s["got"], 16)
                sp.wait_ge(s["out"], 2)
                for a in range(2):
                    for b in range(2):
                        sp.dma_start(k.handed_sums[a, b * TB:(b + 1) * TB, :], total[:, a, b, :])\
                          .then_inc(s["put"], 16)
                sp.wait_ge(s["put"], 64)

            @block.vector
            def _(dve):
                dve.wait_ge(s["made"], 1)
                for a in range(2):
                    nc.vector.tensor_copy(total[:, a, :, :], ps[a][0:TB, :, :]).then_inc(s["out"], 1)

            @block.tensor
            def _(pe):
                pe.wait_ge(s["got"], 64)
                for a in range(2):
                    for out in range(2):
                        for b in range(2):
                            last = nc.tensor.matmul(ps[a][0:TB, out, :], k.handed[:, a, b, out * TB:(out + 1) * TB],
                                                    part[:, 1 - a, b, :], start=(b == 0), stop=(b == 1))
                last.then_inc(s["made"], 1)
        clear_semaphores(nc, list(s.values()))


def routing_phase(k, o, step, last_step, tag):
    nc = k.nc
    first, last = step == 0, step == last_step
    F = GT * D
    with ExitStack() as st:
        def sb(name, shape, dt=F32):
            return k.sb(st, f"{tag}_{name}", shape, dt)

        if not last:
            pair = sb("pair", [P, 2, GT, 2, D])
        if first:
            own = sb("own", [P, 2, GT, D])
            index_s = sb("index", [P, 2, 2, GT], I32)
        else:
            row_b = sb("row_b", [P, 2, GT, P])
            same = sb("same", [P, 2, GT, P])
            ends = sb("ends", [2, 2, GT, P])
            handed = sb("handed", [2, 2, GT, D])
            y_sb = sb("y", [P, 2, GT, D])
            acc = [k.ps(st, f"{tag}_acc{u}", [P, GT, D]) for u in range(2)]
        if last:
            sent = sb("sent", [P, 2, GT, D])
            last_s = sb("last", [P, 2, GT], I32)
        else:
            mask_s = sb("mask", [P, 2, GT, 2])
            end_out = sb("end_out", [2, 2, GT, D])
            end_ps = [k.ps(st, f"{tag}_end{u}", [P, GT, D]) for u in range(2)]
            weight = sb("weight", [P, 2, GT * NH])
        terms = sb("terms", [P, 2, 2, GT, D])
        dots = sb("dots", [P, 2, 2, GT * NH])
        logs = sb("logs", [P, 2, GT * NH])
        inv = sb("inv", [P, 2, GT * NH])
        score = sb("score", [P, 2, GT * NH])
        names = ["index", "free", "rows0", "rows1", "row_free", "same", "ends",
                 "summed", "acc_free", "copied", "squared", "product", "reduced", "log", "inverse", "scored",
                 "weighed", "valued", "paired", "masked", "end_made", "end_copied", "end_put0", "end_put1", "end_free",
                 "sent", "sent_free", "paired_put0", "paired_put1"]
        s = {x: k.sem(st, f"{tag}_{x}") for x in names}
        in0, out0 = k.gather_count, k.scatter_count
        k.gather_count += (EG // 2) * 32 * GT * first
        k.scatter_count += (EG // 2) * 16 * GT * last
        sems = list(s.values())
        s.update(own0=k.gathered[0], own1=k.gathered[1], put0=k.scattered[0], put1=k.scattered[1])

        def tiles(column, g):
            return column[:, bass.ds(g * GT, GT)]

        def edge_rows(table, g, width):
            return table[bass.ds(g * F, F), :].rearrange("(t p) c -> p t c", p=P)

        def by_head(ap):
            return ap.rearrange("p t (h d) -> p t h d", h=NH)

        def per_head(ap):
            return ap.rearrange("p (t h) -> p t h", h=NH).unsqueeze(3).broadcast_to([P, GT, NH, HD])

        with nc.Block() as block:
            @block.sync
            def _(sp):
                def load(g, i, u):
                    sp.wait_ge(s["row_free"], g + 1)
                    sp.dma_start(row_b[:, u, :, :].rearrange("p t e -> p (t e)"),
                                 o.id_row[bass.ds(g * F, F)].partition_broadcast(P)).then_inc(s[f"rows{u}"], 16)
                    sp.dma_start(handed[:, u, :, :], k.handed_sums[:, bass.ds(g * GT, GT), :])\
                      .then_inc(s[f"rows{u}"], 16)
                    if not last:
                        sp.dma_start(pair[:, u, :, :, :].rearrange("p t c d -> p t (c d)"),
                                     edge_rows(k.pairs, g, 2 * D)).then_inc(s[f"rows{u}"], 16)

                def store(g, i, u):
                    if first:
                        sp.wait_ge(s["paired"], g + 1)
                        sp.dma_start(edge_rows(k.pairs, g, 2 * D), pair[:, u, :, :, :]
                                     .rearrange("p t c d -> p t (c d)")).then_inc(s[f"paired_put{u}"], 16)
                    sp.wait_ge(s["end_copied"], g + 1)
                    sp.dma_start(k.end_sums[:, bass.ds(g * GT, GT), :], end_out[:, u, :, :])\
                      .then_inc(s[f"end_put{u}"], 16)

                def stored(g, i, u):
                    sp.wait_ge(s[f"end_put{u}"], i * 16 + 16)
                    if first:
                        sp.wait_ge(s[f"paired_put{u}"], i * 16 + 16)
                    sp.sem_inc(s["end_free"], 1)

                sp.sem_inc(s["end_free"], 2)
                with sp.Fori(0, EG // 2) as i:
                    for stage in ([] if first else [load]) + ([] if last else [store, stored]):
                        for u in range(2):
                            stage(i * 2 + u, i, u)

            @block.gpsimd
            def _(pool):
                def gather(g, i, u):
                    pool.wait_ge(s["free"], g + 1)
                    pool.sem_inc(k.paces, 1)
                    paced(pool, k, s["end_free"], g + 1)
                    nc.gpsimd.tensor_copy(index_s[:, u, 0, :], tiles(o.cap_far, g))
                    nc.gpsimd.tensor_copy(index_s[:, u, 1, :], tiles(o.cap_own, g)).then_inc(s["index"], 1)
                    paced(pool, k, s["index"], g + 1)
                    for j in range(GT):
                        for c, out in ((0, pair[:, u, j, 0, :]), (1, own[:, u, j, :])):
                            nc.gpsimd.indirect_dma_start(
                                out=out, out_offset=None, in_=k.layer1_halves,
                                in_offset=bass.IndirectOffsetOnAxis(ap=index_s[:, u, c, j:j + 1], axis=0))\
                                .then_inc(s[f"own{u}"], 16)

                def values(g, i, u):
                    paced(pool, k, s["weighed"], g + 1)
                    nc.gpsimd.tensor_tensor(
                        by_head(k.vals[:, bass.ds(g * GT, GT), :]), by_head(pair[:, u, :, 1, :]),
                        per_head(weight[:, u, :]), ALU.mult)\
                        .then_inc(s["valued"], 1)
                    paced(pool, k, s["end_made"], g + 1)
                    nc.gpsimd.tensor_copy(mask_s[:, u, :, :], tiles(k.end_mask, g)).then_inc(s["masked"], 1)
                    paced(pool, k, s["valued"], g + 1)
                    if not first:
                        pool.sem_inc(s["row_free"], 1)

                def scatter(g, i, u):
                    paced(pool, k, s["sent"], g + 1)
                    nc.gpsimd.tensor_copy(last_s[:, u, :], tiles(o.last_cap, g)).then_inc(s["index"], 1)
                    paced(pool, k, s["index"], g + 1)
                    for j in range(GT):
                        nc.gpsimd.indirect_dma_start(
                            out=k.layer1_halves,
                            out_offset=bass.IndirectOffsetOnAxis(ap=last_s[:, u, j:j + 1], axis=0),
                            in_=sent[:, u, j, :], in_offset=None, bounds_check=2 * N - 1, oob_is_err=False)\
                            .then_inc(s[f"put{u}"], 16)

                def scattered(g, i, u):
                    pool.wait_ge(s[f"put{u}"], i * (16 * GT) + (out0 + 16 * GT))
                    pool.sem_inc(s["sent_free"], 1)

                if not first and not last:
                    pool.sem_inc(s["row_free"], 2)
                if last:
                    pool.sem_inc(s["sent_free"], 2)
                with pool.Fori(0, EG // 2) as i:
                    for stage in ([gather] if first else []) + ([scatter, scattered] if last else [values]):
                        for u in range(2):
                            stage(i * 2 + u, i, u)

            @block.vector
            def _(dve):
                rows = 32 if last else 48

                def equal(g, i, u):
                    dve.wait_ge(s[f"rows{u}"], i * rows + rows)
                    dve.wait_ge(s["summed"], g + 1)
                    nc.vector.tensor_tensor(same[:, u, :, :], row_b[:, u, :, :],
                                            tiles(o.id_col, g).unsqueeze(2).broadcast_to([P, GT, P]),
                                            ALU.is_equal).then_inc(s["same"], 1)
                    nc.vector.tensor_tensor(ends[:, u, :, :], row_b[0:2, u, :, :],
                                            tiles(k.ends2, g).unsqueeze(2).broadcast_to([2, GT, P]),
                                            ALU.is_equal).then_inc(s["ends"], 1)

                def pairs(g, i, u):
                    dve.wait_ge(s[f"own{u}"], i * (32 * GT) + (in0 + 32 * GT))
                    nc.vector.tensor_tensor(pair[:, u, :, 1, :], pair[:, u, :, 0, :], own[:, u, :, :],
                                            ALU.add).then_inc(s["paired"], 1)

                def reduce(g, i, u):
                    if not last:
                        if not first:
                            dve.wait_ge(s["copied"], g + 1)
                        left = own[:, u, :, :] if first else y_sb[:, u, :, :]
                        nc.vector.tensor_tensor(terms[:, u, 0, :, :], left, pair[:, u, :, 0, :],
                                                ALU.mult).then_inc(s["product"], 1)
                        dve.wait_ge(s["product"], g + 1)
                    lo, hi = (0, 1) if first else (1, 2) if last else (0, 2)
                    if not first:
                        dve.wait_ge(s["squared"], g + 1)
                    nc.vector.tensor_reduce(dots[:, u, lo:hi, :],
                                            terms[:, u, lo:hi, :, :].rearrange("p c t (h d) -> p (c t h) d", h=NH),
                                            AX.X, ALU.add).then_inc(s["reduced"], 1)

                def scored(g, i, u):
                    if first:
                        return
                    dve.wait_ge(s["inverse"], g + 1)
                    if last:
                        dve.wait_ge(s["sent_free"], g + 1)
                        nc.vector.tensor_tensor(by_head(sent[:, u, :, :]), by_head(y_sb[:, u, :, :]),
                                                per_head(inv[:, u, :]),
                                                ALU.mult).then_inc(s["sent"], 1)
                        dve.wait_ge(s["sent"], g + 1)
                        dve.sem_inc(s["row_free"], 1)
                    else:
                        nc.vector.tensor_tensor(score[:, u, :], dots[:, u, 0, :], inv[:, u, :],
                                                ALU.mult).then_inc(s["scored"], 1)

                def freed(g, i, u):
                    if first:
                        dve.wait_ge(s["valued"], g + 1)
                        dve.sem_inc(s["free"], 1)

                if last:
                    dve.sem_inc(s["row_free"], 2)
                if first:
                    dve.sem_inc(s["free"], 2)
                with dve.Fori(0, EG // 2) as i:
                    for stage in ([pairs] if first else [equal]) + [reduce, scored, freed]:
                        for u in range(2):
                            stage(i * 2 + u, i, u)

            @block.scalar
            def _(act):
                def squares(g, i, u):
                    if first:
                        return
                    act.wait_ge(s["summed"], g + 3)
                    nc.scalar.activation(y_sb[:, u, :, :], acc[u][:, :, :], ACT.Copy).then_inc(s["copied"], 1)
                    act.wait_ge(s["copied"], g + 1)
                    nc.scalar.activation(terms[:, u, 1, :, :], y_sb[:, u, :, :], ACT.Square).then_inc(s["squared"], 1)

                def inverse(g, i, u):
                    if first:
                        return
                    act.wait_ge(s["reduced"], g + 1)
                    nc.scalar.activation(logs[:, u, :], dots[:, u, 1, :], ACT.Ln).then_inc(s["log"], 1)
                    act.wait_ge(s["log"], g + 1)
                    nc.scalar.activation(inv[:, u, :], logs[:, u, :], ACT.Exp, scale=-0.5).then_inc(s["inverse"], 1)

                def weigh(g, i, u):
                    if last:
                        return
                    act.wait_ge(s["reduced" if first else "scored"], g + 1)
                    nc.scalar.activation(weight[:, u, :], dots[:, u, 0, :] if first else score[:, u, :],
                                         ACT.Exp).then_inc(s["weighed"], 1)

                def copy_ends(g, i, u):
                    if last:
                        return
                    act.wait_ge(s["end_made"], g + 3)
                    act.wait_ge(s["end_free"], g + 1)
                    nc.scalar.activation(end_out[:, u, :, :], end_ps[u][0:2, :, :], ACT.Copy)\
                        .then_inc(s["end_copied"], 1)

                with act.Fori(0, EG // 2) as i:
                    for stage in (squares, inverse, weigh, copy_ends):
                        for u in range(2):
                            stage(i * 2 + u, i, u)

            @block.tensor
            def _(pe):
                def sums(g, i, u):
                    if first:
                        return
                    pe.wait_ge(s["same"], g + 1)
                    pe.wait_ge(s["ends"], g + 1)
                    for j in range(GT):
                        nc.tensor.matmul(acc[u][:, j, :], same[:, u, j, :], k.vals[:, bass.ds(g * GT + j, 1), :],
                                         start=True, stop=False)
                        mm = nc.tensor.matmul(acc[u][:, j, :], ends[:, u, j, :], handed[:, u, j, :], start=False,
                                              stop=True)
                    mm.then_inc(s["summed"], 1)

                def end_sums(g, i, u):
                    if last:
                        return
                    pe.wait_ge(s["valued"], g + 1)
                    paced(pe, k, s["masked"], g + 1)
                    for j in range(GT):
                        mm = nc.tensor.matmul(end_ps[u][0:2, j, :], mask_s[:, u, j, :],
                                              k.vals[:, bass.ds(g * GT + j, 1), :], start=True, stop=True)
                    mm.then_inc(s["end_made"], 1)

                pe.sem_inc(s["summed"], 2)
                pe.sem_inc(s["end_made"], 2)
                with pe.Fori(0, EG // 2) as i:
                    for stage in (sums, end_sums):
                        for u in range(2):
                            stage(i * 2 + u, i, u)
        clear_semaphores(nc, sems)


CH = 8
CT = T // CH
CE = CT * P
Q = NH * CH


def attention_weights_phase(k):
    nc = k.nc
    a = k.a
    with ExitStack() as st:
        w = k.sb(st, "aw_w", [P, 3, D])
        b = k.sb(st, "aw_b", [1, 3, D])
        g1 = k.sb(st, "aw_g1", [P, 1])
        be1 = k.sb(st, "aw_be1", [P, 1])
        ps = k.ps(st, "aw_ps", [P, 512])
        load_constants(k, [(w[:, i, :], a["L2_gnn_W" + c]) for i, c in enumerate("qkv")]
                       + [(b[:, i, :], a["L2_gnn_b" + c].rearrange("(r d) -> r d", r=1)) for i, c in enumerate("qkv")]
                       + [(g1[:, :], a["L2_gnn_g1"].rearrange("(p r) -> p r", r=1)),
                          (be1[:, :], a["L2_gnn_be1"].rearrange("(p r) -> p r", r=1)),
                          (k.wc[:, :], a["L2_gnn_Wc"]), (k.bc[:, :], a["L2_gnn_bc"].rearrange("(r d) -> r d", r=1)),
                          (k.wo[:, :], a["L2_gnn_Wo"]), (k.bo_row[:, :], a["L2_gnn_bo"].rearrange("(r d) -> r d", r=1))])
        s = {x: k.sem(st, "aw_" + x) for x in ("step", "made")}
        with nc.Block() as block:
            @block.vector
            def _(dve):
                v = nc.vector
                c = Chain(dve, s["step"], 4)
                c.begin(0)
                dve.wait_ge(s["made"], 1)
                c.link(v.tensor_tensor(k.qkv_b[:, :, :], ps[0:1, 0:3 * D].rearrange("p (i d) -> p i d", i=3),
                                       b[:, :, :], ALU.add))
                c.link(v.tensor_scalar(k.qkv_w[:, :, :], w[:, :, :], g1[:, 0:1], None, ALU.mult))
                c.link(v.tensor_scalar(k.qkv_w[:, 0, :], k.qkv_w[:, 0, :], HD ** -0.5, None, ALU.mult))
                c.link(v.tensor_scalar(k.qkv_b[:, 0, :], k.qkv_b[:, 0, :], HD ** -0.5, None, ALU.mult))
                c.end()

            @block.tensor
            def _(pe):
                nc.tensor.matmul(ps[0:1, 0:3 * D], be1[:, 0:1], w[:, :, :].rearrange("p i d -> p (i d)"), start=True,
                                 stop=True).then_inc(s["made"], 1)
        clear_semaphores(nc, list(s.values()))


def scores_phase(k, o):
    nc = k.nc
    C = 2 * GT
    with ExitStack() as st:
        rows = k.sb(st, "sc_rows", [P, 2, C, 2 * D])
        index_s = k.sb(st, "sc_index", [P, 2, 2, GT], I32)
        attr = k.sb(st, "sc_attr", [P, 2, GT, D])
        xin = k.sb(st, "sc_xin", [P, 2, C, D])
        xn = k.sb(st, "sc_xn", [P, 2, C, D])
        x_t = k.sb(st, "sc_x_t", [P, C, P])
        attr_t = k.sb(st, "sc_attr_t", [P, GT, P])
        query = k.sb(st, "sc_query", [P, GT, D])
        value = k.sb(st, "sc_value", [P, 2, GT, D])
        terms = k.sb(st, "sc_terms", [P, GT, D])
        dots = k.sb(st, "sc_dots", [P, GT, NH])
        norm = Norm(k, st, "sc_norm", cols=C, eps=EPS * EPS)
        t_ps = [k.ps(st, f"sc_t{b}", [P, GT, P]) for b in range(3)]
        out_ps = [k.ps(st, f"sc_o{b}", [P, GT, D]) for b in range(3)]
        attr_ps = k.ps(st, "sc_attr_ps", [P, 512])
        names = ["index", "free", "attr0", "attr1", "attr_tail", "attr_free", "added", "normed", "turned", "copied",
                 "made", "query", "value", "value_put0", "value_put1", "value_free", "product", "dots", "scored",
                 "emptied", "cleared"]
        s = {x: k.sem(st, "sc_" + x) for x in names}
        in0 = k.gather_count
        k.gather_count += (EG // 2) * 32 * GT
        full = E // (GT * P)
        assert full % 2 == 0 and full + 2 == EG

        with nc.Block() as block:
            @block.sync
            def _(sp):
                edge_attr = k.a["edge_attr_128"]

                def put(g, i, u):
                    sp.wait_ge(s["value"], g + 1)
                    sp.dma_start(k.values[bass.ds(g * (GT * P), GT * P), 0:D].rearrange("(t p) d -> p t d", p=P),
                                 value[:, u, :, :]).then_inc(s[f"value_put{u}"], 16)

                def done(g, i, u):
                    sp.wait_ge(s[f"value_put{u}"], i * 16 + 16)
                    sp.sem_inc(s["value_free"], 1)

                sp.wait_ge(s["cleared"], 1)
                sp.sem_inc(s["value_free"], 2)
                with sp.Fori(0, full // 2) as i:
                    for u in range(2):
                        g = i * 2 + u
                        sp.wait_ge(s["attr_free"], g + 1)
                        sp.dma_start(attr[:, u, :, :], edge_attr[bass.ds(g * (GT * P), GT * P), :]
                                     .rearrange("(t p) d -> p t d", p=P)).then_inc(s[f"attr{u}"], 16)
                    for stage in (put, done):
                        for u in range(2):
                            stage(i * 2 + u, i, u)
                at, left = full * GT * P, E - full * GT * P
                sp.wait_ge(s["attr_free"], full + 2)
                sp.dma_start(attr[0:left % P, 0, left // P, :], edge_attr[E - left % P:E, :]).then_inc(s["attr_tail"], 16)
                sp.wait_ge(s["attr_tail"], 16)
                sp.dma_start(attr[:, 0, 0:left // P, :], edge_attr[at:at + left // P * P, :]
                             .rearrange("(t p) d -> p t d", p=P)).then_inc(s["attr0"], 16)
                sp.sem_inc(s["attr1"], 16)
                for stage in (put, done):
                    for u in range(2):
                        stage(full + u, full // 2, u)

            @block.gpsimd
            def _(pool):
                with pool.Fori(0, EG // 2) as i:
                    for u in range(2):
                        g = i * 2 + u
                        paced(pool, k, s["free"], g + 1)
                        nc.gpsimd.tensor_copy(index_s[:, u, :, :], k.node_idx[:, :, bass.ds(g * GT, GT)])\
                            .then_inc(s["index"], 1)
                        paced(pool, k, s["index"], g + 1)
                        for c in range(2):
                            for j in range(GT):
                                nc.gpsimd.indirect_dma_start(
                                    out=rows[:, u, c * GT + j, :], out_offset=None, in_=k.layer1,
                                    in_offset=bass.IndirectOffsetOnAxis(ap=index_s[:, u, c, j:j + 1], axis=0))\
                                    .then_inc(k.gathered[u], 16)

            @block.vector
            def _(dve):
                norm.prepare(dve)
                nc.vector.memset(attr[:, :, :, :], 0.0).then_inc(s["cleared"], 1)
                dve.wait_ge(s["cleared"], 1)
                dve.sem_inc(s["free"], 2)
                dve.sem_inc(s["scored"], 1)

                def add(g, i, u):
                    dve.wait_ge(k.gathered[u], i * (32 * GT) + (in0 + 32 * GT))
                    nc.vector.tensor_tensor(xin[:, u, :, :], rows[:, u, :, 0:D], rows[:, u, :, D:2 * D],
                                            ALU.add).then_inc(s["added"], 1)
                    dve.wait_ge(s["added"], g + 1)
                    dve.sem_inc(s["free"], 1)
                    norm.statistics(dve, g, u, P, xin[:, u, :, :])

                def normalise(g, i, u):
                    norm.normalise(dve, g, u, P, xn[:, u, :, :], xin[:, u, :, :]).then_inc(s["normed"], 1)

                def score(g, i, u):
                    dve.wait_ge(s["query"], g + 1)
                    nc.vector.tensor_tensor(terms[:, :, :], query[:, :, :], out_ps[1][:, :, :],
                                            ALU.mult).then_inc(s["product"], 1)
                    dve.wait_ge(s["product"], g + 1)
                    nc.vector.tensor_reduce(dots[:, :, :], terms[:, :, :].rearrange("p t (h d) -> p t h d", h=NH),
                                            AX.X, ALU.add).then_inc(s["dots"], 1)
                    dve.wait_ge(s["dots"], g + 1)
                    nc.vector.tensor_tensor(k.scores[:, bass.ds(g * GT, GT), :], dots[:, :, :],
                                            attr_ps[:, 0:GT * NH].rearrange("p (t h) -> p t h", h=NH),
                                            ALU.add).then_inc(s["scored"], 1)

                with dve.Fori(0, EG // 2) as i:
                    for stage in (add, normalise, score):
                        for u in range(2):
                            stage(i * 2 + u, i, u)

            @block.scalar
            def _(act):
                def root(g, i, u):
                    norm.square_root(act, g, u, P, factor=1.0 + EPS)

                def copy(g, i, u):
                    act.wait_ge(s["turned"], g + 1)
                    act.wait_ge(s["made"], g + 1)
                    for b in range(2):
                        nc.scalar.activation(x_t[:, b * GT:(b + 1) * GT, :], t_ps[b][:, :, :], ACT.Copy)
                    nc.scalar.activation(attr_t[:, :, :], t_ps[2][:, :, :], ACT.Copy).then_inc(s["copied"], 1)

                def values(g, i, u):
                    act.wait_ge(s["made"], g + 2)
                    act.wait_ge(s["scored"], g + 1)
                    nc.scalar.activation(query[:, :, :], out_ps[0][:, :, :], ACT.Copy).then_inc(s["query"], 1)
                    act.wait_ge(s["value_free"], g + 1)
                    nc.scalar.activation(value[:, u, :, :], out_ps[2][:, :, :], ACT.Copy).then_inc(s["value"], 1)

                act.sem_inc(s["copied"], 1)
                with act.Fori(0, EG // 2) as i:
                    for u in range(2):
                        root(i * 2 + u, i, u)
                    for u in range(2):
                        copy(i * 2 + u, i, u)
                        values(i * 2 + u, i, u)

            @block.tensor
            def _(pe):
                pe.sem_inc(s["made"], 1)
                pe.sem_inc(s["attr_free"], 2)

                def turn(g, i, u):
                    pe.wait_ge(s["normed"], g + 1)
                    pe.wait_ge(s["copied"], g + 1)
                    pe.wait_ge(s[f"attr{u}"], i * 16 + 16)
                    for j in range(C):
                        nc.tensor.transpose(t_ps[j // GT][:, j % GT, :], xn[:, u, j, :], k.ident[:, :])
                    for j in range(GT):
                        mm = nc.tensor.transpose(t_ps[2][:, j, :], attr[:, u, j, :], k.ident[:, :])
                    mm.then_inc(s["turned"], 1)
                    pe.wait_ge(s["turned"], g + 1)
                    pe.sem_inc(s["attr_free"], 1)

                def project(g, i, u):
                    pe.wait_ge(s["copied"], g + 2)
                    pe.wait_ge(s["emptied"], g + 1)
                    for c in range(3):
                        for j in range(GT):
                            nc.tensor.matmul(out_ps[c][:, j, :], x_t[:, j if c == 0 else GT + j, :], k.qkv_w[:, c, :],
                                             start=True, stop=False)
                            nc.tensor.matmul(out_ps[c][:, j, :], k.ones[0:1, :], k.qkv_b[:, c, :], start=False,
                                             stop=True)
                    for j in range(GT):
                        nc.tensor.matmul(attr_ps[:, j * NH:(j + 1) * NH], attr_t[:, j, :], k.wc[:, :], start=True,
                                         stop=False)
                        mm = nc.tensor.matmul(attr_ps[:, j * NH:(j + 1) * NH], k.ones[0:1, :], k.bc[:, :],
                                              start=False, stop=True)
                    mm.then_inc(s["made"], 1)
                    pe.wait_ge(s["value"], g + 1)
                    pe.wait_ge(s["scored"], g + 2)
                    pe.sem_inc(s["emptied"], 1)

                pe.sem_inc(s["emptied"], 1)
                with pe.Fori(0, EG // 2) as i:
                    for u in range(2):
                        turn(i * 2 + u, i, u)
                        project(i * 2 + u, i, u)
        clear_semaphores(nc, norm.sems + list(s.values()))


def softmax_phase(k, o):
    nc = k.nc
    with ExitStack() as st:
        def sb(name, shape, dt=F32):
            return k.sb(st, "sm_" + name, shape, dt)

        packed = sb("packed", [P, CT, Q])
        ids = sb("ids", [Q, CE + 2])
        keep = sb("keep", [Q, 2, CE])
        gate = sb("gate", [Q, CE])
        edge = sb("edge", [Q, CE])
        score = sb("score", [Q, CE])
        p = sb("p", [Q, CE])
        run = sb("run", [Q, 2, CE])
        flags = sb("flags", [Q, 6])
        row = sb("row", [1, 6, Q])
        line = sb("line", [1, 4, Q])
        col = sb("col", [Q, 2])
        t_ps = k.ps(st, "sm_t_ps", [P, 4, P])
        row_ps = k.ps(st, "sm_row_ps", [P, 4, Q])
        end_ps = k.ps(st, "sm_end_ps", [P, 512])
        col_ps = k.ps(st, "sm_col_ps", [P, 512])
        back_ps = k.ps(st, "sm_back_ps", [P, 4, Q])
        s = {x: k.sem(st, "sm_" + x) for x in ("loaded", "set", "step", "packed", "turned", "copied", "rows", "ends",
                                               "cols", "exp", "back", "unpacked", "put")}
        with nc.Block() as block:
            @block.sync
            def _(sp):
                sp.wait_ge(s["set"], 1)
                for h in range(NH):
                    q = h * CH
                    sp.dma_start(ids[q:q + CH, 1:CE + 1], o.id_row[0:EP].rearrange("(c e) -> c e", c=CH))\
                      .then_inc(s["loaded"], 16)
                    sp.dma_start(ids[q:q + CH, CE + 1:CE + 2], o.id_row[1:EP + 1].rearrange("(c e) -> c e", c=CH)
                                 [:, CE - 1:CE], allow_slow_non_contiguous=True).then_inc(s["loaded"], 16)
                    sp.dma_start(ids[q + 1:q + CH, 0:1], o.id_row[0:EP].rearrange("(c e) -> c e", c=CH)
                                 [0:CH - 1, CE - 1:CE], allow_slow_non_contiguous=True).then_inc(s["loaded"], 16)
                sp.wait_ge(s["unpacked"], 1)
                sp.dma_start(k.values[:, D:D + NH].rearrange("(t p) h -> p t h", p=P), k.scores[:, :, :])\
                  .then_inc(s["put"], 16)
                sp.wait_ge(s["put"], 16)

            @block.vector
            def _(dve):
                v = nc.vector
                c = Chain(dve, s["step"], 0)
                c.begin(0)
                v.memset(ids[:, 0:1], -7.0).then_inc(s["set"], 1)
                for ch in range(CH):
                    ins = v.tensor_copy(packed[:, :, :].rearrange("p k (h c) -> p k h c", c=CH)[:, :, :, ch],
                                        k.scores[:, ch * CT:(ch + 1) * CT, :])
                ins.then_inc(s["packed"], 1)
                for kt in range(CT):
                    dve.wait_ge(s["turned"], kt + 1)
                    v.tensor_copy(score[:, kt * P:(kt + 1) * P], t_ps[0:Q, kt % 4, :]).then_inc(s["copied"], 1)
                dve.wait_ge(s["copied"], CT)
                dve.wait_ge(s["loaded"], 16 * 3 * NH)
                own = ids[:, 1:CE + 1]
                v.tensor_tensor(keep[:, 0, :], own, ids[:, 0:CE], ALU.is_equal)
                c.link(v.tensor_tensor(keep[:, 1, :], own, ids[:, 2:CE + 2], ALU.is_equal))
                v.tensor_copy(flags[:, 0:1], keep[:, 0, 0:1])
                v.tensor_copy(flags[:, 1:2], keep[:, 1, CE - 1:CE])
                c.link(v.tensor_tensor(flags[:, 2:3], ids[:, 1:2], ids[:, CE:CE + 1], ALU.is_equal))
                v.tensor_tensor(flags[:, 3:4], flags[:, 0:1], flags[:, 2:3], ALU.mult)
                c.link(v.tensor_tensor(flags[:, 4:5], flags[:, 1:2], flags[:, 2:3], ALU.mult))
                v.memset(keep[:, 0, 0:1], 0.0)
                c.link(v.memset(keep[:, 1, CE - 1:CE], 0.0))
                dve.wait_ge(s["rows"], 1)
                c.link(v.tensor_copy(row[:, 0:4, :], row_ps[0:1, :, :]))
                heads = row[:, 0:4, :].rearrange("p a (h c) -> p a h c", c=CH)
                v.memset(heads[:, 0, :, 0], 0.0)
                v.memset(heads[:, 1, :, CH - 1], 0.0)
                v.memset(heads[:, 2, :, 0], 0.0)
                c.link(v.memset(heads[:, 3, :, CH - 1], 0.0))

                def scan(d, data, additive, out):
                    def way(ap):
                        return ap[:, ::-1] if d else ap

                    c.link(v.tensor_scalar(edge[:, :], own, ids[:, (CE if d else 1):(CE + 1 if d else 2)], None,
                                           ALU.is_equal))
                    if additive:
                        c.link(v.tensor_copy(line[:, 0:2, :], row[:, (1 if d else 0):4:2, :]))
                        c.link(v.tensor_tensor_scan(way(out), way(keep[:, d, :]), way(data), 0.0, ALU.mult, ALU.add))
                    else:
                        c.link(v.tensor_scalar(edge[:, :], edge[:, :], BIG, -BIG, ALU.mult, ALU.add))
                        c.link(v.tensor_scalar(gate[:, :], keep[:, d, :], BIG, -BIG, ALU.mult, ALU.add))
                        c.link(v.tensor_scalar(line[:, 0:2, :], row[:, (1 if d else 0):4:2, :], BIG, -BIG, ALU.mult,
                                               ALU.add))
                        c.link(v.tensor_tensor_scan(way(out), way(gate[:, :]), way(data), -BIG, ALU.add, ALU.max))
                    scan.count += 1
                    c.link(v.tensor_copy(col[:, 0:1], out[:, 0:1] if d else out[:, CE - 1:CE]))
                    scan.ready.append(c.count)
                    dve.wait_ge(s["ends"], scan.count)
                    c.link(v.tensor_copy(line[:, 2, :], end_ps[0:1, 0:Q]))
                    ops = (ALU.mult, ALU.add) if additive else (ALU.add, ALU.max)
                    c.link(v.tensor_tensor_scan(way(line[:, 3, :]), way(line[:, 1, :]), way(line[:, 2, :]),
                                                0.0 if additive else -BIG, *ops))
                    c.link(v.memset(line[:, 2, :], 0.0))
                    shift = (line[:, 2, 0:Q - 1], line[:, 3, 1:Q], line[:, 0, 0:Q - 1]) if d else \
                        (line[:, 2, 1:Q], line[:, 3, 0:Q - 1], line[:, 0, 1:Q])
                    if not additive:
                        c.link(v.memset(line[:, 2, :], -BIG))
                    c.link(v.tensor_tensor(*shift, ops[0]))
                    scan.lines.append(c.count)
                    dve.wait_ge(s["cols"], scan.count)
                    c.link(v.tensor_copy(col[:, 1:2], col_ps[0:Q, 0:1]))
                    if additive:
                        c.link(v.scalar_tensor_tensor(out, edge[:, :], col[:, 1:2], out, ALU.mult, ALU.add))
                    else:
                        c.link(v.scalar_tensor_tensor(out, edge[:, :], col[:, 1:2], out, ALU.add, ALU.max))

                scan.count, scan.ready, scan.lines = 0, [], []
                scan(0, score[:, :], False, run[:, 0, :])
                scan(1, score[:, :], False, run[:, 1, :])
                c.link(v.tensor_tensor(run[:, 0, :], run[:, 0, :], run[:, 1, :], ALU.max))
                c.link(v.tensor_tensor(score[:, :], score[:, :], run[:, 0, :], ALU.subtract))
                softmax_phase.shifted = c.count
                dve.wait_ge(s["exp"], 1)
                scan(0, p[:, :], True, run[:, 0, :])
                scan(1, p[:, :], True, run[:, 1, :])
                c.link(v.tensor_tensor(run[:, 0, :], run[:, 0, :], run[:, 1, :], ALU.add))
                c.link(v.tensor_tensor(run[:, 0, :], run[:, 0, :], p[:, :], ALU.subtract))
                c.link(v.reciprocal(run[:, 1, :], run[:, 0, :]))
                c.link(v.tensor_tensor(p[:, :], p[:, :], run[:, 1, :], ALU.mult))
                softmax_phase.probs = c.count
                softmax_phase.ready, softmax_phase.lines = scan.ready, scan.lines
                scores = k.scores[:, :, :].rearrange("p (c k) h -> p k h c", c=CH)
                for kt in range(CT):
                    dve.wait_ge(s["back"], kt + 1)
                    ins = v.tensor_copy(scores[:, kt, :, :],
                                        back_ps[:, kt % 4, :].rearrange("p (h c) -> p h c", c=CH))
                    ins.then_inc(s["copied"], 1)
                dve.wait_ge(s["copied"], 2 * CT)
                dve.sem_inc(s["unpacked"], 1)

            @block.scalar
            def _(act):
                act.wait_ge(s["step"], softmax_phase.shifted)
                nc.scalar.activation(p[:, :], score[:, :], ACT.Exp).then_inc(s["exp"], 1)

            @block.tensor
            def _(pe):
                pe.wait_ge(s["packed"], 1)
                for kt in range(CT):
                    if kt >= 1:
                        pe.wait_ge(s["copied"], kt)
                    nc.tensor.transpose(t_ps[0:Q, kt % 4, :], packed[:, kt, :], k.ident[:, :])\
                        .then_inc(s["turned"], 1)
                pe.wait_ge(s["step"], 3)
                for a, f in enumerate((0, 1, 3, 4)):
                    ins = nc.tensor.transpose(row_ps[0:1, a, :], flags[:, f:f + 1], k.ident[0:Q, 0:Q])
                ins.then_inc(s["rows"], 1)
                for n in range(4):
                    pe.wait_ge(s["step"], softmax_phase.ready[n])
                    nc.tensor.transpose(end_ps[0:1, 0:Q], col[:, 0:1], k.ident[0:Q, 0:Q]).then_inc(s["ends"], 1)
                    pe.wait_ge(s["step"], softmax_phase.lines[n])
                    nc.tensor.transpose(col_ps[0:Q, 0:1], line[:, 2, :], k.ident[0:1, 0:1]).then_inc(s["cols"], 1)
                pe.wait_ge(s["step"], softmax_phase.probs)
                for kt in range(CT):
                    if kt >= 1:
                        pe.wait_ge(s["copied"], CT + kt)
                    nc.tensor.transpose(back_ps[:, kt % 4, :], p[:, kt * P:(kt + 1) * P], k.ident[0:Q, 0:Q])\
                        .then_inc(s["back"], 1)
        clear_semaphores(nc, list(s.values()))


def fill_phase(k, table, row):
    nc = k.nc
    with ExitStack() as st:
        rows = k.sb(st, "fill_rows", [P, NJ, D])
        load_constants(k, [(rows[:, j, :], row.partition_broadcast(P)) for j in range(NJ)])
        stored = k.sem(st, "fill_stored")
        with nc.Block() as block:
            @block.sync
            def _(sp):
                with sp.Fori(0, NG) as g:
                    sp.dma_start(node_rows(table, g, P), rows[:, :, :]).then_inc(stored, 16)
                sp.dma_start(node_rows(table, NG, TAILP), rows[0:TAILP, :, :]).then_inc(stored, 16)
                sp.wait_ge(stored, 16 * (NG + 1))
        clear_semaphores(nc, [stored])


def skewed_groups(front, back):
    def call(f, n):
        f(n, n // 2, n % 2, TAILP if n == NG else P)

    def run(eng):
        call(front, 0)
        with eng.Fori(0, NG // 2 - 1) as i:
            front(i * 2 + 1, i, 1, P)
            back(i * 2, i, 0, P)
            front(i * 2 + 2, i + 1, 0, P)
            back(i * 2 + 1, i, 1, P)
        for n in range(NG - 2, NG):
            call(front, n + 1)
            call(back, n)
        call(back, NG)
    return run


def transformer_phase(k):
    nc = k.nc
    a = k.a
    NB = 4
    with ExitStack() as st:
        def sb(name, shape):
            return k.sb(st, "tf_" + name, shape)

        w1, w2 = sb("w1", [P, NB * D]), sb("w2", [P, NB, D])
        b1, b2 = sb("b1", [P, NB]), sb("b2", [P, D])
        g2, be2 = sb("g2", [P, 1]), sb("be2", [P, 1])
        both = sb("both", [P, 2, NJ, 2 * D])
        msum = sb("msum", [P, 2, NJ, D])
        xin, x2, xm, xn, rest, x3in, x3 = (sb(x, [P, 2, NJ, D]) for x in
                                           ("xin", "x2", "xm", "xn", "rest", "x3in", "x3"))
        x_t = sb("x_t", [P, 2, NJ, P])
        hidden = sb("hidden", [P, 2, NB, 4 * P])
        norms = [Norm(k, st, f"tf_norm{m}") for m in range(3)]
        x_ps = [k.ps(st, f"tf_x_ps{b}", [P, 4, P]) for b in range(2)]
        h_ps = [k.ps(st, f"tf_h_ps{b}", [P, 4 * P]) for b in range(NB)]
        o_ps = [k.ps(st, f"tf_o_ps{b}", [P, 4, D]) for b in range(2)]
        names = ["ready0", "ready1", "free", "added", "x2_made", "xm_made", "rest_made", "rest_half", "normed",
                 "turned", "x_copied", "hidden_made", "bent", "out_made", "out_free", "x3_added", "x3_made",
                 "stored0", "stored1", "w_step", "w_made"]
        s = {x: k.sem(st, "tf_" + x) for x in names}
        load_constants(k, [(w1[:, :], a["L2_gnn_W1"]),
                           (w2[:, :, :], a["L2_gnn_W2"].rearrange("(b p) d -> p b d", p=P)),
                           (b2[:, :], a["L2_gnn_b2"].partition_broadcast(P)),
                           (g2[:, :], a["L2_gnn_g2"].rearrange("(p r) -> p r", r=1)),
                           (be2[:, :], a["L2_gnn_be2"].rearrange("(p r) -> p r", r=1))]
                       + [(b1[:, b:b + 1], a["L2_gnn_b1"][b * P:(b + 1) * P].rearrange("(p r) -> p r", r=1))
                          for b in range(NB)])
        with nc.Block() as block:
            @block.sync
            def _(sp):
                def load(n, i, u, p):
                    sp.wait_ge(s["free"], n + 1)
                    sp.dma_start(both[0:p, u, :, :], node_rows(k.layer1, n, p, 2 * D)).then_inc(s[f"ready{u}"], 16)
                    sp.dma_start(msum[0:p, u, :, :], node_rows(k.msum, n, p)).then_inc(s[f"ready{u}"], 16)

                def store(n, i, u, p):
                    sp.wait_ge(s["x3_made"], n + 1)
                    sp.dma_start(node_rows(k.x3, n, p), x3[0:p, u, :, :]).then_inc(s[f"stored{u}"], 16)

                sp.sem_inc(s["stored0"], 16)
                sp.sem_inc(s["stored1"], 16)
                skewed_groups(load, store)(sp)
                sp.wait_ge(s["stored0"], 16 * (NG // 2 + 2))
                sp.wait_ge(s["stored1"], 16 * (NG // 2 + 1))

            @block.gpsimd
            def _(pool):
                def add(n, i, u, p):
                    paced(pool, k, s[f"ready{u}"], i * 32 + 32)
                    nc.gpsimd.tensor_tensor(xin[0:p, u, :, :], both[0:p, u, :, 0:D], both[0:p, u, :, D:2 * D],
                                            ALU.add).then_inc(s["added"], 1)

                def leave(n, i, u, p):
                    paced(pool, k, s["xm_made"], n + 1)
                    nc.gpsimd.tensor_tensor(rest[0:p, u, :, :], x2[0:p, u, :, :], xm[0:p, u, :, :],
                                            ALU.add).then_inc(s["rest_half"], 1)
                    paced(pool, k, s["rest_half"], n + 1)
                    nc.gpsimd.tensor_tensor(rest[0:p, u, :, :], rest[0:p, u, :, :],
                                            b2[0:p, :].unsqueeze(1).broadcast_to([p, NJ, D]),
                                            ALU.add).then_inc(s["rest_made"], 1)

                skewed_groups(add, leave)(pool)

            @block.vector
            def _(dve):
                v = nc.vector
                for norm in norms:
                    norm.prepare(dve)
                dve.wait_ge(s["w_made"], 1)
                v.tensor_tensor(b1[:, :], b1[:, :], o_ps[0][:, 0, 0:NB], ALU.add).then_inc(s["w_step"], 1)
                v.tensor_scalar(w1[:, :], w1[:, :], g2[:, 0:1], None, ALU.mult).then_inc(s["w_step"], 1)
                dve.wait_ge(s["w_step"], 2)
                dve.sem_inc(s["free"], 2)
                dve.sem_inc(s["out_free"], 1)

                def front(n, i, u, p):
                    dve.wait_ge(s["added"], n + 1)
                    norms[0].statistics(dve, n, u, p, xin[:, u, :, :])
                    norms[0].normalise(dve, n, u, p, x2[:, u, :, :], xin[:, u, :, :]).then_inc(s["x2_made"], 1)
                    dve.wait_ge(s["x2_made"], n + 1)
                    dve.wait_ge(s[f"ready{u}"], i * 32 + 32)
                    v.tensor_tensor(xm[0:p, u, :, :], x2[0:p, u, :, :], msum[0:p, u, :, :],
                                    ALU.add).then_inc(s["xm_made"], 1)
                    dve.wait_ge(s["xm_made"], n + 1)
                    dve.sem_inc(s["free"], 1)
                    norms[1].statistics(dve, n, u, p, xm[:, u, :, :])
                    norms[1].normalise(dve, n, u, p, xn[:, u, :, :], xm[:, u, :, :]).then_inc(s["normed"], 1)

                def back(n, i, u, p):
                    dve.wait_ge(s["rest_made"], n + 1)
                    for b in range(2):
                        dve.wait_ge(s["out_made"], n * 2 + b + 3)
                        ins = v.tensor_tensor(x3in[0:p, u, 4 * b:4 * b + 4, :], rest[0:p, u, 4 * b:4 * b + 4, :],
                                              o_ps[b][0:p, :, :], ALU.add)
                    ins.then_inc(s["x3_added"], 1)
                    dve.wait_ge(s["x3_added"], n + 1)
                    dve.sem_inc(s["out_free"], 1)
                    norms[2].statistics(dve, n, u, p, x3in[:, u, :, :])
                    dve.wait_ge(s[f"stored{u}"], i * 16 + 16)
                    norms[2].normalise(dve, n, u, p, x3[:, u, :, :], x3in[:, u, :, :]).then_inc(s["x3_made"], 1)

                skewed_groups(front, back)(dve)

            @block.scalar
            def _(act):
                act.wait_ge(s["w_step"], 2)
                act.sem_inc(s["x_copied"], 1)
                act.sem_inc(s["bent"], NB)

                def front(n, i, u, p):
                    norms[0].square_root(act, n, u, p)
                    norms[1].square_root(act, n, u, p)
                    act.wait_ge(s["turned"], n + 1)
                    for b in range(2):
                        ins = nc.scalar.activation(x_t[:, u, 4 * b:4 * b + 4, 0:p], x_ps[b][:, :, 0:p], ACT.Copy)
                    ins.then_inc(s["x_copied"], 1)

                def back(n, i, u, p):
                    for h in range(2):
                        act.wait_ge(s["out_made"], n * 2 + h + 1)
                        for b in range(NB):
                            act.wait_ge(s["hidden_made"], n * (2 * NB) + h * NB + b + 1)
                            nc.scalar.activation(hidden[:, h, b, :], h_ps[b][:, :], ACT.Relu,
                                                 bias=b1[:, b:b + 1]).then_inc(s["bent"], 1)
                    norms[2].square_root(act, n, u, p)

                skewed_groups(front, back)(act)

            @block.tensor
            def _(pe):
                for b in range(NB):
                    mm = nc.tensor.matmul(o_ps[0][:, 0, b:b + 1], w1[:, b * P:(b + 1) * P], be2[:, 0:1], start=True,
                                          stop=True)
                mm.then_inc(s["w_made"], 1)
                pe.wait_ge(s["w_step"], 2)
                pe.sem_inc(s["out_made"], 2)

                def turn(n, i, u, p):
                    pe.wait_ge(s["normed"], n + 1)
                    pe.wait_ge(s["x_copied"], n + 1)
                    for j in range(NJ):
                        mm = nc.tensor.transpose(x_ps[j // 4][:, j % 4, 0:p], xn[0:p, u, j, :], k.ident[0:p, 0:p])
                    mm.then_inc(s["turned"], 1)

                def feed_forward(n, i, u, p):
                    pe.wait_ge(s["x_copied"], n + 2)
                    for h in range(2):
                        for b in range(NB):
                            pe.wait_ge(s["bent"], n * (2 * NB) + h * NB + b + 1)
                            nc.tensor.matmul(h_ps[b][:, :], w1[:, b * P:(b + 1) * P],
                                             x_t[:, u, 4 * h:4 * h + 4, :].rearrange("p j e -> p (j e)"), start=True,
                                             stop=True).then_inc(s["hidden_made"], 1)
                    pe.wait_ge(s["out_free"], n + 1)
                    for h in range(2):
                        pe.wait_ge(s["bent"], n * (2 * NB) + (h + 2) * NB)
                        for j in range(4):
                            for b in range(NB):
                                mm = nc.tensor.matmul(o_ps[h][0:p, j, :], hidden[:, h, b, j * P:j * P + p], w2[:, b, :],
                                                      start=b == 0, stop=b == NB - 1)
                        mm.then_inc(s["out_made"], 1)

                skewed_groups(turn, feed_forward)(pe)
        clear_semaphores(nc, [x for norm in norms for x in norm.sems] + list(s.values()))


def mean_layer_phase(k, out):
    nc = k.nc
    a = k.a
    with ExitStack() as st:
        def sb(name, shape):
            return k.sb(st, "ml_" + name, shape)

        w, w_t = sb("w", [P, D]), sb("w_t", [P, D])
        bias = sb("bias", [1, D])
        gamma, beta = sb("gamma", [P, D]), sb("beta", [P, D])
        mix = sb("mix", [P, 4])
        x3, agg, y, z, shifted, scaled, res = (sb(x, [P, 2, NJ, D]) for x in
                                               ("x3", "agg", "y", "z", "shifted", "scaled", "res"))
        norms = [Norm(k, st, f"ml_norm{m}") for m in range(2)]
        conv = Linear(k, st, "ml_conv", w_t[:, :], bias[:, :])
        w_ps = k.ps(st, "ml_w_ps", [P, 512])
        names = ["ready0", "ready1", "free", "summed", "y_made", "shifted", "z_made", "normed", "gained",
                 "added", "res_made", "stored0", "stored1", "w_turned", "w_step", "w_exp"]
        s = {x: k.sem(st, "ml_" + x) for x in names}
        load_constants(k, [(w[:, :], a["L3_gnn_W"]), (bias[:, :], a["L3_gnn_b"].rearrange("(r d) -> r d", r=1)),
                           (gamma[:, :], a["L3_gnn_gamma"].partition_broadcast(P)),
                           (beta[:, :], a["L3_gnn_beta"].partition_broadcast(P)),
                           (mix[:, 0:1], a["L3_gnn_alpha"].partition_broadcast(P))])
        with nc.Block() as block:
            @block.sync
            def _(sp):
                def load(n, i, u, p):
                    sp.wait_ge(s["free"], n + 1)
                    sp.dma_start(x3[0:p, u, :, :], node_rows(k.x3, n, p)).then_inc(s[f"ready{u}"], 16)
                    sp.dma_start(agg[0:p, u, :, :], node_rows(k.agg, n, p)).then_inc(s[f"ready{u}"], 16)

                def store(n, i, u, p):
                    sp.wait_ge(s["res_made"], n + 1)
                    sp.dma_start(node_rows(out, n, p), res[0:p, u, :, :]).then_inc(s[f"stored{u}"], 16)

                sp.sem_inc(s["stored0"], 16)
                sp.sem_inc(s["stored1"], 16)
                skewed_groups(load, store)(sp)
                sp.wait_ge(s["stored0"], 16 * (NG // 2 + 2))
                sp.wait_ge(s["stored1"], 16 * (NG // 2 + 1))

            @block.gpsimd
            def _(pool):
                def add(n, i, u, p):
                    paced(pool, k, s[f"ready{u}"], i * 32 + 32)
                    nc.gpsimd.tensor_tensor(agg[0:p, u, :, :], agg[0:p, u, :, :], x3[0:p, u, :, :],
                                            ALU.add).then_inc(s["summed"], 1)
                    nc.gpsimd.tensor_tensor(shifted[0:p, u, :, :], x3[0:p, u, :, :],
                                            beta[0:p, :].unsqueeze(1).broadcast_to([p, NJ, D]),
                                            ALU.add).then_inc(s["shifted"], 1)

                def gain(n, i, u, p):
                    paced(pool, k, s["normed"], n + 1)
                    nc.gpsimd.tensor_tensor(scaled[0:p, u, :, :], scaled[0:p, u, :, :],
                                            gamma[0:p, :].unsqueeze(1).broadcast_to([p, NJ, D]),
                                            ALU.mult).then_inc(s["gained"], 1)

                skewed_groups(add, gain)(pool)

            @block.vector
            def _(dve):
                v = nc.vector
                for norm in norms:
                    norm.prepare(dve)
                c = Chain(dve, s["w_step"], 5)
                c.begin(0)
                dve.wait_ge(s["w_exp"], 1)
                c.link(v.tensor_scalar(mix[:, 1:2], mix[:, 1:2], 1.0, None, ALU.add))
                c.link(v.reciprocal(mix[:, 2:3], mix[:, 1:2]))
                c.link(v.tensor_scalar(mix[:, 3:4], mix[:, 2:3], -1.0, 1.0, ALU.mult, ALU.add))
                c.link(v.tensor_scalar(bias[:, :], bias[:, :], mix[0:1, 2:3], None, ALU.mult))
                dve.wait_ge(s["w_turned"], 1)
                c.link(v.tensor_scalar(w_t[:, :], w_ps[:, 0:D], mix[:, 2:3], None, ALU.mult))
                c.end()
                dve.sem_inc(s["free"], 2)
                dve.sem_inc(conv.free, 1)

                def front(n, i, u, p):
                    dve.wait_ge(s["summed"], n + 1)
                    c = k.dinv2[0:p, n * NJ:n * NJ + NJ] if isinstance(n, int) else k.dinv2[0:p, bass.ds(n * NJ, NJ)]
                    v.tensor_tensor(y[0:p, u, :, :], agg[0:p, u, :, :], c.unsqueeze(2).broadcast_to([p, NJ, D]),
                                    ALU.mult).then_inc(s["y_made"], 1)

                def back(n, i, u, p):
                    dve.wait_ge(conv.made, n + 2)
                    dve.wait_ge(s[f"ready{u}"], i * 32 + 32)
                    for b in range(2):
                        ins = v.scalar_tensor_tensor(z[0:p, u, 4 * b:4 * b + 4, :], x3[0:p, u, 4 * b:4 * b + 4, :],
                                                     mix[0:p, 3:4], conv.out[b][0:p, :, :], ALU.mult, ALU.add)
                    ins.then_inc(s["z_made"], 1)
                    dve.wait_ge(s["z_made"], n + 1)
                    dve.wait_ge(s["shifted"], n + 1)
                    dve.sem_inc(conv.free, 1)
                    norms[0].statistics(dve, n, u, p, z[:, u, :, :])
                    norms[0].normalise(dve, n, u, p, scaled[:, u, :, :], z[:, u, :, :]).then_inc(s["normed"], 1)
                    dve.wait_ge(s["gained"], n + 1)
                    v.tensor_tensor(z[0:p, u, :, :], scaled[0:p, u, :, :], shifted[0:p, u, :, :],
                                    ALU.add).then_inc(s["added"], 1)
                    dve.wait_ge(s["added"], n + 1)
                    dve.sem_inc(s["free"], 1)
                    norms[1].statistics(dve, n, u, p, z[:, u, :, :])
                    dve.wait_ge(s[f"stored{u}"], i * 16 + 16)
                    norms[1].normalise(dve, n, u, p, res[:, u, :, :], z[:, u, :, :]).then_inc(s["res_made"], 1)

                skewed_groups(front, back)(dve)

            @block.scalar
            def _(act):
                nc.scalar.activation(mix[:, 1:2], mix[:, 0:1], ACT.Exp, scale=-1.0).then_inc(s["w_exp"], 1)
                act.sem_inc(conv.copied, 1)

                def back(n, i, u, p):
                    norms[0].square_root(act, n, u, p)
                    norms[1].square_root(act, n, u, p)

                skewed_groups(lambda n, i, u, p: conv.copy(act, n, p), back)(act)

            @block.tensor
            def _(pe):
                nc.tensor.transpose(w_ps[:, 0:D], w[:, :], k.ident[:, :]).then_inc(s["w_turned"], 1)
                pe.wait_ge(s["w_step"], 5)
                pe.sem_inc(conv.made, 1)

                def turn(n, i, u, p):
                    pe.wait_ge(s["y_made"], n + 1)
                    conv.turn(pe, n, p, y[:, u, :, :])

                skewed_groups(turn, lambda n, i, u, p: conv.product(pe, n, p))(pe)
        clear_semaphores(nc, [x for norm in norms for x in norm.sems] + conv.sems + list(s.values()))


ROUTING_STEPS = 4


def build(nc, a, out):
    k = Ctx(nc, None)
    k.a = a
    k.x, k.src, k.dst = a["x"], a["src"], a["dst"]
    with ExitStack() as st:
        k.paces = k.sem(st, "paces")
        k.gather_count = k.scatter_count = 0
        k.gathered = [k.sem(st, f"gathered{u}") for u in range(2)]
        k.scattered = [k.sem(st, f"scattered{u}") for u in range(2)]
        k.src_row = nc.dram_tensor("src_row", (EP + 1,), F32, kind="Internal").ap()
        k.dst_row = nc.dram_tensor("dst_row", (EP + 1,), F32, kind="Internal").ap()
        k.low_row = nc.dram_tensor("low_row", (EP,), F32, kind="Internal").ap()
        k.sorted4 = nc.dram_tensor("sorted4", (EP, 4), I32, kind="Internal").ap()
        k.sorted_row = nc.dram_tensor("sorted_row", (EP + 1,), F32, kind="Internal").ap()
        k.agg = nc.dram_tensor("agg", (N, D), F32, kind="Internal").ap()
        k.layer1 = nc.dram_tensor("layer1", (N, 2 * D), F32, kind="Internal").ap()
        k.layer1_halves = k.layer1.rearrange("n (c d) -> (n c) d", c=2)
        k.pairs = nc.dram_tensor("pairs", (EP, 2 * D), F32, kind="Internal").ap()
        k.end_sums = nc.dram_tensor("end_sums", (2, T, D), F32, kind="Internal").ap()
        k.handed_sums = nc.dram_tensor("handed_sums", (2, T, D), F32, kind="Internal").ap()
        k.values = nc.dram_tensor("values", (EP, D + NH), F32, kind="Internal").ap()
        k.msum = nc.dram_tensor("msum", (N, D), F32, kind="Internal").ap()
        k.x3 = nc.dram_tensor("x3", (N, D), F32, kind="Internal").ap()
        k.qkv_w = k.sb(st, "qkv_w", [P, 3, D])
        k.qkv_b = k.sb(st, "qkv_b", [1, 3, D])
        k.wc = k.sb(st, "wc", [P, NH])
        k.bc = k.sb(st, "bc", [1, NH])
        k.wo = k.sb(st, "wo", [P, D])
        k.bo_row = k.sb(st, "bo_row", [1, D])
        k.scores = k.sb(st, "scores", [P, T, NH])
        k.gcn_w = k.sb(st, "gcn_w", [P, D])
        k.gcn_c = k.sb(st, "gcn_c", [P, D])
        k.ones = k.sb(st, "ones", [P, P])
        k.zeros = k.sb(st, "zeros", [P, NJ * D])
        k.eps = k.sb(st, "eps", [P, 1])
        k.iota_row = k.sb(st, "iota_row", [P, P])
        k.iota_high = k.sb(st, "iota_high", [P, NCOL])
        k.iota_part = k.sb(st, "iota_part", [P, 1])
        k.ident = k.sb(st, "ident", [P, P])
        k.before = k.sb(st, "before", [P, P])
        k.earlier = k.sb(st, "earlier", [P, P])
        k.last_part = k.sb(st, "last_part", [P, 1])
        k.id_col = k.sb(st, "id_col", [P, 1, 2, T])
        k.node_idx = k.sb(st, "node_idx", [P, 2, T], I32)
        k.low_col = k.sb(st, "low_col", [P, 2, T])
        k.high_col = k.sb(st, "high_col", [P, 2, T])
        k.degree = k.sb(st, "degree", [P, NCOL])
        k.dinv = k.sb(st, "dinv", [P, NCOL])
        k.dinv2 = k.sb(st, "dinv2", [P, NCOL])
        k.start = k.sb(st, "start", [P, NCOL])
        k.dinv_src = k.sb(st, "dinv_src", [P, T])
        by_dst = Order(k.dst_row, k.id_col[:, 0, 1, :], k.sb(st, "d_prev", [P, T]), k.sb(st, "d_last", [P, T], I32))
        by_src = Order(k.sorted_row, k.sb(st, "s_id", [P, T]), k.sb(st, "s_prev", [P, T]),
                       k.sb(st, "s_last", [P, T], I32), k.sorted4, k.sb(st, "s_eid", [P, T], I32),
                       k.sb(st, "s_own", [P, T], I32), k.sb(st, "s_far", [P, T], I32),
                       k.sb(st, "s_last_cap", [P, T], I32))
        constants_phase(k)
        ids_phase(k)
        count_phase(k)
        rank_phase(k)
        order_phase(k, by_dst, "ord_d")
        order_phase(k, by_src, "ord_s")
        zero_phase(k, [k.agg])

        def by_degree(dve, out, rows, g):
            w = k.dinv_src[:, bass.ds(g * GT, GT)].unsqueeze(2).broadcast_to([P, GT, D])
            return nc.vector.tensor_tensor(out, rows, w, ALU.mult)

        segment_sum_phase(k, by_dst, k.x, D, k.node_idx[:, 0, :], k.agg, "gcn", by_degree)
        moments_phase(k)
        capsules_phase(k)
        with ExitStack() as routing:
            k.vals = k.sb(routing, "vals", [P, T, D])
            k.end_mask = k.sb(routing, "end_mask", [P, T, 2])
            k.ends2 = k.sb(routing, "ends2", [2, T])
            k.handed = k.sb(routing, "handed", [TB, 2, 2, T])
            routing_setup_phase(k, by_src)
            for step in range(ROUTING_STEPS + 1):
                if step:
                    exchange_phase(k, f"ex{step}")
                routing_phase(k, by_src, step, ROUTING_STEPS, f"ro{step}")
        attention_weights_phase(k)
        scores_phase(k, by_dst)
        softmax_phase(k, by_dst)
        fill_phase(k, k.msum, a["L2_gnn_bo"])

        def by_head(dve, out, rows, g):
            return nc.vector.tensor_tensor(
                out.rearrange("p t (h d) -> p t h d", h=NH), rows[:, :, 0:D].rearrange("p t (h d) -> p t h d", h=NH),
                rows[:, :, D:D + NH].unsqueeze(3).broadcast_to([P, GT, NH, HD]), ALU.mult)

        segment_sum_phase(k, by_src, k.values, D + NH, by_src.eid, k.msum, "msg", by_head, k.wo[:, :],
                          k.bo_row[:, :])
        transformer_phase(k)
        segment_sum_phase(k, by_dst, k.x3, D, k.node_idx[:, 0, :], k.agg, "mean", None)
        mean_layer_phase(k, out)


_INS = ["x", "src", "dst", "edge_attr_128"] + ["L0_gnn_W", "L0_gnn_b", "L0_gnn_gamma", "L0_gnn_beta", "L1_gnn_weight",
    "L1_gnn_bias"] + ["L2_gnn_" + x for x in ("Wq bq Wk bk Wv bv Wo bo Wc bc W1 b1 W2 b2 g1 be1 g2 be2").split()] + [
    "L3_gnn_" + x for x in "W b alpha gamma beta".split()]


def kernel(**inputs):
    import numpy as _np
    import concourse.bacc as _bacc
    from concourse import mybir as _mybir
    from concourse.bass_utils import run_bass_kernel_spmd as _run

    nc = _bacc.Bacc("TRN2", target_bir_lowering=False, num_devices=1)
    arrays, aps = {}, {}
    for name in _INS:
        v = _np.ascontiguousarray(inputs[name])
        arrays[f"in_{name}_dram"] = v
        aps[name] = nc.dram_tensor(f"in_{name}_dram", v.shape, _mybir.dt.from_np(v.dtype), kind="ExternalInput").ap()
    out = nc.dram_tensor("out_0_dram", (50000, 128), _mybir.dt.float32, kind="ExternalOutput").ap()
    build(nc, aps, out)
    r = _run(nc, [arrays], core_ids=[0])
    return r.results[0]["out_0_dram"]
```

```python
from contextlib import ExitStack

import concourse.bass as bass
from concourse import mybir

F32 = mybir.dt.float32
BF16 = mybir.dt.bfloat16
I32 = mybir.dt.int32
ALU = mybir.AluOpType
ACT = mybir.ActivationFunctionType
AX = mybir.AxisListType

P = 128
D = 128
N = 50000
E = 25000
NH = 8
HD = D // NH
T = 200
EP = T * P
TB = 100
GT = 4
EG = T // GT
NJ = 8
NG = N // (P * NJ)
TAILP = (N - NG * P * NJ) // NJ
NCOL = (NG + 1) * NJ
PAD_ID = N
EPS = 1e-5
BIG = 1.0e30
FAR = 1 << 20


def after(n, k=1):
    return n * k + k


class Ctx:

    def __init__(self, nc, stack):
        self.nc, self.stack = nc, stack
        self.sems = []
        self.dram = {}

    def sb(self, stack, name, shape, dt=F32):
        return stack.enter_context(self.nc.sbuf_tensor(name, shape, dt))

    def ps(self, stack, name, shape, dt=F32):
        return stack.enter_context(self.nc.psum_tensor(name, shape, dt))

    def sem(self, stack, name):
        return stack.enter_context(self.nc.semaphore(name))


def clear_semaphores(nc, sems):
    with nc.Block() as block:
        @block.gpsimd
        def _(pool):
            for s in sems:
                pool.sem_clear(s)


def ids_phase(k):
    nc = k.nc
    with ExitStack() as st:
        rows = k.sb(st, "ids_rows_i", [TB, 2, 2, P], I32)
        rows_f = k.sb(st, "ids_rows_f", [TB, 2, 2, P])
        low = k.sb(st, "ids_low_i", [TB, 2, 2, P], I32)
        low_f = k.sb(st, "ids_low_f", [TB, 2, 2, P])
        cols_i = k.sb(st, "ids_cols_i", [P, 2, T], I32)
        part = k.sb(st, "ids_part_i", [P, 2, 2, T], I32)
        minus = k.sb(st, "ids_minus", [1, 1])
        pt = k.ps(st, "ids_pt", [P, 2, 2, 256])
        padded = k.sem(st, "ids_padded")
        loaded = k.sem(st, "ids_loaded")
        step = k.sem(st, "ids_step")
        turned = k.sem(st, "ids_turned")
        stored = k.sem(st, "ids_stored")
        with nc.Block() as block:
            @block.sync
            def _(sp):
                sp.wait_ge(padded, 1)
                full = (E // P - TB)
                for a, ids in enumerate((k.src, k.dst)):
                    sp.dma_start(rows[:, a, 0, :], ids[0:TB * P].rearrange("(r e) -> r e", e=P)).then_inc(loaded, 16)
                    sp.dma_start(rows[0:full, a, 1, :],
                                 ids[TB * P:(TB + full) * P].rearrange("(r e) -> r e", e=P)).then_inc(loaded, 16)
                    sp.dma_start(rows[full:full + 1, a, 1, 0:E - (TB + full) * P],
                                 ids[(TB + full) * P:E].rearrange("(r e) -> r e", r=1)).then_inc(loaded, 16)
                sp.wait_ge(step, 3)
                for a, row in enumerate((k.src_row, k.dst_row)):
                    sp.dma_start(row[0:EP].rearrange("(b r e) -> r b e", b=2, e=P), rows_f[:, a]).then_inc(stored, 16)
                sp.dma_start(k.low_row[0:EP].rearrange("(b r e) -> r b e", b=2, e=P), low_f[:, 0]).then_inc(stored, 16)
                sp.dma_start(k.dst_row[EP:EP + 1].rearrange("(r e) -> r e", r=1), minus[:, :]).then_inc(stored, 16)
                sp.wait_ge(stored, 64)

            @block.vector
            def _(dve):
                nc.vector.memset(minus[:, :], -1.0)
                nc.vector.memset(rows[:, :, :, :], PAD_ID).then_inc(padded, 1)
                dve.wait_ge(loaded, 96)
                nc.vector.tensor_copy(rows_f[:, :, :, :], rows[:, :, :, :]).then_inc(step, 1)
                nc.vector.tensor_scalar(low[:, :, :, :], rows[:, :, :, :], 3, 127, ALU.arith_shift_right,
                                        ALU.bitwise_and).then_inc(step, 1)
                dve.wait_ge(step, 2)
                nc.vector.tensor_copy(low_f[:, :, :, :], low[:, :, :, :]).then_inc(step, 1)
                dve.wait_ge(turned, 1)
                nc.vector.tensor_copy(k.id_col[:, 0, :, :], pt[:, :, 0, 0:T]).then_inc(step, 1)
                nc.vector.tensor_copy(cols_i[:, :, :], pt[:, :, 0, 0:T]).then_inc(step, 1)
                nc.vector.tensor_copy(k.low_col[:, :, :], pt[:, :, 1, 0:T]).then_inc(step, 1)
                dve.wait_ge(step, 5)
                nc.vector.tensor_scalar(part[:, 0, :, :], cols_i[:, :, :], 10, 3, ALU.arith_shift_right,
                                        ALU.arith_shift_left).then_inc(step, 1)
                nc.vector.tensor_scalar(part[:, 1, :, :], cols_i[:, :, :], 7, None, ALU.bitwise_and).then_inc(step, 1)
                nc.vector.tensor_scalar(k.node_idx[:, :, :], k.id_col[:, 0, :, :], float(N - 1), None, ALU.min)
                dve.wait_ge(step, 8)
                nc.vector.tensor_tensor(k.high_col[:, :, :], part[:, 0, :, :], part[:, 1, :, :],
                                        ALU.add).then_inc(step, 1)
                dve.wait_ge(step, 9)

            @block.tensor
            def _(pe):
                pe.wait_ge(step, 3)
                for a in range(2):
                    for b in range(2):
                        nc.tensor.transpose(pt[:, a, 0, b * TB:(b + 1) * TB], rows_f[:, a, b, :], k.ident[0:TB, 0:TB])
                        last = nc.tensor.transpose(pt[:, a, 1, b * TB:(b + 1) * TB], low_f[:, a, b, :],
                                                   k.ident[0:TB, 0:TB])
                last.then_inc(turned, 1)
        k.done = [padded, loaded, step, turned, stored]
        clear_semaphores(nc, k.done)


def constants_phase(k):
    nc = k.nc
    with ExitStack() as st:
        it = k.sb(st, "cst_iota", [P, P], I32)
        ih = k.sb(st, "cst_iota_high", [P, NCOL], I32)
        ip = k.sb(st, "cst_iota_part", [P, 1], I32)
        made = k.sem(st, "cst_made")
        step = k.sem(st, "cst_step")
        with nc.Block() as block:
            @block.gpsimd
            def _(pool):
                nc.gpsimd.iota(it[:, :], pattern=[[1, P]], base=0, channel_multiplier=0).then_inc(made, 1)
                nc.gpsimd.iota(ih[:, :], pattern=[[1, NCOL]], base=0, channel_multiplier=0).then_inc(made, 1)
                nc.gpsimd.iota(ip[:, :], pattern=[[0, 1]], base=0, channel_multiplier=1).then_inc(made, 1)

            @block.vector
            def _(dve):
                nc.vector.memset(k.ones[:, :], 1.0).then_inc(step, 1)
                nc.vector.memset(k.ones3[:, :], 1.0)
                nc.vector.memset(k.zeros[:, :], 0.0).then_inc(step, 1)
                nc.vector.memset(k.eps[:, :], EPS).then_inc(step, 1)
                dve.wait_ge(made, 3)
                nc.vector.tensor_copy(k.iota_row[:, :], it[:, :]).then_inc(step, 1)
                nc.vector.tensor_copy(k.iota_high[:, :], ih[:, :]).then_inc(step, 1)
                nc.vector.tensor_copy(k.iota_part[:, :], ip[:, :]).then_inc(step, 1)
                dve.wait_ge(step, 6)
                nc.vector.tensor_scalar(k.ident[:, :], k.iota_row[:, :], k.iota_part[:, 0:1], None,
                                        ALU.is_equal).then_inc(step, 1)
                nc.vector.tensor_scalar(k.before[:, :], k.iota_row[:, :], k.iota_part[:, 0:1], None,
                                        ALU.is_gt).then_inc(step, 1)
                nc.vector.tensor_scalar(k.earlier[:, :], k.iota_row[:, :], k.iota_part[:, 0:1], None,
                                        ALU.is_lt).then_inc(step, 1)
                nc.vector.tensor_scalar(k.last_part[:, :], k.iota_part[:, :], float(P - 1), None,
                                        ALU.is_equal).then_inc(step, 1)
                dve.wait_ge(step, 10)
        clear_semaphores(nc, [made, step])


def count_phase(k):
    nc = k.nc
    with ExitStack() as st:
        hot_low = k.sb(st, "cnt_hot_low", [P, 2, 2, P], BF16)
        hot_high = k.sb(st, "cnt_hot_high", [P, 2, 2, NCOL], BF16)
        scan = k.sb(st, "cnt_scan", [P, NCOL])
        count = k.sb(st, "cnt_count", [P, NCOL])
        root = k.sb(st, "cnt_root", [P, NCOL])
        one_col = k.sb(st, "cnt_one", [P, NCOL])
        table = [k.ps(st, f"cnt_table{a}", [P, 512]) for a in range(2)]
        base = k.ps(st, "cnt_base", [P, 512])
        hot = k.sem(st, "cnt_hot")
        used = k.sem(st, "cnt_used")
        step = k.sem(st, "cnt_step")
        based = k.sem(st, "cnt_based")
        rooted = k.sem(st, "cnt_rooted")
        with nc.Block() as block:
            @block.vector
            def _(dve):
                with dve.Fori(0, T // 2) as i:
                    for u in range(2):
                        n = i * 2 + u
                        dve.wait_ge(used, after(n))
                        for a in range(2):
                            nc.vector.tensor_scalar(hot_low[:, u, a, :], k.iota_row[:, :],
                                                    k.low_col[:, a, bass.ds(n, 1)], None, ALU.is_equal)
                            nc.vector.tensor_scalar(hot_high[:, u, a, :], k.iota_high[:, :],
                                                    k.high_col[:, a, bass.ds(n, 1)], None,
                                                    ALU.is_equal).then_inc(hot, 1)
                nc.vector.memset(one_col[:, :], 1.0).then_inc(step, 1)
                dve.wait_ge(used, T + 2)
                nc.vector.tensor_copy(count[:, :], table[0][:, 0:NCOL]).then_inc(step, 1)
                nc.vector.tensor_scalar(k.degree[:, :], table[1][:, 0:NCOL], 1.0, None, ALU.add).then_inc(step, 1)
                dve.wait_ge(step, 3)
                nc.vector.tensor_tensor_scan(scan[:, :], one_col[:, :], count[:, :], 0.0, ALU.mult,
                                             ALU.add).then_inc(step, 1)
                dve.wait_ge(rooted, 1)
                nc.vector.reciprocal(k.dinv[:, :], root[:, :]).then_inc(step, 1)
                nc.vector.reciprocal(k.dinv2[:, :], k.degree[:, :]).then_inc(step, 1)
                dve.wait_ge(step, 6)
                dve.wait_ge(based, 1)
                nc.vector.tensor_tensor(scan[:, :], scan[:, :], count[:, :], ALU.subtract).then_inc(step, 1)
                dve.wait_ge(step, 7)
                nc.vector.tensor_scalar(k.start[:, :], scan[:, :], base[:, 0:1], None, ALU.add).then_inc(step, 1)
                dve.wait_ge(step, 8)

            @block.scalar
            def _(act):
                act.wait_ge(step, 3)
                nc.scalar.activation(root[:, :], k.degree[:, :], ACT.Sqrt).then_inc(rooted, 1)

            @block.tensor
            def _(pe):
                for a in range(2):
                    nc.tensor.matmul(table[a][:, 0:NCOL], k.zeros[:, 0:P], k.zeros[:, 0:NCOL], start=True, stop=False,
                                     skip_group_check=True)
                pe.sem_inc(used, 2)
                with pe.Fori(0, T // 2) as i:
                    for u in range(2):
                        n = i * 2 + u
                        pe.wait_ge(hot, after(n, 2))
                        for a in range(2):
                            mm = nc.tensor.matmul(table[a][:, 0:NCOL], hot_low[:, u, a, :], hot_high[:, u, a, :],
                                                  start=False, stop=False, skip_group_check=True)
                        mm.then_inc(used, 1)
                pe.wait_ge(step, 4)
                nc.tensor.matmul(base[:, 0:1], k.before[:, :], scan[:, NCOL - 1:NCOL], start=True,
                                 stop=True).then_inc(based, 1)
        clear_semaphores(nc, [hot, used, step, based, rooted])


def paced(eng, k, sem, value):
    eng.wait_ge(sem, value)
    eng.sem_inc(k.paces, 1)


def rank_phase(k):
    nc = k.nc
    with ExitStack() as st:
        row_b = k.sb(st, "rank_row_b", [P, 2, 2, GT * P])
        hot_low = k.sb(st, "rank_hot_low", [P, 2, P], BF16)
        hot_high = k.sb(st, "rank_hot_high", [P, 2, NCOL], BF16)
        low_hot = k.sb(st, "rank_low_hot", [P, 2, P])
        twin = k.sb(st, "rank_twin", [P, 2, P])
        table_sb = k.sb(st, "rank_table_sb", [P, 2, NCOL])
        picked = k.sb(st, "rank_picked", [P, 2, NCOL])
        parts = k.sb(st, "rank_parts", [P, 2, 2])
        ids_s = k.sb(st, "rank_ids_s", [P, 2 * GT])
        dinv_s = k.sb(st, "rank_dinv_s", [P, 2 * GT])
        eid = k.sb(st, "rank_eid", [P, T], I32)
        load4 = k.sb(st, "rank_payload", [P, T, 4], I32)
        rank = k.sb(st, "rank_rank", [P, 2 * GT], I32)
        load_s = k.sb(st, "rank_payload_slot", [P, 2 * GT, 4], I32)
        table = k.ps(st, "rank_table", [P, 512])
        look = [k.ps(st, f"rank_look{b}", [P, 2, 512]) for b in range(2)]
        names = ["numbered", "filled", "row_ready0", "row_ready1", "row_free", "hot", "marked", "copied", "added",
                 "looked", "look_free", "ids", "twins", "picks", "ranked", "slot_free0", "slot_free1"]
        s = {x: k.sem(st, "rank_" + x) for x in names}
        out0 = list(k.scatter_base)
        k.scatter_base = [x + (EG // 2) * 16 * GT for x in k.scatter_base]
        sems = list(s.values())
        s.update(sent0=k.scattered[0], sent1=k.scattered[1])
        with nc.Block() as block:
            @block.sync
            def _(sp):
                with sp.Fori(0, EG // 2) as i:
                    for u in range(2):
                        g = i * 2 + u
                        sp.wait_ge(s["row_free"], after(g))
                        for a, row in enumerate((k.low_row, k.src_row)):
                            sp.dma_start(row_b[:, u, a, :],
                                         row[bass.ds(g * (GT * P), GT * P)].partition_broadcast(P))\
                              .then_inc(s[f"row_ready{u}"], 16)

            @block.gpsimd
            def _(pool):
                nc.gpsimd.iota(eid[:, :], pattern=[[P, T]], base=0, channel_multiplier=1).then_inc(s["numbered"], 1)
                with pool.Fori(0, EG // 2) as i:
                    for u in range(2):
                        paced(pool, k, s["ranked"], after(i * 2 + u, GT))
                        for j in range(GT):
                            q = u * GT + j
                            nc.gpsimd.indirect_dma_start(
                                out=k.sorted4[:, :], out_offset=bass.IndirectOffsetOnAxis(ap=rank[:, q:q + 1], axis=0),
                                in_=load_s[:, q, :], in_offset=None).then_inc(s[f"sent{u}"], 16)
                    for u in range(2):
                        pool.wait_ge(s[f"sent{u}"], i * (16 * GT) + (out0[u] + 16 * GT))
                        pool.sem_inc(s[f"slot_free{u}"], 1)

            @block.vector
            def _(dve):
                dve.wait_ge(s["numbered"], 1)
                nc.vector.memset(load4[:, :, 3], 0)
                nc.vector.tensor_copy(load4[:, :, 2], eid[:, :])
                for a in range(2):
                    nc.vector.tensor_copy(load4[:, :, a], k.id_col[:, 0, a, :]).then_inc(s["filled"], 1)
                dve.wait_ge(s["filled"], 2)
                dve.sem_inc(s["row_free"], 2)
                dve.sem_inc(s["look_free"], 2)

                def one_hots(i, u, j):
                    n = i * (2 * GT) + u * GT + j
                    b = j % 2
                    dve.wait_ge(s["added"], n + 1)
                    nc.vector.tensor_scalar(hot_low[:, b, :], k.iota_row[:, :], k.low_col[:, 0, bass.ds(n, 1)],
                                            None, ALU.is_equal)
                    nc.vector.tensor_scalar(hot_high[:, b, :], k.iota_high[:, :], k.high_col[:, 0, bass.ds(n, 1)],
                                            None, ALU.is_equal).then_inc(s["hot"], 1)
                    if j == 0:
                        dve.wait_ge(s[f"row_ready{u}"], i * 32 + 32)
                        nc.vector.tensor_copy(ids_s[:, u * GT:(u + 1) * GT],
                                              k.id_col[:, 0, 0, bass.ds(n, GT)]).then_inc(s["ids"], 1)
                        dve.wait_ge(s["ids"], i * 2 + u + 1)
                    nc.vector.tensor_scalar(low_hot[:, b, :], row_b[:, u, 0, j * P:(j + 1) * P],
                                            k.iota_part[:, 0:1], None, ALU.is_equal).then_inc(s["marked"], 1)
                    nc.vector.scalar_tensor_tensor(
                        twin[:, b, :], row_b[:, u, 1, j * P:(j + 1) * P], ids_s[:, u * GT + j:u * GT + j + 1],
                        k.earlier[:, :], ALU.is_equal, ALU.mult,
                        accum_out=parts[:, b, 0:1]).then_inc(s["twins"], 1)
                    if j == GT - 1:
                        dve.wait_ge(s["twins"], n + 1)
                        dve.sem_inc(s["row_free"], 1)

                def read_back(i, u, j):
                    n = i * (2 * GT) + u * GT + j
                    b = j % 2
                    q = u * GT + j
                    dve.wait_ge(s["looked"], n + 1)
                    nc.vector.tensor_tensor_reduce(picked[:, 0, :], look[b][:, 0, 0:NCOL], hot_high[:, b, :], 1.0, 0.0,
                                                   ALU.mult, ALU.add, parts[:, b, 1:2]).then_inc(s["picks"], 1)
                    nc.vector.tensor_tensor_reduce(picked[:, 1, :], look[b][:, 1, 0:NCOL], hot_high[:, b, :], 1.0, 0.0,
                                                   ALU.mult, ALU.add, dinv_s[:, q:q + 1])\
                        .then_inc(s["look_free"], 1)
                    if j == 0:
                        dve.wait_ge(s[f"slot_free{u}"], i + 1)
                    dve.wait_ge(s["picks"], n + 1)
                    dve.wait_ge(s["twins"], n + 1)
                    if j == GT - 1:
                        dve.wait_ge(s["look_free"], n + 3)
                        nc.vector.tensor_copy(k.dinv_src[:, bass.ds(n - (GT - 1), GT)],
                                              dinv_s[:, u * GT:(u + 1) * GT])
                    nc.vector.tensor_copy(load_s[:, q, :], load4[:, bass.ds(n, 1), :])
                    nc.vector.tensor_tensor(rank[:, q:q + 1], parts[:, b, 0:1], parts[:, b, 1:2],
                                            ALU.add).then_inc(s["ranked"], 1)

                dve.sem_inc(s["slot_free0"], 1)
                dve.sem_inc(s["slot_free1"], 1)
                with dve.Fori(0, EG // 2) as i:
                    for u in range(2):
                        for j in range(GT):
                            one_hots(i, u, j)
                            read_back(i, u, j)

            @block.scalar
            def _(act):
                with act.Fori(0, T // 2) as i:
                    for b in range(2):
                        n = i * 2 + b
                        act.wait_ge(s["added"], n + 2)
                        nc.scalar.activation(table_sb[:, b, :], table[:, 0:NCOL], ACT.Copy).then_inc(s["copied"], 1)

            @block.tensor
            def _(pe):
                pe.sem_inc(s["added"], 1)
                nc.tensor.matmul(table[:, 0:NCOL], k.ident[:, :], k.start[:, :], start=True, stop=False,
                                 skip_group_check=True).then_inc(s["added"], 1)
                with pe.Fori(0, T // 2) as i:
                    for b in range(2):
                        n = i * 2 + b
                        pe.wait_ge(s["hot"], n + 1)
                        pe.wait_ge(s["copied"], n + 1)
                        pe.wait_ge(s["look_free"], n + 1)
                        pe.wait_ge(s["marked"], n + 1)
                        nc.tensor.matmul(look[b][:, 0, 0:NCOL], low_hot[:, b, :], table_sb[:, b, :], start=True,
                                         stop=True)
                        nc.tensor.matmul(look[b][:, 1, 0:NCOL], low_hot[:, b, :], k.dinv[:, :], start=True,
                                         stop=True).then_inc(s["looked"], 1)
                        nc.tensor.matmul(table[:, 0:NCOL], hot_low[:, b, :], hot_high[:, b, :], start=False,
                                         stop=False, skip_group_check=True).then_inc(s["added"], 1)
        clear_semaphores(nc, sems)


def order_phase(k, order, tag):
    nc = k.nc
    sorted_ = order.payload is not None
    with ExitStack() as st:
        row4 = k.sb(st, tag + "_row4", [TB, 2, P, 4], I32)
        row3 = k.sb(st, tag + "_row3", [TB, 2, 3, P])
        nxt = k.sb(st, tag + "_next", [TB, 2, P])
        minus = k.sb(st, tag + "_minus", [1, 1])
        cols = k.sb(st, tag + "_cols", [P, 4, T])
        same = k.sb(st, tag + "_same", [P, T])
        pt = k.ps(st, tag + "_pt", [P, 4, 512])
        s = {x: k.sem(st, f"{tag}_{x}") for x in ("loaded", "stored", "step", "turned", "shifted")}
        with nc.Block() as block:
            @block.sync
            def _(sp):
                if sorted_:
                    sp.dma_start(row4[:, :, :, :], order.payload.rearrange("(b r e) c -> r b e c", b=2, e=P))\
                      .then_inc(s["loaded"], 16)
                    sp.wait_ge(s["step"], 4)
                    sp.dma_start(order.id_row[0:EP].rearrange("(b r e) -> r b e", b=2, e=P), row3[:, :, 0, :])\
                      .then_inc(s["stored"], 16)
                    sp.dma_start(order.id_row[EP:EP + 1].rearrange("(r e) -> r e", r=1), minus[:, :])\
                      .then_inc(s["stored"], 16)
                    sp.wait_ge(s["stored"], 32)
                sp.dma_start(nxt[:, :, :], order.id_row[1:EP + 1].rearrange("(b r e) -> r b e", b=2, e=P))\
                  .then_inc(s["shifted"], 16)
                sp.wait_ge(s["shifted"], 16)

            @block.vector
            def _(dve):
                at = 0
                if sorted_:
                    nc.vector.memset(minus[:, :], -1.0).then_inc(s["step"], 1)
                    dve.wait_ge(s["loaded"], 16)
                    for c in range(3):
                        nc.vector.tensor_copy(row3[:, :, c, :], row4[:, :, :, c]).then_inc(s["step"], 1)
                    dve.wait_ge(s["turned"], 1)
                    for c in range(3):
                        nc.vector.tensor_copy(cols[:, c, :], pt[:, c, 0:T]).then_inc(s["step"], 1)
                    dve.wait_ge(s["step"], 7)
                    nc.vector.tensor_copy(order.id_col[:, :], cols[:, 0, :]).then_inc(s["step"], 1)
                    nc.vector.tensor_copy(order.eid[:, :], cols[:, 2, :]).then_inc(s["step"], 1)
                    for c, out in ((0, order.cap_own), (1, order.cap_far)):
                        nc.vector.tensor_scalar(same[:, :], cols[:, c, :], float(N - 1), None,
                                                ALU.min).then_inc(s["step"], 1)
                        at = 10 + 2 * c
                        dve.wait_ge(s["step"], at)
                        nc.vector.tensor_scalar(out[:, :], same[:, :], 2.0, 1.0, ALU.mult,
                                                ALU.add).then_inc(s["step"], 1)
                        dve.wait_ge(s["step"], at + 1)
                    at = 13
                dve.wait_ge(s["turned"], 2)
                nc.vector.tensor_copy(cols[:, 3, :], pt[:, 3, 0:T]).then_inc(s["step"], 1)
                nc.vector.memset(order.prev_col[:, 0:1], -5.0).then_inc(s["step"], 1)
                nc.vector.tensor_scalar(order.prev_col[:, 1:T], order.id_col[:, 0:T - 1], 5.0, k.last_part[:, 0:1],
                                        ALU.add, ALU.mult).then_inc(s["step"], 1)
                dve.wait_ge(s["step"], at + 3)
                nc.vector.tensor_scalar(order.prev_col[:, 1:T], order.prev_col[:, 1:T], -5.0, None,
                                        ALU.add).then_inc(s["step"], 1)
                nc.vector.tensor_tensor(same[:, :], order.id_col[:, :], cols[:, 3, :],
                                        ALU.is_equal).then_inc(s["step"], 1)
                dve.wait_ge(s["step"], at + 5)
                nc.vector.scalar_tensor_tensor(cols[:, 3, :], same[:, :], float(FAR), order.id_col[:, :], ALU.mult,
                                               ALU.add).then_inc(s["step"], 1)
                dve.wait_ge(s["step"], at + 6)
                nc.vector.tensor_copy(order.last_idx[:, :], cols[:, 3, :]).then_inc(s["step"], 1)
                if sorted_:
                    nc.vector.tensor_scalar(order.last_cap[:, :], cols[:, 3, :], 2.0, 1.0, ALU.mult,
                                            ALU.add).then_inc(s["step"], 1)

            @block.tensor
            def _(pe):
                if sorted_:
                    pe.wait_ge(s["step"], 4)
                    for c in range(3):
                        for b in range(2):
                            last = nc.tensor.transpose(pt[:, c, b * TB:(b + 1) * TB], row3[:, b, c, :],
                                                       k.ident[0:TB, 0:TB])
                    last.then_inc(s["turned"], 1)
                else:
                    pe.sem_inc(s["turned"], 1)
                pe.wait_ge(s["shifted"], 16)
                for b in range(2):
                    last = nc.tensor.transpose(pt[:, 3, b * TB:(b + 1) * TB], nxt[:, b, :], k.ident[0:TB, 0:TB])
                last.then_inc(s["turned"], 1)
        clear_semaphores(nc, list(s.values()))


def segment_sum_phase(k, order, table, width, index, dest, tag, weigh, project=None, bias=None):
    nc = k.nc
    with ExitStack() as st:
        rows = k.sb(st, tag + "_rows", [P, 2, GT, width])
        index_s = k.sb(st, tag + "_index", [P, 2, GT], I32)
        last_s = k.sb(st, tag + "_last", [P, 2, GT], I32)
        row_b = k.sb(st, tag + "_row_b", [P, 2, GT, P])
        same = k.sb(st, tag + "_same", [P, 2, GT, P])
        cross = k.sb(st, tag + "_cross", [P, 2, GT, P])
        vals = k.sb(st, tag + "_vals", [P, 2, GT, D]) if weigh else rows
        sums = k.sb(st, tag + "_sums", [P, 2, GT, D])
        acc = [k.ps(st, f"{tag}_acc{j}", [P, 512]) for j in range(GT)]
        if project is not None:
            turned_sb = k.sb(st, tag + "_turned_sb", [P, 2, GT, P])
            sent = k.sb(st, tag + "_sent", [P, 2, GT, D])
            pt = [k.ps(st, f"{tag}_pt{u}", [P, GT, P]) for u in range(2)]
            pp = [k.ps(st, f"{tag}_pp{u}", [P, GT, D]) for u in range(2)]
        else:
            sent = sums
        names = ["index", "rows_free", "row_ready0", "row_ready1", "row_free", "masks", "masks_free",
                 "weighed", "summed", "copied", "sent_free", "start", "turned", "turned_copied",
                 "projected", "project_copied", "picked"]
        s = {x: k.sem(st, f"{tag}_{x}") for x in names}
        in0, out0 = list(k.gather_base), list(k.scatter_base)
        k.gather_base = [x + (EG // 2) * 16 * GT for x in k.gather_base]
        k.scatter_base = [x + (EG // 2) * 16 * GT for x in k.scatter_base]
        sems = list(s.values())
        s.update(got0=k.gathered[0], got1=k.gathered[1], put0=k.scattered[0], put1=k.scattered[1])
        with nc.Block() as block:
            @block.sync
            def _(sp):
                with sp.Fori(0, EG // 2) as i:
                    for u in range(2):
                        g = i * 2 + u
                        sp.wait_ge(s["row_free"], after(g))
                        sp.dma_start(row_b[:, u, :, :].rearrange("p t e -> p (t e)"),
                                     order.id_row[bass.ds(g * (GT * P), GT * P)].partition_broadcast(P))\
                          .then_inc(s[f"row_ready{u}"], 16)

            @block.gpsimd
            def _(pool):
                pool.sem_inc(s["sent_free"], 2)
                with pool.Fori(0, EG // 2) as i:
                    for u in range(2):
                        g = i * 2 + u
                        pool.wait_ge(s["rows_free"], after(g))
                        pool.sem_inc(k.paces, 1)
                        nc.gpsimd.tensor_copy(index_s[:, u, :], index[:, bass.ds(g * GT, GT)])
                        nc.gpsimd.tensor_copy(last_s[:, u, :], order.last_idx[:, bass.ds(g * GT, GT)])\
                            .then_inc(s["index"], 1)
                        paced(pool, k, s["index"], after(g))
                        for j in range(GT):
                            nc.gpsimd.indirect_dma_start(
                                out=rows[:, u, j, :], out_offset=None, in_=table,
                                in_offset=bass.IndirectOffsetOnAxis(ap=index_s[:, u, j:j + 1], axis=0))\
                                .then_inc(s[f"got{u}"], 16)
                    for u in range(2):
                        paced(pool, k, s["project_copied" if project is not None else "copied"],
                              after(i * 2 + u) if project is not None else after(i * 2 + u, GT) + 1)
                        for j in range(GT):
                            nc.gpsimd.indirect_dma_start(
                                out=dest, out_offset=bass.IndirectOffsetOnAxis(ap=last_s[:, u, j:j + 1], axis=0),
                                in_=sent[:, u, j, :], in_offset=None, bounds_check=N - 1, oob_is_err=False)\
                                .then_inc(s[f"put{u}"], 16)
                    for u in range(2):
                        pool.wait_ge(s[f"put{u}"], i * (16 * GT) + (out0[u] + 16 * GT))
                        pool.sem_inc(s["sent_free"], 1)

            @block.vector
            def _(dve):
                nc.vector.memset(sums[:, 1, GT - 1, :], 0.0).then_inc(s["start"], 1)
                dve.wait_ge(s["start"], 1)
                dve.sem_inc(s["row_free"], 2)
                if weigh:
                    dve.sem_inc(s["rows_free"], 2)
                with dve.Fori(0, EG // 2) as i:
                    for u in range(2):
                        g = i * 2 + u
                        dve.wait_ge(s["masks_free"], after(g))
                        dve.wait_ge(s[f"row_ready{u}"], i * 16 + 16)
                        cols = [c[:, bass.ds(g * GT, GT)].unsqueeze(2).broadcast_to([P, GT, P])
                                for c in (order.id_col, order.prev_col)]
                        nc.vector.tensor_tensor(same[:, u, :, :], row_b[:, u, :, :], cols[0], ALU.is_equal)
                        nc.vector.tensor_tensor(cross[:, u, :, :], row_b[:, u, :, :], cols[1],
                                                ALU.is_equal).then_inc(s["masks"], 1)
                        dve.wait_ge(s["masks"], after(g))
                        dve.sem_inc(s["row_free"], 1)
                        dve.wait_ge(s[f"got{u}"], i * (16 * GT) + (in0[u] + 16 * GT))
                        if weigh:
                            weigh(dve, vals[:, u, :, :], rows[:, u, :, :], g).then_inc(s["weighed"], 1)
                            dve.wait_ge(s["weighed"], after(g))
                            dve.sem_inc(s["rows_free"], 1)

            @block.scalar
            def _(act):
                act.sem_inc(s["copied"], 1)
                with act.Fori(0, EG // 2) as i:
                    for u in range(2):
                        g = i * 2 + u
                        for j in range(GT):
                            if j == 0:
                                act.wait_ge(s["sent_free"], after(g))
                            act.wait_ge(s["summed"], g * GT + j + 1)
                            nc.scalar.activation(sums[:, u, j, :], acc[j][:, 0:D], ACT.Copy)\
                                .then_inc(s["copied"], 1)
                        if project is not None:
                            act.wait_ge(s["turned"], after(g))
                            nc.scalar.activation(turned_sb[:, u, :, :], pt[u][:, :, :], ACT.Copy)\
                                .then_inc(s["turned_copied"], 1)
                            act.wait_ge(s["projected"], after(g))
                            nc.scalar.activation(sent[:, u, :, :], pp[u][:, :, :], ACT.Copy)\
                                .then_inc(s["project_copied"], 1)

            @block.tensor
            def _(pe):
                pe.wait_ge(s["start"], 1)
                pe.sem_inc(s["masks_free"], 2)
                if not weigh:
                    pe.sem_inc(s["rows_free"], 2)
                with pe.Fori(0, EG // 2) as i:
                    for u in range(2):
                        g = i * 2 + u
                        pe.wait_ge(s["masks"], after(g))
                        if weigh:
                            pe.wait_ge(s["weighed"], after(g))
                        else:
                            pe.wait_ge(s[f"got{u}"], i * (16 * GT) + (in0[u] + 16 * GT))
                        for j in range(GT):
                            nc.tensor.matmul(acc[j][:, 0:D], same[:, u, j, :], vals[:, u, j, :], start=True,
                                             stop=False)
                            before = sums[:, u, j - 1, :] if j else sums[:, 1 - u, GT - 1, :]
                            pe.wait_ge(s["copied"], g * GT + j + 1)
                            mm = nc.tensor.matmul(acc[j][:, 0:D], cross[:, u, j, :], before, start=False, stop=True)
                            mm.then_inc(s["summed"], 1)
                        pe.wait_ge(s["summed"], after(g, GT))
                        pe.sem_inc(s["masks_free"], 1)
                        if not weigh:
                            pe.sem_inc(s["rows_free"], 1)
                        if project is not None:
                            pe.wait_ge(s["copied"], after(g, GT) + 1)
                            for j in range(GT):
                                mm = nc.tensor.transpose(pt[u][:, j, :], sums[:, u, j, :], k.ident[:, :])
                            mm.then_inc(s["turned"], 1)
                            pe.wait_ge(s["turned_copied"], after(g))
                            for j in range(GT):
                                nc.tensor.matmul(pp[u][:, j, :], turned_sb[:, u, j, :], project, start=True, stop=False)
                                mm = nc.tensor.matmul(pp[u][:, j, :], k.ones[0:1, :], bias, start=False, stop=True)
                            mm.then_inc(s["projected"], 1)
        clear_semaphores(nc, sems)


def zero_phase(k, tables):
    nc = k.nc
    with ExitStack() as st:
        stored = k.sem(st, "zero_stored")
        with nc.Block() as block:
            @block.sync
            def _(sp):
                for m, table in enumerate(tables):
                    with sp.Fori(0, NG) as g:
                        sp.dma_start(table[bass.ds(g * (P * NJ), P * NJ), :].rearrange("(p j) d -> p (j d)", p=P),
                                     k.zeros[:, :]).then_inc(stored, 16)
                    sp.dma_start(table[NG * P * NJ:N, :].rearrange("(p j) d -> p (j d)", p=TAILP),
                                 k.zeros[0:TAILP, :]).then_inc(stored, 16)
                sp.wait_ge(stored, 16 * (NG + 1) * len(tables))
        clear_semaphores(nc, [stored])


class Order:

    def __init__(self, id_row, id_col, prev_col, last_idx, payload=None, eid=None, cap_own=None, cap_far=None,
                 last_cap=None):
        self.id_row, self.id_col, self.prev_col, self.last_idx = id_row, id_col, prev_col, last_idx
        self.payload, self.eid, self.cap_own, self.cap_far, self.last_cap = payload, eid, cap_own, cap_far, last_cap


class Chain:

    def __init__(self, eng, sem, steps):
        self.eng, self.sem, self.steps = eng, sem, steps

    def begin(self, n):
        self.n, self.count = n, 0

    def link(self, ins):
        self.count += 1
        ins.then_inc(self.sem, 1)
        self.eng.wait_ge(self.sem, self.n * self.steps + self.count)

    def end(self):
        assert self.count == self.steps


def staggered(eng, *stages, full=NG, tail=TAILP):
    most = max(lag for _, lag in stages)

    def static(m):
        for stage, lag in stages:
            n = m - lag
            if 0 <= n < full or (n == full and tail):
                stage(n, n // 2, n % 2, tail if n == full else P)

    pairs = (full - most) // 2
    for m in range(most):
        static(m)
    with eng.Fori(0, pairs) as i:
        for m in (most, most + 1):
            for stage, lag in stages:
                n = m - lag
                stage(i * 2 + n, i + n // 2, n % 2, P)
    for m in range(most + 2 * pairs, full + 1 + most):
        static(m)


def node_rows(table, n, p, width=D):
    at = slice(n * P * NJ, n * P * NJ + p * NJ) if isinstance(n, int) else bass.ds(n * (P * NJ), P * NJ)
    return table[at, :].rearrange("(p j) d -> p j d", p=p)


class Linear:

    def __init__(self, k, st, tag, weight, bias=None, cols=NJ, out=None, spare=None):
        self.k, self.weight, self.bias, self.cols = k, weight, bias, cols
        banks = cols // 4
        self.turned_ps = spare or [k.ps(st, f"{tag}_tps{b}", [P, 4, P]) for b in range(banks)]
        self.out = out or [k.ps(st, f"{tag}_out{b}", [P, 4, D]) for b in range(banks)]
        self.turned_sb = k.sb(st, f"{tag}_tsb", [P, cols, P])
        self.turned = k.sem(st, tag + "_turned")
        self.copied = k.sem(st, tag + "_copied")
        self.made = k.sem(st, tag + "_made")
        self.free = k.sem(st, tag + "_free")
        self.sems = [self.turned, self.copied, self.made, self.free]

    def turn(self, pe, n, p, rows):
        pe.wait_ge(self.copied, n + 1)
        for j in range(self.cols):
            mm = self.k.nc.tensor.transpose(self.turned_ps[j // 4][:, j % 4, 0:p], rows[0:p, j, :],
                                            self.k.ident[0:p, 0:p])
        mm.then_inc(self.turned, 1)

    def copy(self, act, n, p):
        act.wait_ge(self.turned, n + 1)
        act.wait_ge(self.made, n + 1)
        for b in range(self.cols // 4):
            ins = self.k.nc.scalar.activation(self.turned_sb[:, 4 * b:4 * b + 4, 0:p],
                                              self.turned_ps[b][:, :, 0:p], ACT.Copy)
        ins.then_inc(self.copied, 1)

    def product(self, pe, n, p):
        pe.wait_ge(self.copied, n + 2)
        pe.wait_ge(self.free, n + 1)
        for b in range(self.cols // 4):
            self.k.nc.tensor.matmul(self.out[b][0:p, :, :].rearrange("p j d -> p (j d)"), self.k.ones3[:, 0:p],
                                    self.bias[:, :, :].rearrange("p j d -> p (j d)"), start=True, stop=False,
                                    skip_group_check=True)
            for j in range(4):
                mm = self.k.nc.tensor.matmul(self.out[b][0:p, j, :], self.turned_sb[:, 4 * b + j, 0:p], self.weight,
                                             start=False, stop=j == 3, skip_group_check=True)
        mm.then_inc(self.made, 1)


class Norm:

    STEPS = 4

    def __init__(self, k, st, tag, cols=NJ, eps=EPS, factor=1.0, slots=2):
        self.k, self.cols, self.eps, self.factor = k, cols, eps, factor
        self.stats = k.sb(st, tag + "_stats", [P, slots, cols, 6])
        self.mean, self.gap, self.var, self.root, self.scale, self.shift = (
            k.sb(st, f"{tag}_{x}", [P, slots, cols]) for x in ("mean", "gap", "var", "root", "scale", "shift"))
        self.bias = k.sb(st, tag + "_bias", [P, 1])
        self.seen = k.sem(st, tag + "_seen")
        self.rooted = k.sem(st, tag + "_rooted")
        self.scaled = k.sem(st, tag + "_scaled")
        self.shifted = k.sem(st, tag + "_shifted")
        self.steps = k.sem(st, tag + "_steps")
        self.set = k.sem(st, tag + "_set")
        self.sems = [self.seen, self.rooted, self.scaled, self.shifted, self.steps, self.set]

    def prepare(self, dve):
        self.chain = Chain(dve, self.steps, self.STEPS)
        self.k.nc.vector.memset(self.bias[:, :], self.eps).then_inc(self.set, 1)

    def statistics(self, dve, n, u, p, rows):
        v, c, s = self.k.nc.vector, self.chain, self.stats
        mean, gap, var = self.mean[0:p, u, :], self.gap[0:p, u, :], self.var[0:p, u, :]
        c.begin(n)
        for j in range(self.cols):
            ins = v.bn_stats(s[0:p, u, j, :], rows[0:p, j, :])
        c.link(ins)
        v.tensor_tensor(gap, s[0:p, u, :, 1], s[0:p, u, :, 4], ALU.subtract)
        v.tensor_tensor(var, s[0:p, u, :, 2], s[0:p, u, :, 5], ALU.add)
        c.link(v.tensor_tensor(mean, s[0:p, u, :, 1], s[0:p, u, :, 4], ALU.add))
        c.link(v.tensor_tensor(gap, gap, gap, ALU.mult))
        v.tensor_scalar(mean, mean, 0.5, None, ALU.mult)
        c.link(v.scalar_tensor_tensor(var, gap, D / 4.0, var, ALU.mult, ALU.add))
        c.end()
        dve.sem_inc(self.seen, 1)

    def square_root(self, act, n, u, p):
        act.wait_ge(self.seen, n + 1)
        act.wait_ge(self.set, 1)
        self.k.nc.scalar.activation(self.root[0:p, u, :], self.var[0:p, u, :], ACT.Sqrt, bias=self.bias[0:p, 0:1],
                                    scale=self.factor / D).then_inc(self.rooted, 1)

    def invert(self, dve, n, u, p):
        dve.wait_ge(self.rooted, n + 1)
        self.k.nc.vector.reciprocal(self.scale[0:p, u, :], self.root[0:p, u, :]).then_inc(self.scaled, 1)
        dve.wait_ge(self.scaled, n + 1)

    def normalise(self, dve, n, u, p, out, rows):
        self.invert(dve, n, u, p)
        for j in range(self.cols):
            ins = self.k.nc.vector.tensor_scalar(out[0:p, j, :], rows[0:p, j, :], self.mean[0:p, u, j:j + 1],
                                                 self.scale[0:p, u, j:j + 1], ALU.subtract, ALU.mult)
        return ins

    def negate(self, dve, n, u, p):
        self.invert(dve, n, u, p)
        self.k.nc.vector.scalar_tensor_tensor(self.shift[0:p, u, :], self.mean[0:p, u, :], -1.0,
                                              self.scale[0:p, u, :], ALU.mult, ALU.mult).then_inc(self.shifted, 1)

    def normalise_on_act(self, act, n, u, p, out, rows):
        act.wait_ge(self.shifted, n + 1)
        for j in range(self.cols):
            ins = self.k.nc.scalar.activation(out[0:p, j, :], rows[0:p, j, :], ACT.Identity,
                                              bias=self.shift[0:p, u, j:j + 1], scale=self.scale[0:p, u, j:j + 1])
        return ins


class Propagated:

    def __init__(self, k, st, tag):
        self.k = k
        self.x = k.sb(st, tag + "_x", [P, 2, NJ, D])
        self.agg = k.sb(st, tag + "_agg", [P, 2, NJ, D])
        self.y = k.sb(st, tag + "_y", [P, 2, NJ, D + 1])
        self.ready = [k.sem(st, f"{tag}_ready{u}") for u in range(2)]
        self.free = k.sem(st, tag + "_free")
        self.scaled = k.sem(st, tag + "_scaled")
        self.owned = k.sem(st, tag + "_owned")
        self.made = k.sem(st, tag + "_made")
        self.used = k.sem(st, tag + "_used")
        self.sems = self.ready + [self.free, self.scaled, self.owned, self.made, self.used]

    def load(self, sp, n, i, u, p):
        sp.wait_ge(self.free, n + 1)
        sp.dma_start(self.x[0:p, u, :, :], node_rows(self.k.x, n, p)).then_inc(self.ready[u], 16)
        sp.dma_start(self.agg[0:p, u, :, :], node_rows(self.k.agg, n, p)).then_inc(self.ready[u], 16)

    def per_node(self, column, n, p):
        c = column[0:p, n * NJ:n * NJ + NJ] if isinstance(n, int) else column[0:p, bass.ds(n * NJ, NJ)]
        return c.unsqueeze(2).broadcast_to([p, NJ, D])

    def scale(self, pool, n, i, u, p):
        paced(pool, self.k, self.ready[u], i * 32 + 32)
        self.k.nc.gpsimd.tensor_tensor(self.agg[0:p, u, :, :], self.agg[0:p, u, :, :],
                                       self.per_node(self.k.dinv, n, p), ALU.mult).then_inc(self.scaled, 1)

    def make(self, dve, n, i, u, p):
        dve.wait_ge(self.ready[u], i * 32 + 32)
        dve.wait_ge(self.used, n + 1)
        y = self.y[0:p, u, :, 0:D]
        self.k.nc.vector.tensor_tensor(y, self.x[0:p, u, :, :], self.per_node(self.k.dinv2, n, p),
                                       ALU.mult).then_inc(self.owned, 1)
        dve.wait_ge(self.scaled, n + 1)
        dve.wait_ge(self.owned, n + 1)
        self.k.nc.vector.tensor_tensor(y, y, self.agg[0:p, u, :, :], ALU.add).then_inc(self.made, 1)


def moments_phase(k):
    nc = k.nc
    with ExitStack() as st:
        prop = Propagated(k, st, "mom_y")
        w = k.sb(st, "mom_w", [P, D])
        gb = k.sb(st, "mom_gb", [P, 2, D])
        cov = k.sb(st, "mom_cov", [P, D + 1])
        mean = k.sb(st, "mom_mean", [P, 1])
        mean_b = k.sb(st, "mom_mean_b", [P, P])
        mean_r = k.sb(st, "mom_mean_r", [1, P])
        wz = k.sb(st, "mom_wz", [P, D])
        work = k.sb(st, "mom_work", [P, 4, D])
        acc = k.ps(st, "mom_acc", [P, 512])
        tps = k.ps(st, "mom_tps", [P, 512])
        outer = k.ps(st, "mom_outer", [P, 512])
        zp = k.ps(st, "mom_z", [P, 512])
        vb = k.ps(st, "mom_var", [P, 512])
        mb = k.ps(st, "mom_mean_h", [P, 512])
        s = {x: k.sem(st, "mom_" + x) for x in ("wloaded", "summed", "step", "pstep", "astep", "begun")}
        with nc.Block() as block:
            @block.sync
            def _(sp):
                sp.dma_start(w[:, :], k.a["L0_gnn_W"]).then_inc(s["wloaded"], 16)
                sp.dma_start(gb[:, 0, :], k.a["L0_gnn_gamma"].partition_broadcast(P)).then_inc(s["wloaded"], 16)
                sp.dma_start(gb[:, 1, :], k.a["L0_gnn_beta"].partition_broadcast(P)).then_inc(s["wloaded"], 16)
                staggered(sp, (lambda *g: prop.load(sp, *g), 0))

            @block.gpsimd
            def _(pool):
                staggered(pool, (lambda *g: prop.scale(pool, *g), 0))

            @block.vector
            def _(dve):
                dve.sem_inc(prop.free, 2)
                nc.vector.memset(prop.y[:, :, :, D:D + 1], 1.0).then_inc(s["begun"], 1)

                def make(n, i, u, p):
                    prop.make(dve, n, i, u, p)
                    dve.wait_ge(prop.made, n + 1)
                    dve.sem_inc(prop.free, 1)

                staggered(dve, (make, 0))
                dve.wait_ge(s["summed"], 1)
                dve.wait_ge(s["wloaded"], 48)
                c = Chain(dve, s["step"], 13)
                c.begin(0)
                c.link(nc.vector.tensor_scalar(cov[:, :], acc[:, 0:D + 1], 1.0 / N, None, ALU.mult))
                c.link(nc.vector.tensor_copy(mean[:, :], cov[:, D:D + 1]))
                c.link(nc.vector.tensor_scalar(mean_b[:, :], k.ones[:, :], mean[:, 0:1], None, ALU.mult))
                dve.wait_ge(s["pstep"], 1)
                c.link(nc.vector.tensor_copy(mean_r[:, :], tps[0:1, 0:P]))
                dve.wait_ge(s["pstep"], 2)
                c.link(nc.vector.tensor_tensor(cov[:, 0:D], cov[:, 0:D], outer[:, 0:P], ALU.subtract))
                dve.wait_ge(s["pstep"], 3)
                c.link(nc.vector.tensor_tensor(wz[:, :], w[:, :], zp[:, 0:D], ALU.mult))
                dve.wait_ge(s["astep"], 1)
                c.link(nc.vector.reciprocal(work[:, 1, :], work[:, 0, :]))
                c.link(nc.vector.tensor_tensor(work[:, 2, :], work[:, 1, :], gb[:, 0, :], ALU.mult))
                c.link(nc.vector.tensor_scalar(work[:, 2, :], work[:, 2, :], 0.5, None, ALU.mult))
                c.link(nc.vector.tensor_tensor(k.gcn_w[:, :], w[:, :], work[:, 2, :], ALU.mult))
                dve.wait_ge(s["pstep"], 5)
                c.link(nc.vector.tensor_tensor(work[:, 3, :], mb[:, 0:D], work[:, 2, :], ALU.mult))
                c.link(nc.vector.tensor_scalar(gb[:, 1, :], gb[:, 1, :], 0.5, None, ALU.mult))
                c.link(nc.vector.tensor_tensor(k.gcn_c[:, :], gb[:, 1, :], work[:, 3, :], ALU.subtract))
                c.end()

            @block.scalar
            def _(act):
                act.wait_ge(s["pstep"], 4)
                nc.scalar.activation(work[:, 0, :], vb[:, 0:D], ACT.Sqrt, bias=k.eps[:, 0:1]).then_inc(s["astep"], 1)

            @block.tensor
            def _(pe):
                nc.tensor.matmul(acc[:, 0:D + 1], k.zeros[:, 0:P], k.zeros[:, 0:D + 1], start=True, stop=False,
                                 skip_group_check=True)
                pe.sem_inc(prop.used, 2)
                pe.wait_ge(s["begun"], 1)

                def add(n, i, u, p):
                    pe.wait_ge(prop.made, n + 1)
                    for j in range(NJ):
                        mm = nc.tensor.matmul(acc[:, 0:D + 1], prop.y[0:p, u, j, 0:D], prop.y[0:p, u, j, :],
                                              start=False, stop=False, skip_group_check=True)
                    mm.then_inc(prop.used, 1)

                staggered(pe, (add, 0))
                pe.wait_ge(prop.used, NG + 3)
                pe.sem_inc(s["summed"], 1)
                pe.wait_ge(s["step"], 3)
                nc.tensor.transpose(tps[0:1, 0:P], mean[:, 0:1], k.ident[:, :]).then_inc(s["pstep"], 1)
                pe.wait_ge(s["step"], 4)
                nc.tensor.matmul(outer[:, 0:P], mean_r[:, :], mean_r[:, :], start=True, stop=True)\
                    .then_inc(s["pstep"], 1)
                pe.wait_ge(s["step"], 5)
                nc.tensor.matmul(zp[:, 0:D], cov[:, 0:D], w[:, :], start=True, stop=True).then_inc(s["pstep"], 1)
                pe.wait_ge(s["step"], 6)
                nc.tensor.matmul(vb[:, 0:D], k.ones[:, :], wz[:, :], start=True, stop=True).then_inc(s["pstep"], 1)
                nc.tensor.matmul(mb[:, 0:D], mean_b[:, :], w[:, :], start=True, stop=True).then_inc(s["pstep"], 1)
        clear_semaphores(nc, prop.sems + list(s.values()))


def load_constants(k, names):
    nc = k.nc
    with ExitStack() as st:
        got = k.sem(st, "const_got")
        with nc.Block() as block:
            @block.sync
            def _(sp):
                for dst, src in names:
                    sp.dma_start(dst, src).then_inc(got, 16)
                sp.wait_ge(got, 16 * len(names))
        clear_semaphores(nc, [got])


def split_bias(k, st, dve, tag, rows):
    v = k.nc.vector
    parts = k.sb(st, tag + "_parts", [3, 4, D], BF16)
    work = k.sb(st, tag + "_split", [3, 4, D])
    half = k.sb(st, tag + "_half", [3, 3, D], BF16)
    c = Chain(dve, k.sem(st, tag + "_split_steps"), 9)
    c.begin(0)
    c.link(v.tensor_copy(half[:, 0, :], rows))
    c.link(v.tensor_tensor(work[:, 0, :], rows, half[:, 0, :], ALU.subtract))
    c.link(v.tensor_copy(half[:, 1, :], work[:, 0, :]))
    c.link(v.tensor_tensor(work[:, 1, :], work[:, 0, :], half[:, 1, :], ALU.subtract))
    c.link(v.tensor_copy(half[:, 2, :], work[:, 1, :]))
    c.link(v.tensor_scalar(work[:, 2, :], half[:, 0, :], k.ident[0:3, 0:1], None, ALU.mult))
    c.link(v.scalar_tensor_tensor(work[:, 3, :], half[:, 1, :], k.ident[0:3, 1:2], work[:, 2, :], ALU.mult, ALU.add))
    c.link(v.scalar_tensor_tensor(work[:, 0, :], half[:, 2, :], k.ident[0:3, 2:3], work[:, 3, :], ALU.mult, ALU.add))
    c.link(v.tensor_copy(parts[:, :, :], work[:, 0, :].unsqueeze(1).broadcast_to([3, 4, D])))
    c.end()
    return parts, c.sem


def split_bias_phase(k, st, tag, rows):
    with k.nc.Block() as block:
        made = []

        @block.vector
        def _(dve):
            made.append(split_bias(k, st, dve, tag, rows))
    clear_semaphores(k.nc, [made[0][1]])
    return made[0][0]


def capsules_phase(k):
    nc = k.nc
    with ExitStack() as st:
        w1 = k.sb(st, "cap_w1", [P, D])
        b1 = k.sb(st, "cap_b1", [3, D])
        load_constants(k, [(w1[:, :], k.a["L1_gnn_weight"]), (b1[:, :], k.a["L1_gnn_bias"].partition_broadcast(3))])
        gcn_b = split_bias_phase(k, st, "cap_gcn_b", k.gcn_c[0:3, :])
        caps_b = split_bias_phase(k, st, "cap_caps_b", b1[:, :])
        prop = Propagated(k, st, "cap_y")
        conv = Linear(k, st, "cap_conv", k.gcn_w[:, :], gcn_b)
        caps = Linear(k, st, "cap_caps", w1[:, :], caps_b)
        norm = Norm(k, st, "cap_norm", eps=EPS / 4)
        u1, x1, cap, plain, leak = (k.sb(st, "cap_" + x, [P, 2, NJ, D]) for x in ("u", "x1", "cap", "plain", "leak"))
        square = k.sb(st, "cap_square", [P, NJ, D])
        length = k.sb(st, "cap_length", [P, 2, 3, NJ * NH])
        names = ["added", "normed", "x1_stored0", "x1_stored1", "cap_stored0", "cap_stored1", "leaked",
                 "bent", "squared", "reduced", "inverted", "scaled", "sized"]
        s = {x: k.sem(st, "cap_" + x) for x in names}
        with nc.Block() as block:
            @block.sync
            def _(sp):
                def store(what, c, rows):
                    def stage(n, i, u, p):
                        sp.wait_ge(s["normed" if c == 0 else "scaled"], n + 1)
                        sp.dma_start(node_rows(k.layer1, n, p, 2 * D)[:, :, c * D:(c + 1) * D], rows[0:p, u, :, :])\
                          .then_inc(s[f"{what}_stored{u}"], 16)
                    return stage

                for what in ("x1", "cap"):
                    for u in range(2):
                        sp.sem_inc(s[f"{what}_stored{u}"], 16)
                staggered(sp, (lambda *g: prop.load(sp, *g), 0), (store("x1", 0, x1), 3), (store("cap", 1, cap), 6))
                for what in ("x1", "cap"):
                    sp.wait_ge(s[f"{what}_stored0"], 16 * (NG // 2 + 2))
                    sp.wait_ge(s[f"{what}_stored1"], 16 * (NG // 2 + 1))

            @block.gpsimd
            def _(pool):
                staggered(pool, (lambda *g: prop.scale(pool, *g), 0))

            @block.vector
            def _(dve):
                dve.sem_inc(prop.free, 2)
                dve.sem_inc(conv.free, 1)
                dve.sem_inc(s["reduced"], 1)
                norm.prepare(dve)

                def add(n, i, u, p):
                    dve.wait_ge(conv.made, n + 2)
                    for b in range(2):
                        ins = nc.vector.scalar_tensor_tensor(
                            u1[0:p, u, 4 * b:4 * b + 4, :], conv.out[b][0:p, :, :], 0.0,
                            prop.x[0:p, u, 4 * b:4 * b + 4, :], ALU.max, ALU.add)
                    ins.then_inc(s["added"], 1)
                    dve.wait_ge(s["added"], n + 1)
                    dve.sem_inc(conv.free, 1)
                    dve.sem_inc(prop.free, 1)
                    norm.statistics(dve, n, u, p, u1[:, u, :, :])

                def normalise(n, i, u, p):
                    dve.wait_ge(s[f"x1_stored{u}"], i * 16 + 16)
                    norm.normalise(dve, n, u, p, x1[:, u, :, :], u1[:, u, :, :]).then_inc(s["normed"], 1)

                def reduce(n, i, u, p):
                    dve.wait_ge(s["squared"], n + 1)
                    nc.vector.tensor_reduce(length[0:p, u, 0, :],
                                            square[0:p, :, :].rearrange("p j (h d) -> p (j h) d", h=NH), AX.X,
                                            ALU.add).then_inc(s["reduced"], 1)

                def scale(n, i, u, p):
                    dve.wait_ge(s["sized"], n + 1)
                    nc.vector.reciprocal(length[0:p, u, 2, :], length[0:p, u, 1, :]).then_inc(s["inverted"], 1)
                    dve.wait_ge(s["inverted"], n + 1)
                    for b in range(2):
                        half = cap[0:p, u, 4 * b:4 * b + 4, :].rearrange("p j (h d) -> p j h d", h=NH)
                        size = length[0:p, u, 2, 4 * b * NH:(4 * b + 4) * NH].rearrange("p (j h) -> p j h", h=NH)\
                            .unsqueeze(3).broadcast_to([p, 4, NH, HD])
                        ins = nc.vector.tensor_tensor(half, half, size, ALU.mult)
                    ins.then_inc(s["scaled"], 1)

                def bend(n, i, u, p):
                    dve.wait_ge(s["leaked"], n + 1)
                    dve.wait_ge(s[f"cap_stored{u}"], i * 16 + 16)
                    nc.vector.tensor_tensor(cap[0:p, u, :, :], plain[0:p, u, :, :], leak[0:p, u, :, :], ALU.max)\
                        .then_inc(s["bent"], 1)

                staggered(dve, (scale, 5), (normalise, 2), (add, 1), (lambda *g: prop.make(dve, *g), 0), (reduce, 4),
                          (bend, 3))

            @block.scalar
            def _(act):
                act.sem_inc(conv.copied, 1)
                act.sem_inc(caps.copied, 1)
                act.sem_inc(caps.free, 1)

                def leaked(n, i, u, p):
                    act.wait_ge(caps.made, n + 2)
                    for out, scale in ((plain, 1.0), (leak, 0.01)):
                        for b in range(2):
                            ins = nc.scalar.activation(out[0:p, u, 4 * b:4 * b + 4, :], caps.out[b][0:p, :, :],
                                                       ACT.Copy, scale=scale)
                    ins.then_inc(s["leaked"], 1)
                    act.wait_ge(s["leaked"], n + 1)
                    act.sem_inc(caps.free, 1)

                def squared(n, i, u, p):
                    act.wait_ge(s["bent"], n + 1)
                    act.wait_ge(s["reduced"], n + 1)
                    nc.scalar.activation(square[0:p, :, :], cap[0:p, u, :, :], ACT.Square).then_inc(s["squared"], 1)

                def size(n, i, u, p):
                    act.wait_ge(s["reduced"], n + 2)
                    nc.scalar.activation(length[0:p, u, 1, :], length[0:p, u, 0, :], ACT.Sqrt).then_inc(s["sized"], 1)

                staggered(act, (squared, 4), (lambda n, i, u, p: caps.copy(act, n, p), 2),
                          (lambda n, i, u, p: conv.copy(act, n, p), 0), (leaked, 2),
                          (lambda n, i, u, p: norm.square_root(act, n, u, p), 1), (size, 4))

            @block.tensor
            def _(pe):
                pe.sem_inc(conv.made, 1)
                pe.sem_inc(caps.made, 1)
                pe.sem_inc(prop.used, 2)

                def conv_turn(n, i, u, p):
                    pe.wait_ge(prop.made, n + 1)
                    conv.turn(pe, n, p, prop.y[:, u, :, 0:D])
                    pe.wait_ge(conv.turned, n + 1)
                    pe.sem_inc(prop.used, 1)

                def caps_turn(n, i, u, p):
                    pe.wait_ge(s["normed"], n + 1)
                    caps.turn(pe, n, p, x1[:, u, :, :])

                staggered(pe, (caps_turn, 2), (conv_turn, 0), (lambda n, i, u, p: caps.product(pe, n, p), 2),
                          (lambda n, i, u, p: conv.product(pe, n, p), 0))
        clear_semaphores(nc, prop.sems + conv.sems + caps.sems + norm.sems + list(s.values()))


def routing_setup_phase(k, o):
    nc = k.nc
    with ExitStack() as st:
        pick = k.sb(st, "rs_pick", [P, 2, P])
        pick2 = k.sb(st, "rs_pick2", [P, 2])
        ends = k.sb(st, "rs_ends", [P, 2, T])
        ends_t = k.sb(st, "rs_ends_t", [TB, 2, 2])
        place = k.sb(st, "rs_place", [P, 2])
        order = k.sb(st, "rs_order", [TB, 2, 2, T])
        pe_ends = [k.ps(st, f"rs_ends_ps{a}", [P, 512]) for a in range(2)]
        pe_two = k.ps(st, "rs_two_ps", [P, 512])
        pe_t = k.ps(st, "rs_t_ps", [P, 2, 2, P])
        s = {x: k.sem(st, "rs_" + x) for x in ("step", "picked", "turned")}
        with nc.Block() as block:
            @block.vector
            def _(dve):
                v = nc.vector
                c = Chain(dve, s["step"], 14)
                c.begin(0)
                c.link(v.tensor_scalar(pick2[:, 0:1], k.iota_part[:, :], 0.0, None, ALU.is_equal))
                c.link(v.tensor_copy(pick2[:, 1:2], k.last_part[:, :]))
                c.link(v.tensor_scalar(pick[:, 0, :], k.ones[:, :], pick2[:, 0:1], None, ALU.mult))
                c.link(v.tensor_scalar(pick[:, 1, :], k.ones[:, :], pick2[:, 1:2], None, ALU.mult))
                dve.wait_ge(s["picked"], 1)
                c.link(v.tensor_copy(ends[:, 0, :], pe_ends[0][:, 0:T]))
                c.link(v.tensor_copy(ends[:, 1, :], pe_ends[1][:, 0:T]))
                c.link(v.tensor_copy(k.ends2[:, :], pe_two[0:2, 0:T]))
                c.link(v.tensor_tensor(k.end_mask[:, :, 0], o.id_col[:, :], ends[:, 0, :], ALU.is_equal))
                c.link(v.tensor_tensor(k.end_mask[:, :, 1], o.id_col[:, :], ends[:, 1, :], ALU.is_equal))
                dve.wait_ge(s["turned"], 1)
                c.link(v.tensor_copy(ends_t[:, :, :], pe_t[0:TB, :, :, 0]))
                c.link(v.tensor_copy(place[:, 0:1], k.iota_part[:, :]))
                c.link(v.tensor_scalar(place[:, 1:2], k.iota_part[:, :], float(TB), None, ALU.add))
                for b in range(2):
                    v.tensor_scalar(order[:, 0, b, :], k.iota_high[0:TB, 0:T], place[0:TB, b:b + 1], None, ALU.is_gt)
                    ins = v.tensor_scalar(order[:, 1, b, :], k.iota_high[0:TB, 0:T], place[0:TB, b:b + 1], None,
                                          ALU.is_lt)
                c.link(ins)
                for b in range(2):
                    v.scalar_tensor_tensor(k.handed[:, 0, b, :], ends[0:TB, 0, :], ends_t[:, 1, b:b + 1],
                                           order[:, 0, b, :], ALU.is_equal, ALU.mult)
                    ins = v.scalar_tensor_tensor(k.handed[:, 1, b, :], ends[0:TB, 1, :], ends_t[:, 0, b:b + 1],
                                                 order[:, 1, b, :], ALU.is_equal, ALU.mult)
                c.link(ins)
                c.end()

            @block.tensor
            def _(pe):
                pe.wait_ge(s["step"], 4)
                for a in range(2):
                    nc.tensor.matmul(pe_ends[a][:, 0:T], pick[:, a, :], o.id_col[:, :], start=True, stop=True)
                nc.tensor.matmul(pe_two[0:2, 0:T], pick2[:, :], o.id_col[:, :], start=True, stop=True)\
                    .then_inc(s["picked"], 1)
                pe.wait_ge(s["step"], 6)
                for a in range(2):
                    for b in range(2):
                        last = nc.tensor.transpose(pe_t[0:TB, a, b, :], ends[:, a, b * TB:(b + 1) * TB], k.ident[:, :])
                last.then_inc(s["turned"], 1)
        clear_semaphores(nc, list(s.values()))


def exchange_phase(k, tag):
    nc = k.nc
    with ExitStack() as st:
        part = k.sb(st, tag + "_part", [TB, 2, 2, D])
        total = k.sb(st, tag + "_total", [TB, 2, 2, D])
        ps = [k.ps(st, f"{tag}_ps{a}", [P, 2, D]) for a in range(2)]
        s = {x: k.sem(st, f"{tag}_{x}") for x in ("got", "made", "out", "put")}
        with nc.Block() as block:
            @block.sync
            def _(sp):
                for a in range(2):
                    for b in range(2):
                        sp.dma_start(part[:, a, b, :], k.end_sums[a, b * TB:(b + 1) * TB, :]).then_inc(s["got"], 16)
                sp.wait_ge(s["out"], 2)
                for a in range(2):
                    for b in range(2):
                        sp.dma_start(k.handed_sums[a, b * TB:(b + 1) * TB, :], total[:, a, b, :])\
                          .then_inc(s["put"], 16)
                sp.wait_ge(s["put"], 64)

            @block.vector
            def _(dve):
                dve.wait_ge(s["made"], 1)
                for a in range(2):
                    nc.vector.tensor_copy(total[:, a, :, :], ps[a][0:TB, :, :]).then_inc(s["out"], 1)

            @block.tensor
            def _(pe):
                pe.wait_ge(s["got"], 64)
                for a in range(2):
                    for out in range(2):
                        for b in range(2):
                            last = nc.tensor.matmul(ps[a][0:TB, out, :], k.handed[:, a, b, out * TB:(out + 1) * TB],
                                                    part[:, 1 - a, b, :], start=(b == 0), stop=(b == 1))
                last.then_inc(s["made"], 1)
        clear_semaphores(nc, list(s.values()))


RT = 2 * GT
RU = T // RT


def routing_phase(k, o, step, last_step, tag):
    nc = k.nc
    first, last = step == 0, step == last_step
    F = RT * D
    with ExitStack() as st:
        def sb(name, shape, dt=F32):
            return k.sb(st, f"{tag}_{name}", shape, dt)

        if first:
            pair = sb("pair", [P, 2, RT, 2, D])
            own = sb("own", [P, 2, RT, D])
            index_s = sb("index", [P, 2, 2, RT], I32)
        else:
            same = sb("same", [P, 2, RT, P])
            ends = sb("ends", [2, 2, RT, P])
            handed = sb("handed", [2, 2, RT, D])
            y_sb = sb("y", [P, 2, RT, D])
            acc = [k.ps(st, f"{tag}_acc{u}", [P, RT, D]) for u in range(2)]
        if last:
            sent = sb("sent", [P, 2, RT, D])
            last_s = sb("last", [P, 2, RT], I32)
        else:
            if not first:
                far = sb("far", [P, 2, RT, D])
                both = sb("both", [P, 2, RT, D])
            mask_s = sb("mask", [P, 2, RT, 2])
            end_out = sb("end_out", [2, RT, D])
            end_ps = [k.ps(st, f"{tag}_end{u}", [P, RT, D]) for u in range(2)]
            weight = sb("weight", [P, 2, RT * NH])
        terms = sb("terms", [P, 2, RT, D])
        dots = sb("dots", [P, 2, 2, RT * NH])
        logs = sb("logs", [P, 2, RT * NH])
        inv = sb("inv", [P, 2, RT * NH])
        score = sb("score", [P, 2, RT * NH])
        names = ["index", "free", "rows0", "rows1", "far0", "far1", "both0", "both1", "row_free", "same", "ends",
                 "summed", "copied", "squared", "product", "reduced", "log", "inverse", "scored", "masked",
                 "weighed", "valued", "paired", "end_made", "end_copied", "end_put", "sent", "sent_free",
                 "paired_put0", "paired_put1"]
        s = {x: k.sem(st, f"{tag}_{x}") for x in names}
        even, odd = (RU + 1) // 2, RU // 2
        in0, out0 = list(k.gather_base), list(k.scatter_base)
        for u, units in enumerate((even, odd)):
            k.gather_base[u] += units * 32 * RT * first
            k.scatter_base[u] += units * 16 * RT * last
        sems = list(s.values())
        s.update(own0=k.gathered[0], own1=k.gathered[1], put0=k.scattered[0], put1=k.scattered[1])

        def tiles(column, n):
            return column[:, n * RT:n * RT + RT] if isinstance(n, int) else column[:, bass.ds(n * RT, RT)]

        def rows_at(n, width):
            return slice(n * width, n * width + width) if isinstance(n, int) else bass.ds(n * width, width)

        def edge_rows(table, n):
            return table[rows_at(n, F), :].rearrange("(t p) c -> p t c", p=P)

        def by_head(ap):
            return ap.rearrange("p t (h d) -> p t h d", h=NH)

        def per_head(ap):
            return ap.rearrange("p (t h) -> p t h", h=NH).unsqueeze(3).broadcast_to([P, RT, NH, HD])

        def run(eng, *stages):
            staggered(eng, *stages, full=RU, tail=None)

        with nc.Block() as block:
            @block.sync
            def _(sp):
                def load_rows(n, i, u, p):
                    sp.wait_ge(s["row_free"], n + 1)
                    sp.dma_start(same[:, u, :, :].rearrange("p t e -> p (t e)"),
                                 o.id_row[rows_at(n, F)].partition_broadcast(P)).then_inc(s[f"rows{u}"], 16)
                    sp.dma_start(handed[:, u, :, :], k.handed_sums[:, rows_at(n, RT), :])\
                      .then_inc(s[f"rows{u}"], 16)

                def load_far(n, i, u, p):
                    sp.wait_ge(s["reduced"], n + 1)
                    sp.dma_start(far[:, u, :, :], edge_rows(k.pairs, n)[:, :, 0:D]).then_inc(s[f"far{u}"], 16)

                def load_both(n, i, u, p):
                    sp.wait_ge(s["valued"], n + 1)
                    sp.dma_start(both[:, u, :, :], edge_rows(k.pairs, n)[:, :, D:2 * D]).then_inc(s[f"both{u}"], 16)

                def store_pair(n, i, u, p):
                    sp.wait_ge(s["paired"], n + 1)
                    sp.dma_start(edge_rows(k.pairs, n), pair[:, u, :, :, :].rearrange("p t c d -> p t (c d)"))\
                      .then_inc(s[f"paired_put{u}"], 16)

                def store_ends(n, i, u, p):
                    sp.wait_ge(s["end_copied"], n + 1)
                    sp.dma_start(k.end_sums[:, rows_at(n, RT), :], end_out[:, :, :]).then_inc(s["end_put"], 16)

                if first:
                    sp.sem_inc(s["end_put"], 16)
                    run(sp, (store_pair, 1), (store_ends, 2))
                    sp.wait_ge(s["paired_put0"], 16 * even)
                    sp.wait_ge(s["paired_put1"], 16 * odd)
                    sp.wait_ge(s["end_put"], 16 * RU + 16)
                elif last:
                    run(sp, (load_rows, 0))
                else:
                    sp.sem_inc(s["end_put"], 16)
                    run(sp, (load_rows, 0), (load_far, 0), (load_both, 0), (store_ends, 3))
                    sp.wait_ge(s["end_put"], 16 * RU + 16)

            @block.gpsimd
            def _(pool):
                def gather(n, i, u, p):
                    paced(pool, k, s["free"], n + 1)
                    nc.gpsimd.tensor_copy(index_s[:, u, 0, :], tiles(o.cap_far, n))
                    nc.gpsimd.tensor_copy(index_s[:, u, 1, :], tiles(o.cap_own, n)).then_inc(s["index"], 1)
                    paced(pool, k, s["index"], n + 1)
                    for j in range(RT):
                        for c, out in ((0, pair[:, u, j, 0, :]), (1, own[:, u, j, :])):
                            nc.gpsimd.indirect_dma_start(
                                out=out, out_offset=None, in_=k.layer1_halves,
                                in_offset=bass.IndirectOffsetOnAxis(ap=index_s[:, u, c, j:j + 1], axis=0))\
                                .then_inc(s[f"own{u}"], 16)

                def values(n, i, u, p):
                    paced(pool, k, s["weighed"], n + 1)
                    paced(pool, k, s[f"both{u}"], i * 16 + 16)
                    nc.gpsimd.tensor_tensor(by_head(tiles(k.vals, n)), by_head(both[:, u, :, :]),
                                            per_head(weight[:, u, :]), ALU.mult).then_inc(s["valued"], 1)
                    paced(pool, k, s["end_made"], n + 1)
                    nc.gpsimd.tensor_copy(mask_s[:, u, :, :], tiles(k.end_mask, n)).then_inc(s["masked"], 1)

                def scatter(n, i, u, p):
                    paced(pool, k, s["sent"], n + 3)
                    nc.gpsimd.tensor_copy(last_s[:, u, :], tiles(o.last_cap, n)).then_inc(s["index"], 1)
                    paced(pool, k, s["index"], n + 1)
                    for j in range(RT):
                        nc.gpsimd.indirect_dma_start(
                            out=k.layer1_halves,
                            out_offset=bass.IndirectOffsetOnAxis(ap=last_s[:, u, j:j + 1], axis=0),
                            in_=sent[:, u, j, :], in_offset=None, bounds_check=2 * N - 1, oob_is_err=False)\
                            .then_inc(s[f"put{u}"], 16)

                def scattered(n, i, u, p):
                    pool.wait_ge(s[f"put{u}"], i * (16 * RT) + (out0[u] + 16 * RT))
                    pool.sem_inc(s["sent_free"], 1)

                if first:
                    run(pool, (gather, 0))
                elif last:
                    pool.sem_inc(s["sent_free"], 2)
                    run(pool, (scatter, 0), (scattered, 1))
                else:
                    pool.sem_inc(s["valued"], 2)
                    run(pool, (values, 0))

            @block.vector
            def _(dve):
                def equal(n, i, u, p):
                    dve.wait_ge(s[f"rows{u}"], i * 32 + 32)
                    nc.vector.tensor_tensor(ends[:, u, :, :], same[0:2, u, :, :],
                                            tiles(k.ends2, n).unsqueeze(2).broadcast_to([2, RT, P]),
                                            ALU.is_equal).then_inc(s["ends"], 1)
                    dve.wait_ge(s["ends"], n + 1)
                    nc.vector.tensor_tensor(same[:, u, :, :], same[:, u, :, :],
                                            tiles(o.id_col, n).unsqueeze(2).broadcast_to([P, RT, P]),
                                            ALU.is_equal).then_inc(s["same"], 1)

                def pairs(n, i, u, p):
                    dve.wait_ge(s[f"own{u}"], i * (32 * RT) + (in0[u] + 32 * RT))
                    nc.vector.tensor_tensor(pair[:, u, :, 1, :], pair[:, u, :, 0, :], own[:, u, :, :],
                                            ALU.add).then_inc(s["paired"], 1)

                def reduce(n, i, u, p):
                    if not last:
                        if not first:
                            dve.wait_ge(s["copied"], n + 3)
                            dve.wait_ge(s["reduced"], n + 2)
                            dve.wait_ge(s[f"far{u}"], i * 16 + 16)
                        nc.vector.tensor_tensor(terms[:, 0, :, :], own[:, u, :, :] if first else y_sb[:, u, :, :],
                                                pair[:, u, :, 0, :] if first else far[:, u, :, :],
                                                ALU.mult).then_inc(s["product"], 1)
                        dve.wait_ge(s["product"], n + 1)
                    lo, hi = (0, 1) if first else (1, 2) if last else (0, 2)
                    if not first:
                        dve.wait_ge(s["squared"], n + 1)
                    nc.vector.tensor_reduce(dots[:, u, lo:hi, :],
                                            terms[:, lo:hi, :, :].rearrange("p c t (h d) -> p (c t h) d", h=NH),
                                            AX.X, ALU.add).then_inc(s["reduced"], 1)

                def scored(n, i, u, p):
                    dve.wait_ge(s["inverse"], n + 1)
                    if last:
                        dve.wait_ge(s["sent_free"], n + 1)
                        nc.vector.tensor_tensor(by_head(sent[:, u, :, :]), by_head(y_sb[:, u, :, :]),
                                                per_head(inv[:, u, :]), ALU.mult).then_inc(s["sent"], 1)
                    else:
                        nc.vector.tensor_tensor(score[:, u, :], dots[:, u, 0, :], inv[:, u, :],
                                                ALU.mult).then_inc(s["scored"], 1)

                def first_values(n, i, u, p):
                    dve.wait_ge(s["end_made"], n + 1)
                    nc.vector.tensor_copy(mask_s[:, u, :, :], tiles(k.end_mask, n)).then_inc(s["masked"], 1)
                    dve.wait_ge(s["weighed"], n + 1)
                    nc.vector.tensor_tensor(by_head(tiles(k.vals, n)), by_head(pair[:, u, :, 1, :]),
                                            per_head(weight[:, u, :]), ALU.mult).then_inc(s["valued"], 1)
                    dve.wait_ge(s["valued"], n + 3)
                    dve.wait_ge(s[f"paired_put{u}"], i * 16 + 16)
                    dve.sem_inc(s["free"], 1)

                if first:
                    dve.sem_inc(s["free"], 2)
                    dve.sem_inc(s["valued"], 2)
                    run(dve, (pairs, 0), (reduce, 0), (first_values, 0))
                else:
                    dve.sem_inc(s["reduced"], 2)
                    if last:
                        dve.sem_inc(s["sent"], 2)
                    run(dve, (scored, 2), (equal, 0), (reduce, 1))

            @block.scalar
            def _(act):
                def squares(n, i, u, p):
                    act.wait_ge(s["summed"], n + 1)
                    if last:
                        act.wait_ge(s["sent"], n + 1)
                    nc.scalar.activation(y_sb[:, u, :, :], acc[u][:, :, :], ACT.Copy).then_inc(s["copied"], 1)
                    act.wait_ge(s["copied"], n + 3)
                    act.wait_ge(s["reduced"], n + 2)
                    nc.scalar.activation(terms[:, 1, :, :], y_sb[:, u, :, :], ACT.Square).then_inc(s["squared"], 1)

                def inverse(n, i, u, p):
                    act.wait_ge(s["reduced"], n + 3)
                    nc.scalar.activation(logs[:, u, :], dots[:, u, 1, :], ACT.Ln).then_inc(s["log"], 1)
                    act.wait_ge(s["log"], n + 1)
                    nc.scalar.activation(inv[:, u, :], logs[:, u, :], ACT.Exp, scale=-0.5).then_inc(s["inverse"], 1)

                def weigh(n, i, u, p):
                    act.wait_ge(s["reduced" if first else "scored"], n + 1)
                    nc.scalar.activation(weight[:, u, :], dots[:, u, 0, :] if first else score[:, u, :],
                                         ACT.Exp).then_inc(s["weighed"], 1)

                def copy_ends(n, i, u, p):
                    act.wait_ge(s["end_made"], n + 3)
                    act.wait_ge(s["end_put"], n * 16 + 16)
                    nc.scalar.activation(end_out[:, :, :], end_ps[u][0:2, :, :], ACT.Copy)\
                        .then_inc(s["end_copied"], 1)

                if not first:
                    act.sem_inc(s["copied"], 2)
                if first:
                    run(act, (weigh, 0), (copy_ends, 1))
                elif last:
                    run(act, (squares, 0), (inverse, 0))
                else:
                    run(act, (squares, 1), (weigh, 2), (copy_ends, 3), (inverse, 1))

            @block.tensor
            def _(pe):
                def sums(n, i, u, p):
                    pe.wait_ge(s["same"], n + 1)
                    pe.wait_ge(s["copied"], n + 1)
                    for j in range(RT):
                        nc.tensor.matmul(acc[u][:, j, :], same[:, u, j, :], k.vals[:, rows_at_tile(n, j), :],
                                         start=True, stop=False)
                        mm = nc.tensor.matmul(acc[u][:, j, :], ends[:, u, j, :], handed[:, u, j, :], start=False,
                                              stop=True)
                    mm.then_inc(s["summed"], 1)
                    pe.wait_ge(s["summed"], n + 1)
                    pe.sem_inc(s["row_free"], 1)

                def end_sums(n, i, u, p):
                    pe.wait_ge(s["valued"], n + 3)
                    paced(pe, k, s["masked"], n + 1)
                    for j in range(RT):
                        mm = nc.tensor.matmul(end_ps[u][0:2, j, :], mask_s[:, u, j, :], k.vals[:, rows_at_tile(n, j), :],
                                              start=True, stop=True)
                    mm.then_inc(s["end_made"], 1)

                def rows_at_tile(n, j):
                    return slice(n * RT + j, n * RT + j + 1) if isinstance(n, int) else bass.ds(n * RT + j, 1)

                if not last:
                    pe.sem_inc(s["end_made"], 2)
                if not first:
                    pe.sem_inc(s["row_free"], 2)
                if first:
                    run(pe, (end_sums, 0))
                elif last:
                    run(pe, (sums, 0))
                else:
                    run(pe, (sums, 0), (end_sums, 3))
        clear_semaphores(nc, sems)


CH = 8
CT = T // CH
CE = CT * P
Q = NH * CH


def attention_weights_phase(k):
    nc = k.nc
    a = k.a
    with ExitStack() as st:
        w = k.sb(st, "aw_w", [P, 3, D])
        b = k.sb(st, "aw_b", [1, 3, D])
        g1 = k.sb(st, "aw_g1", [P, 1])
        be1 = k.sb(st, "aw_be1", [P, 1])
        ps = k.ps(st, "aw_ps", [P, 512])
        load_constants(k, [(w[:, i, :], a["L2_gnn_W" + c]) for i, c in enumerate("qkv")]
                       + [(b[:, i, :], a["L2_gnn_b" + c].rearrange("(r d) -> r d", r=1)) for i, c in enumerate("qkv")]
                       + [(g1[:, :], a["L2_gnn_g1"].rearrange("(p r) -> p r", r=1)),
                          (be1[:, :], a["L2_gnn_be1"].rearrange("(p r) -> p r", r=1)),
                          (k.wc[:, :], a["L2_gnn_Wc"]), (k.bc[:, :], a["L2_gnn_bc"].rearrange("(r d) -> r d", r=1)),
                          (k.wo[:, :], a["L2_gnn_Wo"]), (k.bo_row[:, :], a["L2_gnn_bo"].rearrange("(r d) -> r d", r=1))])
        s = {x: k.sem(st, "aw_" + x) for x in ("step", "made")}
        with nc.Block() as block:
            @block.vector
            def _(dve):
                v = nc.vector
                c = Chain(dve, s["step"], 4)
                c.begin(0)
                dve.wait_ge(s["made"], 1)
                c.link(v.tensor_tensor(k.qkv_b[:, :, :], ps[0:1, 0:3 * D].rearrange("p (i d) -> p i d", i=3),
                                       b[:, :, :], ALU.add))
                c.link(v.tensor_scalar(k.qkv_w[:, :, :], w[:, :, :], g1[:, 0:1], None, ALU.mult))
                c.link(v.tensor_scalar(k.qkv_w[:, 0, :], k.qkv_w[:, 0, :], HD ** -0.5, None, ALU.mult))
                c.link(v.tensor_scalar(k.qkv_b[:, 0, :], k.qkv_b[:, 0, :], HD ** -0.5, None, ALU.mult))
                c.end()

            @block.tensor
            def _(pe):
                nc.tensor.matmul(ps[0:1, 0:3 * D], be1[:, 0:1], w[:, :, :].rearrange("p i d -> p (i d)"), start=True,
                                 stop=True).then_inc(s["made"], 1)
        clear_semaphores(nc, list(s.values()))


def scores_phase(k, o):
    nc = k.nc
    C = 2 * GT
    with ExitStack() as st:
        rows = k.sb(st, "sc_rows", [P, 2, C, 2 * D])
        index_s = k.sb(st, "sc_index", [P, 2, 2, GT], I32)
        attr = k.sb(st, "sc_attr", [P, 2, GT, D])
        xin = k.sb(st, "sc_xin", [P, 2, C, D])
        xn = k.sb(st, "sc_xn", [P, 2, C, D])
        x_t = k.sb(st, "sc_x_t", [P, C, P])
        attr_t = k.sb(st, "sc_attr_t", [P, GT, P])
        query = k.sb(st, "sc_query", [P, GT, D])
        value = k.sb(st, "sc_value", [P, 2, GT, D])
        terms = k.sb(st, "sc_terms", [P, GT, D])
        dots = k.sb(st, "sc_dots", [P, GT, NH])
        norm = Norm(k, st, "sc_norm", cols=C, eps=EPS * EPS, factor=1.0 + EPS)
        t_ps = [k.ps(st, f"sc_t{b}", [P, GT, P]) for b in range(3)]
        out_ps = [k.ps(st, f"sc_o{b}", [P, GT, D]) for b in range(3)]
        attr_ps = k.ps(st, "sc_attr_ps", [P, 512])
        names = ["index", "free", "attr0", "attr1", "attr_tail", "attr_free", "added", "normed", "turned", "copied",
                 "made", "query", "value", "value_put0", "value_put1", "value_free", "product", "dots", "scored",
                 "emptied", "cleared"]
        s = {x: k.sem(st, "sc_" + x) for x in names}
        in0 = list(k.gather_base)
        k.gather_base = [x + (EG // 2) * 32 * GT for x in k.gather_base]
        full = E // (GT * P)
        assert full % 2 == 0 and full + 2 == EG

        with nc.Block() as block:
            @block.sync
            def _(sp):
                edge_attr = k.a["edge_attr_128"]

                def put(g, i, u):
                    sp.wait_ge(s["value"], g + 1)
                    sp.dma_start(k.values[bass.ds(g * (GT * P), GT * P), 0:D].rearrange("(t p) d -> p t d", p=P),
                                 value[:, u, :, :]).then_inc(s[f"value_put{u}"], 16)

                def done(g, i, u):
                    sp.wait_ge(s[f"value_put{u}"], i * 16 + 16)
                    sp.sem_inc(s["value_free"], 1)

                sp.wait_ge(s["cleared"], 1)
                sp.sem_inc(s["value_free"], 2)
                with sp.Fori(0, full // 2) as i:
                    for u in range(2):
                        g = i * 2 + u
                        sp.wait_ge(s["attr_free"], g + 1)
                        sp.dma_start(attr[:, u, :, :], edge_attr[bass.ds(g * (GT * P), GT * P), :]
                                     .rearrange("(t p) d -> p t d", p=P)).then_inc(s[f"attr{u}"], 16)
                    for stage in (put, done):
                        for u in range(2):
                            stage(i * 2 + u, i, u)
                at, left = full * GT * P, E - full * GT * P
                sp.wait_ge(s["attr_free"], full + 2)
                sp.dma_start(attr[0:left % P, 0, left // P, :], edge_attr[E - left % P:E, :]).then_inc(s["attr_tail"], 16)
                sp.wait_ge(s["attr_tail"], 16)
                sp.dma_start(attr[:, 0, 0:left // P, :], edge_attr[at:at + left // P * P, :]
                             .rearrange("(t p) d -> p t d", p=P)).then_inc(s["attr0"], 16)
                sp.sem_inc(s["attr1"], 16)
                for stage in (put, done):
                    for u in range(2):
                        stage(full + u, full // 2, u)

            @block.gpsimd
            def _(pool):
                with pool.Fori(0, EG // 2) as i:
                    for u in range(2):
                        g = i * 2 + u
                        paced(pool, k, s["free"], g + 1)
                        nc.gpsimd.tensor_copy(index_s[:, u, :, :], k.node_idx[:, :, bass.ds(g * GT, GT)])\
                            .then_inc(s["index"], 1)
                        paced(pool, k, s["index"], g + 1)
                        for c in range(2):
                            for j in range(GT):
                                nc.gpsimd.indirect_dma_start(
                                    out=rows[:, u, c * GT + j, :], out_offset=None, in_=k.layer1,
                                    in_offset=bass.IndirectOffsetOnAxis(ap=index_s[:, u, c, j:j + 1], axis=0))\
                                    .then_inc(k.gathered[u], 16)

            @block.vector
            def _(dve):
                norm.prepare(dve)
                nc.vector.memset(attr[:, :, :, :], 0.0).then_inc(s["cleared"], 1)
                dve.wait_ge(s["cleared"], 1)
                dve.sem_inc(s["free"], 2)
                dve.sem_inc(s["scored"], 1)

                def add(g, i, u):
                    dve.wait_ge(k.gathered[u], i * (32 * GT) + (in0[u] + 32 * GT))
                    nc.vector.tensor_tensor(xin[:, u, :, :], rows[:, u, :, 0:D], rows[:, u, :, D:2 * D],
                                            ALU.add).then_inc(s["added"], 1)
                    dve.wait_ge(s["added"], g + 1)
                    dve.sem_inc(s["free"], 1)
                    norm.statistics(dve, g, u, P, xin[:, u, :, :])

                def normalise(g, i, u):
                    norm.normalise(dve, g, u, P, xn[:, u, :, :], xin[:, u, :, :]).then_inc(s["normed"], 1)

                def score(g, i, u):
                    dve.wait_ge(s["query"], g + 1)
                    nc.vector.tensor_tensor(terms[:, :, :], query[:, :, :], out_ps[1][:, :, :],
                                            ALU.mult).then_inc(s["product"], 1)
                    dve.wait_ge(s["product"], g + 1)
                    nc.vector.tensor_reduce(dots[:, :, :], terms[:, :, :].rearrange("p t (h d) -> p t h d", h=NH),
                                            AX.X, ALU.add).then_inc(s["dots"], 1)
                    dve.wait_ge(s["dots"], g + 1)
                    nc.vector.tensor_tensor(k.scores[:, bass.ds(g * GT, GT), :], dots[:, :, :],
                                            attr_ps[:, 0:GT * NH].rearrange("p (t h) -> p t h", h=NH),
                                            ALU.add).then_inc(s["scored"], 1)

                with dve.Fori(0, EG // 2) as i:
                    for stage in (add, normalise, score):
                        for u in range(2):
                            stage(i * 2 + u, i, u)

            @block.scalar
            def _(act):
                def copy(g, i, u):
                    act.wait_ge(s["turned"], g + 1)
                    act.wait_ge(s["made"], g + 1)
                    for b in range(2):
                        nc.scalar.activation(x_t[:, b * GT:(b + 1) * GT, :], t_ps[b][:, :, :], ACT.Copy)
                    nc.scalar.activation(attr_t[:, :, :], t_ps[2][:, :, :], ACT.Copy).then_inc(s["copied"], 1)

                def values(g, i, u):
                    act.wait_ge(s["made"], g + 2)
                    act.wait_ge(s["scored"], g + 1)
                    nc.scalar.activation(query[:, :, :], out_ps[0][:, :, :], ACT.Copy).then_inc(s["query"], 1)
                    act.wait_ge(s["value_free"], g + 1)
                    nc.scalar.activation(value[:, u, :, :], out_ps[2][:, :, :], ACT.Copy).then_inc(s["value"], 1)

                act.sem_inc(s["copied"], 1)
                with act.Fori(0, EG // 2) as i:
                    for u in range(2):
                        norm.square_root(act, i * 2 + u, u, P)
                    for u in range(2):
                        copy(i * 2 + u, i, u)
                        values(i * 2 + u, i, u)

            @block.tensor
            def _(pe):
                pe.sem_inc(s["made"], 1)
                pe.sem_inc(s["attr_free"], 2)

                def turn(g, i, u):
                    pe.wait_ge(s["normed"], g + 1)
                    pe.wait_ge(s["copied"], g + 1)
                    pe.wait_ge(s[f"attr{u}"], i * 16 + 16)
                    for j in range(C):
                        nc.tensor.transpose(t_ps[j // GT][:, j % GT, :], xn[:, u, j, :], k.ident[:, :])
                    for j in range(GT):
                        mm = nc.tensor.transpose(t_ps[2][:, j, :], attr[:, u, j, :], k.ident[:, :])
                    mm.then_inc(s["turned"], 1)
                    pe.wait_ge(s["turned"], g + 1)
                    pe.sem_inc(s["attr_free"], 1)

                def project(g, i, u):
                    pe.wait_ge(s["copied"], g + 2)
                    pe.wait_ge(s["emptied"], g + 1)
                    for c in range(3):
                        for j in range(GT):
                            nc.tensor.matmul(out_ps[c][:, j, :], x_t[:, j if c == 0 else GT + j, :], k.qkv_w[:, c, :],
                                             start=True, stop=False)
                            nc.tensor.matmul(out_ps[c][:, j, :], k.ones[0:1, :], k.qkv_b[:, c, :], start=False,
                                             stop=True)
                    for j in range(GT):
                        nc.tensor.matmul(attr_ps[:, j * NH:(j + 1) * NH], attr_t[:, j, :], k.wc[:, :], start=True,
                                         stop=False)
                        mm = nc.tensor.matmul(attr_ps[:, j * NH:(j + 1) * NH], k.ones[0:1, :], k.bc[:, :],
                                              start=False, stop=True)
                    mm.then_inc(s["made"], 1)
                    pe.wait_ge(s["value"], g + 1)
                    pe.wait_ge(s["scored"], g + 2)
                    pe.sem_inc(s["emptied"], 1)

                pe.sem_inc(s["emptied"], 1)
                with pe.Fori(0, EG // 2) as i:
                    for u in range(2):
                        turn(i * 2 + u, i, u)
                        project(i * 2 + u, i, u)
        clear_semaphores(nc, norm.sems + list(s.values()))


def softmax_phase(k, o):
    nc = k.nc
    with ExitStack() as st:
        def sb(name, shape, dt=F32):
            return k.sb(st, "sm_" + name, shape, dt)

        packed = sb("packed", [P, CT, Q])
        ids = sb("ids", [Q, CE + 2])
        keep = sb("keep", [Q, 2, CE])
        gate = sb("gate", [Q, CE])
        edge = sb("edge", [Q, CE])
        score = sb("score", [Q, CE])
        p = sb("p", [Q, CE])
        run = sb("run", [Q, 2, CE])
        flags = sb("flags", [Q, 6])
        row = sb("row", [1, 6, Q])
        line = sb("line", [1, 4, Q])
        col = sb("col", [Q, 2])
        t_ps = k.ps(st, "sm_t_ps", [P, 4, P])
        row_ps = k.ps(st, "sm_row_ps", [P, 4, Q])
        end_ps = k.ps(st, "sm_end_ps", [P, 512])
        col_ps = k.ps(st, "sm_col_ps", [P, 512])
        back_ps = k.ps(st, "sm_back_ps", [P, 4, Q])
        s = {x: k.sem(st, "sm_" + x) for x in ("loaded", "set", "step", "packed", "turned", "copied", "rows", "ends",
                                               "cols", "exp", "back", "unpacked", "put")}
        with nc.Block() as block:
            @block.sync
            def _(sp):
                sp.wait_ge(s["set"], 1)
                for h in range(NH):
                    q = h * CH
                    sp.dma_start(ids[q:q + CH, 1:CE + 1], o.id_row[0:EP].rearrange("(c e) -> c e", c=CH))\
                      .then_inc(s["loaded"], 16)
                    sp.dma_start(ids[q:q + CH, CE + 1:CE + 2], o.id_row[1:EP + 1].rearrange("(c e) -> c e", c=CH)
                                 [:, CE - 1:CE], allow_slow_non_contiguous=True).then_inc(s["loaded"], 16)
                    sp.dma_start(ids[q + 1:q + CH, 0:1], o.id_row[0:EP].rearrange("(c e) -> c e", c=CH)
                                 [0:CH - 1, CE - 1:CE], allow_slow_non_contiguous=True).then_inc(s["loaded"], 16)
                sp.wait_ge(s["unpacked"], 1)
                sp.dma_start(k.values[:, D:D + NH].rearrange("(t p) h -> p t h", p=P), k.scores[:, :, :])\
                  .then_inc(s["put"], 16)
                sp.wait_ge(s["put"], 16)

            @block.vector
            def _(dve):
                v = nc.vector
                c = Chain(dve, s["step"], 0)
                c.begin(0)
                v.memset(ids[:, 0:1], -7.0).then_inc(s["set"], 1)
                for ch in range(CH):
                    ins = v.tensor_copy(packed[:, :, :].rearrange("p k (h c) -> p k h c", c=CH)[:, :, :, ch],
                                        k.scores[:, ch * CT:(ch + 1) * CT, :])
                ins.then_inc(s["packed"], 1)
                for kt in range(CT):
                    dve.wait_ge(s["turned"], kt + 1)
                    v.tensor_copy(score[:, kt * P:(kt + 1) * P], t_ps[0:Q, kt % 4, :]).then_inc(s["copied"], 1)
                dve.wait_ge(s["copied"], CT)
                dve.wait_ge(s["loaded"], 16 * 3 * NH)
                own = ids[:, 1:CE + 1]
                v.tensor_tensor(keep[:, 0, :], own, ids[:, 0:CE], ALU.is_equal)
                c.link(v.tensor_tensor(keep[:, 1, :], own, ids[:, 2:CE + 2], ALU.is_equal))
                v.tensor_copy(flags[:, 0:1], keep[:, 0, 0:1])
                v.tensor_copy(flags[:, 1:2], keep[:, 1, CE - 1:CE])
                c.link(v.tensor_tensor(flags[:, 2:3], ids[:, 1:2], ids[:, CE:CE + 1], ALU.is_equal))
                v.tensor_tensor(flags[:, 3:4], flags[:, 0:1], flags[:, 2:3], ALU.mult)
                c.link(v.tensor_tensor(flags[:, 4:5], flags[:, 1:2], flags[:, 2:3], ALU.mult))
                v.memset(keep[:, 0, 0:1], 0.0)
                c.link(v.memset(keep[:, 1, CE - 1:CE], 0.0))
                dve.wait_ge(s["rows"], 1)
                c.link(v.tensor_copy(row[:, 0:4, :], row_ps[0:1, :, :]))
                heads = row[:, 0:4, :].rearrange("p a (h c) -> p a h c", c=CH)
                v.memset(heads[:, 0, :, 0], 0.0)
                v.memset(heads[:, 1, :, CH - 1], 0.0)
                v.memset(heads[:, 2, :, 0], 0.0)
                c.link(v.memset(heads[:, 3, :, CH - 1], 0.0))

                def scan(d, data, additive, out):
                    def way(ap):
                        return ap[:, ::-1] if d else ap

                    c.link(v.tensor_scalar(edge[:, :], own, ids[:, (CE if d else 1):(CE + 1 if d else 2)], None,
                                           ALU.is_equal))
                    if additive:
                        c.link(v.tensor_copy(line[:, 0:2, :], row[:, (1 if d else 0):4:2, :]))
                        c.link(v.tensor_tensor_scan(way(out), way(keep[:, d, :]), way(data), 0.0, ALU.mult, ALU.add))
                    else:
                        c.link(v.tensor_scalar(edge[:, :], edge[:, :], BIG, -BIG, ALU.mult, ALU.add))
                        c.link(v.tensor_scalar(gate[:, :], keep[:, d, :], BIG, -BIG, ALU.mult, ALU.add))
                        c.link(v.tensor_scalar(line[:, 0:2, :], row[:, (1 if d else 0):4:2, :], BIG, -BIG, ALU.mult,
                                               ALU.add))
                        c.link(v.tensor_tensor_scan(way(out), way(gate[:, :]), way(data), -BIG, ALU.add, ALU.max))
                    scan.count += 1
                    c.link(v.tensor_copy(col[:, 0:1], out[:, 0:1] if d else out[:, CE - 1:CE]))
                    scan.ready.append(c.count)
                    dve.wait_ge(s["ends"], scan.count)
                    c.link(v.tensor_copy(line[:, 2, :], end_ps[0:1, 0:Q]))
                    ops = (ALU.mult, ALU.add) if additive else (ALU.add, ALU.max)
                    c.link(v.tensor_tensor_scan(way(line[:, 3, :]), way(line[:, 1, :]), way(line[:, 2, :]),
                                                0.0 if additive else -BIG, *ops))
                    c.link(v.memset(line[:, 2, :], 0.0))
                    shift = (line[:, 2, 0:Q - 1], line[:, 3, 1:Q], line[:, 0, 0:Q - 1]) if d else \
                        (line[:, 2, 1:Q], line[:, 3, 0:Q - 1], line[:, 0, 1:Q])
                    if not additive:
                        c.link(v.memset(line[:, 2, :], -BIG))
                    c.link(v.tensor_tensor(*shift, ops[0]))
                    scan.lines.append(c.count)
                    dve.wait_ge(s["cols"], scan.count)
                    c.link(v.tensor_copy(col[:, 1:2], col_ps[0:Q, 0:1]))
                    if additive:
                        c.link(v.scalar_tensor_tensor(out, edge[:, :], col[:, 1:2], out, ALU.mult, ALU.add))
                    else:
                        c.link(v.scalar_tensor_tensor(out, edge[:, :], col[:, 1:2], out, ALU.add, ALU.max))

                scan.count, scan.ready, scan.lines = 0, [], []
                scan(0, score[:, :], False, run[:, 0, :])
                scan(1, score[:, :], False, run[:, 1, :])
                c.link(v.tensor_tensor(run[:, 0, :], run[:, 0, :], run[:, 1, :], ALU.max))
                c.link(v.tensor_tensor(score[:, :], score[:, :], run[:, 0, :], ALU.subtract))
                softmax_phase.shifted = c.count
                dve.wait_ge(s["exp"], 1)
                scan(0, p[:, :], True, run[:, 0, :])
                scan(1, p[:, :], True, run[:, 1, :])
                c.link(v.tensor_tensor(run[:, 0, :], run[:, 0, :], run[:, 1, :], ALU.add))
                c.link(v.tensor_tensor(run[:, 0, :], run[:, 0, :], p[:, :], ALU.subtract))
                c.link(v.reciprocal(run[:, 1, :], run[:, 0, :]))
                c.link(v.tensor_tensor(p[:, :], p[:, :], run[:, 1, :], ALU.mult))
                softmax_phase.probs = c.count
                softmax_phase.ready, softmax_phase.lines = scan.ready, scan.lines
                scores = k.scores[:, :, :].rearrange("p (c k) h -> p k h c", c=CH)
                for kt in range(CT):
                    dve.wait_ge(s["back"], kt + 1)
                    ins = v.tensor_copy(scores[:, kt, :, :],
                                        back_ps[:, kt % 4, :].rearrange("p (h c) -> p h c", c=CH))
                    ins.then_inc(s["copied"], 1)
                dve.wait_ge(s["copied"], 2 * CT)
                dve.sem_inc(s["unpacked"], 1)

            @block.scalar
            def _(act):
                act.wait_ge(s["step"], softmax_phase.shifted)
                nc.scalar.activation(p[:, :], score[:, :], ACT.Exp).then_inc(s["exp"], 1)

            @block.tensor
            def _(pe):
                pe.wait_ge(s["packed"], 1)
                for kt in range(CT):
                    if kt >= 1:
                        pe.wait_ge(s["copied"], kt)
                    nc.tensor.transpose(t_ps[0:Q, kt % 4, :], packed[:, kt, :], k.ident[:, :])\
                        .then_inc(s["turned"], 1)
                pe.wait_ge(s["step"], 3)
                for a, f in enumerate((0, 1, 3, 4)):
                    ins = nc.tensor.transpose(row_ps[0:1, a, :], flags[:, f:f + 1], k.ident[0:Q, 0:Q])
                ins.then_inc(s["rows"], 1)
                for n in range(4):
                    pe.wait_ge(s["step"], softmax_phase.ready[n])
                    nc.tensor.transpose(end_ps[0:1, 0:Q], col[:, 0:1], k.ident[0:Q, 0:Q]).then_inc(s["ends"], 1)
                    pe.wait_ge(s["step"], softmax_phase.lines[n])
                    nc.tensor.transpose(col_ps[0:Q, 0:1], line[:, 2, :], k.ident[0:1, 0:1]).then_inc(s["cols"], 1)
                pe.wait_ge(s["step"], softmax_phase.probs)
                for kt in range(CT):
                    if kt >= 1:
                        pe.wait_ge(s["copied"], CT + kt)
                    nc.tensor.transpose(back_ps[:, kt % 4, :], p[:, kt * P:(kt + 1) * P], k.ident[0:Q, 0:Q])\
                        .then_inc(s["back"], 1)
        clear_semaphores(nc, list(s.values()))


def fill_phase(k, table, row):
    nc = k.nc
    with ExitStack() as st:
        rows = k.sb(st, "fill_rows", [P, NJ, D])
        load_constants(k, [(rows[:, j, :], row.partition_broadcast(P)) for j in range(NJ)])
        stored = k.sem(st, "fill_stored")
        with nc.Block() as block:
            @block.sync
            def _(sp):
                with sp.Fori(0, NG) as g:
                    sp.dma_start(node_rows(table, g, P), rows[:, :, :]).then_inc(stored, 16)
                sp.dma_start(node_rows(table, NG, TAILP), rows[0:TAILP, :, :]).then_inc(stored, 16)
                sp.wait_ge(stored, 16 * (NG + 1))
        clear_semaphores(nc, [stored])


def transformer_phase(k):
    nc = k.nc
    a = k.a
    NB = 4
    with ExitStack() as st:
        def sb(name, shape):
            return k.sb(st, "tf_" + name, shape)

        w1, w2 = sb("w1", [P, NB * D]), sb("w2", [P, NB, D])
        b1, b2 = sb("b1", [P, NB]), sb("b2", [P, D])
        g2, be2 = sb("g2", [P, 1]), sb("be2", [P, 1])
        both = sb("both", [P, 2, NJ, 2 * D])
        msum = sb("msum", [P, 2, NJ, D])
        xin, x2, xm, xn, rest, x3in, x3 = (sb(x, [P, 2, NJ, D]) for x in
                                           ("xin", "x2", "xm", "xn", "rest", "x3in", "x3"))
        x_t = sb("x_t", [P, 2, NJ, P])
        hidden = sb("hidden", [P, 2, NB, 4 * P])
        norms = [Norm(k, st, f"tf_norm{m}") for m in range(3)]
        x_ps = [k.ps(st, f"tf_x_ps{b}", [P, 4, P]) for b in range(2)]
        h_ps = [k.ps(st, f"tf_h_ps{b}", [P, 4 * P]) for b in range(NB)]
        o_ps = [k.ps(st, f"tf_o_ps{b}", [P, 4, D]) for b in range(2)]
        names = ["ready0", "ready1", "msum_ready0", "msum_ready1", "free", "msum_free", "rest_used", "added", "x2_made", "xm_made", "rest_made", "rest_half", "normed",
                 "turned", "x_copied", "hidden_made", "bent", "out_made", "out_free", "x3_added", "x3_made",
                 "stored0", "stored1", "w_step", "w_made"]
        s = {x: k.sem(st, "tf_" + x) for x in names}
        load_constants(k, [(w1[:, :], a["L2_gnn_W1"]),
                           (w2[:, :, :], a["L2_gnn_W2"].rearrange("(b p) d -> p b d", p=P)),
                           (b2[:, :], a["L2_gnn_b2"].partition_broadcast(P)),
                           (g2[:, :], a["L2_gnn_g2"].rearrange("(p r) -> p r", r=1)),
                           (be2[:, :], a["L2_gnn_be2"].rearrange("(p r) -> p r", r=1))]
                       + [(b1[:, b:b + 1], a["L2_gnn_b1"][b * P:(b + 1) * P].rearrange("(p r) -> p r", r=1))
                          for b in range(NB)])
        with nc.Block() as block:
            @block.sync
            def _(sp):
                def load(n, i, u, p):
                    sp.wait_ge(s["free"], n + 1)
                    sp.dma_start(both[0:p, u, :, :], node_rows(k.layer1, n, p, 2 * D)).then_inc(s[f"ready{u}"], 16)

                def load_msum(n, i, u, p):
                    sp.wait_ge(s["msum_free"], n + 1)
                    sp.dma_start(msum[0:p, u, :, :], node_rows(k.msum, n, p)).then_inc(s[f"msum_ready{u}"], 16)

                def store(n, i, u, p):
                    sp.wait_ge(s["x3_made"], n + 3)
                    sp.dma_start(node_rows(k.x3, n, p), x3[0:p, u, :, :]).then_inc(s[f"stored{u}"], 16)

                sp.sem_inc(s["stored0"], 16)
                sp.sem_inc(s["stored1"], 16)
                staggered(sp, (load_msum, 1), (load, 0), (store, 6))
                sp.wait_ge(s["stored0"], 16 * (NG // 2 + 2))
                sp.wait_ge(s["stored1"], 16 * (NG // 2 + 1))

            @block.gpsimd
            def _(pool):
                def add(n, i, u, p):
                    paced(pool, k, s[f"ready{u}"], i * 16 + 16)
                    paced(pool, k, s["x2_made"], n + 1)
                    nc.gpsimd.tensor_tensor(xin[0:p, u, :, :], both[0:p, u, :, 0:D], both[0:p, u, :, D:2 * D],
                                            ALU.add).then_inc(s["added"], 1)

                def freed(n, i, u, p):
                    pool.wait_ge(s["added"], n + 1)
                    pool.sem_inc(s["free"], 1)

                def leave(n, i, u, p):
                    paced(pool, k, s["xm_made"], n + 1)
                    paced(pool, k, s["rest_used"], n + 1)
                    nc.gpsimd.tensor_tensor(rest[0:p, u, :, :], x2[0:p, u, :, :], xm[0:p, u, :, :],
                                            ALU.add).then_inc(s["rest_half"], 1)
                    paced(pool, k, s["rest_half"], n + 1)
                    nc.gpsimd.tensor_tensor(rest[0:p, u, :, :], rest[0:p, u, :, :],
                                            b2[0:p, :].unsqueeze(1).broadcast_to([p, NJ, D]),
                                            ALU.add).then_inc(s["rest_made"], 1)

                pool.sem_inc(s["free"], 2)
                pool.sem_inc(s["rest_made"], 2)
                staggered(pool, (add, 0), (freed, 0), (leave, 2))

            @block.vector
            def _(dve):
                v = nc.vector
                for norm in norms:
                    norm.prepare(dve)
                dve.wait_ge(s["w_made"], 1)
                v.tensor_tensor(b1[:, :], b1[:, :], o_ps[0][:, 0, 0:NB], ALU.add).then_inc(s["w_step"], 1)
                v.tensor_scalar(w1[:, :], w1[:, :], g2[:, 0:1], None, ALU.mult).then_inc(s["w_step"], 1)
                dve.wait_ge(s["w_step"], 2)
                dve.sem_inc(s["msum_free"], 2)
                dve.sem_inc(s["x2_made"], 2)
                dve.sem_inc(s["rest_used"], 2)
                dve.sem_inc(s["out_free"], 1)

                def first(n, i, u, p):
                    dve.wait_ge(s["added"], n + 1)
                    norms[0].statistics(dve, n, u, p, xin[:, u, :, :])

                def second(n, i, u, p):
                    dve.wait_ge(s["rest_made"], n + 1)
                    norms[0].normalise(dve, n, u, p, x2[:, u, :, :], xin[:, u, :, :]).then_inc(s["x2_made"], 1)
                    dve.wait_ge(s["x2_made"], n + 3)
                    dve.wait_ge(s[f"msum_ready{u}"], i * 16 + 16)
                    v.tensor_tensor(xm[0:p, u, :, :], x2[0:p, u, :, :], msum[0:p, u, :, :],
                                    ALU.add).then_inc(s["xm_made"], 1)
                    dve.wait_ge(s["xm_made"], n + 1)
                    dve.sem_inc(s["msum_free"], 1)
                    norms[1].statistics(dve, n, u, p, xm[:, u, :, :])

                def third(n, i, u, p):
                    dve.wait_ge(s["turned"], n + 1)
                    norms[1].normalise(dve, n, u, p, xn[:, u, :, :], xm[:, u, :, :]).then_inc(s["normed"], 1)

                def fourth(n, i, u, p):
                    dve.wait_ge(s["rest_made"], n + 3)
                    dve.wait_ge(s["x3_made"], n + 1)
                    for b in range(2):
                        dve.wait_ge(s["out_made"], n * 2 + b + 3)
                        ins = v.tensor_tensor(x3in[0:p, u, 4 * b:4 * b + 4, :], rest[0:p, u, 4 * b:4 * b + 4, :],
                                              o_ps[b][0:p, :, :], ALU.add)
                    ins.then_inc(s["x3_added"], 1)
                    dve.wait_ge(s["x3_added"], n + 1)
                    dve.sem_inc(s["out_free"], 1)
                    norms[2].statistics(dve, n, u, p, x3in[:, u, :, :])
                    dve.sem_inc(s["rest_used"], 1)

                staggered(dve, (lambda n, i, u, p: norms[2].negate(dve, n, u, p), 5), (third, 2), (second, 1),
                          (first, 0), (fourth, 3))

            @block.scalar
            def _(act):
                act.wait_ge(s["w_step"], 2)
                act.sem_inc(s["x_copied"], 1)
                act.sem_inc(s["bent"], NB)
                act.sem_inc(s["x3_made"], 2)

                def front(n, i, u, p):
                    act.wait_ge(s["turned"], n + 3)
                    for b in range(2):
                        ins = nc.scalar.activation(x_t[:, u, 4 * b:4 * b + 4, 0:p], x_ps[b][:, :, 0:p], ACT.Copy)
                    ins.then_inc(s["x_copied"], 1)

                def back(n, i, u, p):
                    for h in range(2):
                        act.wait_ge(s["out_made"], n * 2 + h + 1)
                        for b in range(NB):
                            act.wait_ge(s["hidden_made"], n * (2 * NB) + h * NB + b + 1)
                            nc.scalar.activation(hidden[:, h, b, :], h_ps[b][:, :], ACT.Relu,
                                                 bias=b1[:, b:b + 1]).then_inc(s["bent"], 1)

                def finish(n, i, u, p):
                    act.wait_ge(s[f"stored{u}"], i * 16 + 16)
                    norms[2].normalise_on_act(act, n, u, p, x3[:, u, :, :], x3in[:, u, :, :]).then_inc(s["x3_made"], 1)

                staggered(act, (front, 2), (back, 2), (lambda n, i, u, p: norms[1].square_root(act, n, u, p), 1),
                          (lambda n, i, u, p: norms[0].square_root(act, n, u, p), 0),
                          (lambda n, i, u, p: norms[2].square_root(act, n, u, p), 4), (finish, 5))

            @block.tensor
            def _(pe):
                for b in range(NB):
                    mm = nc.tensor.matmul(o_ps[0][:, 0, b:b + 1], w1[:, b * P:(b + 1) * P], be2[:, 0:1], start=True,
                                          stop=True)
                mm.then_inc(s["w_made"], 1)
                pe.wait_ge(s["w_step"], 2)
                pe.sem_inc(s["out_made"], 2)
                pe.sem_inc(s["turned"], 2)

                def turn(n, i, u, p):
                    pe.wait_ge(s["normed"], n + 1)
                    pe.wait_ge(s["x_copied"], n + 1)
                    for j in range(NJ):
                        mm = nc.tensor.transpose(x_ps[j // 4][:, j % 4, 0:p], xn[0:p, u, j, :], k.ident[0:p, 0:p])
                    mm.then_inc(s["turned"], 1)

                def feed_forward(n, i, u, p):
                    pe.wait_ge(s["x_copied"], n + 2)
                    for h in range(2):
                        for b in range(NB):
                            pe.wait_ge(s["bent"], n * (2 * NB) + h * NB + b + 1)
                            nc.tensor.matmul(h_ps[b][:, :], w1[:, b * P:(b + 1) * P],
                                             x_t[:, u, 4 * h:4 * h + 4, :].rearrange("p j e -> p (j e)"), start=True,
                                             stop=True).then_inc(s["hidden_made"], 1)
                    pe.wait_ge(s["out_free"], n + 1)
                    for h in range(2):
                        pe.wait_ge(s["bent"], n * (2 * NB) + (h + 2) * NB)
                        for j in range(4):
                            for b in range(NB):
                                mm = nc.tensor.matmul(o_ps[h][0:p, j, :], hidden[:, h, b, j * P:j * P + p], w2[:, b, :],
                                                      start=b == 0, stop=b == NB - 1)
                        mm.then_inc(s["out_made"], 1)

                staggered(pe, (turn, 2), (feed_forward, 2))
        clear_semaphores(nc, [x for norm in norms for x in norm.sems] + list(s.values()))


def mean_layer_phase(k, out):
    nc = k.nc
    a = k.a
    with ExitStack() as st:
        def sb(name, shape):
            return k.sb(st, "ml_" + name, shape)

        w, w_t = sb("w", [P, D]), sb("w_t", [P, D])
        bias = sb("bias", [3, D])
        gamma, beta = sb("gamma", [P, D]), sb("beta", [P, D])
        mix = sb("mix", [P, 4])
        x3, agg, y, z, shifted, scaled, total, res = (sb(x, [P, 2, NJ, D]) for x in
                                               ("x3", "agg", "y", "z", "shifted", "scaled", "total", "res"))
        norms = [Norm(k, st, f"ml_norm{m}") for m in range(2)]
        w_ps = k.ps(st, "ml_w_ps", [P, 512])
        names = ["ready0", "ready1", "free", "summed", "y_made", "shifted", "z_made", "normed", "gained",
                 "added", "res_made", "stored0", "stored1", "w_turned", "w_step", "w_exp"]
        s = {x: k.sem(st, "ml_" + x) for x in names}
        load_constants(k, [(w[:, :], a["L3_gnn_W"]), (bias[:, :], a["L3_gnn_b"].partition_broadcast(3)),
                           (gamma[:, :], a["L3_gnn_gamma"].partition_broadcast(P)),
                           (beta[:, :], a["L3_gnn_beta"].partition_broadcast(P)),
                           (mix[:, 0:1], a["L3_gnn_alpha"].partition_broadcast(P))])
        with nc.Block() as block:
            @block.vector
            def _(dve):
                v = nc.vector
                c = Chain(dve, s["w_step"], 5)
                c.begin(0)
                dve.wait_ge(s["w_exp"], 1)
                c.link(v.tensor_scalar(mix[:, 1:2], mix[:, 1:2], 1.0, None, ALU.add))
                c.link(v.reciprocal(mix[:, 2:3], mix[:, 1:2]))
                c.link(v.tensor_scalar(mix[:, 3:4], mix[:, 2:3], -1.0, 1.0, ALU.mult, ALU.add))
                c.link(v.tensor_scalar(bias[:, :], bias[:, :], mix[0:3, 2:3], None, ALU.mult))
                dve.wait_ge(s["w_turned"], 1)
                c.link(v.tensor_scalar(w_t[:, :], w_ps[:, 0:D], mix[:, 2:3], None, ALU.mult))
                c.end()

            @block.scalar
            def _(act):
                nc.scalar.activation(mix[:, 1:2], mix[:, 0:1], ACT.Exp, scale=-1.0).then_inc(s["w_exp"], 1)

            @block.tensor
            def _(pe):
                nc.tensor.transpose(w_ps[:, 0:D], w[:, :], k.ident[:, :]).then_inc(s["w_turned"], 1)
        conv = Linear(k, st, "ml_conv", w_t[:, :], split_bias_phase(k, st, "ml_bias", bias[:, :]))
        with nc.Block() as block:
            @block.sync
            def _(sp):
                def load(n, i, u, p):
                    sp.wait_ge(s["free"], n + 1)
                    sp.wait_ge(s["shifted"], n + 1)
                    sp.dma_start(x3[0:p, u, :, :], node_rows(k.x3, n, p)).then_inc(s[f"ready{u}"], 16)
                    sp.dma_start(agg[0:p, u, :, :], node_rows(k.agg, n, p)).then_inc(s[f"ready{u}"], 16)

                def store(n, i, u, p):
                    sp.wait_ge(s["res_made"], n + 3)
                    sp.dma_start(node_rows(out, n, p), res[0:p, u, :, :]).then_inc(s[f"stored{u}"], 16)

                sp.sem_inc(s["stored0"], 16)
                sp.sem_inc(s["stored1"], 16)
                staggered(sp, (load, 0), (store, 5))
                sp.wait_ge(s["stored0"], 16 * (NG // 2 + 2))
                sp.wait_ge(s["stored1"], 16 * (NG // 2 + 1))

            @block.gpsimd
            def _(pool):
                def add(n, i, u, p):
                    paced(pool, k, s[f"ready{u}"], i * 32 + 32)
                    nc.gpsimd.tensor_tensor(agg[0:p, u, :, :], agg[0:p, u, :, :], x3[0:p, u, :, :],
                                            ALU.add).then_inc(s["summed"], 1)

                def shift(n, i, u, p):
                    paced(pool, k, s["added"], n + 1)
                    nc.gpsimd.tensor_tensor(shifted[0:p, u, :, :], x3[0:p, u, :, :],
                                            beta[0:p, :].unsqueeze(1).broadcast_to([p, NJ, D]),
                                            ALU.add).then_inc(s["shifted"], 1)

                def gain(n, i, u, p):
                    paced(pool, k, s["normed"], n + 1)
                    nc.gpsimd.tensor_tensor(scaled[0:p, u, :, :], scaled[0:p, u, :, :],
                                            gamma[0:p, :].unsqueeze(1).broadcast_to([p, NJ, D]),
                                            ALU.mult).then_inc(s["gained"], 1)

                pool.sem_inc(s["shifted"], 2)
                staggered(pool, (add, 0), (shift, 1), (gain, 2))

            @block.vector
            def _(dve):
                v = nc.vector
                for norm in norms:
                    norm.prepare(dve)
                dve.sem_inc(s["free"], 2)
                dve.sem_inc(s["added"], 2)
                dve.sem_inc(conv.free, 1)

                def front(n, i, u, p):
                    dve.wait_ge(s["summed"], n + 1)
                    c = k.dinv2[0:p, n * NJ:n * NJ + NJ] if isinstance(n, int) else k.dinv2[0:p, bass.ds(n * NJ, NJ)]
                    v.tensor_tensor(y[0:p, u, :, :], agg[0:p, u, :, :], c.unsqueeze(2).broadcast_to([p, NJ, D]),
                                    ALU.mult).then_inc(s["y_made"], 1)

                def back(n, i, u, p):
                    dve.wait_ge(conv.made, n + 2)
                    dve.wait_ge(s[f"ready{u}"], i * 32 + 32)
                    for b in range(2):
                        ins = v.scalar_tensor_tensor(z[0:p, u, 4 * b:4 * b + 4, :], x3[0:p, u, 4 * b:4 * b + 4, :],
                                                     mix[0:p, 3:4], conv.out[b][0:p, :, :], ALU.mult, ALU.add)
                    ins.then_inc(s["z_made"], 1)
                    dve.wait_ge(s["z_made"], n + 1)
                    dve.sem_inc(s["free"], 1)
                    dve.sem_inc(conv.free, 1)
                    norms[0].statistics(dve, n, u, p, z[:, u, :, :])

                def middle(n, i, u, p):
                    norms[0].normalise(dve, n, u, p, scaled[:, u, :, :], z[:, u, :, :]).then_inc(s["normed"], 1)

                def last(n, i, u, p):
                    dve.wait_ge(s["shifted"], n + 3)
                    dve.wait_ge(s["gained"], n + 1)
                    dve.wait_ge(s["res_made"], n + 1)
                    v.tensor_tensor(total[0:p, u, :, :], scaled[0:p, u, :, :], shifted[0:p, u, :, :],
                                    ALU.add).then_inc(s["added"], 1)
                    dve.wait_ge(s["added"], n + 3)
                    norms[1].statistics(dve, n, u, p, total[:, u, :, :])

                staggered(dve, (lambda n, i, u, p: norms[1].negate(dve, n, u, p), 4), (last, 3), (middle, 2), (back, 1),
                          (front, 0))

            @block.scalar
            def _(act):
                act.sem_inc(conv.copied, 1)
                act.sem_inc(s["res_made"], 2)

                def finish(n, i, u, p):
                    act.wait_ge(s[f"stored{u}"], i * 16 + 16)
                    norms[1].normalise_on_act(act, n, u, p, res[:, u, :, :], total[:, u, :, :]).then_inc(s["res_made"], 1)

                staggered(act, (lambda n, i, u, p: norms[1].square_root(act, n, u, p), 4),
                          (lambda n, i, u, p: norms[0].square_root(act, n, u, p), 2),
                          (lambda n, i, u, p: conv.copy(act, n, p), 0), (finish, 4))

            @block.tensor
            def _(pe):
                pe.sem_inc(conv.made, 1)

                def turn(n, i, u, p):
                    pe.wait_ge(s["y_made"], n + 1)
                    conv.turn(pe, n, p, y[:, u, :, :])

                staggered(pe, (turn, 0), (lambda n, i, u, p: conv.product(pe, n, p), 0))
        clear_semaphores(nc, [x for norm in norms for x in norm.sems] + conv.sems + list(s.values()))


ROUTING_STEPS = 4


def build(nc, a, out):
    k = Ctx(nc, None)
    k.a = a
    k.x, k.src, k.dst = a["x"], a["src"], a["dst"]
    with ExitStack() as st:
        k.paces = k.sem(st, "paces")
        k.gather_base, k.scatter_base = [0, 0], [0, 0]
        k.gathered = [k.sem(st, f"gathered{u}") for u in range(2)]
        k.scattered = [k.sem(st, f"scattered{u}") for u in range(2)]
        k.src_row = nc.dram_tensor("src_row", (EP + 1,), F32, kind="Internal").ap()
        k.dst_row = nc.dram_tensor("dst_row", (EP + 1,), F32, kind="Internal").ap()
        k.low_row = nc.dram_tensor("low_row", (EP,), F32, kind="Internal").ap()
        k.sorted4 = nc.dram_tensor("sorted4", (EP, 4), I32, kind="Internal").ap()
        k.sorted_row = nc.dram_tensor("sorted_row", (EP + 1,), F32, kind="Internal").ap()
        k.agg = nc.dram_tensor("agg", (N, D), F32, kind="Internal").ap()
        k.layer1 = nc.dram_tensor("layer1", (N, 2 * D), F32, kind="Internal").ap()
        k.layer1_halves = k.layer1.rearrange("n (c d) -> (n c) d", c=2)
        k.pairs = nc.dram_tensor("pairs", (EP, 2 * D), F32, kind="Internal").ap()
        k.end_sums = nc.dram_tensor("end_sums", (2, T, D), F32, kind="Internal").ap()
        k.handed_sums = nc.dram_tensor("handed_sums", (2, T, D), F32, kind="Internal").ap()
        k.values = nc.dram_tensor("values", (EP, D + NH), F32, kind="Internal").ap()
        k.msum = nc.dram_tensor("msum", (N, D), F32, kind="Internal").ap()
        k.x3 = nc.dram_tensor("x3", (N, D), F32, kind="Internal").ap()
        k.qkv_w = k.sb(st, "qkv_w", [P, 3, D])
        k.qkv_b = k.sb(st, "qkv_b", [1, 3, D])
        k.wc = k.sb(st, "wc", [P, NH])
        k.bc = k.sb(st, "bc", [1, NH])
        k.wo = k.sb(st, "wo", [P, D])
        k.bo_row = k.sb(st, "bo_row", [1, D])
        k.gcn_w = k.sb(st, "gcn_w", [P, D])
        k.gcn_c = k.sb(st, "gcn_c", [P, D])
        k.ones = k.sb(st, "ones", [P, P])
        k.ones3 = k.sb(st, "ones3", [3, P], BF16)
        k.zeros = k.sb(st, "zeros", [P, NJ * D])
        k.eps = k.sb(st, "eps", [P, 1])
        k.iota_row = k.sb(st, "iota_row", [P, P])
        k.iota_high = k.sb(st, "iota_high", [P, NCOL])
        k.iota_part = k.sb(st, "iota_part", [P, 1])
        k.ident = k.sb(st, "ident", [P, P])
        k.before = k.sb(st, "before", [P, P])
        k.earlier = k.sb(st, "earlier", [P, P])
        k.last_part = k.sb(st, "last_part", [P, 1])
        k.id_col = k.sb(st, "id_col", [P, 1, 2, T])
        k.node_idx = k.sb(st, "node_idx", [P, 2, T], I32)
        k.low_col = k.sb(st, "low_col", [P, 2, T])
        k.high_col = k.sb(st, "high_col", [P, 2, T])
        k.degree = k.sb(st, "degree", [P, NCOL])
        k.dinv = k.sb(st, "dinv", [P, NCOL])
        k.dinv2 = k.sb(st, "dinv2", [P, NCOL])
        k.start = k.sb(st, "start", [P, NCOL])
        k.dinv_src = k.sb(st, "dinv_src", [P, T])
        by_dst = Order(k.dst_row, k.id_col[:, 0, 1, :], k.sb(st, "d_prev", [P, T]), k.sb(st, "d_last", [P, T], I32))
        by_src = Order(k.sorted_row, k.sb(st, "s_id", [P, T]), k.sb(st, "s_prev", [P, T]),
                       k.sb(st, "s_last", [P, T], I32), k.sorted4, k.sb(st, "s_eid", [P, T], I32),
                       k.sb(st, "s_own", [P, T], I32), k.sb(st, "s_far", [P, T], I32),
                       k.sb(st, "s_last_cap", [P, T], I32))
        constants_phase(k)
        ids_phase(k)
        count_phase(k)
        rank_phase(k)
        order_phase(k, by_dst, "ord_d")
        order_phase(k, by_src, "ord_s")
        zero_phase(k, [k.agg])

        def by_degree(dve, out, rows, g):
            w = k.dinv_src[:, bass.ds(g * GT, GT)].unsqueeze(2).broadcast_to([P, GT, D])
            return nc.vector.tensor_tensor(out, rows, w, ALU.mult)

        segment_sum_phase(k, by_dst, k.x, D, k.node_idx[:, 0, :], k.agg, "gcn", by_degree)
        moments_phase(k)
        capsules_phase(k)
        with ExitStack() as routing:
            k.vals = k.sb(routing, "vals", [P, T, D])
            k.end_mask = k.sb(routing, "end_mask", [P, T, 2])
            k.ends2 = k.sb(routing, "ends2", [2, T])
            k.handed = k.sb(routing, "handed", [TB, 2, 2, T])
            routing_setup_phase(k, by_src)
            for step in range(ROUTING_STEPS + 1):
                if step:
                    exchange_phase(k, f"ex{step}")
                routing_phase(k, by_src, step, ROUTING_STEPS, f"ro{step}")
        k.scores = k.sb(st, "scores", [P, T, NH])
        attention_weights_phase(k)
        scores_phase(k, by_dst)
        softmax_phase(k, by_dst)
        fill_phase(k, k.msum, a["L2_gnn_bo"])

        def by_head(dve, out, rows, g):
            return nc.vector.tensor_tensor(
                out.rearrange("p t (h d) -> p t h d", h=NH), rows[:, :, 0:D].rearrange("p t (h d) -> p t h d", h=NH),
                rows[:, :, D:D + NH].unsqueeze(3).broadcast_to([P, GT, NH, HD]), ALU.mult)

        segment_sum_phase(k, by_src, k.values, D + NH, by_src.eid, k.msum, "msg", by_head, k.wo[:, :],
                          k.bo_row[:, :])
        transformer_phase(k)
        segment_sum_phase(k, by_dst, k.x3, D, k.node_idx[:, 0, :], k.agg, "mean", None)
        mean_layer_phase(k, out)


_INS = ["x", "src", "dst", "edge_attr_128"] + ["L0_gnn_W", "L0_gnn_b", "L0_gnn_gamma", "L0_gnn_beta", "L1_gnn_weight",
    "L1_gnn_bias"] + ["L2_gnn_" + x for x in ("Wq bq Wk bk Wv bv Wo bo Wc bc W1 b1 W2 b2 g1 be1 g2 be2").split()] + [
    "L3_gnn_" + x for x in "W b alpha gamma beta".split()]


def kernel(**inputs):
    import numpy as _np
    import concourse.bacc as _bacc
    from concourse import mybir as _mybir
    from concourse.bass_utils import run_bass_kernel_spmd as _run

    nc = _bacc.Bacc("TRN2", target_bir_lowering=False, num_devices=1)
    arrays, aps = {}, {}
    for name in _INS:
        v = _np.ascontiguousarray(inputs[name])
        arrays[f"in_{name}_dram"] = v
        aps[name] = nc.dram_tensor(f"in_{name}_dram", v.shape, _mybir.dt.from_np(v.dtype), kind="ExternalInput").ap()
    out = nc.dram_tensor("out_0_dram", (50000, 128), _mybir.dt.float32, kind="ExternalOutput").ap()
    build(nc, aps, out)
    r = _run(nc, [arrays], core_ids=[0])
    return r.results[0]["out_0_dram"]
```

```python
from contextlib import ExitStack

import concourse.bass as bass
from concourse import mybir

F32 = mybir.dt.float32
BF16 = mybir.dt.bfloat16
FP16 = mybir.dt.float16
I32 = mybir.dt.int32
ALU = mybir.AluOpType
ACT = mybir.ActivationFunctionType
AX = mybir.AxisListType

P = 128
D = 128
N = 50000
E = 25000
NH = 8
HD = D // NH
T = 200
EP = T * P
TB = 100
GT = 4
EG = T // GT
NJ = 8
NG = N // (P * NJ)
TAILP = (N - NG * P * NJ) // NJ
NCOL = (NG + 1) * NJ
PAD_ID = N
EPS = 1e-5
BIG = 1.0e30
FAR = 1 << 20


def span(n, size):
    return slice(n * size, n * size + size) if isinstance(n, int) else bass.ds(n * size, size)


def after(n, k=1):
    return n * k + k


class Ctx:

    def __init__(self, nc):
        self.nc = nc

    def sb(self, stack, name, shape, dt=F32):
        return stack.enter_context(self.nc.sbuf_tensor(name, shape, dt))

    def ps(self, stack, name, shape, dt=F32):
        return stack.enter_context(self.nc.psum_tensor(name, shape, dt))

    def sem(self, stack, name):
        return stack.enter_context(self.nc.semaphore(name))


def clear_semaphores(nc, sems):
    with nc.Block() as block:
        @block.gpsimd
        def _(pool):
            for s in sems:
                pool.sem_clear(s)


def ids_phase(k):
    nc = k.nc
    with ExitStack() as st:
        rows = k.sb(st, "ids_rows_i", [TB, 2, 2, P], I32)
        rows_f = k.sb(st, "ids_rows_f", [TB, 2, 2, P])
        low = k.sb(st, "ids_low_i", [TB, 2, 2, P], I32)
        low_f = k.sb(st, "ids_low_f", [TB, 2, 2, P])
        cols_i = k.sb(st, "ids_cols_i", [P, 2, T], I32)
        part = k.sb(st, "ids_part_i", [P, 2, 2, T], I32)
        minus = k.sb(st, "ids_minus", [1, 1])
        pt = k.ps(st, "ids_pt", [P, 2, 2, 256])
        padded = k.sem(st, "ids_padded")
        loaded = k.sem(st, "ids_loaded")
        step = k.sem(st, "ids_step")
        turned = k.sem(st, "ids_turned")
        stored = k.sem(st, "ids_stored")
        with nc.Block() as block:
            @block.sync
            def _(sp):
                sp.wait_ge(padded, 1)
                full = (E // P - TB)
                for a, ids in enumerate((k.src, k.dst)):
                    sp.dma_start(rows[:, a, 0, :], ids[0:TB * P].rearrange("(r e) -> r e", e=P)).then_inc(loaded, 16)
                    sp.dma_start(rows[0:full, a, 1, :],
                                 ids[TB * P:(TB + full) * P].rearrange("(r e) -> r e", e=P)).then_inc(loaded, 16)
                    sp.dma_start(rows[full:full + 1, a, 1, 0:E - (TB + full) * P],
                                 ids[(TB + full) * P:E].rearrange("(r e) -> r e", r=1)).then_inc(loaded, 16)
                sp.wait_ge(step, 3)
                for a, row in enumerate((k.src_row, k.dst_row)):
                    sp.dma_start(row[0:EP].rearrange("(b r e) -> r b e", b=2, e=P), rows_f[:, a]).then_inc(stored, 16)
                sp.dma_start(k.low_row[0:EP].rearrange("(b r e) -> r b e", b=2, e=P), low_f[:, 0]).then_inc(stored, 16)
                sp.dma_start(k.dst_row[EP:EP + 1].rearrange("(r e) -> r e", r=1), minus[:, :]).then_inc(stored, 16)
                sp.wait_ge(stored, 64)

            @block.vector
            def _(dve):
                nc.vector.memset(minus[:, :], -1.0)
                nc.vector.memset(rows[:, :, :, :], PAD_ID).then_inc(padded, 1)
                dve.wait_ge(loaded, 96)
                nc.vector.tensor_copy(rows_f[:, :, :, :], rows[:, :, :, :]).then_inc(step, 1)
                nc.vector.tensor_scalar(low[:, :, :, :], rows[:, :, :, :], 3, 127, ALU.arith_shift_right,
                                        ALU.bitwise_and).then_inc(step, 1)
                dve.wait_ge(step, 2)
                nc.vector.tensor_copy(low_f[:, :, :, :], low[:, :, :, :]).then_inc(step, 1)
                dve.wait_ge(turned, 1)
                nc.vector.tensor_copy(k.id_col[:, 0, :, :], pt[:, :, 0, 0:T]).then_inc(step, 1)
                nc.vector.tensor_copy(cols_i[:, :, :], pt[:, :, 0, 0:T]).then_inc(step, 1)
                nc.vector.tensor_copy(k.low_col[:, :, :], pt[:, :, 1, 0:T]).then_inc(step, 1)
                dve.wait_ge(step, 5)
                nc.vector.tensor_scalar(part[:, 0, :, :], cols_i[:, :, :], 10, 3, ALU.arith_shift_right,
                                        ALU.arith_shift_left).then_inc(step, 1)
                nc.vector.tensor_scalar(part[:, 1, :, :], cols_i[:, :, :], 7, None, ALU.bitwise_and).then_inc(step, 1)
                nc.vector.tensor_scalar(k.node_idx[:, :, :], k.id_col[:, 0, :, :], float(N - 1), None, ALU.min)
                dve.wait_ge(step, 8)
                nc.vector.tensor_tensor(k.high_col[:, :, :], part[:, 0, :, :], part[:, 1, :, :],
                                        ALU.add).then_inc(step, 1)
                dve.wait_ge(step, 9)

            @block.tensor
            def _(pe):
                pe.wait_ge(step, 3)
                for a in range(2):
                    for b in range(2):
                        nc.tensor.transpose(pt[:, a, 0, b * TB:(b + 1) * TB], rows_f[:, a, b, :], k.ident[0:TB, 0:TB])
                        last = nc.tensor.transpose(pt[:, a, 1, b * TB:(b + 1) * TB], low_f[:, a, b, :],
                                                   k.ident[0:TB, 0:TB])
                last.then_inc(turned, 1)
        clear_semaphores(nc, [padded, loaded, step, turned, stored])


def constants_phase(k):
    nc = k.nc
    with ExitStack() as st:
        it = k.sb(st, "cst_iota", [P, P], I32)
        ih = k.sb(st, "cst_iota_high", [P, NCOL], I32)
        ip = k.sb(st, "cst_iota_part", [P, 1], I32)
        made = k.sem(st, "cst_made")
        step = k.sem(st, "cst_step")
        with nc.Block() as block:
            @block.gpsimd
            def _(pool):
                nc.gpsimd.iota(it[:, :], pattern=[[1, P]], base=0, channel_multiplier=0).then_inc(made, 1)
                nc.gpsimd.iota(ih[:, :], pattern=[[1, NCOL]], base=0, channel_multiplier=0).then_inc(made, 1)
                nc.gpsimd.iota(ip[:, :], pattern=[[0, 1]], base=0, channel_multiplier=1).then_inc(made, 1)

            @block.vector
            def _(dve):
                nc.vector.memset(k.ones[:, :], 1.0).then_inc(step, 1)
                nc.vector.memset(k.ones3[:, :], 1.0)
                nc.vector.memset(k.zeros[:, :], 0.0).then_inc(step, 1)
                nc.vector.memset(k.eps[:, :], EPS).then_inc(step, 1)
                dve.wait_ge(made, 3)
                nc.vector.tensor_copy(k.iota_row16[:, :], it[:, :])
                nc.vector.tensor_copy(k.iota_high16[:, :], ih[:, :])
                nc.vector.tensor_copy(k.iota_row[:, :], it[:, :]).then_inc(step, 1)
                nc.vector.tensor_copy(k.iota_high[:, :], ih[:, :]).then_inc(step, 1)
                nc.vector.tensor_copy(k.iota_part[:, :], ip[:, :]).then_inc(step, 1)
                dve.wait_ge(step, 6)
                nc.vector.tensor_scalar(k.ident[:, :], k.iota_row[:, :], k.iota_part[:, 0:1], None,
                                        ALU.is_equal).then_inc(step, 1)
                nc.vector.tensor_scalar(k.before[:, :], k.iota_row[:, :], k.iota_part[:, 0:1], None,
                                        ALU.is_gt).then_inc(step, 1)
                nc.vector.tensor_scalar(k.earlier[:, :], k.iota_row[:, :], k.iota_part[:, 0:1], None,
                                        ALU.is_lt).then_inc(step, 1)
                nc.vector.tensor_scalar(k.last_part[:, :], k.iota_part[:, :], float(P - 1), None,
                                        ALU.is_equal).then_inc(step, 1)
                dve.wait_ge(step, 10)
        clear_semaphores(nc, [made, step])


def count_phase(k, fills):
    nc = k.nc
    with ExitStack() as st:
        hot_low = k.sb(st, "cnt_hot_low", [P, 2, 2, P], FP16)
        hot_high = k.sb(st, "cnt_hot_high", [P, 2, 2, NCOL], FP16)
        scan = k.sb(st, "cnt_scan", [P, NCOL])
        count = k.sb(st, "cnt_count", [P, NCOL])
        root = k.sb(st, "cnt_root", [P, NCOL])
        one_col = k.sb(st, "cnt_one", [P, NCOL])
        table = [k.ps(st, f"cnt_table{a}", [P, 512]) for a in range(2)]
        base = k.ps(st, "cnt_base", [P, 512])
        hot = k.sem(st, "cnt_hot")
        used = k.sem(st, "cnt_used")
        step = k.sem(st, "cnt_step")
        based = k.sem(st, "cnt_based")
        filled = k.sem(st, "cnt_filled")
        rooted = k.sem(st, "cnt_rooted")
        with nc.Block() as block:
            @block.sync
            def _(sp):
                for table, rows in fills:
                    with sp.Fori(0, NG) as n:
                        sp.dma_start(node_rows(table, n, P), rows[:, :, :]).then_inc(filled, 16)
                    sp.dma_start(node_rows(table, NG, TAILP), rows[0:TAILP, :, :]).then_inc(filled, 16)
                sp.wait_ge(filled, 16 * (NG + 1) * len(fills))

            @block.vector
            def _(dve):
                with dve.Fori(0, T // 2) as i:
                    for u in range(2):
                        n = i * 2 + u
                        dve.wait_ge(used, after(n))
                        for a in range(2):
                            nc.vector.tensor_scalar(hot_low[:, u, a, :], k.iota_row16[:, :],
                                                    k.low_col[:, a, bass.ds(n, 1)], None, ALU.is_equal)
                            nc.vector.tensor_scalar(hot_high[:, u, a, :], k.iota_high16[:, :],
                                                    k.high_col[:, a, bass.ds(n, 1)], None,
                                                    ALU.is_equal).then_inc(hot, 1)
                nc.vector.memset(one_col[:, :], 1.0).then_inc(step, 1)
                dve.wait_ge(used, T + 2)
                nc.vector.tensor_copy(count[:, :], table[0][:, 0:NCOL]).then_inc(step, 1)
                nc.vector.tensor_scalar(k.degree[:, :], table[1][:, 0:NCOL], 1.0, None, ALU.add).then_inc(step, 1)
                dve.wait_ge(step, 3)
                nc.vector.tensor_tensor_scan(scan[:, :], one_col[:, :], count[:, :], 0.0, ALU.mult,
                                             ALU.add).then_inc(step, 1)
                dve.wait_ge(rooted, 1)
                nc.vector.reciprocal(k.dinv[:, :], root[:, :]).then_inc(step, 1)
                nc.vector.reciprocal(k.dinv2[:, :], k.degree[:, :]).then_inc(step, 1)
                dve.wait_ge(step, 6)
                dve.wait_ge(based, 1)
                nc.vector.tensor_tensor(scan[:, :], scan[:, :], count[:, :], ALU.subtract).then_inc(step, 1)
                dve.wait_ge(step, 7)
                nc.vector.tensor_scalar(k.start[:, :], scan[:, :], base[:, 0:1], None, ALU.add).then_inc(step, 1)
                dve.wait_ge(step, 8)

            @block.scalar
            def _(act):
                act.wait_ge(step, 3)
                nc.scalar.activation(root[:, :], k.degree[:, :], ACT.Sqrt).then_inc(rooted, 1)

            @block.tensor
            def _(pe):
                for a in range(2):
                    nc.tensor.matmul(table[a][:, 0:NCOL], k.zeros[:, 0:P], k.zeros[:, 0:NCOL], start=True, stop=False,
                                     skip_group_check=True)
                pe.sem_inc(used, 2)
                with pe.Fori(0, T // 2) as i:
                    for u in range(2):
                        n = i * 2 + u
                        pe.wait_ge(hot, after(n, 2))
                        for a in range(2):
                            mm = nc.tensor.matmul(table[a][:, 0:NCOL], hot_low[:, u, a, :], hot_high[:, u, a, :],
                                                  start=False, stop=False, skip_group_check=True)
                        mm.then_inc(used, 1)
                pe.wait_ge(step, 4)
                nc.tensor.matmul(base[:, 0:1], k.before[:, :], scan[:, NCOL - 1:NCOL], start=True,
                                 stop=True).then_inc(based, 1)
        clear_semaphores(nc, [hot, used, step, based, rooted, filled])


def paced(eng, k, sem, value):
    eng.wait_ge(sem, value)
    eng.sem_inc(k.paces, 1)


def rank_phase(k):
    nc = k.nc
    with ExitStack() as st:
        row_b = k.sb(st, "rank_row_b", [P, 2, 2, GT * P])
        hot_low = k.sb(st, "rank_hot_low", [P, 2, P], FP16)
        hot_high = k.sb(st, "rank_hot_high", [P, 2, NCOL], FP16)
        low_hot = k.sb(st, "rank_low_hot", [P, 2, P])
        twin = k.sb(st, "rank_twin", [P, 2, P])
        table_sb = k.sb(st, "rank_table_sb", [P, 2, NCOL])
        picked = k.sb(st, "rank_picked", [P, 2, 2, NCOL])
        parts = k.sb(st, "rank_parts", [P, 2, 2])
        ids_s = k.sb(st, "rank_ids_s", [P, 2 * GT])
        dinv_s = k.sb(st, "rank_dinv_s", [P, 2 * GT])
        eid = k.sb(st, "rank_eid", [P, T], I32)
        load4 = k.sb(st, "rank_payload", [P, T, 4], I32)
        rank = k.sb(st, "rank_rank", [P, 2 * GT], I32)
        load_s = k.sb(st, "rank_payload_slot", [P, 2 * GT, 4], I32)
        table = k.ps(st, "rank_table", [P, 512])
        look = [k.ps(st, f"rank_look{b}", [P, 2, 512]) for b in range(2)]
        names = ["numbered", "filled", "row_ready0", "row_ready1", "row_free", "hot", "marked", "copied", "added",
                 "looked", "look_free", "ids", "twins", "picks", "ranked", "slot_free0", "slot_free1"]
        s = {x: k.sem(st, "rank_" + x) for x in names}
        out0 = list(k.scatter_base)
        k.scatter_base = [x + (EG // 2) * 16 * GT for x in k.scatter_base]
        sems = list(s.values())
        s.update(sent0=k.scattered[0], sent1=k.scattered[1])
        with nc.Block() as block:
            @block.sync
            def _(sp):
                with sp.Fori(0, EG // 2) as i:
                    for u in range(2):
                        g = i * 2 + u
                        sp.wait_ge(s["row_free"], after(g))
                        for a, row in enumerate((k.low_row, k.src_row)):
                            sp.dma_start(row_b[:, u, a, :],
                                         row[bass.ds(g * (GT * P), GT * P)].partition_broadcast(P))\
                              .then_inc(s[f"row_ready{u}"], 16)

            @block.gpsimd
            def _(pool):
                nc.gpsimd.iota(eid[:, :], pattern=[[P, T]], base=0, channel_multiplier=1).then_inc(s["numbered"], 1)
                with pool.Fori(0, EG // 2) as i:
                    for u in range(2):
                        paced(pool, k, s["ranked"], after(i * 2 + u, GT) + 2)
                        for j in range(GT):
                            q = u * GT + j
                            nc.gpsimd.indirect_dma_start(
                                out=k.sorted4[:, :], out_offset=bass.IndirectOffsetOnAxis(ap=rank[:, q:q + 1], axis=0),
                                in_=load_s[:, q, :], in_offset=None).then_inc(s[f"sent{u}"], 16)
                        pool.wait_ge(s[f"sent{u}"], i * (16 * GT) + (out0[u] + 16 * GT))
                        pool.sem_inc(s[f"slot_free{u}"], 1)

            @block.vector
            def _(dve):
                dve.wait_ge(s["numbered"], 1)
                nc.vector.memset(load4[:, :, 3], 0)
                nc.vector.tensor_copy(load4[:, :, 2], eid[:, :])
                for a in range(2):
                    nc.vector.tensor_copy(load4[:, :, a], k.id_col[:, 0, a, :]).then_inc(s["filled"], 1)
                dve.wait_ge(s["filled"], 2)
                dve.sem_inc(s["row_free"], 2)
                dve.sem_inc(s["look_free"], 2)
                dve.sem_inc(s["ranked"], 2)

                def one_hots(i, u, j):
                    n = i * (2 * GT) + u * GT + j
                    b = j % 2
                    dve.wait_ge(s["added"], n + 1)
                    dve.wait_ge(s["look_free"], n + 1)
                    nc.vector.tensor_scalar(hot_low[:, b, :], k.iota_row16[:, :], k.low_col[:, 0, bass.ds(n, 1)],
                                            None, ALU.is_equal)
                    nc.vector.tensor_scalar(hot_high[:, b, :], k.iota_high16[:, :], k.high_col[:, 0, bass.ds(n, 1)],
                                            None, ALU.is_equal).then_inc(s["hot"], 1)
                    if j == 0:
                        dve.wait_ge(s[f"row_ready{u}"], i * 32 + 32)
                        nc.vector.tensor_copy(ids_s[:, u * GT:(u + 1) * GT],
                                              k.id_col[:, 0, 0, bass.ds(n, GT)]).then_inc(s["ids"], 1)
                        dve.wait_ge(s["ids"], i * 2 + u + 1)
                    dve.wait_ge(s["looked"], n + 1)
                    nc.vector.tensor_scalar(low_hot[:, b, :], row_b[:, u, 0, j * P:(j + 1) * P],
                                            k.iota_part[:, 0:1], None, ALU.is_equal).then_inc(s["marked"], 1)
                    dve.wait_ge(s["ranked"], n + 1)
                    nc.vector.scalar_tensor_tensor(
                        twin[:, b, :], row_b[:, u, 1, j * P:(j + 1) * P], ids_s[:, u * GT + j:u * GT + j + 1],
                        k.earlier[:, :], ALU.is_equal, ALU.mult,
                        accum_out=parts[:, b, 0:1]).then_inc(s["twins"], 1)
                    if j == GT - 1:
                        dve.wait_ge(s["twins"], n + 1)
                        dve.sem_inc(s["row_free"], 1)

                def read_back(i, u, j):
                    n = i * (2 * GT) + u * GT + j
                    b = j % 2
                    q = u * GT + j
                    dve.wait_ge(s["looked"], n + 3)
                    nc.vector.tensor_tensor_reduce(picked[:, b, 0, :], look[b][:, 0, 0:NCOL], hot_high[:, b, :], 1.0, 0.0,
                                                   ALU.mult, ALU.add, parts[:, b, 1:2]).then_inc(s["picks"], 1)
                    nc.vector.tensor_tensor_reduce(picked[:, b, 1, :], look[b][:, 1, 0:NCOL], hot_high[:, b, :], 1.0, 0.0,
                                                   ALU.mult, ALU.add, dinv_s[:, q:q + 1])\
                        .then_inc(s["look_free"], 1)
                    if j == 0:
                        dve.wait_ge(s[f"slot_free{u}"], i + 1)
                    dve.wait_ge(s["picks"], n + 1)
                    dve.wait_ge(s["twins"], n + 1)
                    if j == GT - 1:
                        dve.wait_ge(s["look_free"], n + 3)
                        nc.vector.tensor_copy(k.dinv_src[:, bass.ds(n - (GT - 1), GT)],
                                              dinv_s[:, u * GT:(u + 1) * GT])
                    nc.vector.tensor_copy(load_s[:, q, :], load4[:, bass.ds(n, 1), :])
                    nc.vector.tensor_tensor(rank[:, q:q + 1], parts[:, b, 0:1], parts[:, b, 1:2],
                                            ALU.add).then_inc(s["ranked"], 1)

                dve.sem_inc(s["slot_free0"], 1)
                dve.sem_inc(s["slot_free1"], 1)
                def tiles(i, last):
                    for q in range(2 * GT):
                        if q < 2 * GT - 1:
                            one_hots(i, (q + 1) // GT, (q + 1) % GT)
                        elif not last:
                            one_hots(i + 1, 0, 0)
                        read_back(i, q // GT, q % GT)

                one_hots(0, 0, 0)
                with dve.Fori(0, EG // 2 - 1) as i:
                    tiles(i, False)
                tiles(EG // 2 - 1, True)

            @block.scalar
            def _(act):
                with act.Fori(0, T // 2) as i:
                    for b in range(2):
                        n = i * 2 + b
                        act.wait_ge(s["added"], n + 2)
                        nc.scalar.activation(table_sb[:, b, :], table[:, 0:NCOL], ACT.Copy).then_inc(s["copied"], 1)

            @block.tensor
            def _(pe):
                pe.sem_inc(s["looked"], 2)
                pe.sem_inc(s["added"], 1)
                nc.tensor.matmul(table[:, 0:NCOL], k.ident[:, :], k.start[:, :], start=True, stop=False,
                                 skip_group_check=True).then_inc(s["added"], 1)
                with pe.Fori(0, T // 2) as i:
                    for b in range(2):
                        n = i * 2 + b
                        pe.wait_ge(s["hot"], n + 1)
                        pe.wait_ge(s["copied"], n + 1)
                        pe.wait_ge(s["look_free"], n + 1)
                        pe.wait_ge(s["marked"], n + 1)
                        nc.tensor.matmul(table[:, 0:NCOL], hot_low[:, b, :], hot_high[:, b, :], start=False,
                                         stop=False, skip_group_check=True).then_inc(s["added"], 1)
                        nc.tensor.matmul(look[b][:, 0, 0:NCOL], low_hot[:, b, :], table_sb[:, b, :], start=True,
                                         stop=True)
                        nc.tensor.matmul(look[b][:, 1, 0:NCOL], low_hot[:, b, :], k.dinv[:, :], start=True,
                                         stop=True).then_inc(s["looked"], 1)
        clear_semaphores(nc, sems)


def order_phase(k, order, tag):
    nc = k.nc
    sorted_ = order.payload is not None
    with ExitStack() as st:
        row4 = k.sb(st, tag + "_row4", [TB, 2, P, 4], I32)
        row3 = k.sb(st, tag + "_row3", [TB, 2, 3, P])
        nxt = k.sb(st, tag + "_next", [TB, 2, P])
        minus = k.sb(st, tag + "_minus", [1, 1])
        cols = k.sb(st, tag + "_cols", [P, 4, T])
        same = k.sb(st, tag + "_same", [P, T])
        pt = k.ps(st, tag + "_pt", [P, 4, 512])
        s = {x: k.sem(st, f"{tag}_{x}") for x in ("loaded", "stored", "step", "turned", "shifted")}
        with nc.Block() as block:
            @block.sync
            def _(sp):
                if sorted_:
                    sp.dma_start(row4[:, :, :, :], order.payload.rearrange("(b r e) c -> r b e c", b=2, e=P))\
                      .then_inc(s["loaded"], 16)
                    sp.wait_ge(s["step"], 4)
                    sp.dma_start(order.id_row[0:EP].rearrange("(b r e) -> r b e", b=2, e=P), row3[:, :, 0, :])\
                      .then_inc(s["stored"], 16)
                    sp.dma_start(order.id_row[EP:EP + 1].rearrange("(r e) -> r e", r=1), minus[:, :])\
                      .then_inc(s["stored"], 16)
                    sp.wait_ge(s["stored"], 32)
                sp.dma_start(nxt[:, :, :], order.id_row[1:EP + 1].rearrange("(b r e) -> r b e", b=2, e=P))\
                  .then_inc(s["shifted"], 16)
                sp.wait_ge(s["shifted"], 16)

            @block.vector
            def _(dve):
                at = 0
                if sorted_:
                    nc.vector.memset(minus[:, :], -1.0).then_inc(s["step"], 1)
                    dve.wait_ge(s["loaded"], 16)
                    for c in range(3):
                        nc.vector.tensor_copy(row3[:, :, c, :], row4[:, :, :, c]).then_inc(s["step"], 1)
                    dve.wait_ge(s["turned"], 1)
                    for c in range(3):
                        nc.vector.tensor_copy(cols[:, c, :], pt[:, c, 0:T]).then_inc(s["step"], 1)
                    dve.wait_ge(s["step"], 7)
                    nc.vector.tensor_copy(order.id_col[:, :], cols[:, 0, :]).then_inc(s["step"], 1)
                    nc.vector.tensor_copy(order.eid[:, :], cols[:, 2, :]).then_inc(s["step"], 1)
                    for c, out in ((0, order.cap_own), (1, order.cap_far)):
                        nc.vector.tensor_scalar(same[:, :], cols[:, c, :], float(N - 1), None,
                                                ALU.min).then_inc(s["step"], 1)
                        at = 10 + 2 * c
                        dve.wait_ge(s["step"], at)
                        nc.vector.tensor_scalar(out[:, :], same[:, :], 2.0, 1.0, ALU.mult,
                                                ALU.add).then_inc(s["step"], 1)
                        dve.wait_ge(s["step"], at + 1)
                    at = 13
                dve.wait_ge(s["turned"], 2)
                nc.vector.tensor_copy(cols[:, 3, :], pt[:, 3, 0:T]).then_inc(s["step"], 1)
                nc.vector.memset(order.prev_col[:, 0:1], -5.0).then_inc(s["step"], 1)
                nc.vector.tensor_scalar(order.prev_col[:, 1:T], order.id_col[:, 0:T - 1], 5.0, k.last_part[:, 0:1],
                                        ALU.add, ALU.mult).then_inc(s["step"], 1)
                dve.wait_ge(s["step"], at + 3)
                nc.vector.tensor_scalar(order.prev_col[:, 1:T], order.prev_col[:, 1:T], -5.0, None,
                                        ALU.add).then_inc(s["step"], 1)
                nc.vector.tensor_tensor(same[:, :], order.id_col[:, :], cols[:, 3, :],
                                        ALU.is_equal).then_inc(s["step"], 1)
                dve.wait_ge(s["step"], at + 5)
                nc.vector.scalar_tensor_tensor(cols[:, 3, :], same[:, :], float(FAR), order.id_col[:, :], ALU.mult,
                                               ALU.add).then_inc(s["step"], 1)
                dve.wait_ge(s["step"], at + 6)
                nc.vector.tensor_copy(order.last_idx[:, :], cols[:, 3, :]).then_inc(s["step"], 1)
                if sorted_:
                    nc.vector.tensor_scalar(order.last_cap[:, :], cols[:, 3, :], 2.0, 1.0, ALU.mult,
                                            ALU.add).then_inc(s["step"], 1)

            @block.tensor
            def _(pe):
                if sorted_:
                    pe.wait_ge(s["step"], 4)
                    for c in range(3):
                        for b in range(2):
                            last = nc.tensor.transpose(pt[:, c, b * TB:(b + 1) * TB], row3[:, b, c, :],
                                                       k.ident[0:TB, 0:TB])
                    last.then_inc(s["turned"], 1)
                else:
                    pe.sem_inc(s["turned"], 1)
                pe.wait_ge(s["shifted"], 16)
                for b in range(2):
                    last = nc.tensor.transpose(pt[:, 3, b * TB:(b + 1) * TB], nxt[:, b, :], k.ident[0:TB, 0:TB])
                last.then_inc(s["turned"], 1)
        clear_semaphores(nc, list(s.values()))


def segment_sum_phase(k, order, table, width, index, dest, tag, weigh, project=None, bias=None):
    nc = k.nc
    with ExitStack() as st:
        rows = k.sb(st, tag + "_rows", [P, 2, GT, width])
        index_s = k.sb(st, tag + "_index", [P, 2, GT], I32)
        last_s = k.sb(st, tag + "_last", [P, 2, GT], I32)
        row_b = k.sb(st, tag + "_row_b", [P, 2, GT, P])
        same = k.sb(st, tag + "_same", [P, 2, GT, P])
        cross = k.sb(st, tag + "_cross", [P, 2, GT, P])
        vals = k.sb(st, tag + "_vals", [P, 2, GT, D]) if weigh else rows
        sums = k.sb(st, tag + "_sums", [P, 2, GT, D])
        acc = [k.ps(st, f"{tag}_acc{j}", [P, 512]) for j in range(GT)]
        if project is not None:
            turned_sb = k.sb(st, tag + "_turned_sb", [P, 2, GT, P])
            sent = k.sb(st, tag + "_sent", [P, 2, GT, D])
            pt = [k.ps(st, f"{tag}_pt{u}", [P, GT, P]) for u in range(2)]
            pp = [k.ps(st, f"{tag}_pp{u}", [P, GT, D]) for u in range(2)]
        else:
            sent = sums
        names = ["index", "last", "rows_free", "row_ready0", "row_ready1", "row_free", "masks", "masks_free",
                 "weighed", "summed", "copied", "sent_free", "start", "turned", "turned_copied",
                 "projected", "project_copied"]
        s = {x: k.sem(st, f"{tag}_{x}") for x in names}
        in0, out0 = list(k.gather_base), list(k.scatter_base)
        k.gather_base = [x + (EG // 2) * 16 * GT for x in k.gather_base]
        k.scatter_base = [x + (EG // 2) * 16 * GT for x in k.scatter_base]
        sems = list(s.values())
        s.update(got0=k.gathered[0], got1=k.gathered[1], put0=k.scattered[0], put1=k.scattered[1])
        lag = 1 if project is None else 2

        def tiles(column, g):
            return column[:, g * GT:g * GT + GT] if isinstance(g, int) else column[:, bass.ds(g * GT, GT)]

        def run(eng, *stages):
            staggered(eng, *stages, full=EG, tail=None)

        with nc.Block() as block:
            @block.sync
            def _(sp):
                def load(g, i, u, p):
                    sp.wait_ge(s["row_free"], g + 1)
                    at = span(g, GT * P)
                    sp.dma_start(row_b[:, u, :, :].rearrange("p t e -> p (t e)"),
                                 order.id_row[at].partition_broadcast(P)).then_inc(s[f"row_ready{u}"], 16)

                run(sp, (load, 0))

            @block.gpsimd
            def _(pool):
                def gather(g, i, u, p):
                    paced(pool, k, s["rows_free"], g + 1)
                    nc.gpsimd.tensor_copy(index_s[:, u, :], tiles(index, g)).then_inc(s["index"], 1)
                    paced(pool, k, s["index"], g + 1)
                    for j in range(GT):
                        nc.gpsimd.indirect_dma_start(
                            out=rows[:, u, j, :], out_offset=None, in_=table,
                            in_offset=bass.IndirectOffsetOnAxis(ap=index_s[:, u, j:j + 1], axis=0))\
                            .then_inc(s[f"got{u}"], 16)

                def scatter(g, i, u, p):
                    nc.gpsimd.tensor_copy(last_s[:, u, :], tiles(order.last_idx, g)).then_inc(s["last"], 1)
                    paced(pool, k, s["last"], g + 1)
                    paced(pool, k, s["project_copied" if project is not None else "copied"],
                          g + 3 if project is not None else after(g, GT) + 1)
                    for j in range(GT):
                        nc.gpsimd.indirect_dma_start(
                            out=dest, out_offset=bass.IndirectOffsetOnAxis(ap=last_s[:, u, j:j + 1], axis=0),
                            in_=sent[:, u, j, :], in_offset=None, bounds_check=N - 1, oob_is_err=False)\
                            .then_inc(s[f"put{u}"], 16)

                def scattered(g, i, u, p):
                    pool.wait_ge(s[f"put{u}"], i * (16 * GT) + (out0[u] + 16 * GT))
                    pool.sem_inc(s["sent_free"], 1)

                pool.sem_inc(s["sent_free"], 2)
                run(pool, (gather, 0), (scattered, lag + 2), (scatter, lag + 1))

            @block.vector
            def _(dve):
                def masks(g, i, u, p):
                    dve.wait_ge(s["masks_free"], g + 1)
                    dve.wait_ge(s[f"row_ready{u}"], i * 16 + 16)
                    own, prev = (tiles(c, g).unsqueeze(2).broadcast_to([P, GT, P])
                                 for c in (order.id_col, order.prev_col))
                    nc.vector.tensor_tensor(same[:, u, :, :], row_b[:, u, :, :], own, ALU.is_equal)
                    nc.vector.tensor_tensor(cross[:, u, :, :], row_b[:, u, :, :], prev,
                                            ALU.is_equal).then_inc(s["masks"], 1)
                    dve.wait_ge(s["masks"], g + 1)
                    dve.sem_inc(s["row_free"], 1)

                def weighed(g, i, u, p):
                    dve.wait_ge(s[f"got{u}"], i * (16 * GT) + (in0[u] + 16 * GT))
                    weigh(dve, vals[:, u, :, :], rows[:, u, :, :], g).then_inc(s["weighed"], 1)
                    dve.wait_ge(s["weighed"], g + 1)
                    dve.sem_inc(s["rows_free"], 1)

                nc.vector.memset(sums[:, 1, GT - 1, :], 0.0).then_inc(s["start"], 1)
                dve.wait_ge(s["start"], 1)
                dve.sem_inc(s["row_free"], 2)
                if weigh:
                    dve.sem_inc(s["rows_free"], 2)
                    run(dve, (masks, 0), (weighed, 0))
                else:
                    run(dve, (masks, 0))

            @block.scalar
            def _(act):
                def copy(g, i, u, p):
                    if project is None:
                        act.wait_ge(s["sent_free"], g + 1)
                    else:
                        act.wait_ge(s["turned"], g + 1)
                    for j in range(GT):
                        act.wait_ge(s["summed"], g * GT + j + 1)
                        nc.scalar.activation(sums[:, u, j, :], acc[j][:, 0:D], ACT.Copy).then_inc(s["copied"], 1)

                def copy_turned(g, i, u, p):
                    act.wait_ge(s["turned"], g + 3)
                    act.wait_ge(s["projected"], g + 1)
                    nc.scalar.activation(turned_sb[:, u, :, :], pt[u][:, :, :], ACT.Copy)\
                        .then_inc(s["turned_copied"], 1)

                def copy_projected(g, i, u, p):
                    act.wait_ge(s["projected"], g + 3)
                    act.wait_ge(s["sent_free"], g + 1)
                    nc.scalar.activation(sent[:, u, :, :], pp[u][:, :, :], ACT.Copy).then_inc(s["project_copied"], 1)

                act.sem_inc(s["copied"], 1)
                act.sem_inc(s["project_copied"], 2)
                if project is None:
                    run(act, (copy, 0))
                else:
                    run(act, (copy_turned, 1), (copy_projected, 1), (copy, 0))

            @block.tensor
            def _(pe):
                def sum_up(g, i, u, p):
                    pe.wait_ge(s["masks"], g + 1)
                    if weigh:
                        pe.wait_ge(s["weighed"], g + 1)
                    else:
                        pe.wait_ge(s[f"got{u}"], i * (16 * GT) + (in0[u] + 16 * GT))
                    for j in range(GT):
                        if j == 0:
                            pe.wait_ge(s["copied"], g * GT + 1)
                        nc.tensor.matmul(acc[j][:, 0:D], same[:, u, j, :], vals[:, u, j, :], start=True, stop=False)
                        before = sums[:, u, j - 1, :] if j else sums[:, 1 - u, GT - 1, :]
                        pe.wait_ge(s["copied"], g * GT + j + 1)
                        nc.tensor.matmul(acc[j][:, 0:D], cross[:, u, j, :], before, start=False, stop=True)\
                            .then_inc(s["summed"], 1)
                    pe.wait_ge(s["summed"], after(g, GT))
                    pe.sem_inc(s["masks_free"], 1)
                    if not weigh:
                        pe.sem_inc(s["rows_free"], 1)

                def turn(g, i, u, p):
                    pe.wait_ge(s["copied"], after(g, GT) + 1)
                    for j in range(GT):
                        mm = nc.tensor.transpose(pt[u][:, j, :], sums[:, u, j, :], k.ident[:, :])
                    mm.then_inc(s["turned"], 1)

                def product(g, i, u, p):
                    pe.wait_ge(s["turned_copied"], g + 1)
                    pe.wait_ge(s["project_copied"], g + 1)
                    nc.tensor.matmul(pp[u][:, :, :].rearrange("p t d -> p (t d)"), k.ones3[:, :],
                                     bias[:, :, :].rearrange("r t d -> r (t d)"), start=True, stop=False,
                                     skip_group_check=True)
                    for j in range(GT):
                        mm = nc.tensor.matmul(pp[u][:, j, :], turned_sb[:, u, j, :], project, start=False,
                                              stop=j == GT - 1, skip_group_check=True)
                    mm.then_inc(s["projected"], 1)

                pe.wait_ge(s["start"], 1)
                pe.sem_inc(s["masks_free"], 2)
                if not weigh:
                    pe.sem_inc(s["rows_free"], 2)
                if project is None:
                    run(pe, (sum_up, 0))
                else:
                    pe.sem_inc(s["turned"], 2)
                    pe.sem_inc(s["projected"], 2)
                    run(pe, (turn, 1), (product, 1), (sum_up, 0))
        clear_semaphores(nc, sems)


class Order:

    def __init__(self, id_row, id_col, prev_col, last_idx, payload=None, eid=None, cap_own=None, cap_far=None,
                 last_cap=None):
        self.id_row, self.id_col, self.prev_col, self.last_idx = id_row, id_col, prev_col, last_idx
        self.payload, self.eid, self.cap_own, self.cap_far, self.last_cap = payload, eid, cap_own, cap_far, last_cap


class Chain:

    def __init__(self, eng, sem, steps):
        self.eng, self.sem, self.steps = eng, sem, steps

    def begin(self, n):
        self.n, self.count = n, 0

    def link(self, ins):
        self.count += 1
        ins.then_inc(self.sem, 1)
        self.eng.wait_ge(self.sem, self.n * self.steps + self.count)

    def end(self):
        assert self.count == self.steps


def staggered(eng, *stages, full=NG, tail=TAILP, looped=None):
    most = max(lag for _, lag in stages)
    looped = looped or full

    def static(m):
        for stage, lag in stages:
            n = m - lag
            if 0 <= n < full or (n == full and tail):
                stage(n, n // 2, n % 2, tail if n == full else P)

    pairs = (looped - most) // 2
    for m in range(most):
        static(m)
    with eng.Fori(0, pairs) as i:
        for m in (most, most + 1):
            for stage, lag in stages:
                n = m - lag
                stage(i * 2 + n, i + n // 2, n % 2, P)
    for m in range(most + 2 * pairs, full + 1 + most):
        static(m)


def node_rows(table, n, p, width=D):
    at = slice(n * P * NJ, n * P * NJ + p * NJ) if isinstance(n, int) else bass.ds(n * (P * NJ), P * NJ)
    return table[at, :].rearrange("(p j) d -> p j d", p=p)


class Linear:

    def __init__(self, k, st, tag, weight, bias, cols=NJ):
        self.k, self.weight, self.bias, self.cols = k, weight, bias, cols
        banks = cols // 4
        self.turned_ps = [k.ps(st, f"{tag}_tps{b}", [P, 4, P]) for b in range(banks)]
        self.out = [k.ps(st, f"{tag}_out{b}", [P, 4, D]) for b in range(banks)]
        self.turned_sb = k.sb(st, f"{tag}_tsb", [P, cols, P])
        self.turned = k.sem(st, tag + "_turned")
        self.copied = k.sem(st, tag + "_copied")
        self.made = k.sem(st, tag + "_made")
        self.free = k.sem(st, tag + "_free")
        self.sems = [self.turned, self.copied, self.made, self.free]

    def turn(self, pe, n, p, rows):
        pe.wait_ge(self.copied, n + 1)
        for j in range(self.cols):
            mm = self.k.nc.tensor.transpose(self.turned_ps[j // 4][:, j % 4, 0:p], rows[0:p, j, :],
                                            self.k.ident[0:p, 0:p])
        mm.then_inc(self.turned, 1)

    def copy(self, act, n, p):
        act.wait_ge(self.turned, n + 1)
        act.wait_ge(self.made, n + 1)
        for b in range(self.cols // 4):
            ins = self.k.nc.scalar.activation(self.turned_sb[:, 4 * b:4 * b + 4, 0:p],
                                              self.turned_ps[b][:, :, 0:p], ACT.Copy)
        ins.then_inc(self.copied, 1)

    def product(self, pe, n, p):
        pe.wait_ge(self.copied, n + 2)
        pe.wait_ge(self.free, n + 1)
        for b in range(self.cols // 4):
            self.k.nc.tensor.matmul(self.out[b][0:p, :, :].rearrange("p j d -> p (j d)"), self.k.ones3[:, 0:p],
                                    self.bias[:, :, :].rearrange("p j d -> p (j d)"), start=True, stop=False,
                                    skip_group_check=True)
            for j in range(4):
                mm = self.k.nc.tensor.matmul(self.out[b][0:p, j, :], self.turned_sb[:, 4 * b + j, 0:p], self.weight,
                                             start=False, stop=j == 3, skip_group_check=True)
        mm.then_inc(self.made, 1)


class Norm:

    STEPS = 4

    def __init__(self, k, st, tag, cols=NJ, eps=EPS, factor=1.0, slots=2):
        self.k, self.cols, self.eps, self.factor = k, cols, eps, factor
        self.stats = k.sb(st, tag + "_stats", [P, slots, cols, 6])
        self.mean, self.gap, self.var, self.root, self.scale, self.shift = (
            k.sb(st, f"{tag}_{x}", [P, slots, cols]) for x in ("mean", "gap", "var", "root", "scale", "shift"))
        self.bias = k.sb(st, tag + "_bias", [P, 1])
        self.seen = k.sem(st, tag + "_seen")
        self.rooted = k.sem(st, tag + "_rooted")
        self.scaled = k.sem(st, tag + "_scaled")
        self.shifted = k.sem(st, tag + "_shifted")
        self.steps = k.sem(st, tag + "_steps")
        self.set = k.sem(st, tag + "_set")
        self.sems = [self.seen, self.rooted, self.scaled, self.shifted, self.steps, self.set]

    def prepare(self, dve):
        self.chain = Chain(dve, self.steps, self.STEPS)
        self.k.nc.vector.memset(self.bias[:, :], self.eps).then_inc(self.set, 1)

    def statistics(self, dve, n, u, p, rows):
        v, c, s = self.k.nc.vector, self.chain, self.stats
        mean, gap, var = self.mean[0:p, u, :], self.gap[0:p, u, :], self.var[0:p, u, :]
        c.begin(n)
        for j in range(self.cols):
            ins = v.bn_stats(s[0:p, u, j, :], rows[0:p, j, :])
        c.link(ins)
        v.tensor_tensor(gap, s[0:p, u, :, 1], s[0:p, u, :, 4], ALU.subtract)
        v.tensor_tensor(var, s[0:p, u, :, 2], s[0:p, u, :, 5], ALU.add)
        c.link(v.tensor_tensor(mean, s[0:p, u, :, 1], s[0:p, u, :, 4], ALU.add))
        c.link(v.tensor_tensor(gap, gap, gap, ALU.mult))
        v.tensor_scalar(mean, mean, 0.5, None, ALU.mult)
        c.link(v.scalar_tensor_tensor(var, gap, D / 4.0, var, ALU.mult, ALU.add))
        c.end()
        dve.sem_inc(self.seen, 1)

    def square_root(self, act, n, u, p):
        act.wait_ge(self.seen, n + 1)
        act.wait_ge(self.set, 1)
        self.k.nc.scalar.activation(self.root[0:p, u, :], self.var[0:p, u, :], ACT.Sqrt, bias=self.bias[0:p, 0:1],
                                    scale=self.factor / D).then_inc(self.rooted, 1)

    def invert(self, dve, n, u, p):
        dve.wait_ge(self.rooted, n + 1)
        self.k.nc.vector.reciprocal(self.scale[0:p, u, :], self.root[0:p, u, :]).then_inc(self.scaled, 1)
        dve.wait_ge(self.scaled, n + 1)

    def normalise(self, dve, n, u, p, out, rows):
        self.invert(dve, n, u, p)
        for j in range(self.cols):
            ins = self.k.nc.vector.tensor_scalar(out[0:p, j, :], rows[0:p, j, :], self.mean[0:p, u, j:j + 1],
                                                 self.scale[0:p, u, j:j + 1], ALU.subtract, ALU.mult)
        return ins

    def negate(self, dve, n, u, p):
        self.invert(dve, n, u, p)
        self.k.nc.vector.scalar_tensor_tensor(self.shift[0:p, u, :], self.mean[0:p, u, :], -1.0,
                                              self.scale[0:p, u, :], ALU.mult, ALU.mult).then_inc(self.shifted, 1)

    def normalise_on_act(self, act, n, u, p, out, rows):
        act.wait_ge(self.shifted, n + 1)
        for j in range(self.cols):
            ins = self.k.nc.scalar.activation(out[0:p, j, :], rows[0:p, j, :], ACT.Identity,
                                              bias=self.shift[0:p, u, j:j + 1], scale=self.scale[0:p, u, j:j + 1])
        return ins


class Propagated:

    def __init__(self, k, st, tag):
        self.k = k
        self.x = k.sb(st, tag + "_x", [P, 2, NJ, D])
        self.agg = k.sb(st, tag + "_agg", [P, 2, NJ, D])
        self.y = k.sb(st, tag + "_y", [P, 2, NJ, D + 1])
        self.ready = [k.sem(st, f"{tag}_ready{u}") for u in range(2)]
        self.free = k.sem(st, tag + "_free")
        self.scaled = k.sem(st, tag + "_scaled")
        self.owned = k.sem(st, tag + "_owned")
        self.made = k.sem(st, tag + "_made")
        self.used = k.sem(st, tag + "_used")
        self.sems = self.ready + [self.free, self.scaled, self.owned, self.made, self.used]

    def load(self, sp, n, i, u, p):
        sp.wait_ge(self.free, n + 1)
        sp.dma_start(self.x[0:p, u, :, :], node_rows(self.k.x, n, p)).then_inc(self.ready[u], 16)
        sp.dma_start(self.agg[0:p, u, :, :], node_rows(self.k.agg, n, p)).then_inc(self.ready[u], 16)

    def per_node(self, column, n, p):
        c = column[0:p, n * NJ:n * NJ + NJ] if isinstance(n, int) else column[0:p, bass.ds(n * NJ, NJ)]
        return c.unsqueeze(2).broadcast_to([p, NJ, D])

    def scale(self, pool, n, i, u, p):
        paced(pool, self.k, self.ready[u], i * 32 + 32)
        self.k.nc.gpsimd.tensor_tensor(self.agg[0:p, u, :, :], self.agg[0:p, u, :, :],
                                       self.per_node(self.k.dinv, n, p), ALU.mult).then_inc(self.scaled, 1)

    def make(self, dve, n, i, u, p):
        dve.wait_ge(self.ready[u], i * 32 + 32)
        dve.wait_ge(self.used, n + 1)
        y = self.y[0:p, u, :, 0:D]
        self.k.nc.vector.tensor_tensor(y, self.x[0:p, u, :, :], self.per_node(self.k.dinv2, n, p),
                                       ALU.mult).then_inc(self.owned, 1)
        dve.wait_ge(self.scaled, n + 1)
        dve.wait_ge(self.owned, n + 1)
        self.k.nc.vector.tensor_tensor(y, y, self.agg[0:p, u, :, :], ALU.add).then_inc(self.made, 1)


def moments_phase(k):
    nc = k.nc
    with ExitStack() as st:
        prop = Propagated(k, st, "mom_y")
        w = k.sb(st, "mom_w", [P, D])
        gb = k.sb(st, "mom_gb", [P, 2, D])
        cov = k.sb(st, "mom_cov", [P, D + 1])
        mean = k.sb(st, "mom_mean", [P, 1])
        mean_b = k.sb(st, "mom_mean_b", [P, P])
        mean_r = k.sb(st, "mom_mean_r", [1, P])
        wz = k.sb(st, "mom_wz", [P, D])
        work = k.sb(st, "mom_work", [P, 4, D])
        acc = k.ps(st, "mom_acc", [P, 512])
        tps = k.ps(st, "mom_tps", [P, 512])
        outer = k.ps(st, "mom_outer", [P, 512])
        zp = k.ps(st, "mom_z", [P, 512])
        vb = k.ps(st, "mom_var", [P, 512])
        mb = k.ps(st, "mom_mean_h", [P, 512])
        s = {x: k.sem(st, "mom_" + x) for x in ("wloaded", "summed", "step", "pstep", "astep", "begun")}
        with nc.Block() as block:
            @block.sync
            def _(sp):
                sp.dma_start(w[:, :], k.a["L0_gnn_W"]).then_inc(s["wloaded"], 16)
                sp.dma_start(gb[:, 0, :], k.a["L0_gnn_gamma"].partition_broadcast(P)).then_inc(s["wloaded"], 16)
                sp.dma_start(gb[:, 1, :], k.a["L0_gnn_beta"].partition_broadcast(P)).then_inc(s["wloaded"], 16)
                staggered(sp, (lambda *g: prop.load(sp, *g), 0))

            @block.gpsimd
            def _(pool):
                staggered(pool, (lambda *g: prop.scale(pool, *g), 0))

            @block.vector
            def _(dve):
                dve.sem_inc(prop.free, 2)
                nc.vector.memset(prop.y[:, :, :, D:D + 1], 1.0).then_inc(s["begun"], 1)

                def make(n, i, u, p):
                    prop.make(dve, n, i, u, p)
                    dve.wait_ge(prop.made, n + 1)
                    dve.sem_inc(prop.free, 1)

                staggered(dve, (make, 0))
                dve.wait_ge(s["summed"], 1)
                dve.wait_ge(s["wloaded"], 48)
                c = Chain(dve, s["step"], 13)
                c.begin(0)
                c.link(nc.vector.tensor_scalar(cov[:, :], acc[:, 0:D + 1], 1.0 / N, None, ALU.mult))
                c.link(nc.vector.tensor_copy(mean[:, :], cov[:, D:D + 1]))
                c.link(nc.vector.tensor_scalar(mean_b[:, :], k.ones[:, :], mean[:, 0:1], None, ALU.mult))
                dve.wait_ge(s["pstep"], 1)
                c.link(nc.vector.tensor_copy(mean_r[:, :], tps[0:1, 0:P]))
                dve.wait_ge(s["pstep"], 2)
                c.link(nc.vector.tensor_tensor(cov[:, 0:D], cov[:, 0:D], outer[:, 0:P], ALU.subtract))
                dve.wait_ge(s["pstep"], 3)
                c.link(nc.vector.tensor_tensor(wz[:, :], w[:, :], zp[:, 0:D], ALU.mult))
                dve.wait_ge(s["astep"], 1)
                c.link(nc.vector.reciprocal(work[:, 1, :], work[:, 0, :]))
                c.link(nc.vector.tensor_tensor(work[:, 2, :], work[:, 1, :], gb[:, 0, :], ALU.mult))
                c.link(nc.vector.tensor_scalar(work[:, 2, :], work[:, 2, :], 0.5, None, ALU.mult))
                c.link(nc.vector.tensor_tensor(k.gcn_w[:, :], w[:, :], work[:, 2, :], ALU.mult))
                dve.wait_ge(s["pstep"], 5)
                c.link(nc.vector.tensor_tensor(work[:, 3, :], mb[:, 0:D], work[:, 2, :], ALU.mult))
                c.link(nc.vector.tensor_scalar(gb[:, 1, :], gb[:, 1, :], 0.5, None, ALU.mult))
                c.link(nc.vector.tensor_tensor(k.gcn_c[:, :], gb[:, 1, :], work[:, 3, :], ALU.subtract))
                c.end()

            @block.scalar
            def _(act):
                act.wait_ge(s["pstep"], 4)
                nc.scalar.activation(work[:, 0, :], vb[:, 0:D], ACT.Sqrt, bias=k.eps[:, 0:1]).then_inc(s["astep"], 1)

            @block.tensor
            def _(pe):
                nc.tensor.matmul(acc[:, 0:D + 1], k.zeros[:, 0:P], k.zeros[:, 0:D + 1], start=True, stop=False,
                                 skip_group_check=True)
                pe.sem_inc(prop.used, 2)
                pe.wait_ge(s["begun"], 1)

                def add(n, i, u, p):
                    pe.wait_ge(prop.made, n + 1)
                    for j in range(NJ):
                        mm = nc.tensor.matmul(acc[:, 0:D + 1], prop.y[0:p, u, j, 0:D], prop.y[0:p, u, j, :],
                                              start=False, stop=False, skip_group_check=True)
                    mm.then_inc(prop.used, 1)

                staggered(pe, (add, 0))
                pe.wait_ge(prop.used, NG + 3)
                pe.sem_inc(s["summed"], 1)
                pe.wait_ge(s["step"], 3)
                nc.tensor.transpose(tps[0:1, 0:P], mean[:, 0:1], k.ident[:, :]).then_inc(s["pstep"], 1)
                pe.wait_ge(s["step"], 4)
                nc.tensor.matmul(outer[:, 0:P], mean_r[:, :], mean_r[:, :], start=True, stop=True)\
                    .then_inc(s["pstep"], 1)
                pe.wait_ge(s["step"], 5)
                nc.tensor.matmul(zp[:, 0:D], cov[:, 0:D], w[:, :], start=True, stop=True).then_inc(s["pstep"], 1)
                pe.wait_ge(s["step"], 6)
                nc.tensor.matmul(vb[:, 0:D], k.ones[:, :], wz[:, :], start=True, stop=True).then_inc(s["pstep"], 1)
                nc.tensor.matmul(mb[:, 0:D], mean_b[:, :], w[:, :], start=True, stop=True).then_inc(s["pstep"], 1)
        clear_semaphores(nc, prop.sems + list(s.values()))


def load_constants(k, names):
    nc = k.nc
    with ExitStack() as st:
        got = k.sem(st, "const_got")
        with nc.Block() as block:
            @block.sync
            def _(sp):
                for dst, src in names:
                    sp.dma_start(dst, src).then_inc(got, 16)
                sp.wait_ge(got, 16 * len(names))
        clear_semaphores(nc, [got])


def split_biases(k, st, tag, biases, parts=None):
    nc = k.nc
    v = nc.vector
    widths = [rows.shape[-1] for rows in biases]
    parts = parts or [k.sb(st, f"{tag}_parts{m}", [3, 4, w], BF16) for m, w in enumerate(widths)]
    with ExitStack() as inner:
        step = k.sem(inner, tag + "_step")
        work = k.sb(inner, tag + "_work", [3, 5, D])
        half = k.sb(inner, tag + "_half", [3, 3, D], BF16)
        with nc.Block() as block:
            @block.vector
            def _(dve):
                c = Chain(dve, step, 9 * len(biases))
                c.begin(0)
                for rows, w, out in zip(biases, widths, parts):
                    h, r = half[:, :, 0:w], work[:, :, 0:w]
                    c.link(v.tensor_copy(h[:, 0, :], rows))
                    c.link(v.tensor_tensor(r[:, 0, :], rows, h[:, 0, :], ALU.subtract))
                    c.link(v.tensor_copy(h[:, 1, :], r[:, 0, :]))
                    c.link(v.tensor_tensor(r[:, 1, :], r[:, 0, :], h[:, 1, :], ALU.subtract))
                    c.link(v.tensor_copy(h[:, 2, :], r[:, 1, :]))
                    c.link(v.tensor_scalar(r[:, 2, :], h[:, 0, :], k.ident[0:3, 0:1], None, ALU.mult))
                    c.link(v.scalar_tensor_tensor(r[:, 3, :], h[:, 1, :], k.ident[0:3, 1:2], r[:, 2, :], ALU.mult,
                                                  ALU.add))
                    c.link(v.scalar_tensor_tensor(r[:, 4, :], h[:, 2, :], k.ident[0:3, 2:3], r[:, 3, :], ALU.mult,
                                                  ALU.add))
                    c.link(v.tensor_copy(out[:, :, :], r[:, 4, :].unsqueeze(1).broadcast_to([3, 4, w])))
                c.end()
        clear_semaphores(nc, [step])
    return parts


def capsules_phase(k):
    nc = k.nc
    with ExitStack() as st:
        w1 = k.sb(st, "cap_w1", [P, D])
        b1 = k.sb(st, "cap_b1", [3, D])
        load_constants(k, [(w1[:, :], k.a["L1_gnn_weight"]), (b1[:, :], k.a["L1_gnn_bias"].partition_broadcast(3))])
        gcn_b, caps_b = split_biases(k, st, "cap_bias", [k.gcn_c[0:3, :], b1[:, :]])
        prop = Propagated(k, st, "cap_y")
        conv = Linear(k, st, "cap_conv", k.gcn_w[:, :], gcn_b)
        caps = Linear(k, st, "cap_caps", w1[:, :], caps_b)
        norm = Norm(k, st, "cap_norm", eps=EPS / 4)
        u1, x1, cap, plain, leak = (k.sb(st, "cap_" + x, [P, 2, NJ, D]) for x in ("u", "x1", "cap", "plain", "leak"))
        square = k.sb(st, "cap_square", [P, NJ, D])
        length = k.sb(st, "cap_length", [P, 2, 3, NJ * NH])
        names = ["added", "normed", "x1_stored0", "x1_stored1", "cap_stored0", "cap_stored1", "leaked",
                 "bent", "squared", "reduced", "inverted", "scaled", "sized"]
        s = {x: k.sem(st, "cap_" + x) for x in names}
        with nc.Block() as block:
            @block.sync
            def _(sp):
                def store(what, c, rows):
                    def stage(n, i, u, p):
                        sp.wait_ge(s["normed" if c == 0 else "scaled"], n + 1)
                        sp.dma_start(node_rows(k.layer1, n, p, 2 * D)[:, :, c * D:(c + 1) * D], rows[0:p, u, :, :])\
                          .then_inc(s[f"{what}_stored{u}"], 16)
                    return stage

                for what in ("x1", "cap"):
                    for u in range(2):
                        sp.sem_inc(s[f"{what}_stored{u}"], 16)
                staggered(sp, (lambda *g: prop.load(sp, *g), 0), (store("x1", 0, x1), 3), (store("cap", 1, cap), 6))
                for what in ("x1", "cap"):
                    sp.wait_ge(s[f"{what}_stored0"], 16 * (NG // 2 + 2))
                    sp.wait_ge(s[f"{what}_stored1"], 16 * (NG // 2 + 1))

            @block.gpsimd
            def _(pool):
                staggered(pool, (lambda *g: prop.scale(pool, *g), 0))

            @block.vector
            def _(dve):
                dve.sem_inc(prop.free, 2)
                dve.sem_inc(conv.free, 1)
                dve.sem_inc(s["reduced"], 1)
                norm.prepare(dve)

                def add(n, i, u, p):
                    dve.wait_ge(conv.made, n + 2)
                    for b in range(2):
                        ins = nc.vector.scalar_tensor_tensor(
                            u1[0:p, u, 4 * b:4 * b + 4, :], conv.out[b][0:p, :, :], 0.0,
                            prop.x[0:p, u, 4 * b:4 * b + 4, :], ALU.max, ALU.add)
                    ins.then_inc(s["added"], 1)
                    dve.wait_ge(s["added"], n + 1)
                    dve.sem_inc(conv.free, 1)
                    dve.sem_inc(prop.free, 1)
                    norm.statistics(dve, n, u, p, u1[:, u, :, :])

                def normalise(n, i, u, p):
                    dve.wait_ge(s[f"x1_stored{u}"], i * 16 + 16)
                    norm.normalise(dve, n, u, p, x1[:, u, :, :], u1[:, u, :, :]).then_inc(s["normed"], 1)

                def reduce(n, i, u, p):
                    dve.wait_ge(s["squared"], n + 1)
                    nc.vector.tensor_reduce(length[0:p, u, 0, :],
                                            square[0:p, :, :].rearrange("p j (h d) -> p (j h) d", h=NH), AX.X,
                                            ALU.add).then_inc(s["reduced"], 1)

                def scale(n, i, u, p):
                    dve.wait_ge(s["sized"], n + 1)
                    nc.vector.reciprocal(length[0:p, u, 2, :], length[0:p, u, 1, :]).then_inc(s["inverted"], 1)
                    dve.wait_ge(s["inverted"], n + 1)
                    for b in range(2):
                        half = cap[0:p, u, 4 * b:4 * b + 4, :].rearrange("p j (h d) -> p j h d", h=NH)
                        size = length[0:p, u, 2, 4 * b * NH:(4 * b + 4) * NH].rearrange("p (j h) -> p j h", h=NH)\
                            .unsqueeze(3).broadcast_to([p, 4, NH, HD])
                        ins = nc.vector.tensor_tensor(half, half, size, ALU.mult)
                    ins.then_inc(s["scaled"], 1)

                def bend(n, i, u, p):
                    dve.wait_ge(s["leaked"], n + 1)
                    dve.wait_ge(s[f"cap_stored{u}"], i * 16 + 16)
                    nc.vector.tensor_tensor(cap[0:p, u, :, :], plain[0:p, u, :, :], leak[0:p, u, :, :], ALU.max)\
                        .then_inc(s["bent"], 1)

                staggered(dve, (normalise, 2), (scale, 5), (add, 1), (lambda *g: prop.make(dve, *g), 0), (reduce, 4),
                          (bend, 3))

            @block.scalar
            def _(act):
                act.sem_inc(conv.copied, 1)
                act.sem_inc(caps.copied, 1)
                act.sem_inc(caps.free, 1)

                def leaked(n, i, u, p):
                    act.wait_ge(caps.made, n + 2)
                    for out, scale in ((plain, 1.0), (leak, 0.01)):
                        for b in range(2):
                            ins = nc.scalar.activation(out[0:p, u, 4 * b:4 * b + 4, :], caps.out[b][0:p, :, :],
                                                       ACT.Copy, scale=scale)
                    ins.then_inc(s["leaked"], 1)
                    act.wait_ge(s["leaked"], n + 1)
                    act.sem_inc(caps.free, 1)

                def squared(n, i, u, p):
                    act.wait_ge(s["bent"], n + 1)
                    act.wait_ge(s["reduced"], n + 1)
                    nc.scalar.activation(square[0:p, :, :], cap[0:p, u, :, :], ACT.Square).then_inc(s["squared"], 1)

                def size(n, i, u, p):
                    act.wait_ge(s["reduced"], n + 2)
                    nc.scalar.activation(length[0:p, u, 1, :], length[0:p, u, 0, :], ACT.Sqrt).then_inc(s["sized"], 1)

                staggered(act, (squared, 4), (lambda n, i, u, p: caps.copy(act, n, p), 2),
                          (lambda n, i, u, p: norm.square_root(act, n, u, p), 1), (leaked, 2),
                          (lambda n, i, u, p: conv.copy(act, n, p), 0), (size, 4))

            @block.tensor
            def _(pe):
                pe.sem_inc(conv.made, 1)
                pe.sem_inc(caps.made, 1)
                pe.sem_inc(prop.used, 2)

                def conv_turn(n, i, u, p):
                    pe.wait_ge(prop.made, n + 1)
                    conv.turn(pe, n, p, prop.y[:, u, :, 0:D])
                    pe.wait_ge(conv.turned, n + 1)
                    pe.sem_inc(prop.used, 1)

                def caps_turn(n, i, u, p):
                    pe.wait_ge(s["normed"], n + 1)
                    caps.turn(pe, n, p, x1[:, u, :, :])

                staggered(pe, (caps_turn, 2), (lambda n, i, u, p: caps.product(pe, n, p), 2), (conv_turn, 0),
                          (lambda n, i, u, p: conv.product(pe, n, p), 0))
        clear_semaphores(nc, prop.sems + conv.sems + caps.sems + norm.sems + list(s.values()))


def routing_setup_phase(k, o):
    nc = k.nc
    with ExitStack() as st:
        pick = k.sb(st, "rs_pick", [P, 2, P])
        pick2 = k.sb(st, "rs_pick2", [P, 2])
        ends = k.sb(st, "rs_ends", [P, 2, T])
        ends_t = k.sb(st, "rs_ends_t", [TB, 2, 2])
        place = k.sb(st, "rs_place", [P, 2])
        order = k.sb(st, "rs_order", [TB, 2, 2, T])
        pe_ends = [k.ps(st, f"rs_ends_ps{a}", [P, 512]) for a in range(2)]
        pe_two = k.ps(st, "rs_two_ps", [P, 512])
        pe_t = k.ps(st, "rs_t_ps", [P, 2, 2, P])
        s = {x: k.sem(st, "rs_" + x) for x in ("step", "picked", "turned")}
        with nc.Block() as block:
            @block.vector
            def _(dve):
                v = nc.vector
                c = Chain(dve, s["step"], 14)
                c.begin(0)
                c.link(v.tensor_scalar(pick2[:, 0:1], k.iota_part[:, :], 0.0, None, ALU.is_equal))
                c.link(v.tensor_copy(pick2[:, 1:2], k.last_part[:, :]))
                c.link(v.tensor_scalar(pick[:, 0, :], k.ones[:, :], pick2[:, 0:1], None, ALU.mult))
                c.link(v.tensor_scalar(pick[:, 1, :], k.ones[:, :], pick2[:, 1:2], None, ALU.mult))
                dve.wait_ge(s["picked"], 1)
                c.link(v.tensor_copy(ends[:, 0, :], pe_ends[0][:, 0:T]))
                c.link(v.tensor_copy(ends[:, 1, :], pe_ends[1][:, 0:T]))
                c.link(v.tensor_copy(k.ends2[:, :], pe_two[0:2, 0:T]))
                c.link(v.tensor_tensor(k.end_mask[:, :, 0], o.id_col[:, :], ends[:, 0, :], ALU.is_equal))
                c.link(v.tensor_tensor(k.end_mask[:, :, 1], o.id_col[:, :], ends[:, 1, :], ALU.is_equal))
                dve.wait_ge(s["turned"], 1)
                c.link(v.tensor_copy(ends_t[:, :, :], pe_t[0:TB, :, :, 0]))
                c.link(v.tensor_copy(place[:, 0:1], k.iota_part[:, :]))
                c.link(v.tensor_scalar(place[:, 1:2], k.iota_part[:, :], float(TB), None, ALU.add))
                for b in range(2):
                    v.tensor_scalar(order[:, 0, b, :], k.iota_high[0:TB, 0:T], place[0:TB, b:b + 1], None, ALU.is_gt)
                    ins = v.tensor_scalar(order[:, 1, b, :], k.iota_high[0:TB, 0:T], place[0:TB, b:b + 1], None,
                                          ALU.is_lt)
                c.link(ins)
                for b in range(2):
                    v.scalar_tensor_tensor(k.handed[:, 0, b, :], ends[0:TB, 0, :], ends_t[:, 1, b:b + 1],
                                           order[:, 0, b, :], ALU.is_equal, ALU.mult)
                    ins = v.scalar_tensor_tensor(k.handed[:, 1, b, :], ends[0:TB, 1, :], ends_t[:, 0, b:b + 1],
                                                 order[:, 1, b, :], ALU.is_equal, ALU.mult)
                c.link(ins)
                c.end()

            @block.tensor
            def _(pe):
                pe.wait_ge(s["step"], 4)
                for a in range(2):
                    nc.tensor.matmul(pe_ends[a][:, 0:T], pick[:, a, :], o.id_col[:, :], start=True, stop=True)
                nc.tensor.matmul(pe_two[0:2, 0:T], pick2[:, :], o.id_col[:, :], start=True, stop=True)\
                    .then_inc(s["picked"], 1)
                pe.wait_ge(s["step"], 6)
                for a in range(2):
                    for b in range(2):
                        last = nc.tensor.transpose(pe_t[0:TB, a, b, :], ends[:, a, b * TB:(b + 1) * TB], k.ident[:, :])
                last.then_inc(s["turned"], 1)
        clear_semaphores(nc, list(s.values()))


def exchange_phase(k, tag):
    nc = k.nc
    with ExitStack() as st:
        part = k.sb(st, tag + "_part", [TB, 2, 2, D])
        total = k.sb(st, tag + "_total", [TB, 2, 2, D])
        ps = [k.ps(st, f"{tag}_ps{a}", [P, 2, D]) for a in range(2)]
        s = {x: k.sem(st, f"{tag}_{x}") for x in ("got", "made", "out", "put")}
        with nc.Block() as block:
            @block.sync
            def _(sp):
                for a in range(2):
                    for b in range(2):
                        sp.dma_start(part[:, a, b, :], k.end_sums[a, b * TB:(b + 1) * TB, :]).then_inc(s["got"], 16)
                sp.wait_ge(s["out"], 2)
                for a in range(2):
                    for b in range(2):
                        sp.dma_start(k.handed_sums[a, b * TB:(b + 1) * TB, :], total[:, a, b, :])\
                          .then_inc(s["put"], 16)
                sp.wait_ge(s["put"], 64)

            @block.vector
            def _(dve):
                dve.wait_ge(s["made"], 1)
                for a in range(2):
                    nc.vector.tensor_copy(total[:, a, :, :], ps[a][0:TB, :, :]).then_inc(s["out"], 1)

            @block.tensor
            def _(pe):
                pe.wait_ge(s["got"], 64)
                for a in range(2):
                    for out in range(2):
                        for b in range(2):
                            last = nc.tensor.matmul(ps[a][0:TB, out, :], k.handed[:, a, b, out * TB:(out + 1) * TB],
                                                    part[:, 1 - a, b, :], start=(b == 0), stop=(b == 1))
                last.then_inc(s["made"], 1)
        clear_semaphores(nc, list(s.values()))


RT = 2 * GT
RU = T // RT


def routing_phase(k, o, step, last_step, tag):
    nc = k.nc
    first, last = step == 0, step == last_step
    F = RT * D
    with ExitStack() as st:
        def sb(name, shape, dt=F32):
            return k.sb(st, f"{tag}_{name}", shape, dt)

        if first:
            pair = sb("pair", [P, 2, RT, 2, D])
            own = sb("own", [P, 2, RT, D])
            index_s = sb("index", [P, 2, 2, RT], I32)
        else:
            same = sb("same", [P, 2, RT, P])
            ends = sb("ends", [2, 2, RT, P])
            handed = sb("handed", [2, 2, RT, D])
            y_sb = sb("y", [P, 2, RT, D])
            acc = [k.ps(st, f"{tag}_acc{u}", [P, RT, D]) for u in range(2)]
        if last:
            sent = sb("sent", [P, 2, RT, D])
            last_s = sb("last", [P, 2, RT], I32)
        else:
            if not first:
                far = sb("far", [P, 2, RT, D])
                both = sb("both", [P, 2, RT, D])
            mask_s = sb("mask", [P, 2, RT, 2])
            end_out = sb("end_out", [2, RT, D])
            end_ps = [k.ps(st, f"{tag}_end{u}", [P, RT, D]) for u in range(2)]
            weight = sb("weight", [P, 2, RT * NH])
        terms = sb("terms", [P, 2, RT, D])
        dots = sb("dots", [P, 2, 2, RT * NH])
        logs = sb("logs", [P, 2, RT * NH])
        inv = sb("inv", [P, 2, RT * NH])
        score = sb("score", [P, 2, RT * NH])
        names = ["index", "free", "rows0", "rows1", "far0", "far1", "both0", "both1", "row_free", "same", "ends",
                 "summed", "copied", "squared", "product", "reduced", "log", "inverse", "scored", "masked",
                 "weighed", "valued", "paired", "end_made", "end_copied", "end_put", "sent", "sent_free",
                 "paired_put0", "paired_put1"]
        s = {x: k.sem(st, f"{tag}_{x}") for x in names}
        even, odd = (RU + 1) // 2, RU // 2
        in0, out0 = list(k.gather_base), list(k.scatter_base)
        for u, units in enumerate((even, odd)):
            k.gather_base[u] += units * 32 * RT * first
            k.scatter_base[u] += units * 16 * RT * last
        sems = list(s.values())
        s.update(own0=k.gathered[0], own1=k.gathered[1], put0=k.scattered[0], put1=k.scattered[1])

        def tiles(column, n):
            return column[:, n * RT:n * RT + RT] if isinstance(n, int) else column[:, bass.ds(n * RT, RT)]

        def rows_at(n, width):
            return slice(n * width, n * width + width) if isinstance(n, int) else bass.ds(n * width, width)

        def edge_rows(table, n):
            return table[rows_at(n, F), :].rearrange("(t p) c -> p t c", p=P)

        def by_head(ap):
            return ap.rearrange("p t (h d) -> p t h d", h=NH)

        def per_head(ap):
            return ap.rearrange("p (t h) -> p t h", h=NH).unsqueeze(3).broadcast_to([P, RT, NH, HD])

        def run(eng, *stages):
            staggered(eng, *stages, full=RU, tail=None)

        with nc.Block() as block:
            @block.sync
            def _(sp):
                def load_rows(n, i, u, p):
                    sp.wait_ge(s["row_free"], n + 1)
                    sp.dma_start(same[:, u, :, :].rearrange("p t e -> p (t e)"),
                                 o.id_row[rows_at(n, F)].partition_broadcast(P)).then_inc(s[f"rows{u}"], 16)
                    sp.dma_start(handed[:, u, :, :], k.handed_sums[:, rows_at(n, RT), :])\
                      .then_inc(s[f"rows{u}"], 16)

                def load_far(n, i, u, p):
                    sp.wait_ge(s["reduced"], n + 1)
                    sp.dma_start(far[:, u, :, :], edge_rows(k.pairs, n)[:, :, 0:D]).then_inc(s[f"far{u}"], 16)

                def load_both(n, i, u, p):
                    sp.wait_ge(s["valued"], n + 1)
                    sp.dma_start(both[:, u, :, :], edge_rows(k.pairs, n)[:, :, D:2 * D]).then_inc(s[f"both{u}"], 16)

                def store_pair(n, i, u, p):
                    sp.wait_ge(s["paired"], n + 1)
                    sp.dma_start(edge_rows(k.pairs, n), pair[:, u, :, :, :].rearrange("p t c d -> p t (c d)"))\
                      .then_inc(s[f"paired_put{u}"], 16)

                def store_ends(n, i, u, p):
                    sp.wait_ge(s["end_copied"], n + 1)
                    sp.dma_start(k.end_sums[:, rows_at(n, RT), :], end_out[:, :, :]).then_inc(s["end_put"], 16)

                if first:
                    sp.sem_inc(s["end_put"], 16)
                    run(sp, (store_pair, 1), (store_ends, 2))
                    sp.wait_ge(s["paired_put0"], 16 * even)
                    sp.wait_ge(s["paired_put1"], 16 * odd)
                    sp.wait_ge(s["end_put"], 16 * RU + 16)
                elif last:
                    run(sp, (load_rows, 0))
                else:
                    sp.sem_inc(s["end_put"], 16)
                    run(sp, (load_rows, 0), (load_far, 1), (load_both, 1), (store_ends, 4))
                    sp.wait_ge(s["end_put"], 16 * RU + 16)

            @block.gpsimd
            def _(pool):
                def gather(n, i, u, p):
                    paced(pool, k, s["free"], n + 1)
                    nc.gpsimd.tensor_copy(index_s[:, u, 0, :], tiles(o.cap_far, n))
                    nc.gpsimd.tensor_copy(index_s[:, u, 1, :], tiles(o.cap_own, n)).then_inc(s["index"], 1)
                    paced(pool, k, s["index"], n + 1)
                    for j in range(RT):
                        for c, out in ((0, pair[:, u, j, 0, :]), (1, own[:, u, j, :])):
                            nc.gpsimd.indirect_dma_start(
                                out=out, out_offset=None, in_=k.layer1_halves,
                                in_offset=bass.IndirectOffsetOnAxis(ap=index_s[:, u, c, j:j + 1], axis=0))\
                                .then_inc(s[f"own{u}"], 16)

                def values(n, i, u, p):
                    paced(pool, k, s["weighed"], n + 1)
                    paced(pool, k, s[f"both{u}"], i * 16 + 16)
                    nc.gpsimd.tensor_tensor(by_head(tiles(k.vals, n)), by_head(both[:, u, :, :]),
                                            per_head(weight[:, u, :]), ALU.mult).then_inc(s["valued"], 1)
                    paced(pool, k, s["end_made"], n + 1)
                    nc.gpsimd.tensor_copy(mask_s[:, u, :, :], tiles(k.end_mask, n)).then_inc(s["masked"], 1)

                def scatter(n, i, u, p):
                    paced(pool, k, s["sent"], n + 3)
                    nc.gpsimd.tensor_copy(last_s[:, u, :], tiles(o.last_cap, n)).then_inc(s["index"], 1)
                    paced(pool, k, s["index"], n + 1)
                    for j in range(RT):
                        nc.gpsimd.indirect_dma_start(
                            out=k.layer1_halves,
                            out_offset=bass.IndirectOffsetOnAxis(ap=last_s[:, u, j:j + 1], axis=0),
                            in_=sent[:, u, j, :], in_offset=None, bounds_check=2 * N - 1, oob_is_err=False)\
                            .then_inc(s[f"put{u}"], 16)

                def scattered(n, i, u, p):
                    pool.wait_ge(s[f"put{u}"], i * (16 * RT) + (out0[u] + 16 * RT))
                    pool.sem_inc(s["sent_free"], 1)

                if first:
                    run(pool, (gather, 0))
                elif last:
                    pool.sem_inc(s["sent_free"], 2)
                    run(pool, (scatter, 0), (scattered, 1))
                else:
                    pool.sem_inc(s["valued"], 2)
                    run(pool, (values, 0))

            @block.vector
            def _(dve):
                def equal(n, i, u, p):
                    dve.wait_ge(s[f"rows{u}"], i * 32 + 32)
                    nc.vector.tensor_tensor(ends[:, u, :, :], same[0:2, u, :, :],
                                            tiles(k.ends2, n).unsqueeze(2).broadcast_to([2, RT, P]),
                                            ALU.is_equal).then_inc(s["ends"], 1)
                    dve.wait_ge(s["ends"], n + 1)
                    nc.vector.tensor_tensor(same[:, u, :, :], same[:, u, :, :],
                                            tiles(o.id_col, n).unsqueeze(2).broadcast_to([P, RT, P]),
                                            ALU.is_equal).then_inc(s["same"], 1)

                def pairs(n, i, u, p):
                    dve.wait_ge(s[f"own{u}"], i * (32 * RT) + (in0[u] + 32 * RT))
                    nc.vector.tensor_tensor(pair[:, u, :, 1, :], pair[:, u, :, 0, :], own[:, u, :, :],
                                            ALU.add).then_inc(s["paired"], 1)

                def reduce(n, i, u, p):
                    if not last:
                        if not first:
                            dve.wait_ge(s["copied"], n + 3)
                            dve.wait_ge(s["reduced"], n + 2)
                            dve.wait_ge(s[f"far{u}"], i * 16 + 16)
                        nc.vector.tensor_tensor(terms[:, 0, :, :], own[:, u, :, :] if first else y_sb[:, u, :, :],
                                                pair[:, u, :, 0, :] if first else far[:, u, :, :],
                                                ALU.mult).then_inc(s["product"], 1)
                        dve.wait_ge(s["product"], n + 1)
                    lo, hi = (0, 1) if first else (1, 2) if last else (0, 2)
                    if not first:
                        dve.wait_ge(s["squared"], n + 1)
                    nc.vector.tensor_reduce(dots[:, u, lo:hi, :],
                                            terms[:, lo:hi, :, :].rearrange("p c t (h d) -> p (c t h) d", h=NH),
                                            AX.X, ALU.add).then_inc(s["reduced"], 1)

                def scored(n, i, u, p):
                    dve.wait_ge(s["inverse"], n + 1)
                    if last:
                        dve.wait_ge(s["sent_free"], n + 1)
                        nc.vector.tensor_tensor(by_head(sent[:, u, :, :]), by_head(y_sb[:, u, :, :]),
                                                per_head(inv[:, u, :]), ALU.mult).then_inc(s["sent"], 1)
                    else:
                        nc.vector.tensor_tensor(score[:, u, :], dots[:, u, 0, :], inv[:, u, :],
                                                ALU.mult).then_inc(s["scored"], 1)

                def first_values(n, i, u, p):
                    dve.wait_ge(s["end_made"], n + 1)
                    nc.vector.tensor_copy(mask_s[:, u, :, :], tiles(k.end_mask, n)).then_inc(s["masked"], 1)
                    dve.wait_ge(s["weighed"], n + 1)
                    nc.vector.tensor_tensor(by_head(tiles(k.vals, n)), by_head(pair[:, u, :, 1, :]),
                                            per_head(weight[:, u, :]), ALU.mult).then_inc(s["valued"], 1)
                    dve.wait_ge(s["valued"], n + 3)
                    dve.wait_ge(s[f"paired_put{u}"], i * 16 + 16)
                    dve.sem_inc(s["free"], 1)

                if first:
                    dve.sem_inc(s["free"], 2)
                    dve.sem_inc(s["valued"], 2)
                    run(dve, (pairs, 0), (reduce, 0), (first_values, 0))
                else:
                    dve.sem_inc(s["reduced"], 2)
                    if last:
                        dve.sem_inc(s["sent"], 2)
                    run(dve, (equal, 0), (scored, 2), (reduce, 1))

            @block.scalar
            def _(act):
                def squares(n, i, u, p):
                    act.wait_ge(s["summed"], n + 1)
                    if last:
                        act.wait_ge(s["sent"], n + 1)
                    nc.scalar.activation(y_sb[:, u, :, :], acc[u][:, :, :], ACT.Copy).then_inc(s["copied"], 1)
                    act.wait_ge(s["copied"], n + 3)
                    act.wait_ge(s["reduced"], n + 2)
                    nc.scalar.activation(terms[:, 1, :, :], y_sb[:, u, :, :], ACT.Square).then_inc(s["squared"], 1)

                def inverse(n, i, u, p):
                    act.wait_ge(s["reduced"], n + 3)
                    nc.scalar.activation(logs[:, u, :], dots[:, u, 1, :], ACT.Ln).then_inc(s["log"], 1)
                    act.wait_ge(s["log"], n + 1)
                    nc.scalar.activation(inv[:, u, :], logs[:, u, :], ACT.Exp, scale=-0.5).then_inc(s["inverse"], 1)

                def weigh(n, i, u, p):
                    act.wait_ge(s["reduced" if first else "scored"], n + 1)
                    nc.scalar.activation(weight[:, u, :], dots[:, u, 0, :] if first else score[:, u, :],
                                         ACT.Exp).then_inc(s["weighed"], 1)

                def copy_ends(n, i, u, p):
                    act.wait_ge(s["end_made"], n + 3)
                    act.wait_ge(s["end_put"], n * 16 + 16)
                    nc.scalar.activation(end_out[:, :, :], end_ps[u][0:2, :, :], ACT.Copy)\
                        .then_inc(s["end_copied"], 1)

                if not first:
                    act.sem_inc(s["copied"], 2)
                if first:
                    run(act, (weigh, 0), (copy_ends, 1))
                elif last:
                    run(act, (squares, 0), (inverse, 0))
                else:
                    run(act, (squares, 1), (weigh, 2), (inverse, 1), (copy_ends, 3))

            @block.tensor
            def _(pe):
                def sums(n, i, u, p):
                    pe.wait_ge(s["same"], n + 1)
                    pe.wait_ge(s["copied"], n + 1)
                    for j in range(RT):
                        nc.tensor.matmul(acc[u][:, j, :], same[:, u, j, :], k.vals[:, rows_at_tile(n, j), :],
                                         start=True, stop=False)
                        mm = nc.tensor.matmul(acc[u][:, j, :], ends[:, u, j, :], handed[:, u, j, :], start=False,
                                              stop=True)
                    mm.then_inc(s["summed"], 1)
                    pe.wait_ge(s["summed"], n + 1)
                    pe.sem_inc(s["row_free"], 1)

                def end_sums(n, i, u, p):
                    pe.wait_ge(s["valued"], n + 3)
                    paced(pe, k, s["masked"], n + 1)
                    for j in range(RT):
                        mm = nc.tensor.matmul(end_ps[u][0:2, j, :], mask_s[:, u, j, :], k.vals[:, rows_at_tile(n, j), :],
                                              start=True, stop=True)
                    mm.then_inc(s["end_made"], 1)

                def rows_at_tile(n, j):
                    return slice(n * RT + j, n * RT + j + 1) if isinstance(n, int) else bass.ds(n * RT + j, 1)

                if not last:
                    pe.sem_inc(s["end_made"], 2)
                if not first:
                    pe.sem_inc(s["row_free"], 2)
                if first:
                    run(pe, (end_sums, 0))
                elif last:
                    run(pe, (sums, 0))
                else:
                    run(pe, (sums, 0), (end_sums, 3))
        clear_semaphores(nc, sems)


CH = 8
CT = T // CH
CE = CT * P
Q = NH * CH


def attention_weights_phase(k, stack):
    nc = k.nc
    a = k.a
    k.qkv_parts = [k.sb(stack, f"{name}_parts", [3, 4, D], BF16) for name in ("query", "key", "value")]
    k.bc_parts = k.sb(stack, "bc_parts", [3, 4, NH], BF16)
    k.bo_parts = k.sb(stack, "bo_parts", [3, 4, D], BF16)
    with ExitStack() as st:
        w = k.sb(st, "aw_w", [P, 3, D])
        b = k.sb(st, "aw_b", [3, 3, D])
        bc = k.sb(st, "aw_bc", [3, NH])
        bo = k.sb(st, "aw_bo", [3, D])
        g1 = k.sb(st, "aw_g1", [P, 1])
        be1 = k.sb(st, "aw_be1", [P, 3])
        ps = k.ps(st, "aw_ps", [P, 512])
        load_constants(k, [(w[:, i, :], a["L2_gnn_W" + c]) for i, c in enumerate("qkv")]
                       + [(b[:, i, :], a["L2_gnn_b" + c].partition_broadcast(3)) for i, c in enumerate("qkv")]
                       + [(be1[:, r:r + 1], a["L2_gnn_be1"].rearrange("(p r) -> p r", r=1)) for r in range(3)]
                       + [(g1[:, :], a["L2_gnn_g1"].rearrange("(p r) -> p r", r=1)),
                          (k.wc[:, :], a["L2_gnn_Wc"]), (bc[:, :], a["L2_gnn_bc"].partition_broadcast(3)),
                          (k.wo[:, :], a["L2_gnn_Wo"]), (bo[:, :], a["L2_gnn_bo"].partition_broadcast(3))])
        s = {x: k.sem(st, "aw_" + x) for x in ("step", "made")}
        with nc.Block() as block:
            @block.vector
            def _(dve):
                v = nc.vector
                c = Chain(dve, s["step"], 4)
                c.begin(0)
                dve.wait_ge(s["made"], 1)
                c.link(v.tensor_tensor(b[:, :, :], ps[0:3, 0:3 * D].rearrange("p (i d) -> p i d", i=3),
                                       b[:, :, :], ALU.add))
                c.link(v.tensor_scalar(k.qkv_w[:, :, :], w[:, :, :], g1[:, 0:1], None, ALU.mult))
                c.link(v.tensor_scalar(k.qkv_w[:, 0, :], k.qkv_w[:, 0, :], HD ** -0.5, None, ALU.mult))
                c.link(v.tensor_scalar(b[:, 0, :], b[:, 0, :], HD ** -0.5, None, ALU.mult))
                c.end()

            @block.tensor
            def _(pe):
                nc.tensor.matmul(ps[0:3, 0:3 * D], be1[:, :], w[:, :, :].rearrange("p i d -> p (i d)"), start=True,
                                 stop=True).then_inc(s["made"], 1)
        clear_semaphores(nc, list(s.values()))
        split_biases(k, st, "aw_bias", [b[:, 0, :], b[:, 1, :], b[:, 2, :], bc[:, :], bo[:, :]],
                     k.qkv_parts + [k.bc_parts, k.bo_parts])


def scores_phase(k, o):
    nc = k.nc
    C = 2 * GT
    with ExitStack() as st:
        rows = k.sb(st, "sc_rows", [P, 2, C, 2 * D])
        index_s = k.sb(st, "sc_index", [P, 2, 2, GT], I32)
        attr = k.sb(st, "sc_attr", [P, 2, GT, D])
        xin = k.sb(st, "sc_xin", [P, 2, C, D])
        xn = k.sb(st, "sc_xn", [P, 2, C, D])
        x_t = k.sb(st, "sc_x_t", [P, C, P])
        attr_t = k.sb(st, "sc_attr_t", [P, GT, P])
        query = k.sb(st, "sc_query", [P, GT, D])
        value = k.sb(st, "sc_value", [P, 2, GT, D])
        terms = k.sb(st, "sc_terms", [P, GT, D])
        dots = k.sb(st, "sc_dots", [P, GT, NH])
        norm = Norm(k, st, "sc_norm", cols=C, eps=EPS * EPS, factor=1.0 + EPS)
        t_ps = [k.ps(st, f"sc_t{b}", [P, GT, P]) for b in range(3)]
        out_ps = [k.ps(st, f"sc_o{b}", [P, GT, D]) for b in range(3)]
        attr_ps = k.ps(st, "sc_attr_ps", [P, 512])
        names = ["index", "free", "attr0", "attr1", "attr_tail", "attr_free", "added", "normed", "turned", "copied",
                 "made", "query", "value", "value_put0", "value_put1", "product", "dots", "scored", "cleared"]
        s = {x: k.sem(st, "sc_" + x) for x in names}
        in0 = list(k.gather_base)
        k.gather_base = [x + (EG // 2) * 32 * GT for x in k.gather_base]
        full = E // (GT * P)
        assert full % 2 == 0 and full + 2 == EG

        with nc.Block() as block:
            @block.sync
            def _(sp):
                edge_attr = k.a["edge_attr_128"]

                def load(g, i, u, p):
                    sp.wait_ge(s["attr_free"], g + 1)
                    if not isinstance(g, int) or g < full:
                        at = span(g, GT * P)
                        sp.dma_start(attr[:, u, :, :], edge_attr[at, :].rearrange("(t p) d -> p t d", p=P))\
                          .then_inc(s[f"attr{u}"], 16)
                    elif g == full:
                        at, left = full * GT * P, E - full * GT * P
                        sp.dma_start(attr[0:left % P, u, left // P, :], edge_attr[E - left % P:E, :])\
                          .then_inc(s["attr_tail"], 16)
                        sp.wait_ge(s["attr_tail"], 16)
                        sp.dma_start(attr[:, u, 0:left // P, :], edge_attr[at:at + left // P * P, :]
                                     .rearrange("(t p) d -> p t d", p=P)).then_inc(s[f"attr{u}"], 16)
                    else:
                        sp.sem_inc(s[f"attr{u}"], 16)

                def put(g, i, u, p):
                    sp.wait_ge(s["value"], g + 2)
                    at = span(g, GT * P)
                    sp.dma_start(k.values[at, 0:D].rearrange("(t p) d -> p t d", p=P), value[:, u, :, :])\
                      .then_inc(s[f"value_put{u}"], 16)

                sp.wait_ge(s["cleared"], 1)
                for u in range(2):
                    sp.sem_inc(s[f"value_put{u}"], 16)
                staggered(sp, (load, 0), (put, 3), full=EG, tail=None, looped=full)
                for u in range(2):
                    sp.wait_ge(s[f"value_put{u}"], 16 * (EG // 2) + 16)

            @block.gpsimd
            def _(pool):
                with pool.Fori(0, EG // 2) as i:
                    for u in range(2):
                        g = i * 2 + u
                        paced(pool, k, s["free"], g + 1)
                        nc.gpsimd.tensor_copy(index_s[:, u, :, :], k.node_idx[:, :, bass.ds(g * GT, GT)])\
                            .then_inc(s["index"], 1)
                        paced(pool, k, s["index"], g + 1)
                        for c in range(2):
                            for j in range(GT):
                                nc.gpsimd.indirect_dma_start(
                                    out=rows[:, u, c * GT + j, :], out_offset=None, in_=k.layer1,
                                    in_offset=bass.IndirectOffsetOnAxis(ap=index_s[:, u, c, j:j + 1], axis=0))\
                                    .then_inc(k.gathered[u], 16)

            @block.vector
            def _(dve):
                norm.prepare(dve)
                nc.vector.memset(attr[:, :, :, :], 0.0).then_inc(s["cleared"], 1)
                dve.wait_ge(s["cleared"], 1)
                dve.sem_inc(s["free"], 2)
                dve.sem_inc(s["scored"], 1)

                def add(g, i, u, p):
                    dve.wait_ge(k.gathered[u], i * (32 * GT) + (in0[u] + 32 * GT))
                    nc.vector.tensor_tensor(xin[:, u, :, :], rows[:, u, :, 0:D], rows[:, u, :, D:2 * D],
                                            ALU.add).then_inc(s["added"], 1)
                    dve.wait_ge(s["added"], g + 1)
                    dve.sem_inc(s["free"], 1)
                    norm.statistics(dve, g, u, P, xin[:, u, :, :])

                def normalise(g, i, u, p):
                    norm.normalise(dve, g, u, P, xn[:, u, :, :], xin[:, u, :, :]).then_inc(s["normed"], 1)

                def score(g, i, u, p):
                    dve.wait_ge(s["query"], g + 1)
                    nc.vector.tensor_tensor(terms[:, :, :], query[:, :, :], out_ps[1][:, :, :],
                                            ALU.mult).then_inc(s["product"], 1)
                    dve.wait_ge(s["product"], g + 1)
                    nc.vector.tensor_reduce(dots[:, :, :], terms[:, :, :].rearrange("p t (h d) -> p t h d", h=NH),
                                            AX.X, ALU.add).then_inc(s["dots"], 1)
                    dve.wait_ge(s["dots"], g + 1)
                    nc.vector.tensor_tensor(k.scores[:, span(g, GT), :],
                                            dots[:, :, :],
                                            attr_ps[:, 0:GT * NH].rearrange("p (t h) -> p t h", h=NH),
                                            ALU.add).then_inc(s["scored"], 1)

                staggered(dve, (normalise, 1), (score, 2), (add, 0), full=EG, tail=None)

            @block.scalar
            def _(act):
                def copy(g, i, u, p):
                    act.wait_ge(s["turned"], g + 1)
                    act.wait_ge(s["made"], g + 1)
                    for b in range(2):
                        nc.scalar.activation(x_t[:, b * GT:(b + 1) * GT, :], t_ps[b][:, :, :], ACT.Copy)
                    nc.scalar.activation(attr_t[:, :, :], t_ps[2][:, :, :], ACT.Copy).then_inc(s["copied"], 1)

                def values(g, i, u, p):
                    act.wait_ge(s["made"], g + 2)
                    act.wait_ge(s["scored"], g + 1)
                    nc.scalar.activation(query[:, :, :], out_ps[0][:, :, :], ACT.Copy).then_inc(s["query"], 1)
                    act.wait_ge(s[f"value_put{u}"], i * 16 + 16)
                    nc.scalar.activation(value[:, u, :, :], out_ps[2][:, :, :], ACT.Copy).then_inc(s["value"], 1)

                act.sem_inc(s["copied"], 1)
                act.sem_inc(s["value"], 1)
                staggered(act, (values, 2), (copy, 1), (lambda g, i, u, p: norm.square_root(act, g, u, p), 0),
                          full=EG, tail=None)

            @block.tensor
            def _(pe):
                pe.sem_inc(s["made"], 1)
                pe.sem_inc(s["attr_free"], 2)

                def turn(g, i, u, p):
                    pe.wait_ge(s["normed"], g + 1)
                    pe.wait_ge(s["copied"], g + 1)
                    pe.wait_ge(s[f"attr{u}"], i * 16 + 16)
                    for j in range(C):
                        nc.tensor.transpose(t_ps[j // GT][:, j % GT, :], xn[:, u, j, :], k.ident[:, :])
                    for j in range(GT):
                        mm = nc.tensor.transpose(t_ps[2][:, j, :], attr[:, u, j, :], k.ident[:, :])
                    mm.then_inc(s["turned"], 1)
                    pe.wait_ge(s["turned"], g + 1)
                    pe.sem_inc(s["attr_free"], 1)

                def project(g, i, u, p):
                    pe.wait_ge(s["copied"], g + 2)
                    pe.wait_ge(s["value"], g + 1)
                    pe.wait_ge(s["scored"], g + 1)
                    for c in range(3):
                        add_bias(out_ps[c][:, :, :].rearrange("p t d -> p (t d)"), k.qkv_parts[c])
                        for j in range(GT):
                            nc.tensor.matmul(out_ps[c][:, j, :], x_t[:, j if c == 0 else GT + j, :], k.qkv_w[:, c, :],
                                             start=False, stop=j == GT - 1, skip_group_check=True)
                    add_bias(attr_ps[:, 0:GT * NH], k.bc_parts)
                    for j in range(GT):
                        mm = nc.tensor.matmul(attr_ps[:, j * NH:(j + 1) * NH], attr_t[:, j, :], k.wc[:, :],
                                              start=False, stop=j == GT - 1, skip_group_check=True)
                    mm.then_inc(s["made"], 1)

                def add_bias(out, parts):
                    nc.tensor.matmul(out, k.ones3[:, :], parts[:, :, :].rearrange("r t d -> r (t d)"), start=True,
                                     stop=False, skip_group_check=True)

                staggered(pe, (turn, 1), (project, 1), full=EG, tail=None)
        clear_semaphores(nc, norm.sems + list(s.values()))


def softmax_phase(k, o):
    nc = k.nc
    with ExitStack() as st:
        def sb(name, shape, dt=F32):
            return k.sb(st, "sm_" + name, shape, dt)

        packed = sb("packed", [P, CT, Q])
        ids = sb("ids", [Q, CE + 2])
        keep = sb("keep", [Q, 2, CE])
        gate = sb("gate", [Q, CE])
        edge = sb("edge", [Q, CE])
        score = sb("score", [Q, CE])
        p = sb("p", [Q, CE])
        run = sb("run", [Q, 2, CE])
        flags = sb("flags", [Q, 6])
        row = sb("row", [1, 6, Q])
        line = sb("line", [1, 4, Q])
        col = sb("col", [Q, 2])
        t_ps = k.ps(st, "sm_t_ps", [P, 4, P])
        row_ps = k.ps(st, "sm_row_ps", [P, 4, Q])
        end_ps = k.ps(st, "sm_end_ps", [P, 512])
        col_ps = k.ps(st, "sm_col_ps", [P, 512])
        back_ps = k.ps(st, "sm_back_ps", [P, 4, Q])
        s = {x: k.sem(st, "sm_" + x) for x in ("loaded", "set", "step", "packed", "turned", "copied", "rows", "ends",
                                               "cols", "exp", "back", "unpacked", "put")}
        with nc.Block() as block:
            @block.sync
            def _(sp):
                sp.wait_ge(s["set"], 1)
                for h in range(NH):
                    q = h * CH
                    sp.dma_start(ids[q:q + CH, 1:CE + 1], o.id_row[0:EP].rearrange("(c e) -> c e", c=CH))\
                      .then_inc(s["loaded"], 16)
                    sp.dma_start(ids[q:q + CH, CE + 1:CE + 2], o.id_row[1:EP + 1].rearrange("(c e) -> c e", c=CH)
                                 [:, CE - 1:CE], allow_slow_non_contiguous=True).then_inc(s["loaded"], 16)
                    sp.dma_start(ids[q + 1:q + CH, 0:1], o.id_row[0:EP].rearrange("(c e) -> c e", c=CH)
                                 [0:CH - 1, CE - 1:CE], allow_slow_non_contiguous=True).then_inc(s["loaded"], 16)
                sp.wait_ge(s["unpacked"], 1)
                sp.dma_start(k.values[:, D:D + NH].rearrange("(t p) h -> p t h", p=P), k.scores[:, :, :])\
                  .then_inc(s["put"], 16)
                sp.wait_ge(s["put"], 16)

            @block.vector
            def _(dve):
                v = nc.vector
                c = Chain(dve, s["step"], 0)
                c.begin(0)
                v.memset(ids[:, 0:1], -7.0).then_inc(s["set"], 1)
                for ch in range(CH):
                    ins = v.tensor_copy(packed[:, :, :].rearrange("p k (h c) -> p k h c", c=CH)[:, :, :, ch],
                                        k.scores[:, ch * CT:(ch + 1) * CT, :])
                ins.then_inc(s["packed"], 1)
                for kt in range(CT):
                    dve.wait_ge(s["turned"], kt + 1)
                    v.tensor_copy(score[:, kt * P:(kt + 1) * P], t_ps[0:Q, kt % 4, :]).then_inc(s["copied"], 1)
                dve.wait_ge(s["copied"], CT)
                dve.wait_ge(s["loaded"], 16 * 3 * NH)
                own = ids[:, 1:CE + 1]
                v.tensor_tensor(keep[:, 0, :], own, ids[:, 0:CE], ALU.is_equal)
                c.link(v.tensor_tensor(keep[:, 1, :], own, ids[:, 2:CE + 2], ALU.is_equal))
                v.tensor_copy(flags[:, 0:1], keep[:, 0, 0:1])
                v.tensor_copy(flags[:, 1:2], keep[:, 1, CE - 1:CE])
                c.link(v.tensor_tensor(flags[:, 2:3], ids[:, 1:2], ids[:, CE:CE + 1], ALU.is_equal))
                v.tensor_tensor(flags[:, 3:4], flags[:, 0:1], flags[:, 2:3], ALU.mult)
                c.link(v.tensor_tensor(flags[:, 4:5], flags[:, 1:2], flags[:, 2:3], ALU.mult))
                v.memset(keep[:, 0, 0:1], 0.0)
                c.link(v.memset(keep[:, 1, CE - 1:CE], 0.0))
                dve.wait_ge(s["rows"], 1)
                c.link(v.tensor_copy(row[:, 0:4, :], row_ps[0:1, :, :]))
                heads = row[:, 0:4, :].rearrange("p a (h c) -> p a h c", c=CH)
                v.memset(heads[:, 0, :, 0], 0.0)
                v.memset(heads[:, 1, :, CH - 1], 0.0)
                v.memset(heads[:, 2, :, 0], 0.0)
                c.link(v.memset(heads[:, 3, :, CH - 1], 0.0))

                def scan(d, data, additive, out):
                    def way(ap):
                        return ap[:, ::-1] if d else ap

                    c.link(v.tensor_scalar(edge[:, :], own, ids[:, (CE if d else 1):(CE + 1 if d else 2)], None,
                                           ALU.is_equal))
                    if additive:
                        c.link(v.tensor_copy(line[:, 0:2, :], row[:, (1 if d else 0):4:2, :]))
                        c.link(v.tensor_tensor_scan(way(out), way(keep[:, d, :]), way(data), 0.0, ALU.mult, ALU.add))
                    else:
                        c.link(v.tensor_scalar(edge[:, :], edge[:, :], BIG, -BIG, ALU.mult, ALU.add))
                        c.link(v.tensor_scalar(gate[:, :], keep[:, d, :], BIG, -BIG, ALU.mult, ALU.add))
                        c.link(v.tensor_scalar(line[:, 0:2, :], row[:, (1 if d else 0):4:2, :], BIG, -BIG, ALU.mult,
                                               ALU.add))
                        c.link(v.tensor_tensor_scan(way(out), way(gate[:, :]), way(data), -BIG, ALU.add, ALU.max))
                    scan.count += 1
                    c.link(v.tensor_copy(col[:, 0:1], out[:, 0:1] if d else out[:, CE - 1:CE]))
                    scan.ready.append(c.count)
                    dve.wait_ge(s["ends"], scan.count)
                    c.link(v.tensor_copy(line[:, 2, :], end_ps[0:1, 0:Q]))
                    ops = (ALU.mult, ALU.add) if additive else (ALU.add, ALU.max)
                    c.link(v.tensor_tensor_scan(way(line[:, 3, :]), way(line[:, 1, :]), way(line[:, 2, :]),
                                                0.0 if additive else -BIG, *ops))
                    c.link(v.memset(line[:, 2, :], 0.0))
                    shift = (line[:, 2, 0:Q - 1], line[:, 3, 1:Q], line[:, 0, 0:Q - 1]) if d else \
                        (line[:, 2, 1:Q], line[:, 3, 0:Q - 1], line[:, 0, 1:Q])
                    if not additive:
                        c.link(v.memset(line[:, 2, :], -BIG))
                    c.link(v.tensor_tensor(*shift, ops[0]))
                    scan.lines.append(c.count)
                    dve.wait_ge(s["cols"], scan.count)
                    c.link(v.tensor_copy(col[:, 1:2], col_ps[0:Q, 0:1]))
                    if additive:
                        c.link(v.scalar_tensor_tensor(out, edge[:, :], col[:, 1:2], out, ALU.mult, ALU.add))
                    else:
                        c.link(v.scalar_tensor_tensor(out, edge[:, :], col[:, 1:2], out, ALU.add, ALU.max))

                scan.count, scan.ready, scan.lines = 0, [], []
                scan(0, score[:, :], False, run[:, 0, :])
                scan(1, score[:, :], False, run[:, 1, :])
                c.link(v.tensor_tensor(run[:, 0, :], run[:, 0, :], run[:, 1, :], ALU.max))
                c.link(v.tensor_tensor(score[:, :], score[:, :], run[:, 0, :], ALU.subtract))
                softmax_phase.shifted = c.count
                dve.wait_ge(s["exp"], 1)
                scan(0, p[:, :], True, run[:, 0, :])
                scan(1, p[:, :], True, run[:, 1, :])
                c.link(v.tensor_tensor(run[:, 0, :], run[:, 0, :], run[:, 1, :], ALU.add))
                c.link(v.tensor_tensor(run[:, 0, :], run[:, 0, :], p[:, :], ALU.subtract))
                c.link(v.reciprocal(run[:, 1, :], run[:, 0, :]))
                c.link(v.tensor_tensor(p[:, :], p[:, :], run[:, 1, :], ALU.mult))
                softmax_phase.probs = c.count
                softmax_phase.ready, softmax_phase.lines = scan.ready, scan.lines
                scores = k.scores[:, :, :].rearrange("p (c k) h -> p k h c", c=CH)
                for kt in range(CT):
                    dve.wait_ge(s["back"], kt + 1)
                    ins = v.tensor_copy(scores[:, kt, :, :],
                                        back_ps[:, kt % 4, :].rearrange("p (h c) -> p h c", c=CH))
                    ins.then_inc(s["copied"], 1)
                dve.wait_ge(s["copied"], 2 * CT)
                dve.sem_inc(s["unpacked"], 1)

            @block.scalar
            def _(act):
                act.wait_ge(s["step"], softmax_phase.shifted)
                nc.scalar.activation(p[:, :], score[:, :], ACT.Exp).then_inc(s["exp"], 1)

            @block.tensor
            def _(pe):
                pe.wait_ge(s["packed"], 1)
                for kt in range(CT):
                    if kt >= 1:
                        pe.wait_ge(s["copied"], kt)
                    nc.tensor.transpose(t_ps[0:Q, kt % 4, :], packed[:, kt, :], k.ident[:, :])\
                        .then_inc(s["turned"], 1)
                pe.wait_ge(s["step"], 3)
                for a, f in enumerate((0, 1, 3, 4)):
                    ins = nc.tensor.transpose(row_ps[0:1, a, :], flags[:, f:f + 1], k.ident[0:Q, 0:Q])
                ins.then_inc(s["rows"], 1)
                for n in range(4):
                    pe.wait_ge(s["step"], softmax_phase.ready[n])
                    nc.tensor.transpose(end_ps[0:1, 0:Q], col[:, 0:1], k.ident[0:Q, 0:Q]).then_inc(s["ends"], 1)
                    pe.wait_ge(s["step"], softmax_phase.lines[n])
                    nc.tensor.transpose(col_ps[0:Q, 0:1], line[:, 2, :], k.ident[0:1, 0:1]).then_inc(s["cols"], 1)
                pe.wait_ge(s["step"], softmax_phase.probs)
                for kt in range(CT):
                    if kt >= 1:
                        pe.wait_ge(s["copied"], CT + kt)
                    nc.tensor.transpose(back_ps[:, kt % 4, :], p[:, kt * P:(kt + 1) * P], k.ident[0:Q, 0:Q])\
                        .then_inc(s["back"], 1)
        clear_semaphores(nc, list(s.values()))


def transformer_phase(k):
    nc = k.nc
    a = k.a
    NB = 4
    with ExitStack() as st:
        def sb(name, shape):
            return k.sb(st, "tf_" + name, shape)

        w1, w2 = sb("w1", [P, NB * D]), sb("w2", [P, NB, D])
        b1, b2 = sb("b1", [P, NB]), sb("b2", [P, D])
        g2, be2 = sb("g2", [P, 1]), sb("be2", [P, 1])
        both = sb("both", [P, 2, NJ, 2 * D])
        msum = sb("msum", [P, 2, NJ, D])
        xin, x2, xm, xn, rest, x3in, x3 = (sb(x, [P, 2, NJ, D]) for x in
                                           ("xin", "x2", "xm", "xn", "rest", "x3in", "x3"))
        x_t = sb("x_t", [P, 2, NJ, P])
        hidden = sb("hidden", [P, 2, NB, 4 * P])
        norms = [Norm(k, st, f"tf_norm{m}") for m in range(3)]
        x_ps = [k.ps(st, f"tf_x_ps{b}", [P, 4, P]) for b in range(2)]
        h_ps = [k.ps(st, f"tf_h_ps{b}", [P, 4 * P]) for b in range(NB)]
        o_ps = [k.ps(st, f"tf_o_ps{b}", [P, 4, D]) for b in range(2)]
        names = ["ready0", "ready1", "msum_ready0", "msum_ready1", "free", "msum_free", "rest_used", "added",
                 "x2_made", "xm_made", "rest_made", "rest_half", "normed", "turned", "x_copied", "hidden_made",
                 "bent", "out_made", "out_free", "x3_added", "x3_made", "stored0", "stored1", "w_step", "w_made"]
        s = {x: k.sem(st, "tf_" + x) for x in names}
        load_constants(k, [(w1[:, :], a["L2_gnn_W1"]),
                           (w2[:, :, :], a["L2_gnn_W2"].rearrange("(b p) d -> p b d", p=P)),
                           (b2[:, :], a["L2_gnn_b2"].partition_broadcast(P)),
                           (g2[:, :], a["L2_gnn_g2"].rearrange("(p r) -> p r", r=1)),
                           (be2[:, :], a["L2_gnn_be2"].rearrange("(p r) -> p r", r=1))]
                       + [(b1[:, b:b + 1], a["L2_gnn_b1"][b * P:(b + 1) * P].rearrange("(p r) -> p r", r=1))
                          for b in range(NB)])
        with nc.Block() as block:
            @block.sync
            def _(sp):
                def load(n, i, u, p):
                    sp.wait_ge(s["free"], n + 1)
                    sp.dma_start(both[0:p, u, :, :], node_rows(k.layer1, n, p, 2 * D)).then_inc(s[f"ready{u}"], 16)

                def load_msum(n, i, u, p):
                    sp.wait_ge(s["msum_free"], n + 1)
                    sp.dma_start(msum[0:p, u, :, :], node_rows(k.msum, n, p)).then_inc(s[f"msum_ready{u}"], 16)

                def store(n, i, u, p):
                    sp.wait_ge(s["x3_made"], n + 3)
                    sp.dma_start(node_rows(k.x3, n, p), x3[0:p, u, :, :]).then_inc(s[f"stored{u}"], 16)

                sp.sem_inc(s["stored0"], 16)
                sp.sem_inc(s["stored1"], 16)
                staggered(sp, (load_msum, 1), (load, 0), (store, 5))
                sp.wait_ge(s["stored0"], 16 * (NG // 2 + 2))
                sp.wait_ge(s["stored1"], 16 * (NG // 2 + 1))

            @block.gpsimd
            def _(pool):
                def add(n, i, u, p):
                    paced(pool, k, s[f"ready{u}"], i * 16 + 16)
                    paced(pool, k, s["x2_made"], n + 1)
                    nc.gpsimd.tensor_tensor(xin[0:p, u, :, :], both[0:p, u, :, 0:D], both[0:p, u, :, D:2 * D],
                                            ALU.add).then_inc(s["added"], 1)

                def freed(n, i, u, p):
                    pool.wait_ge(s["added"], n + 1)
                    pool.sem_inc(s["free"], 1)

                def leave(n, i, u, p):
                    paced(pool, k, s["xm_made"], n + 1)
                    paced(pool, k, s["rest_used"], n + 1)
                    nc.gpsimd.tensor_tensor(rest[0:p, u, :, :], x2[0:p, u, :, :], xm[0:p, u, :, :],
                                            ALU.add).then_inc(s["rest_half"], 1)
                    paced(pool, k, s["rest_half"], n + 1)
                    nc.gpsimd.tensor_tensor(rest[0:p, u, :, :], rest[0:p, u, :, :],
                                            b2[0:p, :].unsqueeze(1).broadcast_to([p, NJ, D]),
                                            ALU.add).then_inc(s["rest_made"], 1)

                pool.sem_inc(s["free"], 2)
                pool.sem_inc(s["rest_made"], 2)
                staggered(pool, (add, 0), (freed, 0), (leave, 2))

            @block.vector
            def _(dve):
                v = nc.vector
                for norm in norms:
                    norm.prepare(dve)
                dve.wait_ge(s["w_made"], 1)
                v.tensor_tensor(b1[:, :], b1[:, :], o_ps[0][:, 0, 0:NB], ALU.add).then_inc(s["w_step"], 1)
                v.tensor_scalar(w1[:, :], w1[:, :], g2[:, 0:1], None, ALU.mult).then_inc(s["w_step"], 1)
                dve.wait_ge(s["w_step"], 2)
                dve.sem_inc(s["msum_free"], 2)
                dve.sem_inc(s["x2_made"], 2)
                dve.sem_inc(s["rest_used"], 2)
                dve.sem_inc(s["out_free"], 1)

                def first(n, i, u, p):
                    dve.wait_ge(s["added"], n + 1)
                    norms[0].statistics(dve, n, u, p, xin[:, u, :, :])

                def second(n, i, u, p):
                    dve.wait_ge(s["rest_made"], n + 1)
                    norms[0].normalise(dve, n, u, p, x2[:, u, :, :], xin[:, u, :, :]).then_inc(s["x2_made"], 1)
                    dve.wait_ge(s["x2_made"], n + 3)
                    dve.wait_ge(s[f"msum_ready{u}"], i * 16 + 16)
                    v.tensor_tensor(xm[0:p, u, :, :], x2[0:p, u, :, :], msum[0:p, u, :, :],
                                    ALU.add).then_inc(s["xm_made"], 1)
                    dve.wait_ge(s["xm_made"], n + 1)
                    dve.sem_inc(s["msum_free"], 1)
                    norms[1].statistics(dve, n, u, p, xm[:, u, :, :])

                def third(n, i, u, p):
                    dve.wait_ge(s["turned"], n + 1)
                    norms[1].normalise(dve, n, u, p, xn[:, u, :, :], xm[:, u, :, :]).then_inc(s["normed"], 1)

                def fourth(n, i, u, p):
                    dve.wait_ge(s["rest_made"], n + 3)
                    dve.wait_ge(s["x3_made"], n + 1)
                    for b in range(2):
                        dve.wait_ge(s["out_made"], n * 2 + b + 3)
                        ins = v.tensor_tensor(x3in[0:p, u, 4 * b:4 * b + 4, :], rest[0:p, u, 4 * b:4 * b + 4, :],
                                              o_ps[b][0:p, :, :], ALU.add)
                    ins.then_inc(s["x3_added"], 1)
                    dve.wait_ge(s["x3_added"], n + 1)
                    dve.sem_inc(s["out_free"], 1)
                    norms[2].statistics(dve, n, u, p, x3in[:, u, :, :])
                    dve.sem_inc(s["rest_used"], 1)

                staggered(dve, (third, 2), (lambda n, i, u, p: norms[2].negate(dve, n, u, p), 4), (fourth, 3),
                          (second, 1), (first, 0))

            @block.scalar
            def _(act):
                act.wait_ge(s["w_step"], 2)
                act.sem_inc(s["x_copied"], 1)
                act.sem_inc(s["bent"], NB)
                act.sem_inc(s["x3_made"], 2)

                def front(n, i, u, p):
                    act.wait_ge(s["turned"], n + 3)
                    for b in range(2):
                        ins = nc.scalar.activation(x_t[:, u, 4 * b:4 * b + 4, 0:p], x_ps[b][:, :, 0:p], ACT.Copy)
                    ins.then_inc(s["x_copied"], 1)

                def back(n, i, u, p):
                    for h in range(2):
                        act.wait_ge(s["out_made"], n * 2 + h + 1)
                        for b in range(NB):
                            act.wait_ge(s["hidden_made"], n * (2 * NB) + h * NB + b + 1)
                            nc.scalar.activation(hidden[:, h, b, :], h_ps[b][:, :], ACT.Relu,
                                                 bias=b1[:, b:b + 1]).then_inc(s["bent"], 1)

                def finish(n, i, u, p):
                    act.wait_ge(s[f"stored{u}"], i * 16 + 16)
                    norms[2].normalise_on_act(act, n, u, p, x3[:, u, :, :], x3in[:, u, :, :]).then_inc(s["x3_made"], 1)

                staggered(act, (front, 2), (back, 2), (finish, 4),
                          (lambda n, i, u, p: norms[2].square_root(act, n, u, p), 3),
                          (lambda n, i, u, p: norms[1].square_root(act, n, u, p), 1),
                          (lambda n, i, u, p: norms[0].square_root(act, n, u, p), 0))

            @block.tensor
            def _(pe):
                for b in range(NB):
                    mm = nc.tensor.matmul(o_ps[0][:, 0, b:b + 1], w1[:, b * P:(b + 1) * P], be2[:, 0:1], start=True,
                                          stop=True)
                mm.then_inc(s["w_made"], 1)
                pe.wait_ge(s["w_step"], 2)
                pe.sem_inc(s["out_made"], 2)
                pe.sem_inc(s["turned"], 2)

                def turn(n, i, u, p):
                    pe.wait_ge(s["normed"], n + 1)
                    pe.wait_ge(s["x_copied"], n + 1)
                    for j in range(NJ):
                        mm = nc.tensor.transpose(x_ps[j // 4][:, j % 4, 0:p], xn[0:p, u, j, :], k.ident[0:p, 0:p])
                    mm.then_inc(s["turned"], 1)

                def feed_forward(n, i, u, p):
                    pe.wait_ge(s["x_copied"], n + 2)
                    for h in range(2):
                        for b in range(NB):
                            pe.wait_ge(s["bent"], n * (2 * NB) + h * NB + b + 1)
                            nc.tensor.matmul(h_ps[b][:, :], w1[:, b * P:(b + 1) * P],
                                             x_t[:, u, 4 * h:4 * h + 4, :].rearrange("p j e -> p (j e)"), start=True,
                                             stop=True).then_inc(s["hidden_made"], 1)
                    pe.wait_ge(s["out_free"], n + 1)
                    for h in range(2):
                        pe.wait_ge(s["bent"], n * (2 * NB) + (h + 2) * NB)
                        for j in range(4):
                            for b in range(NB):
                                mm = nc.tensor.matmul(o_ps[h][0:p, j, :], hidden[:, h, b, j * P:j * P + p], w2[:, b, :],
                                                      start=b == 0, stop=b == NB - 1)
                        mm.then_inc(s["out_made"], 1)

                staggered(pe, (turn, 2), (feed_forward, 2))
        clear_semaphores(nc, [x for norm in norms for x in norm.sems] + list(s.values()))


def mean_layer_phase(k, out):
    nc = k.nc
    a = k.a
    with ExitStack() as st:
        def sb(name, shape):
            return k.sb(st, "ml_" + name, shape)

        w, w_t = sb("w", [P, D]), sb("w_t", [P, D])
        bias = sb("bias", [3, D])
        gamma, beta = sb("gamma", [P, D]), sb("beta", [P, D])
        mix = sb("mix", [P, 4])
        x3, agg, y, z, shifted, scaled, total, res = (sb(x, [P, 2, NJ, D]) for x in
                                               ("x3", "agg", "y", "z", "shifted", "scaled", "total", "res"))
        norms = [Norm(k, st, f"ml_norm{m}") for m in range(2)]
        w_ps = k.ps(st, "ml_w_ps", [P, 512])
        names = ["ready0", "ready1", "free", "summed", "y_made", "shifted", "z_made", "normed", "gained",
                 "added", "res_made", "stored0", "stored1", "w_turned", "w_step", "w_exp"]
        s = {x: k.sem(st, "ml_" + x) for x in names}
        load_constants(k, [(w[:, :], a["L3_gnn_W"]), (bias[:, :], a["L3_gnn_b"].partition_broadcast(3)),
                           (gamma[:, :], a["L3_gnn_gamma"].partition_broadcast(P)),
                           (beta[:, :], a["L3_gnn_beta"].partition_broadcast(P)),
                           (mix[:, 0:1], a["L3_gnn_alpha"].partition_broadcast(P))])
        with nc.Block() as block:
            @block.vector
            def _(dve):
                v = nc.vector
                c = Chain(dve, s["w_step"], 5)
                c.begin(0)
                dve.wait_ge(s["w_exp"], 1)
                c.link(v.tensor_scalar(mix[:, 1:2], mix[:, 1:2], 1.0, None, ALU.add))
                c.link(v.reciprocal(mix[:, 2:3], mix[:, 1:2]))
                c.link(v.tensor_scalar(mix[:, 3:4], mix[:, 2:3], -1.0, 1.0, ALU.mult, ALU.add))
                c.link(v.tensor_scalar(bias[:, :], bias[:, :], mix[0:3, 2:3], None, ALU.mult))
                dve.wait_ge(s["w_turned"], 1)
                c.link(v.tensor_scalar(w_t[:, :], w_ps[:, 0:D], mix[:, 2:3], None, ALU.mult))
                c.end()

            @block.scalar
            def _(act):
                nc.scalar.activation(mix[:, 1:2], mix[:, 0:1], ACT.Exp, scale=-1.0).then_inc(s["w_exp"], 1)

            @block.tensor
            def _(pe):
                nc.tensor.transpose(w_ps[:, 0:D], w[:, :], k.ident[:, :]).then_inc(s["w_turned"], 1)
        conv = Linear(k, st, "ml_conv", w_t[:, :], split_biases(k, st, "ml_bias", [bias[:, :]])[0])
        with nc.Block() as block:
            @block.sync
            def _(sp):
                def load(n, i, u, p):
                    sp.wait_ge(s["free"], n + 1)
                    sp.wait_ge(s["shifted"], n + 1)
                    sp.dma_start(x3[0:p, u, :, :], node_rows(k.x3, n, p)).then_inc(s[f"ready{u}"], 16)
                    sp.dma_start(agg[0:p, u, :, :], node_rows(k.agg, n, p)).then_inc(s[f"ready{u}"], 16)

                def store(n, i, u, p):
                    sp.wait_ge(s["res_made"], n + 3)
                    sp.dma_start(node_rows(out, n, p), res[0:p, u, :, :]).then_inc(s[f"stored{u}"], 16)

                sp.sem_inc(s["stored0"], 16)
                sp.sem_inc(s["stored1"], 16)
                staggered(sp, (load, 0), (store, 4))
                sp.wait_ge(s["stored0"], 16 * (NG // 2 + 2))
                sp.wait_ge(s["stored1"], 16 * (NG // 2 + 1))

            @block.gpsimd
            def _(pool):
                def add(n, i, u, p):
                    paced(pool, k, s[f"ready{u}"], i * 32 + 32)
                    nc.gpsimd.tensor_tensor(agg[0:p, u, :, :], agg[0:p, u, :, :], x3[0:p, u, :, :],
                                            ALU.add).then_inc(s["summed"], 1)

                def shift(n, i, u, p):
                    paced(pool, k, s["added"], n + 1)
                    nc.gpsimd.tensor_tensor(shifted[0:p, u, :, :], x3[0:p, u, :, :],
                                            beta[0:p, :].unsqueeze(1).broadcast_to([p, NJ, D]),
                                            ALU.add).then_inc(s["shifted"], 1)

                def gain(n, i, u, p):
                    paced(pool, k, s["normed"], n + 3)
                    nc.gpsimd.tensor_tensor(scaled[0:p, u, :, :], scaled[0:p, u, :, :],
                                            gamma[0:p, :].unsqueeze(1).broadcast_to([p, NJ, D]),
                                            ALU.mult).then_inc(s["gained"], 1)

                pool.sem_inc(s["shifted"], 2)
                staggered(pool, (gain, 3), (shift, 2), (add, 0))

            @block.vector
            def _(dve):
                v = nc.vector
                for norm in norms:
                    norm.prepare(dve)
                dve.sem_inc(s["free"], 2)
                dve.sem_inc(s["added"], 2)
                dve.sem_inc(s["normed"], 2)
                dve.sem_inc(conv.free, 1)

                def front(n, i, u, p):
                    dve.wait_ge(s["summed"], n + 1)
                    c = k.dinv2[0:p, n * NJ:n * NJ + NJ] if isinstance(n, int) else k.dinv2[0:p, bass.ds(n * NJ, NJ)]
                    v.tensor_tensor(y[0:p, u, :, :], agg[0:p, u, :, :], c.unsqueeze(2).broadcast_to([p, NJ, D]),
                                    ALU.mult).then_inc(s["y_made"], 1)

                def back(n, i, u, p):
                    dve.wait_ge(s["normed"], n + 1)
                    dve.wait_ge(conv.made, n + 2)
                    dve.wait_ge(s[f"ready{u}"], i * 32 + 32)
                    for b in range(2):
                        ins = v.scalar_tensor_tensor(z[0:p, u, 4 * b:4 * b + 4, :], x3[0:p, u, 4 * b:4 * b + 4, :],
                                                     mix[0:p, 3:4], conv.out[b][0:p, :, :], ALU.mult, ALU.add)
                    ins.then_inc(s["z_made"], 1)
                    dve.wait_ge(s["z_made"], n + 1)
                    dve.sem_inc(s["free"], 1)
                    dve.sem_inc(conv.free, 1)
                    norms[0].statistics(dve, n, u, p, z[:, u, :, :])

                def middle(n, i, u, p):
                    norms[0].normalise(dve, n, u, p, scaled[:, u, :, :], z[:, u, :, :]).then_inc(s["normed"], 1)

                def last(n, i, u, p):
                    dve.wait_ge(s["shifted"], n + 3)
                    dve.wait_ge(s["gained"], n + 1)
                    dve.wait_ge(s["res_made"], n + 1)
                    v.tensor_tensor(total[0:p, u, :, :], scaled[0:p, u, :, :], shifted[0:p, u, :, :],
                                    ALU.add).then_inc(s["added"], 1)
                    dve.wait_ge(s["added"], n + 3)
                    norms[1].statistics(dve, n, u, p, total[:, u, :, :])

                staggered(dve, (front, 0), (back, 1), (last, 2), (lambda n, i, u, p: norms[1].negate(dve, n, u, p), 3),
                          (middle, 1))

            @block.scalar
            def _(act):
                act.sem_inc(conv.copied, 1)
                act.sem_inc(s["res_made"], 2)

                def finish(n, i, u, p):
                    act.wait_ge(s[f"stored{u}"], i * 16 + 16)
                    norms[1].normalise_on_act(act, n, u, p, res[:, u, :, :], total[:, u, :, :]).then_inc(s["res_made"], 1)

                staggered(act, (lambda n, i, u, p: norms[1].square_root(act, n, u, p), 3),
                          (lambda n, i, u, p: conv.copy(act, n, p), 0),
                          (lambda n, i, u, p: norms[0].square_root(act, n, u, p), 1), (finish, 3))

            @block.tensor
            def _(pe):
                pe.sem_inc(conv.made, 1)

                def turn(n, i, u, p):
                    pe.wait_ge(s["y_made"], n + 1)
                    conv.turn(pe, n, p, y[:, u, :, :])

                staggered(pe, (turn, 0), (lambda n, i, u, p: conv.product(pe, n, p), 0))
        clear_semaphores(nc, [x for norm in norms for x in norm.sems] + conv.sems + list(s.values()))


ROUTING_STEPS = 4


def build(nc, a, out):
    k = Ctx(nc)
    k.a = a
    k.x, k.src, k.dst = a["x"], a["src"], a["dst"]
    with ExitStack() as st:
        k.paces = k.sem(st, "paces")
        k.gather_base, k.scatter_base = [0, 0], [0, 0]
        k.gathered = [k.sem(st, f"gathered{u}") for u in range(2)]
        k.scattered = [k.sem(st, f"scattered{u}") for u in range(2)]
        k.src_row = nc.dram_tensor("src_row", (EP + 1,), F32, kind="Internal").ap()
        k.dst_row = nc.dram_tensor("dst_row", (EP + 1,), F32, kind="Internal").ap()
        k.low_row = nc.dram_tensor("low_row", (EP,), F32, kind="Internal").ap()
        k.sorted4 = nc.dram_tensor("sorted4", (EP, 4), I32, kind="Internal").ap()
        k.sorted_row = nc.dram_tensor("sorted_row", (EP + 1,), F32, kind="Internal").ap()
        k.agg = nc.dram_tensor("agg", (N, D), F32, kind="Internal").ap()
        k.layer1 = nc.dram_tensor("layer1", (N, 2 * D), F32, kind="Internal").ap()
        k.layer1_halves = k.layer1.rearrange("n (c d) -> (n c) d", c=2)
        k.pairs = nc.dram_tensor("pairs", (EP, 2 * D), F32, kind="Internal").ap()
        k.end_sums = nc.dram_tensor("end_sums", (2, T, D), F32, kind="Internal").ap()
        k.handed_sums = nc.dram_tensor("handed_sums", (2, T, D), F32, kind="Internal").ap()
        k.values = nc.dram_tensor("values", (EP, D + NH), F32, kind="Internal").ap()
        k.msum = nc.dram_tensor("msum", (N, D), F32, kind="Internal").ap()
        k.x3 = nc.dram_tensor("x3", (N, D), F32, kind="Internal").ap()
        k.qkv_w = k.sb(st, "qkv_w", [P, 3, D])
        k.wc = k.sb(st, "wc", [P, NH])
        k.wo = k.sb(st, "wo", [P, D])
        k.gcn_w = k.sb(st, "gcn_w", [P, D])
        k.gcn_c = k.sb(st, "gcn_c", [P, D])
        k.ones = k.sb(st, "ones", [P, P])
        k.ones3 = k.sb(st, "ones3", [3, P], BF16)
        k.zeros = k.sb(st, "zeros", [P, NJ * D])
        k.eps = k.sb(st, "eps", [P, 1])
        k.iota_row = k.sb(st, "iota_row", [P, P])
        k.iota_high = k.sb(st, "iota_high", [P, NCOL])
        k.iota_row16 = k.sb(st, "iota_row16", [P, P], FP16)
        k.iota_high16 = k.sb(st, "iota_high16", [P, NCOL], FP16)
        k.iota_part = k.sb(st, "iota_part", [P, 1])
        k.ident = k.sb(st, "ident", [P, P])
        k.before = k.sb(st, "before", [P, P])
        k.earlier = k.sb(st, "earlier", [P, P])
        k.last_part = k.sb(st, "last_part", [P, 1])
        k.id_col = k.sb(st, "id_col", [P, 1, 2, T])
        k.node_idx = k.sb(st, "node_idx", [P, 2, T], I32)
        k.low_col = k.sb(st, "low_col", [P, 2, T])
        k.high_col = k.sb(st, "high_col", [P, 2, T])
        k.degree = k.sb(st, "degree", [P, NCOL])
        k.dinv = k.sb(st, "dinv", [P, NCOL])
        k.dinv2 = k.sb(st, "dinv2", [P, NCOL])
        k.start = k.sb(st, "start", [P, NCOL])
        k.dinv_src = k.sb(st, "dinv_src", [P, T])
        by_dst = Order(k.dst_row, k.id_col[:, 0, 1, :], k.sb(st, "d_prev", [P, T]), k.sb(st, "d_last", [P, T], I32))
        by_src = Order(k.sorted_row, k.sb(st, "s_id", [P, T]), k.sb(st, "s_prev", [P, T]),
                       k.sb(st, "s_last", [P, T], I32), k.sorted4, k.sb(st, "s_eid", [P, T], I32),
                       k.sb(st, "s_own", [P, T], I32), k.sb(st, "s_far", [P, T], I32),
                       k.sb(st, "s_last_cap", [P, T], I32))
        constants_phase(k)
        ids_phase(k)
        with ExitStack() as filling:
            bo_rows = k.sb(filling, "bo_rows", [P, NJ, D])
            load_constants(k, [(bo_rows[:, j, :], a["L2_gnn_bo"].partition_broadcast(P)) for j in range(NJ)])
            count_phase(k, [(k.agg, k.zeros[:, :].rearrange("p (j d) -> p j d", j=NJ)), (k.msum, bo_rows)])
        rank_phase(k)
        order_phase(k, by_dst, "ord_d")
        order_phase(k, by_src, "ord_s")

        def by_degree(dve, out, rows, g):
            w = k.dinv_src[:, bass.ds(g * GT, GT)].unsqueeze(2).broadcast_to([P, GT, D])
            return nc.vector.tensor_tensor(out, rows, w, ALU.mult)

        segment_sum_phase(k, by_dst, k.x, D, k.node_idx[:, 0, :], k.agg, "gcn", by_degree)
        moments_phase(k)
        capsules_phase(k)
        with ExitStack() as routing:
            k.vals = k.sb(routing, "vals", [P, T, D])
            k.end_mask = k.sb(routing, "end_mask", [P, T, 2])
            k.ends2 = k.sb(routing, "ends2", [2, T])
            k.handed = k.sb(routing, "handed", [TB, 2, 2, T])
            routing_setup_phase(k, by_src)
            for step in range(ROUTING_STEPS + 1):
                if step:
                    exchange_phase(k, f"ex{step}")
                routing_phase(k, by_src, step, ROUTING_STEPS, f"ro{step}")
        k.scores = k.sb(st, "scores", [P, T, NH])
        attention_weights_phase(k, st)
        scores_phase(k, by_dst)
        softmax_phase(k, by_dst)

        def by_head(dve, out, rows, g):
            return nc.vector.tensor_tensor(
                out.rearrange("p t (h d) -> p t h d", h=NH), rows[:, :, 0:D].rearrange("p t (h d) -> p t h d", h=NH),
                rows[:, :, D:D + NH].unsqueeze(3).broadcast_to([P, GT, NH, HD]), ALU.mult)

        segment_sum_phase(k, by_src, k.values, D + NH, by_src.eid, k.msum, "msg", by_head, k.wo[:, :],
                          k.bo_parts)
        transformer_phase(k)
        segment_sum_phase(k, by_dst, k.x3, D, k.node_idx[:, 0, :], k.agg, "mean", None)
        mean_layer_phase(k, out)


INPUTS = (["x", "src", "dst", "edge_attr_128"] + ["L0_gnn_" + x for x in "W b gamma beta".split()]
          + ["L1_gnn_weight", "L1_gnn_bias"]
          + ["L2_gnn_" + x for x in "Wq bq Wk bk Wv bv Wo bo Wc bc W1 b1 W2 b2 g1 be1 g2 be2".split()]
          + ["L3_gnn_" + x for x in "W b alpha gamma beta".split()])


def kernel(**inputs):
    import numpy as _np
    import concourse.bacc as _bacc
    from concourse import mybir as _mybir
    from concourse.bass_utils import run_bass_kernel_spmd as _run

    nc = _bacc.Bacc("TRN2", target_bir_lowering=False, num_devices=1)
    arrays, aps = {}, {}
    for name in INPUTS:
        v = _np.ascontiguousarray(inputs[name])
        arrays[f"in_{name}_dram"] = v
        aps[name] = nc.dram_tensor(f"in_{name}_dram", v.shape, _mybir.dt.from_np(v.dtype), kind="ExternalInput").ap()
    out = nc.dram_tensor("out_0_dram", (N, D), _mybir.dt.float32, kind="ExternalOutput").ap()
    build(nc, aps, out)
    r = _run(nc, [arrays], core_ids=[0])
    return r.results[0]["out_0_dram"]
```
